# Optimizing a Trainium2 kernel written in Bass

```python
import numpy as np
import jax
import jax.numpy as jnp

def _softmax(x, axis=-1):
    return jax.nn.softmax(x, axis=axis)

def _gelu(x):
    return jax.nn.gelu(x, approximate=True)

def _silu(x):
    return jax.nn.silu(x)

def _sigmoid(x):
    return jax.nn.sigmoid(x)

def _layernorm(x, axis=-1, eps=1e-05):
    m = jnp.mean(x, axis=axis, keepdims=True)
    v = jnp.var(x, axis=axis, keepdims=True)
    return (x - m) / jnp.sqrt(v + eps)

def _scatter_add(tgt, idx, src, axis=0):
    return tgt.at[idx].add(src)

def _segment_sum(src, seg, n):
    return jax.ops.segment_sum(src, seg, n)
kernel_name = 'mk_decoder_preln_d4_seqx_r8_ab12ec'

def setup_inputs(seed: int=0):
    np.random.seed(seed)
    _w = jnp.asarray

    def _rec_inputs():
        import jax
        import jax.numpy as jnp
        _rk = jax.random.key(seed)
        x = -0.000125 + 0.9999 * jax.random.normal(jax.random.fold_in(_rk, 1), (8, 128, 256), jnp.float32)
        _lenS = 128 - jax.random.randint(jax.random.fold_in(_rk, 7), (8,), 0, max(1, 128 // 4) + 1, jnp.int32)
        _lenS2 = 128 - jax.random.randint(jax.random.fold_in(_rk, 8), (8,), 0, max(1, 128 // 4) + 1, jnp.int32)
        _ctx_2048P = jax.random.normal(jax.random.fold_in(_rk, 11), (8, 16, 256), jnp.float32)
        _ctx_2048c = jax.random.dirichlet(jax.random.fold_in(_rk, 511), 0.3 * jnp.ones((16,), jnp.float32), (8, 128))
        _ctx_2048t = jnp.einsum('bsk,bkd->bsd', _ctx_2048c, _ctx_2048P)
        _ctx_2048t = _ctx_2048t * jax.lax.rsqrt(jnp.mean(jnp.square(_ctx_2048t)) + 1e-12) * 0.953939
        ctx_2048 = -1.52775e-05 + 0.999936 * (_ctx_2048t + 0.3 * jax.random.normal(jax.random.fold_in(_rk, 611), (8, 128, 256), jnp.float32))
        return (x, ctx_2048)
    x, ctx_2048 = _rec_inputs()

    def _L0_attn_setup():
        import jax, jax.numpy as jnp
        import numpy as np
        D_MODEL = 256
        D_INNER = 256
        D_XB = 64
        D_STATE = 32
        DT_RANK = 128
        D_FF = 704
        BATCH = 2
        SEQ = 128
        EPS = 1e-05

        def _rmsnorm(x, w):
            var = jnp.mean(jnp.square(x), axis=-1, keepdims=True)
            return x * jax.lax.rsqrt(var + EPS) * w

        def _selective_scan(x, dt, A, B, C):
            b, l, g, p = x.shape
            n = A.shape[-1]

            def step(h, inp):
                x_t, dt_t, B_t, C_t = inp
                dA = jnp.exp(dt_t[..., None] * A)
                h = dA * h + (dt_t * x_t)[..., None] * B_t[:, :, None, :]
                y = jnp.einsum('bgpn,bgn->bgp', h, C_t)
                return (h, y)
            h0 = jnp.zeros((b, g, p, n), x.dtype)
            xs = tuple((jnp.moveaxis(a, 1, 0) for a in (x, dt, B, C)))
            _, ys = jax.lax.scan(step, h0, xs)
            return jnp.moveaxis(ys, 0, 1)

        def _mamba(u, in_proj_w, dt_proj_w, dt_proj_b, A_log, D_param, out_proj_w):
            b, l, _ = u.shape
            zxbcdt = u @ in_proj_w.T
            splits = np.cumsum([D_INNER, D_XB, D_XB, D_INNER]).tolist()
            z, x, Bc, Cc, dt_raw = jnp.split(zxbcdt, splits, axis=-1)
            dt = jax.nn.softplus(dt_raw @ dt_proj_w.T + dt_proj_b)
            g = D_INNER // D_STATE
            g_kv = D_XB // D_STATE
            rep = g // g_kv
            x = jnp.repeat(x.reshape(b, l, g_kv, D_STATE), rep, axis=2)
            Bm = jnp.repeat(Bc.reshape(b, l, g_kv, D_STATE), rep, axis=2)
            Cm = Cc.reshape(b, l, g, D_STATE)
            A = -jnp.exp(A_log).reshape(g, D_STATE, D_STATE)
            dt = dt.reshape(b, l, g, D_STATE)
            y = _selective_scan(x, dt, A, Bm, Cm).reshape(b, l, D_INNER)
            y = y + x.reshape(b, l, D_INNER) * D_param
            y = y * jax.nn.silu(z)
            return y @ out_proj_w.T

        def _forward(hidden_states, in_proj_w, dt_proj_w, dt_proj_b, A_log, D_param, out_proj_w, gate_w, up_w, down_w, norm1_w, norm2_w):
            h = hidden_states + _mamba(_rmsnorm(hidden_states, norm1_w), in_proj_w, dt_proj_w, dt_proj_b, A_log, D_param, out_proj_w)
            xn = _rmsnorm(h, norm2_w)
            mlp = jax.nn.silu(xn @ gate_w.T) * (xn @ up_w.T) @ down_w.T
            return h + mlp
        key = jax.random.key(seed)
        ks = jax.random.split(key, 8)
        s = lambda k, shape, scale=0.02: jax.random.normal(k, shape, jnp.float32) * scale
        proj_dim = 2 * D_INNER + 2 * D_XB + DT_RANK
        return {'hidden_states': jax.random.normal(ks[0], (BATCH, SEQ, D_MODEL), jnp.float32), 'in_proj_w': s(ks[1], (proj_dim, D_MODEL)), 'dt_proj_w': s(ks[2], (D_INNER, DT_RANK)), 'dt_proj_b': jnp.full((D_INNER,), -4.6, jnp.float32), 'A_log': jnp.log(jnp.tile(jnp.arange(1, D_STATE + 1, dtype=jnp.float32), (D_INNER, 1))), 'D_param': jnp.ones((D_INNER,), jnp.float32), 'out_proj_w': s(ks[3], (D_MODEL, D_INNER)), 'gate_w': s(ks[4], (D_FF, D_MODEL)), 'up_w': s(ks[5], (D_FF, D_MODEL)), 'down_w': s(ks[6], (D_MODEL, D_FF)), 'norm1_w': jnp.ones((D_MODEL,), jnp.float32), 'norm2_w': jnp.ones((D_MODEL,), jnp.float32)}
    _L0_attn_all = _L0_attn_setup()
    _L0_attn_in = {k: v for k, v in _L0_attn_all.items() if k in ('in_proj_w', 'dt_proj_w', 'dt_proj_b', 'A_log', 'D_param', 'out_proj_w', 'gate_w', 'up_w', 'down_w', 'norm1_w', 'norm2_w')}
    del _L0_attn_all

    def _L0_xattn_setup():
        import jax, jax.numpy as jnp
        import numpy as np
        B, DIM1, DIM2, LATENT, T = (16, 128, 128, 64, 256)
        LN_EPS = 1e-05
        key = jax.random.key(seed)
        ks = jax.random.split(key, 8)

        def xavier(k, shape):
            fan_out, fan_in = shape
            std = float(np.sqrt(2.0 / (fan_in + fan_out)))
            return jax.random.normal(k, shape, dtype=jnp.float32) * std
        return {'input1': jax.random.normal(ks[0], (B, DIM1, T), dtype=jnp.float32), 'input2': jax.random.normal(ks[1], (B, DIM2, T), dtype=jnp.float32), 'theta_w': xavier(ks[2], (LATENT, DIM2)), 'theta_b': jnp.zeros((LATENT,), jnp.float32), 'phi_w': xavier(ks[3], (LATENT, DIM1)), 'phi_b': jnp.zeros((LATENT,), jnp.float32), 'g_w': xavier(ks[4], (LATENT, DIM1)), 'g_b': jnp.zeros((LATENT,), jnp.float32), 'ln_gamma': jnp.ones((LATENT, T), jnp.float32), 'ln_beta': jnp.zeros((LATENT, T), jnp.float32), 'out_w': xavier(ks[5], (DIM2, LATENT)), 'out_b': jnp.zeros((DIM2,), jnp.float32)}
    _L0_xattn_all = _L0_xattn_setup()
    _L0_xattn_in = {k: v for k, v in _L0_xattn_all.items() if k in ('theta_w', 'theta_b', 'phi_w', 'phi_b', 'g_w', 'g_b', 'ln_gamma', 'ln_beta', 'out_w', 'out_b')}
    del _L0_xattn_all

    def _L0_ffn_setup():
        import jax, jax.numpy as jnp
        import numpy as np
        N, S, D = (8, 256, 256)
        O = 256
        E = 8
        K = 2
        key = jax.random.key(seed)
        ks = jax.random.split(key, 5)
        scale_in = 1.0 / np.sqrt(D)
        x = jax.random.normal(ks[0], (N, S, D), dtype=jnp.float32)
        gate_w = jax.random.uniform(ks[1], (D, E), dtype=jnp.float32, minval=-scale_in, maxval=scale_in)
        gate_b = jax.random.uniform(ks[2], (E,), dtype=jnp.float32, minval=-scale_in, maxval=scale_in)
        expert_w = jax.random.uniform(ks[3], (E, D, O), dtype=jnp.float32, minval=-scale_in, maxval=scale_in)
        expert_b = jax.random.uniform(ks[4], (E, O), dtype=jnp.float32, minval=-scale_in, maxval=scale_in)
        return {'x': x, 'gate_w': gate_w, 'gate_b': gate_b, 'expert_w': expert_w, 'expert_b': expert_b}
    _L0_ffn_all = _L0_ffn_setup()
    _L0_ffn_in = {k: v for k, v in _L0_ffn_all.items() if k in ('gate_w', 'gate_b', 'expert_w', 'expert_b')}
    del _L0_ffn_all

    def _L1_attn_setup():
        import jax, jax.numpy as jnp
        import numpy as np
        D = 256
        key = jax.random.key(seed)
        ks = jax.random.split(key, 5)
        scale = 1.0 / np.sqrt(D)
        x = jax.random.normal(ks[0], (4, 512, D), dtype=jnp.float32)
        Wq = jax.random.normal(ks[1], (D, D), dtype=jnp.float32) * scale
        Wk = jax.random.normal(ks[2], (D, D), dtype=jnp.float32) * scale
        Wv = jax.random.normal(ks[3], (D, D), dtype=jnp.float32) * scale
        Wo = jax.random.normal(ks[4], (D, D), dtype=jnp.float32) * scale
        return {'x': x, 'Wq': Wq, 'Wk': Wk, 'Wv': Wv, 'Wo': Wo}
    _L1_attn_all = _L1_attn_setup()
    _L1_attn_in = {k: v for k, v in _L1_attn_all.items() if k in ('Wq', 'Wk', 'Wv', 'Wo')}
    del _L1_attn_all

    def _L1_xattn_setup():
        import jax, jax.numpy as jnp
        import numpy as np
        from jax import lax
        LN_EPS = 1e-05
        key = jax.random.key(seed)
        ks = jax.random.split(key, 8)
        B, S, T, D = (4, 128, 256, 256)
        scale = 0.02
        return {'Z': jax.random.normal(ks[0], (B, S, D), dtype=jnp.float32), 'kv': jax.random.normal(ks[1], (B, T, D), dtype=jnp.float32), 'decay': jnp.float32(0.9), 'W_in': jax.random.normal(ks[2], (D, D), dtype=jnp.float32) * scale, 'b_in': jnp.zeros((D,), dtype=jnp.float32), 'W_out': jax.random.normal(ks[3], (D, D), dtype=jnp.float32) * scale, 'b_out': jnp.zeros((D,), dtype=jnp.float32), 'gamma': jnp.ones((D,), dtype=jnp.float32), 'beta': jnp.zeros((D,), dtype=jnp.float32)}
    _L1_xattn_all = _L1_xattn_setup()
    _L1_xattn_in = {k: v for k, v in _L1_xattn_all.items() if k in ('decay', 'W_in', 'b_in', 'W_out', 'b_out', 'gamma', 'beta')}
    del _L1_xattn_all

    def _L1_ffn_setup():
        import jax, jax.numpy as jnp
        import numpy as np
        NUM_ROUTED = 7
        TOP_K = 3
        D = 256
        H = 256
        B, S = (4, 256)

        def _expert_ffn(x, w1, wg, w2):
            return jax.nn.silu(x @ w1) * (x @ wg) @ w2
        key = jax.random.key(seed)
        ks = jax.random.split(key, 8)
        s = 0.02
        return {'x': jax.random.normal(ks[0], (B, S, D), jnp.float32), 'W1': jax.random.normal(ks[1], (NUM_ROUTED, D, H), jnp.float32) * s, 'Wg': jax.random.normal(ks[2], (NUM_ROUTED, D, H), jnp.float32) * s, 'W2': jax.random.normal(ks[3], (NUM_ROUTED, H, D), jnp.float32) * s, 'Ws1': jax.random.normal(ks[4], (D, H), jnp.float32) * s, 'Wsg': jax.random.normal(ks[5], (D, H), jnp.float32) * s, 'Ws2': jax.random.normal(ks[6], (H, D), jnp.float32) * s, 'gate_w': jax.random.normal(ks[7], (D, NUM_ROUTED), jnp.float32) * s, 'gate_b': jnp.zeros((NUM_ROUTED,), jnp.float32), 'biases': jnp.zeros((NUM_ROUTED,), jnp.float32)}
    _L1_ffn_all = _L1_ffn_setup()
    _L1_ffn_in = {k: v for k, v in _L1_ffn_all.items() if k in ('W1', 'Wg', 'W2', 'Ws1', 'Wsg', 'Ws2', 'gate_w', 'gate_b', 'biases')}
    del _L1_ffn_all

    def _L2_attn_setup():
        import jax, jax.numpy as jnp
        import numpy as np
        import math
        N_EMBD = 256
        N_HEADS = 16
        HEAD_DIM = N_EMBD // N_HEADS
        CTX = 256

        def alibi_bias(seq_len: int, n_heads: int) -> jnp.ndarray:
            i = jnp.arange(seq_len)[:, None]
            j = jnp.arange(seq_len)[None, :]
            pos = jnp.where(j <= i, (j - i).astype(jnp.float32), 0.0)
            slopes = 2.0 ** (-8.0 / jnp.arange(1, n_heads + 1, dtype=jnp.float32))
            return slopes[:, None, None] * pos[None, :, :]

        def causal_mask(seq_len: int) -> jnp.ndarray:
            i = jnp.arange(seq_len)[:, None]
            j = jnp.arange(seq_len)[None, :]
            return jnp.where(j > i, -jnp.inf, 0.0).astype(jnp.float32)
        key = jax.random.key(seed)
        k_x, k_qkv, k_o = jax.random.split(key, 3)
        scale = 1.0 / math.sqrt(N_EMBD)
        x = jax.random.normal(k_x, (2, CTX, N_EMBD), dtype=jnp.float32)
        W_qkv = jax.random.normal(k_qkv, (N_EMBD, 3 * N_EMBD), dtype=jnp.float32) * scale
        W_o = jax.random.normal(k_o, (N_EMBD, N_EMBD), dtype=jnp.float32) * scale
        return {'x': x, 'W_qkv': W_qkv, 'W_o': W_o}
    _L2_attn_all = _L2_attn_setup()
    _L2_attn_in = {k: v for k, v in _L2_attn_all.items() if k in ('W_qkv', 'W_o')}
    del _L2_attn_all

    def _L2_xattn_setup():
        import jax, jax.numpy as jnp
        import numpy as np
        FP8_MAX = 448.0
        EPS = 1e-05

        def _fp8_roundtrip(x):
            return x.astype(jnp.float8_e4m3fn).astype(jnp.float32)

        def _div_clamp_fp8(x, scale):
            y = jnp.clip(x.astype(jnp.float32) / scale, -FP8_MAX, FP8_MAX)
            y = y.astype(jnp.bfloat16).astype(jnp.float32)
            return _fp8_roundtrip(y)

        def _ln(x, w, b):
            mu = jnp.mean(x, axis=-1, keepdims=True)
            var = jnp.mean(jnp.square(x - mu), axis=-1, keepdims=True)
            return (x - mu) * jax.lax.rsqrt(var + EPS) * w + b

        def _fp8_linear_pertensor(x, wq, w_scale, in_scale):
            xq = _div_clamp_fp8(x, in_scale)
            return jnp.einsum('bsi,oi->bso', xq * in_scale, wq) * w_scale

        def _gqa(q, k, v):
            scale = 1.0 / np.sqrt(q.shape[-1])
            scores = jnp.einsum('bsghd,btgd->bghst', q, k) * scale
            p = jax.nn.softmax(scores, axis=-1)
            return jnp.einsum('bghst,btgd->bsghd', p, v)
        key = jax.random.key(seed)
        ks = jax.random.split(key, 8)
        B, S, SC, H, NH, G, D = (2, 256, 64, 256, 16, 8, 128)

        def qw(k, out_f, in_f):
            w = jax.random.normal(k, (out_f, in_f), jnp.float32) * 0.02
            sc = jnp.max(jnp.abs(w)) / FP8_MAX
            return (_fp8_roundtrip(w / sc), sc.astype(jnp.float32))
        wq, wq_s = qw(ks[0], NH * D, H)
        wqx, wqx_s = qw(ks[1], NH * D, H)
        wk, wk_s = qw(ks[2], G * D, H)
        wv, wv_s = qw(ks[3], G * D, H)
        wproj, wp_s = qw(ks[4], H, 2 * NH * D)
        return {'hidden_states': jax.random.normal(ks[5], (B, S, H), jnp.float32), 'cond': jax.random.normal(ks[6], (B, SC, H), jnp.float32), 'ln_w': jnp.ones((H,), jnp.float32), 'ln_b': jnp.zeros((H,), jnp.float32), 'wq': wq, 'wq_scale': wq_s, 'q_in_scale': jnp.full((H,), 0.05, jnp.float32), 'wqx': wqx, 'wqx_scale': wqx_s, 'qx_in_scale': jnp.full((H,), 0.05, jnp.float32), 'wk': wk, 'wk_scale': wk_s, 'k_in_scale': jnp.full((H,), 0.05, jnp.float32), 'wv': wv, 'wv_scale': wv_s, 'v_in_scale': jnp.full((H,), 0.05, jnp.float32), 'w_kv_x': jax.random.normal(ks[7], (2 * G * D, H), jnp.float32) * 0.02, 'qln_w': jnp.ones((D,), jnp.float32), 'qln_b': jnp.zeros((D,), jnp.float32), 'kln_w': jnp.ones((D,), jnp.float32), 'kln_b': jnp.zeros((D,), jnp.float32), 'qxln_w': jnp.ones((D,), jnp.float32), 'qxln_b': jnp.zeros((D,), jnp.float32), 'kxln_w': jnp.ones((D,), jnp.float32), 'kxln_b': jnp.zeros((D,), jnp.float32), 'wproj': wproj, 'proj_w_scale': wp_s, 'proj_in_scale': jnp.asarray(0.05, jnp.float32), 'proj_smooth': jnp.full((2 * NH * D,), 0.05, jnp.float32)}
    _L2_xattn_all = _L2_xattn_setup()
    _L2_xattn_in = {k: v for k, v in _L2_xattn_all.items() if k in ('ln_w', 'ln_b', 'wq', 'wq_scale', 'q_in_scale', 'wqx', 'wqx_scale', 'qx_in_scale', 'wk', 'wk_scale', 'k_in_scale', 'wv', 'wv_scale', 'v_in_scale', 'w_kv_x', 'qln_w', 'qln_b', 'kln_w', 'kln_b', 'qxln_w', 'qxln_b', 'kxln_w', 'kxln_b', 'wproj', 'proj_w_scale', 'proj_in_scale', 'proj_smooth')}
    del _L2_xattn_all

    def _L2_ffn_setup():
        import jax, jax.numpy as jnp
        import numpy as np
        from jax import lax
        D_MODEL = 256
        D_CROSS = 1024
        D_RETR = 128
        D_PRIV = 128
        N_EXPERTS = 2048
        N_HEADS = 8
        K_PER_HEAD = 8
        NUM_KEYS = int(np.sqrt(N_EXPERTS))
        BATCH, SEQ = (2, 256)
        key = jax.random.key(seed)
        ks = jax.random.split(key, 10)
        s = 0.02
        return {'hidden_states': jax.random.normal(ks[0], (BATCH, SEQ, D_MODEL), jnp.float32), 'W_up': jax.random.normal(ks[1], (D_CROSS, D_MODEL), jnp.float32) * s, 'b_up': jnp.zeros((D_CROSS,), jnp.float32), 'W_down': jax.random.normal(ks[2], (D_PRIV, D_CROSS), jnp.float32) * s, 'b_down': jnp.zeros((D_PRIV,), jnp.float32), 'W_q': jax.random.normal(ks[3], (D_RETR * N_HEADS, D_PRIV), jnp.float32) * s, 'keys': jax.random.normal(ks[4], (N_HEADS, NUM_KEYS, 2, D_RETR // 2), jnp.float32) * s, 'down_embed': jax.random.normal(ks[5], (N_EXPERTS, D_PRIV), jnp.float32) * s, 'up_embed': jax.random.normal(ks[6], (N_EXPERTS, D_MODEL), jnp.float32) * s}
    _L2_ffn_all = _L2_ffn_setup()
    _L2_ffn_in = {k: v for k, v in _L2_ffn_all.items() if k in ('W_up', 'b_up', 'W_down', 'b_down', 'W_q', 'keys', 'down_embed', 'up_embed')}
    del _L2_ffn_all

    def _L3_attn_setup():
        import jax, jax.numpy as jnp
        import numpy as np
        B, S, D = (1, 256, 256)
        H, G = (32, 8)
        HPG = H // G
        HD = D // H
        key = jax.random.key(seed)
        ks = jax.random.split(key, 5)
        w_scale = 0.02
        return {'x': jax.random.normal(ks[0], (B, S, D), dtype=jnp.float32), 'Wq': jax.random.normal(ks[1], (D, D), dtype=jnp.float32) * w_scale, 'bq': jnp.zeros((D,), dtype=jnp.float32), 'Wk': jax.random.normal(ks[2], (G * HD, D), dtype=jnp.float32) * w_scale, 'bk': jnp.zeros((G * HD,), dtype=jnp.float32), 'Wv': jax.random.normal(ks[3], (G * HD, D), dtype=jnp.float32) * w_scale, 'bv': jnp.zeros((G * HD,), dtype=jnp.float32), 'Wo': jax.random.normal(ks[4], (D, D), dtype=jnp.float32) * w_scale, 'bo': jnp.zeros((D,), dtype=jnp.float32)}
    _L3_attn_all = _L3_attn_setup()
    _L3_attn_in = {k: v for k, v in _L3_attn_all.items() if k in ('Wq', 'bq', 'Wk', 'bk', 'Wv', 'bv', 'Wo', 'bo')}
    del _L3_attn_all

    def _L3_xattn_setup():
        import jax, jax.numpy as jnp
        import numpy as np
        EPS = 1e-06
        NUM_HEADS = 16

        def _feature_map(x):
            return jnp.where(x > 0, x + 1.0, jnp.exp(x))
        key = jax.random.key(seed)
        ks = jax.random.split(key, 7)
        B, L, S, D = (4, 512, 512, 256)
        sc = 1.0 / np.sqrt(D)
        return {'query': jax.random.normal(ks[0], (B, L, D), jnp.float32), 'kv': jax.random.normal(ks[1], (B, S, D), jnp.float32), 'Wq': jax.random.normal(ks[2], (D, D), jnp.float32) * sc, 'Wg': jax.random.normal(ks[3], (D, D), jnp.float32) * sc, 'bg': jnp.ones((D,), jnp.float32), 'Wkv': jax.random.normal(ks[4], (2 * D, D), jnp.float32) * sc, 'Wo': jax.random.normal(ks[5], (D, D), jnp.float32) * sc}
    _L3_xattn_all = _L3_xattn_setup()
    _L3_xattn_in = {k: v for k, v in _L3_xattn_all.items() if k in ('Wq', 'Wg', 'bg', 'Wkv', 'Wo')}
    del _L3_xattn_all

    def _L3_ffn_setup():
        import jax, jax.numpy as jnp
        import numpy as np
        B_, S, D = (2, 256, 256)
        F_ = 1024
        R = 16
        H = 16
        HD = D // H
        MOD_SCALE = 0.1
        EPS = 1e-06

        def _rmsnorm(x, w):
            v = jnp.mean(x * x, axis=-1, keepdims=True)
            return x * jax.lax.rsqrt(v + EPS) * w

        def _attention(x, Wq, Wk, Wv, Wo):
            b, s, d = x.shape
            q = (x @ Wq.T).reshape(b, s, H, HD)
            k = (x @ Wk.T).reshape(b, s, H, HD)
            v = (x @ Wv.T).reshape(b, s, H, HD)
            scores = jnp.einsum('bqhd,bkhd->bhqk', q, k) / np.sqrt(HD).astype(np.float32)
            causal = jnp.tril(jnp.ones((s, s), bool))
            scores = jnp.where(causal, scores, jnp.finfo(scores.dtype).min)
            probs = jax.nn.softmax(scores, axis=-1)
            out = jnp.einsum('bhqk,bkhd->bqhd', probs, v).reshape(b, s, d)
            return out @ Wo.T
        key = jax.random.key(seed)
        ks = jax.random.split(key, 12)
        sd = 0.02
        return {'hidden_states': jax.random.normal(ks[0], (B_, S, D), jnp.float32), 'ln1_w': jnp.ones((D,), jnp.float32), 'ln2_w': jnp.ones((D,), jnp.float32), 'Wq': jax.random.normal(ks[1], (D, D), jnp.float32) * sd, 'Wk': jax.random.normal(ks[2], (D, D), jnp.float32) * sd, 'Wv': jax.random.normal(ks[3], (D, D), jnp.float32) * sd, 'Wo': jax.random.normal(ks[4], (D, D), jnp.float32) * sd, 'A': jax.random.normal(ks[5], (D, R), jnp.float32) * (0.01 / np.sqrt(D)), 'B': jax.random.normal(ks[6], (R, F_), jnp.float32) * (0.01 / np.sqrt(R)), 'W_in_base': jax.random.normal(ks[7], (F_, D), jnp.float32) * sd, 'W_up_base': jax.random.normal(ks[8], (F_, D), jnp.float32) * sd, 'W_down': jax.random.normal(ks[9], (D, F_), jnp.float32) * sd}
    _L3_ffn_all = _L3_ffn_setup()
    _L3_ffn_in = {k: v for k, v in _L3_ffn_all.items() if k in ('ln1_w', 'ln2_w', 'Wq', 'Wk', 'Wv', 'Wo', 'A', 'B', 'W_in_base', 'W_up_base', 'W_down')}
    del _L3_ffn_all
    return {'x': x, 'ctx_2048': ctx_2048, 'L0_attn_in_proj_w': _L0_attn_in['in_proj_w'], 'L0_attn_dt_proj_w': _L0_attn_in['dt_proj_w'], 'L0_attn_dt_proj_b': _L0_attn_in['dt_proj_b'], 'L0_attn_A_log': _L0_attn_in['A_log'], 'L0_attn_D_param': _L0_attn_in['D_param'], 'L0_attn_out_proj_w': _L0_attn_in['out_proj_w'], 'L0_attn_gate_w': _L0_attn_in['gate_w'], 'L0_attn_up_w': _L0_attn_in['up_w'], 'L0_attn_down_w': _L0_attn_in['down_w'], 'L0_attn_norm1_w': _L0_attn_in['norm1_w'], 'L0_attn_norm2_w': _L0_attn_in['norm2_w'], 'L0_xattn_theta_w': _L0_xattn_in['theta_w'], 'L0_xattn_theta_b': _L0_xattn_in['theta_b'], 'L0_xattn_phi_w': _L0_xattn_in['phi_w'], 'L0_xattn_phi_b': _L0_xattn_in['phi_b'], 'L0_xattn_g_w': _L0_xattn_in['g_w'], 'L0_xattn_g_b': _L0_xattn_in['g_b'], 'L0_xattn_ln_gamma': _L0_xattn_in['ln_gamma'], 'L0_xattn_ln_beta': _L0_xattn_in['ln_beta'], 'L0_xattn_out_w': _L0_xattn_in['out_w'], 'L0_xattn_out_b': _L0_xattn_in['out_b'], 'L0_ffn_gate_w': _L0_ffn_in['gate_w'], 'L0_ffn_gate_b': _L0_ffn_in['gate_b'], 'L0_ffn_expert_w': _L0_ffn_in['expert_w'], 'L0_ffn_expert_b': _L0_ffn_in['expert_b'], 'L1_attn_Wq': _L1_attn_in['Wq'], 'L1_attn_Wk': _L1_attn_in['Wk'], 'L1_attn_Wv': _L1_attn_in['Wv'], 'L1_attn_Wo': _L1_attn_in['Wo'], 'L1_xattn_decay': _L1_xattn_in['decay'], 'L1_xattn_W_in': _L1_xattn_in['W_in'], 'L1_xattn_b_in': _L1_xattn_in['b_in'], 'L1_xattn_W_out': _L1_xattn_in['W_out'], 'L1_xattn_b_out': _L1_xattn_in['b_out'], 'L1_xattn_gamma': _L1_xattn_in['gamma'], 'L1_xattn_beta': _L1_xattn_in['beta'], 'L1_ffn_W1': _L1_ffn_in['W1'], 'L1_ffn_Wg': _L1_ffn_in['Wg'], 'L1_ffn_W2': _L1_ffn_in['W2'], 'L1_ffn_Ws1': _L1_ffn_in['Ws1'], 'L1_ffn_Wsg': _L1_ffn_in['Wsg'], 'L1_ffn_Ws2': _L1_ffn_in['Ws2'], 'L1_ffn_gate_w': _L1_ffn_in['gate_w'], 'L1_ffn_gate_b': _L1_ffn_in['gate_b'], 'L1_ffn_biases': _L1_ffn_in['biases'], 'L2_attn_W_qkv': _L2_attn_in['W_qkv'], 'L2_attn_W_o': _L2_attn_in['W_o'], 'L2_xattn_ln_w': _L2_xattn_in['ln_w'], 'L2_xattn_ln_b': _L2_xattn_in['ln_b'], 'L2_xattn_wq': _L2_xattn_in['wq'], 'L2_xattn_wq_scale': _L2_xattn_in['wq_scale'], 'L2_xattn_q_in_scale': _L2_xattn_in['q_in_scale'], 'L2_xattn_wqx': _L2_xattn_in['wqx'], 'L2_xattn_wqx_scale': _L2_xattn_in['wqx_scale'], 'L2_xattn_qx_in_scale': _L2_xattn_in['qx_in_scale'], 'L2_xattn_wk': _L2_xattn_in['wk'], 'L2_xattn_wk_scale': _L2_xattn_in['wk_scale'], 'L2_xattn_k_in_scale': _L2_xattn_in['k_in_scale'], 'L2_xattn_wv': _L2_xattn_in['wv'], 'L2_xattn_wv_scale': _L2_xattn_in['wv_scale'], 'L2_xattn_v_in_scale': _L2_xattn_in['v_in_scale'], 'L2_xattn_w_kv_x': _L2_xattn_in['w_kv_x'], 'L2_xattn_qln_w': _L2_xattn_in['qln_w'], 'L2_xattn_qln_b': _L2_xattn_in['qln_b'], 'L2_xattn_kln_w': _L2_xattn_in['kln_w'], 'L2_xattn_kln_b': _L2_xattn_in['kln_b'], 'L2_xattn_qxln_w': _L2_xattn_in['qxln_w'], 'L2_xattn_qxln_b': _L2_xattn_in['qxln_b'], 'L2_xattn_kxln_w': _L2_xattn_in['kxln_w'], 'L2_xattn_kxln_b': _L2_xattn_in['kxln_b'], 'L2_xattn_wproj': _L2_xattn_in['wproj'], 'L2_xattn_proj_w_scale': _L2_xattn_in['proj_w_scale'], 'L2_xattn_proj_in_scale': _L2_xattn_in['proj_in_scale'], 'L2_xattn_proj_smooth': _L2_xattn_in['proj_smooth'], 'L2_ffn_W_up': _L2_ffn_in['W_up'], 'L2_ffn_b_up': _L2_ffn_in['b_up'], 'L2_ffn_W_down': _L2_ffn_in['W_down'], 'L2_ffn_b_down': _L2_ffn_in['b_down'], 'L2_ffn_W_q': _L2_ffn_in['W_q'], 'L2_ffn_keys': _L2_ffn_in['keys'], 'L2_ffn_down_embed': _L2_ffn_in['down_embed'], 'L2_ffn_up_embed': _L2_ffn_in['up_embed'], 'L3_attn_Wq': _L3_attn_in['Wq'], 'L3_attn_bq': _L3_attn_in['bq'], 'L3_attn_Wk': _L3_attn_in['Wk'], 'L3_attn_bk': _L3_attn_in['bk'], 'L3_attn_Wv': _L3_attn_in['Wv'], 'L3_attn_bv': _L3_attn_in['bv'], 'L3_attn_Wo': _L3_attn_in['Wo'], 'L3_attn_bo': _L3_attn_in['bo'], 'L3_xattn_Wq': _L3_xattn_in['Wq'], 'L3_xattn_Wg': _L3_xattn_in['Wg'], 'L3_xattn_bg': _L3_xattn_in['bg'], 'L3_xattn_Wkv': _L3_xattn_in['Wkv'], 'L3_xattn_Wo': _L3_xattn_in['Wo'], 'L3_ffn_ln1_w': _L3_ffn_in['ln1_w'], 'L3_ffn_ln2_w': _L3_ffn_in['ln2_w'], 'L3_ffn_Wq': _L3_ffn_in['Wq'], 'L3_ffn_Wk': _L3_ffn_in['Wk'], 'L3_ffn_Wv': _L3_ffn_in['Wv'], 'L3_ffn_Wo': _L3_ffn_in['Wo'], 'L3_ffn_A': _L3_ffn_in['A'], 'L3_ffn_B': _L3_ffn_in['B'], 'L3_ffn_W_in_base': _L3_ffn_in['W_in_base'], 'L3_ffn_W_up_base': _L3_ffn_in['W_up_base'], 'L3_ffn_W_down': _L3_ffn_in['W_down']}

def reference(x, ctx_2048, L0_attn_in_proj_w, L0_attn_dt_proj_w, L0_attn_dt_proj_b, L0_attn_A_log, L0_attn_D_param, L0_attn_out_proj_w, L0_attn_gate_w, L0_attn_up_w, L0_attn_down_w, L0_attn_norm1_w, L0_attn_norm2_w, L0_xattn_theta_w, L0_xattn_theta_b, L0_xattn_phi_w, L0_xattn_phi_b, L0_xattn_g_w, L0_xattn_g_b, L0_xattn_ln_gamma, L0_xattn_ln_beta, L0_xattn_out_w, L0_xattn_out_b, L0_ffn_gate_w, L0_ffn_gate_b, L0_ffn_expert_w, L0_ffn_expert_b, L1_attn_Wq, L1_attn_Wk, L1_attn_Wv, L1_attn_Wo, L1_xattn_decay, L1_xattn_W_in, L1_xattn_b_in, L1_xattn_W_out, L1_xattn_b_out, L1_xattn_gamma, L1_xattn_beta, L1_ffn_W1, L1_ffn_Wg, L1_ffn_W2, L1_ffn_Ws1, L1_ffn_Wsg, L1_ffn_Ws2, L1_ffn_gate_w, L1_ffn_gate_b, L1_ffn_biases, L2_attn_W_qkv, L2_attn_W_o, L2_xattn_ln_w, L2_xattn_ln_b, L2_xattn_wq, L2_xattn_wq_scale, L2_xattn_q_in_scale, L2_xattn_wqx, L2_xattn_wqx_scale, L2_xattn_qx_in_scale, L2_xattn_wk, L2_xattn_wk_scale, L2_xattn_k_in_scale, L2_xattn_wv, L2_xattn_wv_scale, L2_xattn_v_in_scale, L2_xattn_w_kv_x, L2_xattn_qln_w, L2_xattn_qln_b, L2_xattn_kln_w, L2_xattn_kln_b, L2_xattn_qxln_w, L2_xattn_qxln_b, L2_xattn_kxln_w, L2_xattn_kxln_b, L2_xattn_wproj, L2_xattn_proj_w_scale, L2_xattn_proj_in_scale, L2_xattn_proj_smooth, L2_ffn_W_up, L2_ffn_b_up, L2_ffn_W_down, L2_ffn_b_down, L2_ffn_W_q, L2_ffn_keys, L2_ffn_down_embed, L2_ffn_up_embed, L3_attn_Wq, L3_attn_bq, L3_attn_Wk, L3_attn_bk, L3_attn_Wv, L3_attn_bv, L3_attn_Wo, L3_attn_bo, L3_xattn_Wq, L3_xattn_Wg, L3_xattn_bg, L3_xattn_Wkv, L3_xattn_Wo, L3_ffn_ln1_w, L3_ffn_ln2_w, L3_ffn_Wq, L3_ffn_Wk, L3_ffn_Wv, L3_ffn_Wo, L3_ffn_A, L3_ffn_B, L3_ffn_W_in_base, L3_ffn_W_up_base, L3_ffn_W_down):
    import jax
    import jax.numpy as jnp

    def _L0_attn_ref(hidden_states, in_proj_w, dt_proj_w, dt_proj_b, A_log, D_param, out_proj_w, gate_w, up_w, down_w, norm1_w, norm2_w):
        import jax, jax.numpy as jnp
        import numpy as np
        D_MODEL = 256
        D_INNER = 256
        D_XB = 64
        D_STATE = 32
        DT_RANK = 128
        D_FF = 704
        BATCH = 2
        SEQ = 128
        EPS = 1e-05

        def _rmsnorm(x, w):
            var = jnp.mean(jnp.square(x), axis=-1, keepdims=True)
            return x * jax.lax.rsqrt(var + EPS) * w

        def _selective_scan(x, dt, A, B, C):
            b, l, g, p = x.shape
            n = A.shape[-1]

            def step(h, inp):
                x_t, dt_t, B_t, C_t = inp
                dA = jnp.exp(dt_t[..., None] * A)
                h = dA * h + (dt_t * x_t)[..., None] * B_t[:, :, None, :]
                y = jnp.einsum('bgpn,bgn->bgp', h, C_t)
                return (h, y)
            h0 = jnp.zeros((b, g, p, n), x.dtype)
            xs = tuple((jnp.moveaxis(a, 1, 0) for a in (x, dt, B, C)))
            _, ys = jax.lax.scan(step, h0, xs)
            return jnp.moveaxis(ys, 0, 1)

        def _mamba(u, in_proj_w, dt_proj_w, dt_proj_b, A_log, D_param, out_proj_w):
            b, l, _ = u.shape
            zxbcdt = u @ in_proj_w.T
            splits = np.cumsum([D_INNER, D_XB, D_XB, D_INNER]).tolist()
            z, x, Bc, Cc, dt_raw = jnp.split(zxbcdt, splits, axis=-1)
            dt = jax.nn.softplus(dt_raw @ dt_proj_w.T + dt_proj_b)
            g = D_INNER // D_STATE
            g_kv = D_XB // D_STATE
            rep = g // g_kv
            x = jnp.repeat(x.reshape(b, l, g_kv, D_STATE), rep, axis=2)
            Bm = jnp.repeat(Bc.reshape(b, l, g_kv, D_STATE), rep, axis=2)
            Cm = Cc.reshape(b, l, g, D_STATE)
            A = -jnp.exp(A_log).reshape(g, D_STATE, D_STATE)
            dt = dt.reshape(b, l, g, D_STATE)
            y = _selective_scan(x, dt, A, Bm, Cm).reshape(b, l, D_INNER)
            y = y + x.reshape(b, l, D_INNER) * D_param
            y = y * jax.nn.silu(z)
            return y @ out_proj_w.T

        def _forward(hidden_states, in_proj_w, dt_proj_w, dt_proj_b, A_log, D_param, out_proj_w, gate_w, up_w, down_w, norm1_w, norm2_w):
            h = hidden_states + _mamba(_rmsnorm(hidden_states, norm1_w), in_proj_w, dt_proj_w, dt_proj_b, A_log, D_param, out_proj_w)
            xn = _rmsnorm(h, norm2_w)
            mlp = jax.nn.silu(xn @ gate_w.T) * (xn @ up_w.T) @ down_w.T
            return h + mlp
        return _forward(hidden_states, in_proj_w, dt_proj_w, dt_proj_b, A_log, D_param, out_proj_w, gate_w, up_w, down_w, norm1_w, norm2_w)

    def _L0_xattn_ref(input1, input2, theta_w, theta_b, phi_w, phi_b, g_w, g_b, ln_gamma, ln_beta, out_w, out_b):
        import jax, jax.numpy as jnp
        import numpy as np
        B, DIM1, DIM2, LATENT, T = (16, 128, 128, 64, 256)
        LN_EPS = 1e-05
        theta_x = jnp.einsum('ld,bdt->btl', theta_w, input2) + theta_b
        phi_x = jnp.einsum('ld,bdt->blt', phi_w, input1) + phi_b[:, None]
        scores = jnp.einsum('btl,bls->bts', theta_x, phi_x)
        p = jax.nn.softmax(scores, axis=-1)
        g_x = jnp.einsum('ld,bdt->btl', g_w, input1) + g_b
        t_x = jnp.einsum('bts,bsl->blt', p, g_x)
        mu = jnp.mean(t_x, axis=(1, 2), keepdims=True)
        var = jnp.var(t_x, axis=(1, 2), keepdims=True)
        h = (t_x - mu) * jax.lax.rsqrt(var + LN_EPS) * ln_gamma + ln_beta
        h = jax.nn.relu(h)
        w_t = jnp.einsum('ol,blt->bot', out_w, h) + out_b[None, :, None]
        return w_t + input2

    def _L0_ffn_ref(x, gate_w, gate_b, expert_w, expert_b):
        import jax, jax.numpy as jnp
        import numpy as np
        N, S, D = (8, 256, 256)
        O = 256
        E = 8
        K = 2
        gate_logits = jnp.einsum('nsd,de->nse', x, gate_w) + gate_b
        _, top_idx = jax.lax.top_k(gate_logits, K)
        all_out = jax.nn.relu(jnp.einsum('nsd,edo->nseo', x, expert_w) + expert_b)
        sel = jnp.take_along_axis(all_out, top_idx[..., None], axis=2)
        return sel.mean(axis=2)

    def _L1_attn_ref(x, Wq, Wk, Wv, Wo):
        import jax, jax.numpy as jnp
        import numpy as np
        D = 256
        q = jnp.einsum('bsd,ed->bse', x, Wq)
        k = jnp.einsum('bsd,ed->bse', x, Wk)
        v = jnp.einsum('bsd,ed->bse', x, Wv)
        seq = x.shape[-2]
        denom = jnp.sqrt(jnp.float32(x.shape[-1])) / seq
        kvt = jnp.cumsum(k * v, axis=-2) * denom
        vhat = q * kvt
        return jnp.einsum('bse,fe->bsf', vhat, Wo)

    def _L1_xattn_ref(Z, kv, decay, W_in, b_in, W_out, b_out, gamma, beta):
        import jax, jax.numpy as jnp
        import numpy as np
        from jax import lax
        LN_EPS = 1e-05
        B, T, D = kv.shape
        K = jax.nn.sigmoid(decay)
        x = jnp.einsum('btd,ed->bte', kv, W_in) + b_in

        def scan_fn(s, xt):
            s = K * s + xt
            return (s, s)
        s0 = jnp.zeros((B, D), dtype=kv.dtype)
        _, states = lax.scan(scan_fn, s0, jnp.swapaxes(x, 0, 1))
        states = jnp.swapaxes(states, 0, 1)
        proj = jnp.einsum('btd,ed->bte', states, W_out) + b_out
        summary = jnp.mean(proj, axis=1, keepdims=True)
        y = Z + summary
        mu = jnp.mean(y, axis=-1, keepdims=True)
        var = jnp.mean((y - mu) ** 2, axis=-1, keepdims=True)
        return (y - mu) / jnp.sqrt(var + LN_EPS) * gamma + beta

    def _L1_ffn_ref(x, W1, Wg, W2, Ws1, Wsg, Ws2, gate_w, gate_b, biases):
        import jax, jax.numpy as jnp
        import numpy as np
        NUM_ROUTED = 7
        TOP_K = 3
        D = 256
        H = 256
        B, S = (4, 256)

        def _expert_ffn(x, w1, wg, w2):
            return jax.nn.silu(x @ w1) * (x @ wg) @ w2
        output = _expert_ffn(x, Ws1, Wsg, Ws2)
        gate_logits = x @ gate_w + gate_b
        gate_probas = jax.nn.softmax(gate_logits, axis=-1)
        biased_probas = gate_probas + biases
        _, topk_idxs = jax.lax.top_k(biased_probas, TOP_K)
        topk_probas = jnp.take_along_axis(gate_probas, topk_idxs, axis=-1)
        topk_probas = topk_probas / jnp.sum(topk_probas, axis=-1, keepdims=True)
        for e in range(NUM_ROUTED):
            w_e = jnp.sum(topk_probas * (topk_idxs == e), axis=-1)
            output = output + _expert_ffn(x, W1[e], Wg[e], W2[e]) * w_e[..., None]
        return output

    def _L2_attn_ref(x, W_qkv, W_o):
        import jax, jax.numpy as jnp
        import numpy as np
        import math
        N_EMBD = 256
        N_HEADS = 16
        HEAD_DIM = N_EMBD // N_HEADS
        CTX = 256

        def alibi_bias(seq_len: int, n_heads: int) -> jnp.ndarray:
            i = jnp.arange(seq_len)[:, None]
            j = jnp.arange(seq_len)[None, :]
            pos = jnp.where(j <= i, (j - i).astype(jnp.float32), 0.0)
            slopes = 2.0 ** (-8.0 / jnp.arange(1, n_heads + 1, dtype=jnp.float32))
            return slopes[:, None, None] * pos[None, :, :]

        def causal_mask(seq_len: int) -> jnp.ndarray:
            i = jnp.arange(seq_len)[:, None]
            j = jnp.arange(seq_len)[None, :]
            return jnp.where(j > i, -jnp.inf, 0.0).astype(jnp.float32)
        bsz, seq_len, n_embd = x.shape
        qkv = jnp.einsum('bsd,de->bse', x, W_qkv)
        q, k, v = jnp.split(qkv, 3, axis=-1)

        def to_heads(t):
            return t.reshape(bsz, seq_len, N_HEADS, HEAD_DIM).transpose(0, 2, 1, 3)
        q, k, v = (to_heads(q), to_heads(k), to_heads(v))
        attn = jnp.einsum('bhqd,bhkd->bhqk', q, k) / math.sqrt(HEAD_DIM)
        attn = attn + alibi_bias(seq_len, N_HEADS)[None] + causal_mask(seq_len)[None, None]
        attn = jax.nn.softmax(attn, axis=-1)
        y = jnp.einsum('bhqk,bhkd->bhqd', attn, v)
        y = y.transpose(0, 2, 1, 3).reshape(bsz, seq_len, n_embd)
        return jnp.einsum('bsd,de->bse', y, W_o)

    def _L2_xattn_ref(hidden_states, cond, ln_w, ln_b, wq, wq_scale, q_in_scale, wqx, wqx_scale, qx_in_scale, wk, wk_scale, k_in_scale, wv, wv_scale, v_in_scale, w_kv_x, qln_w, qln_b, kln_w, kln_b, qxln_w, qxln_b, kxln_w, kxln_b, wproj, proj_w_scale, proj_in_scale, proj_smooth):
        import jax, jax.numpy as jnp
        import numpy as np
        FP8_MAX = 448.0
        EPS = 1e-05

        def _fp8_roundtrip(x):
            return x.astype(jnp.float8_e4m3fn).astype(jnp.float32)

        def _div_clamp_fp8(x, scale):
            y = jnp.clip(x.astype(jnp.float32) / scale, -FP8_MAX, FP8_MAX)
            y = y.astype(jnp.bfloat16).astype(jnp.float32)
            return _fp8_roundtrip(y)

        def _ln(x, w, b):
            mu = jnp.mean(x, axis=-1, keepdims=True)
            var = jnp.mean(jnp.square(x - mu), axis=-1, keepdims=True)
            return (x - mu) * jax.lax.rsqrt(var + EPS) * w + b

        def _fp8_linear_pertensor(x, wq, w_scale, in_scale):
            xq = _div_clamp_fp8(x, in_scale)
            return jnp.einsum('bsi,oi->bso', xq * in_scale, wq) * w_scale

        def _gqa(q, k, v):
            scale = 1.0 / np.sqrt(q.shape[-1])
            scores = jnp.einsum('bsghd,btgd->bghst', q, k) * scale
            p = jax.nn.softmax(scores, axis=-1)
            return jnp.einsum('bghst,btgd->bsghd', p, v)
        b, s, _ = hidden_states.shape
        sc = cond.shape[1]
        d = qln_w.shape[0]
        nh = wq.shape[0] // d
        g = wk.shape[0] // d
        hpg = nh // g
        ln_out = _ln(hidden_states, ln_w, ln_b)
        q = _fp8_linear_pertensor(ln_out, wq, wq_scale, q_in_scale).reshape(b, s, g, hpg, d)
        q = _ln(q, qln_w, qln_b)
        k = _fp8_linear_pertensor(ln_out, wk, wk_scale, k_in_scale).reshape(b, s, g, d)
        k = _ln(k, kln_w, kln_b)
        v = _fp8_linear_pertensor(ln_out, wv, wv_scale, v_in_scale).reshape(b, s, g, d)
        core = _gqa(q, k, v).reshape(b, s, nh * d)
        qx = _fp8_linear_pertensor(ln_out, wqx, wqx_scale, qx_in_scale).reshape(b, s, g, hpg, d)
        qx = _ln(qx, qxln_w, qxln_b)
        kvx = jnp.einsum('bsi,oi->bso', cond, w_kv_x)
        kx, vx = jnp.split(kvx, 2, axis=-1)
        kx = _ln(kx.reshape(b, sc, g, d), kxln_w, kxln_b)
        vx = vx.reshape(b, sc, g, d)
        xout = _gqa(qx, kx, vx).reshape(b, s, nh * d)
        cat = jnp.concatenate([core, xout], axis=-1)
        catq = _div_clamp_fp8(cat, proj_smooth)
        return jnp.einsum('bsi,oi->bso', catq, wproj) * (proj_in_scale * proj_w_scale)

    def _L2_ffn_ref(hidden_states, W_up, b_up, W_down, b_down, W_q, keys, down_embed, up_embed):
        import jax, jax.numpy as jnp
        import numpy as np
        from jax import lax
        D_MODEL = 256
        D_CROSS = 1024
        D_RETR = 128
        D_PRIV = 128
        N_EXPERTS = 2048
        N_HEADS = 8
        K_PER_HEAD = 8
        NUM_KEYS = int(np.sqrt(N_EXPERTS))
        BATCH, SEQ = (2, 256)
        b, t, _ = hidden_states.shape
        act = jax.nn.silu
        h = act(jnp.einsum('btd,cd->btc', hidden_states, W_up) + b_up)
        h = jnp.einsum('btc,pc->btp', h, W_down) + b_down
        q = jnp.einsum('btp,rp->btr', h, W_q)
        q = q.reshape(b, t, 2, N_HEADS, D_RETR // 2).transpose(2, 0, 1, 3, 4)
        sim = jnp.einsum('pbthn,hkpn->pbthk', q, keys)
        scores, idx = lax.top_k(sim, K_PER_HEAD)
        sx, sy = (scores[0], scores[1])
        ix, iy = (idx[0], idx[1])
        all_scores = (sx[..., :, None] + sy[..., None, :]).reshape(b, t, N_HEADS, K_PER_HEAD * K_PER_HEAD)
        all_indices = (ix[..., :, None] * NUM_KEYS + iy[..., None, :]).reshape(b, t, N_HEADS, K_PER_HEAD * K_PER_HEAD)
        sc, pk = lax.top_k(all_scores, K_PER_HEAD)
        indices = jnp.take_along_axis(all_indices, pk, axis=-1)
        de = down_embed[indices]
        ue = up_embed[indices]
        z = jnp.einsum('btd,bthkd->bthk', h, de)
        z = act(z * jax.nn.softmax(sc, axis=-1))
        out = jnp.einsum('bthk,bthkd->btd', z, ue)
        return out

    def _L3_attn_ref(x, Wq, bq, Wk, bk, Wv, bv, Wo, bo):
        import jax, jax.numpy as jnp
        import numpy as np
        B, S, D = (1, 256, 256)
        H, G = (32, 8)
        HPG = H // G
        HD = D // H
        b, n, _ = x.shape
        q = x @ Wq.T + bq
        k = x @ Wk.T + bk
        v = x @ Wv.T + bv
        q = q.reshape(b, n, H, HD).transpose(0, 2, 1, 3).reshape(b, G, HPG, n, HD)
        k = k.reshape(b, n, G, HD).transpose(0, 2, 1, 3)
        v = v.reshape(b, n, G, HD).transpose(0, 2, 1, 3)
        scale = 1.0 / jnp.sqrt(jnp.asarray(HD, dtype=q.dtype))
        attn_score = jnp.einsum('bghnd,bgsd->bghns', q, k) * scale
        attn_prob = jax.nn.softmax(attn_score, axis=-1)
        out = jnp.einsum('bghns,bgsd->bghnd', attn_prob, v)
        out = out.transpose(0, 3, 2, 1, 4).reshape(b, n, HPG * G * HD)
        return out @ Wo.T + bo

    def _L3_xattn_ref(query, kv, Wq, Wg, bg, Wkv, Wo):
        import jax, jax.numpy as jnp
        import numpy as np
        EPS = 1e-06
        NUM_HEADS = 16

        def _feature_map(x):
            return jnp.where(x > 0, x + 1.0, jnp.exp(x))
        B, L, D = query.shape
        S = kv.shape[1]
        H = NUM_HEADS
        hd = D // H
        q = query @ Wq.T
        gate = jax.nn.sigmoid(query @ Wg.T + bg)
        kvp = kv @ Wkv.T
        k, v = jnp.split(kvp, 2, axis=-1)
        q = _feature_map(q.reshape(B, L, H, hd).transpose(0, 2, 1, 3))
        k = _feature_map(k.reshape(B, S, H, hd).transpose(0, 2, 1, 3))
        v = v.reshape(B, S, H, hd).transpose(0, 2, 1, 3)
        kv_summary = jnp.einsum('bhsd,bhse->bhde', k, v)
        k_sum = k.sum(axis=-2)
        z = 1.0 / (jnp.einsum('bhld,bhd->bhl', q, k_sum)[..., None] + EPS)
        attn = jnp.einsum('bhld,bhde->bhle', q, kv_summary) * z
        attn = attn.transpose(0, 2, 1, 3).reshape(B, L, D)
        out = attn * gate @ Wo.T
        return out

    def _L3_ffn_ref(hidden_states, ln1_w, ln2_w, Wq, Wk, Wv, Wo, A, B, W_in_base, W_up_base, W_down):
        import jax, jax.numpy as jnp
        import numpy as np
        B_, S, D = (2, 256, 256)
        F_ = 1024
        R = 16
        H = 16
        HD = D // H
        MOD_SCALE = 0.1
        EPS = 1e-06

        def _rmsnorm(x, w):
            v = jnp.mean(x * x, axis=-1, keepdims=True)
            return x * jax.lax.rsqrt(v + EPS) * w

        def _attention(x, Wq, Wk, Wv, Wo):
            b, s, d = x.shape
            q = (x @ Wq.T).reshape(b, s, H, HD)
            k = (x @ Wk.T).reshape(b, s, H, HD)
            v = (x @ Wv.T).reshape(b, s, H, HD)
            scores = jnp.einsum('bqhd,bkhd->bhqk', q, k) / np.sqrt(HD).astype(np.float32)
            causal = jnp.tril(jnp.ones((s, s), bool))
            scores = jnp.where(causal, scores, jnp.finfo(scores.dtype).min)
            probs = jax.nn.softmax(scores, axis=-1)
            out = jnp.einsum('bhqk,bkhd->bqhd', probs, v).reshape(b, s, d)
            return out @ Wo.T
        residual = hidden_states
        x = _rmsnorm(hidden_states, ln1_w)
        attn = _attention(x, Wq, Wk, Wv, Wo)
        mod = MOD_SCALE * jnp.tanh(attn @ A)
        h = _rmsnorm(residual, ln2_w)
        gate_pre = h @ W_in_base.T + mod * (h @ A) @ B
        gate = jax.nn.silu(gate_pre)
        up = h @ W_up_base.T
        mlp_out = gate * up @ W_down.T
        return residual + mlp_out
    x = x + _L0_attn_ref(_layernorm(x, axis=-1), L0_attn_in_proj_w, L0_attn_dt_proj_w, L0_attn_dt_proj_b, L0_attn_A_log, L0_attn_D_param, L0_attn_out_proj_w, L0_attn_gate_w, L0_attn_up_w, L0_attn_down_w, L0_attn_norm1_w, L0_attn_norm2_w)
    x = x + _L0_xattn_ref(_layernorm(x, axis=-1), ctx_2048, L0_xattn_theta_w, L0_xattn_theta_b, L0_xattn_phi_w, L0_xattn_phi_b, L0_xattn_g_w, L0_xattn_g_b, L0_xattn_ln_gamma, L0_xattn_ln_beta, L0_xattn_out_w, L0_xattn_out_b)
    x = x + _L0_ffn_ref(_layernorm(x, axis=-1), L0_ffn_gate_w, L0_ffn_gate_b, L0_ffn_expert_w, L0_ffn_expert_b)
    x = x + _L1_attn_ref(_layernorm(x, axis=-1), L1_attn_Wq, L1_attn_Wk, L1_attn_Wv, L1_attn_Wo)
    x = x + _L1_xattn_ref(_layernorm(x, axis=-1), ctx_2048, L1_xattn_decay, L1_xattn_W_in, L1_xattn_b_in, L1_xattn_W_out, L1_xattn_b_out, L1_xattn_gamma, L1_xattn_beta)
    x = x + _L1_ffn_ref(_layernorm(x, axis=-1), L1_ffn_W1, L1_ffn_Wg, L1_ffn_W2, L1_ffn_Ws1, L1_ffn_Wsg, L1_ffn_Ws2, L1_ffn_gate_w, L1_ffn_gate_b, L1_ffn_biases)
    x = x + _L2_attn_ref(_layernorm(x, axis=-1), L2_attn_W_qkv, L2_attn_W_o)
    x = x + _L2_xattn_ref(_layernorm(x, axis=-1), ctx_2048, L2_xattn_ln_w, L2_xattn_ln_b, L2_xattn_wq, L2_xattn_wq_scale, L2_xattn_q_in_scale, L2_xattn_wqx, L2_xattn_wqx_scale, L2_xattn_qx_in_scale, L2_xattn_wk, L2_xattn_wk_scale, L2_xattn_k_in_scale, L2_xattn_wv, L2_xattn_wv_scale, L2_xattn_v_in_scale, L2_xattn_w_kv_x, L2_xattn_qln_w, L2_xattn_qln_b, L2_xattn_kln_w, L2_xattn_kln_b, L2_xattn_qxln_w, L2_xattn_qxln_b, L2_xattn_kxln_w, L2_xattn_kxln_b, L2_xattn_wproj, L2_xattn_proj_w_scale, L2_xattn_proj_in_scale, L2_xattn_proj_smooth)
    x = x + _L2_ffn_ref(_layernorm(x, axis=-1), L2_ffn_W_up, L2_ffn_b_up, L2_ffn_W_down, L2_ffn_b_down, L2_ffn_W_q, L2_ffn_keys, L2_ffn_down_embed, L2_ffn_up_embed)
    x = x + _L3_attn_ref(_layernorm(x, axis=-1), L3_attn_Wq, L3_attn_bq, L3_attn_Wk, L3_attn_bk, L3_attn_Wv, L3_attn_bv, L3_attn_Wo, L3_attn_bo)
    x = x + _L3_xattn_ref(_layernorm(x, axis=-1), ctx_2048, L3_xattn_Wq, L3_xattn_Wg, L3_xattn_bg, L3_xattn_Wkv, L3_xattn_Wo)
    x = x + _L3_ffn_ref(_layernorm(x, axis=-1), L3_ffn_ln1_w, L3_ffn_ln2_w, L3_ffn_Wq, L3_ffn_Wk, L3_ffn_Wv, L3_ffn_Wo, L3_ffn_A, L3_ffn_B, L3_ffn_W_in_base, L3_ffn_W_up_base, L3_ffn_W_down)
    return x

_drawn_inputs = setup_inputs


def setup_inputs(seed=0):
    import zlib

    import numpy as np

    out = dict(_drawn_inputs(seed))
    spreads = {'L0_attn_dt_proj_b': (-4.599999904632568, 0.6),
     'L0_attn_D_param': (1.0, 0.6),
     'L0_attn_norm1_w': (1.0, 0.6),
     'L0_attn_norm2_w': (1.0, 0.6),
     'L0_xattn_theta_b': (0.0, 0.1),
     'L0_xattn_phi_b': (0.0, 2.0),
     'L0_xattn_g_b': (0.0, 0.268),
     'L0_xattn_ln_gamma': (1.0, 0.2),
     'L0_xattn_ln_beta': (0.0, 0.1),
     'L0_xattn_out_b': (0.0, 2.0),
     'L1_xattn_b_in': (0.0, 0.299),
     'L1_xattn_b_out': (0.0, 0.269),
     'L1_xattn_gamma': (1.0, 0.2),
     'L1_xattn_beta': (0.0, 0.288),
     'L1_ffn_gate_b': (0.0, 0.8),
     'L1_ffn_biases': (0.0, 0.8),
     'L2_xattn_ln_w': (1.0, 0.6),
     'L2_xattn_ln_b': (0.0, 0.8),
     'L2_xattn_q_in_scale': (0.05000000074505806, 0.6),
     'L2_xattn_qx_in_scale': (0.05000000074505806, 0.6),
     'L2_xattn_k_in_scale': (0.05000000074505806, 0.6),
     'L2_xattn_v_in_scale': (0.05000000074505806, 0.6),
     'L2_xattn_qln_w': (1.0, 0.6),
     'L2_xattn_qln_b': (0.0, 2.0),
     'L2_xattn_kln_w': (1.0, 0.6),
     'L2_xattn_kln_b': (0.0, 2.0),
     'L2_xattn_qxln_w': (1.0, 0.6),
     'L2_xattn_qxln_b': (0.0, 2.0),
     'L2_xattn_kxln_w': (1.0, 0.6),
     'L2_xattn_kxln_b': (0.0, 2.0),
     'L2_xattn_proj_smooth': (0.05000000074505806, 0.6),
     'L2_ffn_b_up': (0.0, 0.8),
     'L2_ffn_b_down': (0.0, 0.8),
     'L3_attn_bq': (0.0, 0.8),
     'L3_attn_bk': (0.0, 2.0),
     'L3_attn_bv': (0.0, 0.8),
     'L3_attn_bo': (0.0, 1.149),
     'L3_xattn_bg': (1.0, 0.6),
     'L3_ffn_ln1_w': (1.0, 0.6),
     'L3_ffn_ln2_w': (1.0, 0.6)}
    factors = {'L0_attn_dt_proj_w': 8.0,
     'L0_attn_A_log': 8.0,
     'L0_ffn_expert_b': 5.892,
     'L1_ffn_W1': 8.0,
     'L1_ffn_Wg': 8.0,
     'L1_ffn_W2': 8.0,
     'L1_ffn_Ws1': 8.0,
     'L1_ffn_Wsg': 8.0,
     'L1_ffn_Ws2': 8.0,
     'L1_ffn_gate_w': 8.0,
     'L2_xattn_wq': 4.894,
     'L2_xattn_wqx': 3.463,
     'L2_xattn_wk': 4.876,
     'L2_ffn_W_up': 8.0,
     'L2_ffn_W_down': 8.0,
     'L2_ffn_W_q': 8.0,
     'L2_ffn_keys': 8.0,
     'L2_ffn_down_embed': 8.0,
     'L2_ffn_up_embed': 8.0,
     'L3_attn_Wq': 8.0,
     'L3_attn_Wk': 8.0,
     'L3_attn_Wv': 8.0,
     'L3_attn_Wo': 5.715,
     'L3_xattn_Wq': 200.0,
     'L3_ffn_Wq': 200.0,
     'L3_ffn_Wk': 200.0,
     'L3_ffn_Wv': 200.0,
     'L3_ffn_Wo': 200.0,
     'L3_ffn_A': 200.0,
     'L3_ffn_B': 200.0,
     'L3_ffn_W_in_base': 7.683,
     'L3_ffn_W_up_base': 7.604,
     'L3_ffn_W_down': 7.618,
     'L3_xattn_Wg': 24.485}
    for name, (base, spread) in spreads.items():
        noise = np.random.default_rng([zlib.crc32(name.encode()), seed]).standard_normal(out[name].shape)
        drawn = base * np.exp(spread * noise) if base else spread * noise
        out[name] = jnp.asarray(drawn.astype(out[name].dtype))
    for name, factor in factors.items():
        out[name] = (out[name] * factor).astype(out[name].dtype)
    return out
```

```python
from contextlib import ExitStack

import numpy as np
import concourse.bass as bass
from concourse import mybir

ACT = mybir.ActivationFunctionType
ALU = mybir.AluOpType
AX = mybir.AxisListType
F32 = mybir.dt.float32
BF16 = mybir.dt.bfloat16
I32 = mybir.dt.int32
U16 = mybir.dt.uint16
ds = bass.ds

_WEIGHTS = [
    'x_d',
    'ctx_d',
    'ctxT_d',
    'w_in_d',
    'w_dt_d',
    'b_dt_d',
    'A_d',
    'Dp_d',
    'w_mo_d',
    'w_gate_d',
    'w_up_d',
    'w_dn_d',
    'w_dn_rest_d',
    'n1_d',
    'n2_d',
    'w_th_d',
    'w_ph_d',
    'w_g_d',
    'gam0_d',
    'bet0_d',
    'w_xo_d',
    'b_th_d',
    'b_ph_d',
    'b_xo_d',
    'b_g_d',
    'w_e0_d',
    'b_e0_d',
    'w_gt0_d',
    'b_gt0_d',
    'w_qkv1_d',
    'w_o1_d',
    'w_i1_d',
    'w_oo1_d',
    'b_i1_d',
    'b_oo1_d',
    'gam1_d',
    'bet1_d',
    'dec_d',
    'w_gu1_d',
    'w_dn1_d',
    'w_gt1_d',
    'b_gt1_d',
    'bi1_d',
    'w_qkv2_d',
    'w_o2_d',
    'w_q2_d',
    'w_qx2_d',
    'w_k2_d',
    'w_v2_d',
    'w_kv2_d',
    'w_p2_d',
    'insc_d',
    'lnb2_d',
    'nw2_d',
    'smo_d',
    'wsc_d',
    'w_u2_d',
    'b_u2_d',
    'w_d2_d',
    'b_d2_d',
    'w_q2f_d',
    'keys_even_d',
    'keys_odd_d',
    'de_d',
    'ue_d',
    'ue_rest_d',
    'w_q3_d',
    'w_kr3_d',
    'w_v3_d',
    'w_o3_d',
    'b_q3_d',
    'b_k3_d',
    'b_v3_d',
    'b_o3_d',
    'w_qg3_d',
    'w_kv3_d',
    'w_ox3_d',
    'b_gx3_d',
    'w_qkv3_d',
    'w_o3f_d',
    'w_A_d',
    'w_B_d',
    'w_in3_d',
    'w_up3_d',
    'w_dn3_d',
    'l1w_d',
    'l2w_d',
]


def build_program(nc, dram, out_d):
    x_d = dram['x_d']
    ctx_d = dram['ctx_d']
    ctxT_d = dram['ctxT_d']
    w_in_d = dram['w_in_d']
    w_dt_d = dram['w_dt_d']
    b_dt_d = dram['b_dt_d']
    A_d = dram['A_d']
    Dp_d = dram['Dp_d']
    w_mo_d = dram['w_mo_d']
    w_gate_d = dram['w_gate_d']
    w_up_d = dram['w_up_d']
    w_dn_d = dram['w_dn_d']
    w_dn_rest_d = dram['w_dn_rest_d']
    n1_d = dram['n1_d']
    n2_d = dram['n2_d']
    w_th_d = dram['w_th_d']
    w_ph_d = dram['w_ph_d']
    w_g_d = dram['w_g_d']
    gam0_d = dram['gam0_d']
    bet0_d = dram['bet0_d']
    w_xo_d = dram['w_xo_d']
    b_th_d = dram['b_th_d']
    b_ph_d = dram['b_ph_d']
    b_xo_d = dram['b_xo_d']
    b_g_d = dram['b_g_d']
    w_e0_d = dram['w_e0_d']
    b_e0_d = dram['b_e0_d']
    w_gt0_d = dram['w_gt0_d']
    b_gt0_d = dram['b_gt0_d']
    w_qkv1_d = dram['w_qkv1_d']
    w_o1_d = dram['w_o1_d']
    w_i1_d = dram['w_i1_d']
    w_oo1_d = dram['w_oo1_d']
    b_i1_d = dram['b_i1_d']
    b_oo1_d = dram['b_oo1_d']
    gam1_d = dram['gam1_d']
    bet1_d = dram['bet1_d']
    dec_d = dram['dec_d']
    w_gu1_d = dram['w_gu1_d']
    w_dn1_d = dram['w_dn1_d']
    w_gt1_d = dram['w_gt1_d']
    b_gt1_d = dram['b_gt1_d']
    bi1_d = dram['bi1_d']
    w_qkv2_d = dram['w_qkv2_d']
    w_o2_d = dram['w_o2_d']
    w_q2_d = dram['w_q2_d']
    w_qx2_d = dram['w_qx2_d']
    w_k2_d = dram['w_k2_d']
    w_v2_d = dram['w_v2_d']
    w_kv2_d = dram['w_kv2_d']
    w_p2_d = dram['w_p2_d']
    insc_d = dram['insc_d']
    lnb2_d = dram['lnb2_d']
    nw2_d = dram['nw2_d']
    smo_d = dram['smo_d']
    wsc_d = dram['wsc_d']
    w_u2_d = dram['w_u2_d']
    b_u2_d = dram['b_u2_d']
    w_d2_d = dram['w_d2_d']
    b_d2_d = dram['b_d2_d']
    w_q2f_d = dram['w_q2f_d']
    keys_even_d = dram['keys_even_d']
    keys_odd_d = dram['keys_odd_d']
    de_d = dram['de_d']
    ue_d = dram['ue_d']
    ue_rest_d = dram['ue_rest_d']
    w_q3_d = dram['w_q3_d']
    w_kr3_d = dram['w_kr3_d']
    w_v3_d = dram['w_v3_d']
    w_o3_d = dram['w_o3_d']
    b_q3_d = dram['b_q3_d']
    b_k3_d = dram['b_k3_d']
    b_v3_d = dram['b_v3_d']
    b_o3_d = dram['b_o3_d']
    w_qg3_d = dram['w_qg3_d']
    w_kv3_d = dram['w_kv3_d']
    w_ox3_d = dram['w_ox3_d']
    b_gx3_d = dram['b_gx3_d']
    w_qkv3_d = dram['w_qkv3_d']
    w_o3f_d = dram['w_o3f_d']
    w_A_d = dram['w_A_d']
    w_B_d = dram['w_B_d']
    w_in3_d = dram['w_in3_d']
    w_up3_d = dram['w_up3_d']
    w_dn3_d = dram['w_dn3_d']
    l1w_d = dram['l1w_d']
    l2w_d = dram['l2w_d']
    stack = ExitStack()
    with stack:
        sbuf = stack.enter_context(nc.sbuf_tensor('sbuf', [128, 53100], F32))
        psum = stack.enter_context(nc.psum_tensor('psum', [128, 4096], F32))

        def view(memory, start, shape, dtype=F32):
            n = 1
            for d in shape:
                n *= d
            words = n if dtype in (F32, I32) else n // 2
            v = memory[:, start:start + words]
            if dtype is not F32:
                v = v.bitcast(dtype)
            if len(shape) > 1:
                names = 'abcd'[:len(shape)]
                v = v.rearrange(f"p ({' '.join(names)}) -> p {' '.join(names)}", **dict(zip(names, shape)))
            return v

        ident = view(sbuf, 0, [128])
        tri = view(sbuf, 128, [128])
        alibi = view(sbuf, 256, [128])
        causal = view(sbuf, 384, [128])
        ones = view(sbuf, 512, [128])
        mask16 = view(sbuf, 640, [8])
        mask8 = view(sbuf, 648, [16])
        eps5 = view(sbuf, 664, [1])
        eps6 = view(sbuf, 665, [1])
        one = view(sbuf, 666, [1])
        idb = view(sbuf, 667, [128], BF16)
        idb4 = view(sbuf, 667, [4, 32], BF16)
        iot = view(sbuf, 747, [128], I32)
        x = view(sbuf, 1280, [8, 256])
        x_next = view(sbuf, 1792, [8, 256])
        ctx = view(sbuf, 3328, [8, 256])
        ctxT = view(sbuf, 5376, [2, 1024])
        ps0 = view(psum, 0, [4, 512])
        psf0 = view(psum, 0, [2048])
        ps1 = view(psum, 2048, [4, 512])
        psf1 = view(psum, 2048, [2048])
        st0 = view(sbuf, 43976, [64])
        u0 = view(sbuf, 44040, [256])
        un0 = view(sbuf, 44296, [256])
        unT0 = view(sbuf, 44552, [2, 128])
        jk0 = view(sbuf, 44808, [256])
        st1 = view(sbuf, 45064, [64])
        u1 = view(sbuf, 45128, [256])
        un1 = view(sbuf, 45384, [256])
        unT1 = view(sbuf, 45640, [2, 128])
        jk1 = view(sbuf, 45896, [256])
        w_in = view(sbuf, 7424, [2, 1024])
        w_dt = view(sbuf, 9472, [256])
        b_dt = view(sbuf, 9728, [2])
        A = view(sbuf, 9730, [2, 32])
        Dp = view(sbuf, 9794, [2])
        w_mo = view(sbuf, 9796, [2, 256])
        w_gate = view(sbuf, 10308, [2, 768])
        w_up = view(sbuf, 11844, [2, 768])
        w_dn = view(sbuf, 13380, [6, 256])
        n1 = view(sbuf, 14916, [256])
        n2 = view(sbuf, 15172, [256])
        selC = view(sbuf, 15428, [32, 128], BF16)
        w_th = view(sbuf, 18376, [64])
        w_ph = view(sbuf, 18440, [64])
        w_g = view(sbuf, 18504, [64])
        gam0 = view(sbuf, 18568, [256])
        bet0 = view(sbuf, 18824, [256])
        w_xo = view(sbuf, 19080, [128])
        b_th = view(sbuf, 19208, [1])
        b_ph = view(sbuf, 19209, [1])
        b_xo = view(sbuf, 19210, [1])
        b_g = view(sbuf, 19211, [64])
        uall = view(sbuf, 19436, [8, 256])
        zx = view(sbuf, 21484, [4, 8, 128])
        dt = view(sbuf, 25580, [2, 8, 128])
        dtx = view(sbuf, 27628, [2, 8, 128])
        y = view(sbuf, 29676, [2, 8, 128])
        s3 = view(sbuf, 31724, [3, 3, 8, 128], BF16)
        f0 = view(sbuf, 46152, [4, 128])
        r0 = view(sbuf, 46664, [3, 128])
        sp0 = view(sbuf, 47048, [2, 128])
        sa0 = view(sbuf, 47304, [2, 128])
        h0 = view(sbuf, 47560, [256])
        m0 = view(sbuf, 47816, [768])
        tm0 = view(sbuf, 48584, [768])
        f1 = view(sbuf, 49352, [4, 128])
        r1 = view(sbuf, 49864, [3, 128])
        sp1 = view(sbuf, 50248, [2, 128])
        sa1 = view(sbuf, 50504, [2, 128])
        h1 = view(sbuf, 50760, [256])
        m1 = view(sbuf, 51016, [768])
        tm1 = view(sbuf, 51784, [768])
        dA0 = view(sbuf, 43976, [8, 128])
        us0 = view(sbuf, 45000, [8, 128])
        hs0 = view(sbuf, 46024, [8, 128])
        hc0 = view(sbuf, 47048, [8, 128])
        dA1 = view(sbuf, 48072, [8, 128])
        us1 = view(sbuf, 49096, [8, 128])
        hs1 = view(sbuf, 50120, [8, 128])
        hc1 = view(sbuf, 51144, [8, 128])
        dAf0 = view(sbuf, 43976, [1024])
        usf0 = view(sbuf, 45000, [1024])
        hsf0 = view(sbuf, 46024, [1024])
        dAf1 = view(sbuf, 48072, [1024])
        usf1 = view(sbuf, 49096, [1024])
        hsf1 = view(sbuf, 50120, [1024])
        w_e0 = view(sbuf, 7424, [2, 2048])
        b_e0 = view(sbuf, 11520, [2048])
        w_gt0 = view(sbuf, 13568, [2, 8])
        b_gt0 = view(sbuf, 13584, [8])
        thT0 = view(sbuf, 46152, [256])
        phT0 = view(sbuf, 46408, [256])
        S0 = view(sbuf, 46664, [2, 256])
        Pm0 = view(sbuf, 47176, [4, 128])
        g_0 = view(sbuf, 47688, [2, 64])
        t_0 = view(sbuf, 47816, [256])
        thT1 = view(sbuf, 48072, [256])
        phT1 = view(sbuf, 48328, [256])
        S1 = view(sbuf, 48584, [2, 256])
        Pm1 = view(sbuf, 49096, [4, 128])
        g_1 = view(sbuf, 49608, [2, 64])
        t_1 = view(sbuf, 49736, [256])
        w_qkv1 = view(sbuf, 18376, [2, 768])
        w_o1 = view(sbuf, 19912, [2, 256])
        lg0_0 = view(sbuf, 46152, [8])
        mk0_0 = view(sbuf, 46160, [8])
        r0_0 = view(sbuf, 46168, [2, 256])
        acc0_0 = view(sbuf, 46680, [256])
        lg0_1 = view(sbuf, 46936, [8])
        mk0_1 = view(sbuf, 46944, [8])
        r0_1 = view(sbuf, 46952, [2, 256])
        acc0_1 = view(sbuf, 47464, [256])
        w_i1 = view(sbuf, 7424, [2, 256])
        w_oo1 = view(sbuf, 7936, [2, 256])
        b_i1 = view(sbuf, 8448, [2])
        b_oo1 = view(sbuf, 8450, [256])
        gam1 = view(sbuf, 8706, [256])
        bet1 = view(sbuf, 8962, [256])
        dec = view(sbuf, 9218, [1])
        Kt = view(sbuf, 9219, [128])
        k1_0 = view(sbuf, 46152, [256])
        q1_0 = view(sbuf, 46408, [256])
        kv1_0 = view(sbuf, 46664, [256])
        vT1_0 = view(sbuf, 46920, [2, 128])
        k1_1 = view(sbuf, 47176, [256])
        q1_1 = view(sbuf, 47432, [256])
        kv1_1 = view(sbuf, 47688, [256])
        vT1_1 = view(sbuf, 47944, [2, 128])
        w_gu1 = view(sbuf, 18376, [2, 4096])
        w_dn1 = view(sbuf, 26568, [8, 2, 256])
        w_gt1 = view(sbuf, 30664, [2, 7])
        b_gt1 = view(sbuf, 30678, [7])
        bi1 = view(sbuf, 30685, [7])
        xi_0 = view(sbuf, 46152, [2, 128])
        ss_0 = view(sbuf, 46408, [2, 128])
        mn_0 = view(sbuf, 46664, [2, 128])
        xi_1 = view(sbuf, 46920, [2, 128])
        ss_1 = view(sbuf, 47176, [2, 128])
        mn_1 = view(sbuf, 47432, [2, 128])
        w_qkv2 = view(sbuf, 7424, [2, 768])
        w_o2 = view(sbuf, 8960, [2, 256])
        lg1_0 = view(sbuf, 46152, [8])
        pr1_0 = view(sbuf, 46160, [8])
        bp1_0 = view(sbuf, 46168, [8])
        wv1_0 = view(sbuf, 46176, [8])
        m1_0 = view(sbuf, 46184, [2, 256])
        t1_0 = view(sbuf, 46696, [256])
        acc1_0 = view(sbuf, 46952, [256])
        lg1_1 = view(sbuf, 47208, [8])
        pr1_1 = view(sbuf, 47216, [8])
        bp1_1 = view(sbuf, 47224, [8])
        wv1_1 = view(sbuf, 47232, [8])
        m1_1 = view(sbuf, 47240, [2, 256])
        t1_1 = view(sbuf, 47752, [256])
        acc1_1 = view(sbuf, 48008, [256])
        w_q2 = view(sbuf, 18376, [2, 2048])
        w_qx2 = view(sbuf, 22472, [2, 2048])
        w_k2 = view(sbuf, 26568, [2, 1024])
        w_v2 = view(sbuf, 28616, [2, 1024])
        w_kv2 = view(sbuf, 30664, [2, 2048])
        w_p2 = view(sbuf, 34760, [32, 256])
        insc = view(sbuf, 42952, [4, 2])
        inrc = view(sbuf, 42960, [4, 2])
        lnb2 = view(sbuf, 42968, [2, 256])
        nw2 = view(sbuf, 43480, [4, 2])
        smo = view(sbuf, 43488, [32])
        smr = view(sbuf, 43520, [32])
        wsc = view(sbuf, 43552, [8])
        S_0 = view(sbuf, 46152, [4, 128])
        PT_0 = view(sbuf, 46664, [4, 128])
        ao_0 = view(sbuf, 47176, [256])
        qT_0 = view(sbuf, 47432, [2, 128])
        S_1 = view(sbuf, 47688, [4, 128])
        PT_1 = view(sbuf, 48200, [4, 128])
        ao_1 = view(sbuf, 48712, [256])
        qT_1 = view(sbuf, 48968, [2, 128])
        v_0 = view(sbuf, 49224, [16, 17])
        v_1 = view(sbuf, 49496, [16, 17])
        kM_0 = view(sbuf, 11520, [2, 8, 128])
        kM_1 = view(sbuf, 13568, [2, 8, 128])
        w_u2 = view(sbuf, 7424, [2, 1024])
        b_u2 = view(sbuf, 9472, [8])
        w_d2 = view(sbuf, 9480, [8, 128])
        b_d2 = view(sbuf, 10504, [1])
        w_q2f = view(sbuf, 10505, [1024])
        keys = view(sbuf, 11529, [8, 90])
        de = view(sbuf, 12249, [2025])
        ue = view(sbuf, 14274, [16, 256])
        xs_0 = view(sbuf, 46152, [4, 2, 128])
        qk_0 = view(sbuf, 47176, [6, 128])
        qT2_0 = view(sbuf, 47944, [512])
        PT2_0 = view(sbuf, 48456, [512])
        s6_0 = view(sbuf, 48968, [6, 6])
        mv_0 = view(sbuf, 49004, [6, 2])
        xs_1 = view(sbuf, 49016, [4, 2, 128])
        qk_1 = view(sbuf, 50040, [6, 128])
        qT2_1 = view(sbuf, 50808, [512])
        PT2_1 = view(sbuf, 51320, [512])
        s6_1 = view(sbuf, 51832, [6, 6])
        mv_1 = view(sbuf, 51868, [6, 2])
        vv_0 = view(sbuf, 51880, [6])
        rr_0 = view(sbuf, 51886, [6])
        P2_0 = view(sbuf, 51892, [4, 128])
        vv_1 = view(sbuf, 52404, [6])
        rr_1 = view(sbuf, 52410, [6])
        P2_1 = view(sbuf, 52416, [4, 128])
        v2_0 = view(sbuf, 14280, [256])
        kT2_0 = view(sbuf, 14536, [256])
        cx_0 = view(sbuf, 14792, [2, 128])
        y16_0 = view(sbuf, 15048, [1024], BF16)
        v2_1 = view(sbuf, 15560, [256])
        kT2_1 = view(sbuf, 15816, [256])
        cx_1 = view(sbuf, 16072, [2, 128])
        y16_1 = view(sbuf, 16328, [1024], BF16)
        y16u_0 = view(sbuf, 15048, [1024], U16)
        y16u_1 = view(sbuf, 16328, [1024], U16)
        e16_0 = view(sbuf, 16840, [1024], U16)
        e16_1 = view(sbuf, 17352, [1024], U16)
        e16b_0 = view(sbuf, 16840, [1024], BF16)
        e16b_1 = view(sbuf, 17352, [1024], BF16)
        qq_0 = view(sbuf, 47176, [1024])
        P2f_0 = view(sbuf, 51892, [512])
        xsf_0 = view(sbuf, 46152, [1024])
        qq_1 = view(sbuf, 50040, [1024])
        P2f_1 = view(sbuf, 52416, [512])
        xsf_1 = view(sbuf, 49016, [1024])
        srow = view(sbuf, 43576, [2, 6])
        ssq = view(sbuf, 43588, [2, 6])
        wps = view(sbuf, 43600, [1])
        w_q3 = view(sbuf, 18376, [2, 256])
        w_kr3 = view(sbuf, 18888, [2, 256])
        w_v3 = view(sbuf, 19400, [2, 64])
        w_o3 = view(sbuf, 19528, [2, 256])
        b_q3 = view(sbuf, 20040, [2])
        b_k3 = view(sbuf, 20042, [2])
        b_v3 = view(sbuf, 20044, [64])
        b_o3 = view(sbuf, 20108, [256])
        h2T_0 = view(sbuf, 46152, [128])
        sim_0 = view(sbuf, 46280, [2, 8, 45])
        v8_0 = view(sbuf, 47000, [2, 8, 8])
        c_0 = view(sbuf, 47128, [8, 8, 8])
        t8_0 = view(sbuf, 47640, [8, 8])
        d8_0 = view(sbuf, 47704, [8])
        q8_0 = view(sbuf, 47712, [8])
        qc_0 = view(sbuf, 47720, [8, 128])
        h2T_1 = view(sbuf, 48744, [128])
        sim_1 = view(sbuf, 48872, [2, 8, 45])
        v8_1 = view(sbuf, 49592, [2, 8, 8])
        c_1 = view(sbuf, 49720, [8, 8, 8])
        t8_1 = view(sbuf, 50232, [8, 8])
        d8_1 = view(sbuf, 50296, [8])
        q8_1 = view(sbuf, 50304, [8])
        qc_1 = view(sbuf, 50312, [8, 128])
        z_0 = view(sbuf, 20424, [2048])
        Pra_0 = view(sbuf, 22472, [45, 45])
        Prb_0 = view(sbuf, 24497, [45, 45])
        z_1 = view(sbuf, 30572, [2048])
        Pra_1 = view(sbuf, 32620, [45, 45])
        Prb_1 = view(sbuf, 34645, [45, 45])
        Pfa_0 = view(sbuf, 22472, [2025])
        Pfb_0 = view(sbuf, 24497, [2025])
        Qfa_0 = view(sbuf, 26522, [2025])
        Qfb_0 = view(sbuf, 28547, [2025])
        GT_0 = view(sbuf, 26522, [16, 128])
        hb_0 = view(sbuf, 22472, [8, 128])
        he_0 = view(sbuf, 24497, [8, 128])
        Pfa_1 = view(sbuf, 32620, [2025])
        Pfb_1 = view(sbuf, 34645, [2025])
        Qfa_1 = view(sbuf, 36670, [2025])
        Qfb_1 = view(sbuf, 38695, [2025])
        GT_1 = view(sbuf, 36670, [16, 128])
        hb_1 = view(sbuf, 32620, [8, 128])
        he_1 = view(sbuf, 34645, [8, 128])
        w_qg3 = view(sbuf, 7424, [2, 512])
        w_kv3 = view(sbuf, 8448, [2, 512])
        w_ox3 = view(sbuf, 9472, [2, 256])
        b_gx3 = view(sbuf, 9984, [256])
        vg_0 = view(sbuf, 49224, [8, 9])
        vg_1 = view(sbuf, 49296, [8, 9])
        kR_0 = view(sbuf, 34760, [2, 16, 128])
        kR_1 = view(sbuf, 38856, [2, 16, 128])
        kT3_0 = view(sbuf, 49368, [2, 128])
        kT3_1 = view(sbuf, 49624, [2, 128])
        w_qkv3 = view(sbuf, 20424, [2, 768])
        w_o3f = view(sbuf, 21960, [2, 256])
        w_A = view(sbuf, 22472, [2, 16])
        w_B = view(sbuf, 22504, [1024])
        w_in3 = view(sbuf, 23528, [2, 1024])
        w_up3 = view(sbuf, 25576, [2, 1024])
        w_dn3 = view(sbuf, 27624, [8, 256])
        l1w = view(sbuf, 29672, [256])
        l2w = view(sbuf, 29928, [256])
        cT_0 = view(sbuf, 46152, [2, 128])
        q3_0 = view(sbuf, 46408, [256])
        k3_0 = view(sbuf, 46664, [256])
        v3_0 = view(sbuf, 46920, [2, 129])
        ks_0 = view(sbuf, 47178, [256])
        BD_0 = view(sbuf, 47434, [2, 136])
        ga_0 = view(sbuf, 47706, [256])
        a3_0 = view(sbuf, 47962, [256])
        rd_0 = view(sbuf, 48218, [16])
        cT_1 = view(sbuf, 48234, [2, 128])
        q3_1 = view(sbuf, 48490, [256])
        k3_1 = view(sbuf, 48746, [256])
        v3_1 = view(sbuf, 49002, [2, 129])
        ks_1 = view(sbuf, 49260, [256])
        BD_1 = view(sbuf, 49516, [2, 136])
        ga_1 = view(sbuf, 49788, [256])
        a3_1 = view(sbuf, 50044, [256])
        rd_1 = view(sbuf, 50300, [16])
        kM3_0 = view(sbuf, 10924, [2, 8, 128])
        kM3_1 = view(sbuf, 12972, [2, 8, 128])
        md_0 = view(sbuf, 49768, [128])
        hA_0 = view(sbuf, 49896, [128])
        md_1 = view(sbuf, 50024, [128])
        hA_1 = view(sbuf, 50152, [128])
        m3_0 = view(sbuf, 36376, [1024])
        tt_0 = view(sbuf, 37400, [1024])
        m3_1 = view(sbuf, 38424, [1024])
        tt_1 = view(sbuf, 39448, [1024])
        L0a_matmul_done = stack.enter_context(nc.semaphore('L0a_matmul_done'))
        L0a_pool_done = stack.enter_context(nc.semaphore('L0a_pool_done'))
        L0a_scalar_done = stack.enter_context(nc.semaphore('L0a_scalar_done'))
        L0a_vector_done = stack.enter_context(nc.semaphore('L0a_vector_done'))
        L0a_w_loaded = stack.enter_context(nc.semaphore('L0a_w_loaded'))
        L0f_matmul_done = stack.enter_context(nc.semaphore('L0f_matmul_done'))
        L0f_pool_done = stack.enter_context(nc.semaphore('L0f_pool_done'))
        L0f_scalar_done = stack.enter_context(nc.semaphore('L0f_scalar_done'))
        L0f_vector_done = stack.enter_context(nc.semaphore('L0f_vector_done'))
        L0f_w_loaded = stack.enter_context(nc.semaphore('L0f_w_loaded'))
        L0x_matmul_done = stack.enter_context(nc.semaphore('L0x_matmul_done'))
        L0x_pool_done = stack.enter_context(nc.semaphore('L0x_pool_done'))
        L0x_scalar_done = stack.enter_context(nc.semaphore('L0x_scalar_done'))
        L0x_vector_done = stack.enter_context(nc.semaphore('L0x_vector_done'))
        L0x_w_loaded = stack.enter_context(nc.semaphore('L0x_w_loaded'))
        L1a_matmul_done = stack.enter_context(nc.semaphore('L1a_matmul_done'))
        L1a_scalar_done = stack.enter_context(nc.semaphore('L1a_scalar_done'))
        L1a_vector_done = stack.enter_context(nc.semaphore('L1a_vector_done'))
        L1a_w_loaded = stack.enter_context(nc.semaphore('L1a_w_loaded'))
        L1f_matmul_done = stack.enter_context(nc.semaphore('L1f_matmul_done'))
        L1f_pool_done = stack.enter_context(nc.semaphore('L1f_pool_done'))
        L1f_scalar_done = stack.enter_context(nc.semaphore('L1f_scalar_done'))
        L1f_vector_done = stack.enter_context(nc.semaphore('L1f_vector_done'))
        L1f_w_loaded = stack.enter_context(nc.semaphore('L1f_w_loaded'))
        L1x_matmul_done = stack.enter_context(nc.semaphore('L1x_matmul_done'))
        L1x_pool_done = stack.enter_context(nc.semaphore('L1x_pool_done'))
        L1x_scalar_done = stack.enter_context(nc.semaphore('L1x_scalar_done'))
        L1x_vector_done = stack.enter_context(nc.semaphore('L1x_vector_done'))
        L1x_w_loaded = stack.enter_context(nc.semaphore('L1x_w_loaded'))
        L2a_matmul_done = stack.enter_context(nc.semaphore('L2a_matmul_done'))
        L2a_scalar_done = stack.enter_context(nc.semaphore('L2a_scalar_done'))
        L2a_vector_done = stack.enter_context(nc.semaphore('L2a_vector_done'))
        L2a_w_loaded = stack.enter_context(nc.semaphore('L2a_w_loaded'))
        L2f_matmul_done = stack.enter_context(nc.semaphore('L2f_matmul_done'))
        L2f_pool_done = stack.enter_context(nc.semaphore('L2f_pool_done'))
        L2f_scalar_done = stack.enter_context(nc.semaphore('L2f_scalar_done'))
        L2f_ue_loaded = stack.enter_context(nc.semaphore('L2f_ue_loaded'))
        L2f_vector_done = stack.enter_context(nc.semaphore('L2f_vector_done'))
        L2f_w_loaded = stack.enter_context(nc.semaphore('L2f_w_loaded'))
        L2x_matmul_done = stack.enter_context(nc.semaphore('L2x_matmul_done'))
        L2x_pool_done = stack.enter_context(nc.semaphore('L2x_pool_done'))
        L2x_scalar_done = stack.enter_context(nc.semaphore('L2x_scalar_done'))
        L2x_vector_done = stack.enter_context(nc.semaphore('L2x_vector_done'))
        L2x_w_loaded = stack.enter_context(nc.semaphore('L2x_w_loaded'))
        L3a_matmul_done = stack.enter_context(nc.semaphore('L3a_matmul_done'))
        L3a_pool_done = stack.enter_context(nc.semaphore('L3a_pool_done'))
        L3a_scalar_done = stack.enter_context(nc.semaphore('L3a_scalar_done'))
        L3a_vector_done = stack.enter_context(nc.semaphore('L3a_vector_done'))
        L3a_w_loaded = stack.enter_context(nc.semaphore('L3a_w_loaded'))
        L3f_matmul_done = stack.enter_context(nc.semaphore('L3f_matmul_done'))
        L3f_pool_done = stack.enter_context(nc.semaphore('L3f_pool_done'))
        L3f_scalar_done = stack.enter_context(nc.semaphore('L3f_scalar_done'))
        L3f_vector_done = stack.enter_context(nc.semaphore('L3f_vector_done'))
        L3f_w_loaded = stack.enter_context(nc.semaphore('L3f_w_loaded'))
        L3x_matmul_done = stack.enter_context(nc.semaphore('L3x_matmul_done'))
        L3x_pool_done = stack.enter_context(nc.semaphore('L3x_pool_done'))
        L3x_scalar_done = stack.enter_context(nc.semaphore('L3x_scalar_done'))
        L3x_vector_done = stack.enter_context(nc.semaphore('L3x_vector_done'))
        L3x_w_loaded = stack.enter_context(nc.semaphore('L3x_w_loaded'))
        act_waited = stack.enter_context(nc.semaphore('act_waited'))
        ctx_loaded = stack.enter_context(nc.semaphore('ctx_loaded'))
        dve_waited = stack.enter_context(nc.semaphore('dve_waited'))
        out_loaded = stack.enter_context(nc.semaphore('out_loaded'))
        pe_waited = stack.enter_context(nc.semaphore('pe_waited'))
        pool_waited = stack.enter_context(nc.semaphore('pool_waited'))
        setup_pool_done = stack.enter_context(nc.semaphore('setup_pool_done'))
        x_loaded = stack.enter_context(nc.semaphore('x_loaded'))
        block = stack.enter_context(nc.Block())

        @block.sync
        def _(sp):

            sp.dma_start(x[:, :, :], x_d).then_inc(x_loaded, 16)
            sp.dma_start(ctx[:, :, :], ctx_d).then_inc(ctx_loaded, 16)
            sp.dma_start(ctxT[:, :, :], ctxT_d).then_inc(ctx_loaded, 16)
            sp.dma_start(w_in[:, :, :], w_in_d).then_inc(L0a_w_loaded, 16)
            sp.dma_start(w_dt[:, :], w_dt_d).then_inc(L0a_w_loaded, 16)
            sp.dma_start(b_dt[:, :], b_dt_d).then_inc(L0a_w_loaded, 16)
            sp.dma_start(A[:, :, :], A_d).then_inc(L0a_w_loaded, 16)
            sp.dma_start(Dp[:, :], Dp_d).then_inc(L0a_w_loaded, 16)
            sp.dma_start(w_mo[:, :, :], w_mo_d).then_inc(L0a_w_loaded, 16)
            sp.dma_start(w_gate[:, :, 0:704], w_gate_d).then_inc(L0a_w_loaded, 16)
            sp.dma_start(w_up[:, :, 0:704], w_up_d).then_inc(L0a_w_loaded, 16)
            sp.dma_start(w_dn[:, 0:5, :], w_dn_d).then_inc(L0a_w_loaded, 16)
            sp.wait_ge(L0a_pool_done, 1)
            sp.dma_start(w_dn[0:64, 5, :], w_dn_rest_d).then_inc(L0a_w_loaded, 16)
            sp.dma_start(n1[:, :], n1_d.to_broadcast([128, 256])).then_inc(L0a_w_loaded, 16)
            sp.dma_start(n2[:, :], n2_d.to_broadcast([128, 256])).then_inc(L0a_w_loaded, 16)
            sp.dma_start(w_th[:, :], w_th_d).then_inc(L0x_w_loaded, 16)
            sp.dma_start(w_ph[:, :], w_ph_d).then_inc(L0x_w_loaded, 16)
            sp.dma_start(w_g[:, :], w_g_d).then_inc(L0x_w_loaded, 16)
            sp.dma_start(gam0[0:64, :], gam0_d).then_inc(L0x_w_loaded, 16)
            sp.dma_start(bet0[0:64, :], bet0_d).then_inc(L0x_w_loaded, 16)
            sp.dma_start(w_xo[0:64, :], w_xo_d).then_inc(L0x_w_loaded, 16)
            sp.dma_start(b_th[0:64, :], b_th_d).then_inc(L0x_w_loaded, 16)
            sp.dma_start(b_ph[0:64, :], b_ph_d).then_inc(L0x_w_loaded, 16)
            sp.dma_start(b_xo[:, :], b_xo_d).then_inc(L0x_w_loaded, 16)
            sp.dma_start(b_g[:, :], b_g_d.to_broadcast([128, 64])).then_inc(L0x_w_loaded, 16)

            sp.wait_ge(L0a_w_loaded, 192)
            sp.wait_ge(L0a_scalar_done, 154)
            sp.wait_ge(L0a_vector_done, 329)
            sp.wait_ge(L0a_matmul_done, 186)
            sp.dma_start(w_e0[:, :, :], w_e0_d).then_inc(L0f_w_loaded, 16)
            sp.wait_ge(L0a_w_loaded, 192)
            sp.wait_ge(L0a_matmul_done, 190)
            sp.dma_start(b_e0[:, :], b_e0_d.to_broadcast([128, 2048])).then_inc(L0f_w_loaded, 16)
            sp.dma_start(w_gt0[:, :, :], w_gt0_d).then_inc(L0f_w_loaded, 16)
            sp.dma_start(b_gt0[:, :], b_gt0_d.to_broadcast([128, 8])).then_inc(L0f_w_loaded, 16)

            sp.wait_ge(L0x_w_loaded, 160)
            sp.wait_ge(L0a_pool_done, 10)
            sp.wait_ge(L0x_matmul_done, 56)
            sp.wait_ge(L0x_vector_done, 186)
            sp.dma_start(w_qkv1[:, :, :], w_qkv1_d).then_inc(L1a_w_loaded, 16)
            sp.dma_start(w_o1[:, :, :], w_o1_d).then_inc(L1a_w_loaded, 16)

            sp.wait_ge(L0f_w_loaded, 64)
            sp.wait_ge(L0f_matmul_done, 40)
            sp.dma_start(w_i1[:, :, :], w_i1_d).then_inc(L1x_w_loaded, 16)
            sp.wait_ge(L0f_matmul_done, 44)
            sp.dma_start(w_oo1[:, :, :], w_oo1_d).then_inc(L1x_w_loaded, 16)
            sp.wait_ge(L0f_matmul_done, 46)
            sp.dma_start(b_i1[:, :], b_i1_d).then_inc(L1x_w_loaded, 16)
            sp.dma_start(b_oo1[:, :], b_oo1_d.to_broadcast([128, 256])).then_inc(L1x_w_loaded, 16)
            sp.wait_ge(L0f_matmul_done, 48)
            sp.dma_start(gam1[:, :], gam1_d.to_broadcast([128, 256])).then_inc(L1x_w_loaded, 16)
            sp.dma_start(bet1[:, :], bet1_d.to_broadcast([128, 256])).then_inc(L1x_w_loaded, 16)
            sp.dma_start(dec[:, :], dec_d.to_broadcast([128, 1])).then_inc(L1x_w_loaded, 16)

            sp.wait_ge(L0a_scalar_done, 192)
            sp.wait_ge(L1a_w_loaded, 32)
            sp.wait_ge(L1a_matmul_done, 48)
            sp.dma_start(w_gu1[:, :, :], w_gu1_d).then_inc(L1f_w_loaded, 16)
            sp.wait_ge(L0a_pool_done, 73)
            sp.dma_start(w_dn1[:, :, :, :], w_dn1_d).then_inc(L1f_w_loaded, 16)
            sp.dma_start(w_gt1[:, :, :], w_gt1_d).then_inc(L1f_w_loaded, 16)
            sp.dma_start(b_gt1[:, :], b_gt1_d.to_broadcast([128, 7])).then_inc(L1f_w_loaded, 16)
            sp.dma_start(bi1[:, :], bi1_d.to_broadcast([128, 7])).then_inc(L1f_w_loaded, 16)

            sp.wait_ge(L1x_w_loaded, 112)
            sp.wait_ge(L1x_vector_done, 74)
            sp.wait_ge(L1x_matmul_done, 16)
            sp.wait_ge(L1x_pool_done, 26)
            sp.dma_start(w_qkv2[:, :, :], w_qkv2_d).then_inc(L2a_w_loaded, 16)
            sp.wait_ge(L1x_w_loaded, 112)
            sp.wait_ge(L1x_vector_done, 76)
            sp.wait_ge(L1x_pool_done, 27)
            sp.dma_start(w_o2[:, :, :], w_o2_d).then_inc(L2a_w_loaded, 16)

            sp.wait_ge(L1f_w_loaded, 80)
            sp.wait_ge(L1f_matmul_done, 148)
            sp.dma_start(w_q2[:, :, :], w_q2_d).then_inc(L2x_w_loaded, 16)
            sp.dma_start(w_qx2[:, :, :], w_qx2_d).then_inc(L2x_w_loaded, 16)
            sp.wait_ge(L1f_w_loaded, 80)
            sp.dma_start(w_k2[:, :, :], w_k2_d).then_inc(L2x_w_loaded, 16)
            sp.wait_ge(L1f_matmul_done, 154)
            sp.dma_start(w_v2[:, :, :], w_v2_d).then_inc(L2x_w_loaded, 16)
            sp.wait_ge(L1f_w_loaded, 80)
            sp.wait_ge(L1f_vector_done, 247)
            sp.dma_start(w_kv2[:, :, :], w_kv2_d).then_inc(L2x_w_loaded, 16)
            sp.dma_start(w_p2[:, :, :], w_p2_d).then_inc(L2x_w_loaded, 16)
            sp.dma_start(insc[:, :, :], insc_d).then_inc(L2x_w_loaded, 16)
            sp.dma_start(lnb2[:, :, :], lnb2_d.to_broadcast([128, 2, 256])).then_inc(L2x_w_loaded, 16)
            sp.dma_start(nw2[:, :, :], nw2_d).then_inc(L2x_w_loaded, 16)
            sp.dma_start(smo[:, :], smo_d).then_inc(L2x_w_loaded, 16)
            sp.dma_start(wsc[:, 0:6], wsc_d.to_broadcast([128, 6])).then_inc(L2x_w_loaded, 16)

            sp.wait_ge(L2a_w_loaded, 32)
            sp.wait_ge(L2a_matmul_done, 116)
            sp.dma_start(w_u2[:, :, :], w_u2_d).then_inc(L2f_w_loaded, 16)
            sp.dma_start(b_u2[:, :], b_u2_d).then_inc(L2f_w_loaded, 16)
            sp.dma_start(w_d2[:, :, :], w_d2_d).then_inc(L2f_w_loaded, 16)
            sp.dma_start(b_d2[:, :], b_d2_d).then_inc(L2f_w_loaded, 16)
            sp.wait_ge(L0f_w_loaded, 64)
            sp.wait_ge(L2a_vector_done, 191)
            sp.dma_start(w_q2f[:, :], w_q2f_d).then_inc(L2f_w_loaded, 16)
            sp.wait_ge(L2f_pool_done, 4)
            sp.dma_start(keys[0:64, :, 0:45], keys_even_d).then_inc(L2f_w_loaded, 16)
            sp.dma_start(keys[64:128, :, 45:90], keys_odd_d).then_inc(L2f_w_loaded, 16)
            sp.wait_ge(L2a_vector_done, 193)
            sp.dma_start(de[:, :], de_d).then_inc(L2f_w_loaded, 16)

            sp.wait_ge(L2x_scalar_done, 534)
            sp.wait_ge(L2x_matmul_done, 510)
            sp.wait_ge(L2x_vector_done, 1120)
            sp.wait_ge(L2x_pool_done, 210)
            sp.dma_start(ue[:, 0:15, :], ue_d).then_inc(L2f_ue_loaded, 16)
            sp.dma_start(ue[0:105, 15, :], ue_rest_d).then_inc(L2f_ue_loaded, 16)
            sp.wait_ge(L2x_w_loaded, 176)
            sp.dma_start(w_q3[:, :, :], w_q3_d).then_inc(L3a_w_loaded, 16)
            sp.dma_start(w_kr3[:, :, :], w_kr3_d).then_inc(L3a_w_loaded, 16)
            sp.dma_start(w_v3[:, :, :], w_v3_d).then_inc(L3a_w_loaded, 16)
            sp.dma_start(w_o3[:, :, :], w_o3_d).then_inc(L3a_w_loaded, 16)
            sp.dma_start(b_q3[:, :], b_q3_d).then_inc(L3a_w_loaded, 16)
            sp.dma_start(b_k3[:, :], b_k3_d).then_inc(L3a_w_loaded, 16)
            sp.dma_start(b_v3[:, :], b_v3_d.to_broadcast([128, 64])).then_inc(L3a_w_loaded, 16)
            sp.dma_start(b_o3[:, :], b_o3_d.to_broadcast([128, 256])).then_inc(L3a_w_loaded, 16)

            sp.wait_ge(L2f_w_loaded, 128)
            sp.wait_ge(L2f_matmul_done, 91)
            sp.dma_start(w_qg3[:, :, :], w_qg3_d).then_inc(L3x_w_loaded, 16)
            sp.dma_start(w_kv3[:, :, :], w_kv3_d).then_inc(L3x_w_loaded, 16)
            sp.wait_ge(L2f_w_loaded, 128)
            sp.wait_ge(L2f_vector_done, 216)
            sp.wait_ge(L2f_matmul_done, 93)
            sp.dma_start(w_ox3[:, :, :], w_ox3_d).then_inc(L3x_w_loaded, 16)
            sp.dma_start(b_gx3[:, :], b_gx3_d.to_broadcast([128, 256])).then_inc(L3x_w_loaded, 16)

            sp.wait_ge(L2f_scalar_done, 159)
            sp.wait_ge(L2f_vector_done, 260)
            sp.dma_start(w_qkv3[:, :, :], w_qkv3_d).then_inc(L3f_w_loaded, 16)
            sp.dma_start(w_o3f[:, :, :], w_o3f_d).then_inc(L3f_w_loaded, 16)
            sp.wait_ge(L2x_w_loaded, 176)
            sp.wait_ge(L2f_pool_done, 73)
            sp.dma_start(w_A[:, :, :], w_A_d).then_inc(L3f_w_loaded, 16)
            sp.dma_start(w_B[0:16, :], w_B_d).then_inc(L3f_w_loaded, 16)
            sp.wait_ge(L2f_pool_done, 75)
            sp.dma_start(w_in3[:, :, :], w_in3_d).then_inc(L3f_w_loaded, 16)
            sp.wait_ge(L2x_w_loaded, 176)
            sp.wait_ge(L2f_scalar_done, 180)
            sp.wait_ge(L2f_matmul_done, 114)
            sp.dma_start(w_up3[:, :, :], w_up3_d).then_inc(L3f_w_loaded, 16)
            sp.wait_ge(L2x_w_loaded, 176)
            sp.wait_ge(L2f_scalar_done, 182)
            sp.wait_ge(L2f_matmul_done, 115)
            sp.dma_start(w_dn3[:, :, :], w_dn3_d).then_inc(L3f_w_loaded, 16)
            sp.dma_start(l1w[:, :], l1w_d.to_broadcast([128, 256])).then_inc(L3f_w_loaded, 16)
            sp.dma_start(l2w[:, :], l2w_d.to_broadcast([128, 256])).then_inc(L3f_w_loaded, 16)



            sp.wait_ge(L3x_vector_done, 128)
            sp.wait_ge(L3f_pool_done, 8)
            sp.dma_start(out_d, x[:, :, :]).then_inc(out_loaded, 16)
            sp.wait_ge(out_loaded, 16)

        @block.gpsimd
        def _(pool):

            pool.memset(ones[:, :], 1.0)
            pool.memset(ident[:, :], 0.0).then_inc(setup_pool_done, 1)
            pool.memset(causal[:, :], 0.0).then_inc(setup_pool_done, 1)
            pool.memset(mask16[:, :], 1.0)
            pool.memset(mask8[:, :], 1.0)
            pool.memset(eps5[:, :], 1e-5)
            pool.memset(eps6[:, :], 1e-6)
            pool.memset(one[:, :], 1.0)
            pool.wait_ge(setup_pool_done, 1)
            pool.affine_select(out=ident[:, :], in_=ident[:, :], compare_op=ALU.not_equal, fill=1.0, base=0, pattern=[[-1, 128]], channel_multiplier=1)
            pool.affine_select(out=tri[:, :], in_=ones[:, :], compare_op=ALU.is_ge, fill=0.0, base=0, pattern=[[1, 128]], channel_multiplier=-1)
            pool.wait_ge(setup_pool_done, 2)
            pool.affine_select(out=causal[:, :], in_=causal[:, :], compare_op=ALU.is_ge, fill=-1e30, base=0, pattern=[[-1, 128]], channel_multiplier=1)
            pool.iota(iot[:, :], pattern=[[1, 128]], base=0, channel_multiplier=-1).then_inc(setup_pool_done, 1)
            pool.wait_ge(setup_pool_done, 3)
            pool.tensor_copy(alibi[:, :], iot[:, :]).then_inc(setup_pool_done, 1)
            pool.wait_ge(setup_pool_done, 4)
            pool.affine_select(out=alibi[:, :], in_=alibi[:, :], compare_op=ALU.is_ge, fill=-1e30, base=0, pattern=[[-1, 128]], channel_multiplier=1)
            pool.affine_select(out=mask16[:, :], in_=mask16[:, :], compare_op=ALU.is_ge, fill=0.0, base=0, pattern=[[-16, 8]], channel_multiplier=1).then_inc(setup_pool_done, 1)
            pool.wait_ge(setup_pool_done, 5)
            pool.affine_select(out=mask16[:, :], in_=mask16[:, :], compare_op=ALU.is_ge, fill=0.0, base=15, pattern=[[16, 8]], channel_multiplier=-1)
            pool.affine_select(out=mask8[:, :], in_=mask8[:, :], compare_op=ALU.is_ge, fill=0.0, base=0, pattern=[[-8, 16]], channel_multiplier=1).then_inc(setup_pool_done, 1)
            pool.wait_ge(setup_pool_done, 6)
            pool.affine_select(out=mask8[:, :], in_=mask8[:, :], compare_op=ALU.is_ge, fill=0.0, base=7, pattern=[[8, 16]], channel_multiplier=-1)
            pool.tensor_copy(idb[:, :], ident[:, :]).then_inc(setup_pool_done, 1)
            pool.memset(w_gate[:, :, 704:768], 0.0)
            pool.memset(w_up[:, :, 704:768], 0.0)
            pool.memset(w_dn[:, 5, :], 0.0).then_inc(L0a_pool_done, 1)

            pool.memset(y[:, :, :, :], 0.0).then_inc(L0a_pool_done, 1)
            pool.wait_ge(L0a_vector_done, 16)
            with pool.Fori(0, 4) as b:
                pool.wait_ge(L0a_vector_done, 20*b + 3)
                pool.sem_inc(pool_waited, 1)
                pool.tensor_copy(uall[:, 2*b+0, :], u0[:, :]).then_inc(L0a_pool_done, 1)
                pool.wait_ge(L0a_vector_done, 20*b + 10)
                pool.sem_inc(pool_waited, 1)
                pool.tensor_copy(uall[:, 2*b+1, :], u1[:, :]).then_inc(L0a_pool_done, 1)
            pool.wait_ge(L0a_pool_done, 2)
            with pool.Fori(0, 32) as n:
                pool.wait_ge(L0a_vector_done, 6*n + 103)
                pool.tensor_tensor(y[:, 0, :, :], y[:, 0, :, :], hc0[:, :, :], ALU.add).then_inc(L0a_pool_done, 1)
                pool.wait_ge(L0a_vector_done, 6*n + 105)
                pool.tensor_tensor(y[:, 1, :, :], y[:, 1, :, :], hc1[:, :, :], ALU.add).then_inc(L0a_pool_done, 1)
            pool.wait_ge(L0a_vector_done, 290)
            with pool.Fori(0, 4) as b:
                pool.wait_ge(L0a_vector_done, 12*b + 302)
                pool.sem_inc(pool_waited, 1)
                pool.tensor_tensor(x[:, 2*b+0, :], x[:, 2*b+0, :], h0[:, :], ALU.add).then_inc(L0a_pool_done, 1)
                pool.wait_ge(L0a_vector_done, 12*b + 303)
                pool.sem_inc(pool_waited, 1)
                pool.tensor_tensor(x[:, 2*b+1, :], x[:, 2*b+1, :], h1[:, :], ALU.add).then_inc(L0a_pool_done, 1)

            pool.sem_inc(L0x_pool_done, 4)
            pool.wait_ge(L0x_vector_done, 36)
            with pool.Fori(0, 4) as b:
                pool.wait_ge(L0x_vector_done, 38*b + 45)
                pool.tensor_tensor(S0[:, :, :], S0[:, :, :], st0[:, 16:18].unsqueeze(2).to_broadcast([128, 2, 256]), ALU.mult).then_inc(L0x_pool_done, 1)
                pool.wait_ge(L0x_vector_done, 38*b + 46)
                pool.tensor_tensor(S1[:, :, :], S1[:, :, :], st1[:, 16:18].unsqueeze(2).to_broadcast([128, 2, 256]), ALU.mult).then_inc(L0x_pool_done, 1)
                pool.wait_ge(L0x_vector_done, 38*b + 71)
                pool.sem_inc(pool_waited, 1)
                pool.tensor_tensor(x[:, 2*b+0, :], x[:, 2*b+0, :], u0[:, :], ALU.add).then_inc(L0x_pool_done, 1)
                pool.wait_ge(L0x_vector_done, 38*b + 72)
                pool.sem_inc(pool_waited, 1)
                pool.tensor_tensor(x[:, 2*b+1, :], x[:, 2*b+1, :], u1[:, :], ALU.add).then_inc(L0x_pool_done, 1)

            pool.sem_inc(L0f_pool_done, 4)
            pool.wait_ge(L0x_matmul_done, 51)
            pool.wait_ge(L0f_vector_done, 16)
            with pool.Fori(0, 4) as b:
                pool.wait_ge(L0f_scalar_done, 20*b + 25)
                pool.tensor_tensor(acc0_0[:, :], acc0_0[:, :], r0_0[:, 1, :], ALU.add).then_inc(L0f_pool_done, 1)
                pool.wait_ge(L0f_scalar_done, 20*b + 26)
                pool.tensor_tensor(acc0_1[:, :], acc0_1[:, :], r0_1[:, 1, :], ALU.add).then_inc(L0f_pool_done, 1)
                pool.wait_ge(L0f_scalar_done, 20*b + 27)
                pool.tensor_tensor(acc0_0[:, :], acc0_0[:, :], r0_0[:, 0, :], ALU.add).then_inc(L0f_pool_done, 1)
                pool.wait_ge(L0f_scalar_done, 20*b + 28)
                pool.wait_ge(L0f_pool_done, 15*b + 7)
                pool.tensor_tensor(acc0_0[:, :], acc0_0[:, :], r0_0[:, 1, :], ALU.add).then_inc(L0f_pool_done, 1)
                pool.wait_ge(L0f_scalar_done, 20*b + 29)
                pool.tensor_tensor(acc0_1[:, :], acc0_1[:, :], r0_1[:, 0, :], ALU.add).then_inc(L0f_pool_done, 1)
                pool.wait_ge(L0f_scalar_done, 20*b + 30)
                pool.wait_ge(L0f_pool_done, 15*b + 9)
                pool.tensor_tensor(acc0_1[:, :], acc0_1[:, :], r0_1[:, 1, :], ALU.add).then_inc(L0f_pool_done, 1)
                pool.wait_ge(L0f_scalar_done, 20*b + 31)
                pool.tensor_tensor(acc0_0[:, :], acc0_0[:, :], r0_0[:, 0, :], ALU.add).then_inc(L0f_pool_done, 1)
                pool.wait_ge(L0f_scalar_done, 20*b + 32)
                pool.wait_ge(L0f_pool_done, 15*b + 11)
                pool.tensor_tensor(acc0_0[:, :], acc0_0[:, :], r0_0[:, 1, :], ALU.add).then_inc(L0f_pool_done, 1)
                pool.wait_ge(L0f_scalar_done, 20*b + 33)
                pool.tensor_tensor(acc0_1[:, :], acc0_1[:, :], r0_1[:, 0, :], ALU.add).then_inc(L0f_pool_done, 1)
                pool.wait_ge(L0f_scalar_done, 20*b + 34)
                pool.wait_ge(L0f_pool_done, 15*b + 13)
                pool.tensor_tensor(acc0_1[:, :], acc0_1[:, :], r0_1[:, 1, :], ALU.add).then_inc(L0f_pool_done, 1)
                pool.wait_ge(L0f_scalar_done, 20*b + 35)
                pool.tensor_tensor(acc0_0[:, :], acc0_0[:, :], r0_0[:, 0, :], ALU.add).then_inc(L0f_pool_done, 1)
                pool.wait_ge(L0f_scalar_done, 20*b + 36)
                pool.wait_ge(L0f_pool_done, 15*b + 15)
                pool.tensor_tensor(acc0_0[:, :], acc0_0[:, :], r0_0[:, 1, :], ALU.add).then_inc(L0f_pool_done, 1)
                pool.wait_ge(L0f_pool_done, 15*b + 16)
                pool.sem_inc(pool_waited, 1)
                pool.tensor_tensor(x[:, 2*b+0, :], x[:, 2*b+0, :], acc0_0[:, :], ALU.add)
                pool.wait_ge(L0f_scalar_done, 20*b + 39)
                pool.tensor_tensor(acc0_1[:, :], acc0_1[:, :], r0_1[:, 0, :], ALU.add).then_inc(L0f_pool_done, 1)
                pool.wait_ge(L0f_scalar_done, 20*b + 40)
                pool.wait_ge(L0f_pool_done, 15*b + 17)
                pool.tensor_tensor(acc0_1[:, :], acc0_1[:, :], r0_1[:, 1, :], ALU.add).then_inc(L0f_pool_done, 1)
                pool.wait_ge(L0f_pool_done, 15*b + 18)
                pool.sem_inc(pool_waited, 1)
                pool.tensor_tensor(x[:, 2*b+1, :], x[:, 2*b+1, :], acc0_1[:, :], ALU.add).then_inc(L0f_pool_done, 1)

            pool.wait_ge(L1x_vector_done, 18)
            with pool.Fori(0, 4) as b:
                pool.wait_ge(L1x_vector_done, 18*b + 27)
                pool.tensor_tensor(u0[:, :], u0[:, :], b_oo1[:, :], ALU.add).then_inc(L1x_pool_done, 1)
                pool.wait_ge(L1x_vector_done, 18*b + 28)
                pool.tensor_tensor(u1[:, :], u1[:, :], b_oo1[:, :], ALU.add).then_inc(L1x_pool_done, 1)
                pool.wait_ge(L1x_vector_done, 18*b + 33)
                pool.tensor_tensor(un0[:, :], un0[:, :], gam1[:, :], ALU.mult).then_inc(L1x_pool_done, 1)
                pool.wait_ge(L1x_pool_done, 7*b + 3)
                pool.tensor_tensor(un0[:, :], un0[:, :], bet1[:, :], ALU.add).then_inc(L1x_pool_done, 1)
                pool.wait_ge(L1x_vector_done, 18*b + 35)
                pool.tensor_tensor(un1[:, :], un1[:, :], gam1[:, :], ALU.mult).then_inc(L1x_pool_done, 1)
                pool.wait_ge(L1x_pool_done, 7*b + 4)
                pool.sem_inc(pool_waited, 1)
                pool.tensor_tensor(x[:, 2*b+0, :], x[:, 2*b+0, :], un0[:, :], ALU.add)
                pool.wait_ge(L1x_pool_done, 7*b + 5)
                pool.tensor_tensor(un1[:, :], un1[:, :], bet1[:, :], ALU.add).then_inc(L1x_pool_done, 1)
                pool.wait_ge(L1x_pool_done, 7*b + 6)
                pool.sem_inc(pool_waited, 1)
                pool.tensor_tensor(x[:, 2*b+1, :], x[:, 2*b+1, :], un1[:, :], ALU.add).then_inc(L1x_pool_done, 1)

            pool.sem_inc(L1f_pool_done, 2)
            pool.wait_ge(L1f_vector_done, 54)
            with pool.Fori(0, 4) as b:
                pool.wait_ge(L1f_vector_done, 56*b + 109)
                pool.sem_inc(pool_waited, 1)
                pool.tensor_tensor(x[:, 2*b+0, :], x[:, 2*b+0, :], acc1_0[:, :], ALU.add).then_inc(L1f_pool_done, 1)
                pool.wait_ge(L1f_vector_done, 56*b + 110)
                pool.sem_inc(pool_waited, 1)
                pool.tensor_tensor(x[:, 2*b+1, :], x[:, 2*b+1, :], acc1_1[:, :], ALU.add).then_inc(L1f_pool_done, 1)
            pool.wait_ge(L2a_vector_done, 191)
            pool.wait_ge(L2a_matmul_done, 96)
            pool.memset(keys[:, :, :], 0.0).then_inc(L2f_pool_done, 1)

            pool.wait_ge(L2x_vector_done, 216)
            pool.tensor_tensor(xsf_0[:, :], y16_0[:, 0:1024], qq_0[:, :], ALU.add).then_inc(L2x_pool_done, 1)
            pool.wait_ge(L2x_vector_done, 217)
            pool.tensor_tensor(xsf_1[:, :], y16_1[:, 0:1024], qq_1[:, :], ALU.add).then_inc(L2x_pool_done, 1)
            pool.wait_ge(L2x_pool_done, 1)
            pool.tensor_tensor(xsf_0[:, :], xsf_0[:, :], qq_0[:, :], ALU.subtract).then_inc(L2x_pool_done, 1)
            pool.wait_ge(L2x_pool_done, 2)
            pool.tensor_tensor(xsf_1[:, :], xsf_1[:, :], qq_1[:, :], ALU.subtract).then_inc(L2x_pool_done, 1)
            with pool.Fori(0, 4) as b:
                pool.wait_ge(L2x_vector_done, 226*b + 249)
                pool.tensor_tensor(P2_0[:, :, :], P2_0[:, :, :], st0[:, 16:20].unsqueeze(2).to_broadcast([128, 4, 128]), ALU.mult).then_inc(L2x_pool_done, 1)
                pool.wait_ge(L2x_vector_done, 226*b + 250)
                pool.tensor_tensor(P2_1[:, :, :], P2_1[:, :, :], st1[:, 16:20].unsqueeze(2).to_broadcast([128, 4, 128]), ALU.mult).then_inc(L2x_pool_done, 1)
                pool.wait_ge(L2x_vector_done, 226*b + 262)
                pool.tensor_tensor(P2f_0[:, :], y16_0[:, 0:512], PT2_0[:, :], ALU.add).then_inc(L2x_pool_done, 1)
                pool.wait_ge(L2x_vector_done, 226*b + 265)
                pool.tensor_tensor(P2f_1[:, :], y16_1[:, 0:512], PT2_1[:, :], ALU.add).then_inc(L2x_pool_done, 1)
                pool.wait_ge(L2x_pool_done, 52*b + 7)
                pool.tensor_tensor(P2f_0[:, :], P2f_0[:, :], PT2_0[:, :], ALU.subtract).then_inc(L2x_pool_done, 1)
                pool.wait_ge(L2x_pool_done, 52*b + 8)
                pool.tensor_tensor(P2f_1[:, :], P2f_1[:, :], PT2_1[:, :], ALU.subtract).then_inc(L2x_pool_done, 1)
                pool.wait_ge(L2x_vector_done, 226*b + 272)
                pool.tensor_tensor(P2_0[:, :, :], P2_0[:, :, :], st0[:, 16:20].unsqueeze(2).to_broadcast([128, 4, 128]), ALU.mult).then_inc(L2x_pool_done, 1)
                pool.wait_ge(L2x_vector_done, 226*b + 274)
                pool.tensor_tensor(P2_1[:, :, :], P2_1[:, :, :], st1[:, 16:20].unsqueeze(2).to_broadcast([128, 4, 128]), ALU.mult).then_inc(L2x_pool_done, 1)
                pool.wait_ge(L2x_vector_done, 226*b + 286)
                pool.tensor_tensor(P2f_0[:, :], y16_0[:, 0:512], PT2_0[:, :], ALU.add).then_inc(L2x_pool_done, 1)
                pool.wait_ge(L2x_vector_done, 226*b + 287)
                pool.tensor_tensor(P2f_1[:, :], y16_1[:, 0:512], PT2_1[:, :], ALU.add).then_inc(L2x_pool_done, 1)
                pool.wait_ge(L2x_pool_done, 52*b + 13)
                pool.tensor_tensor(P2f_0[:, :], P2f_0[:, :], PT2_0[:, :], ALU.subtract).then_inc(L2x_pool_done, 1)
                pool.wait_ge(L2x_pool_done, 52*b + 14)
                pool.tensor_tensor(P2f_1[:, :], P2f_1[:, :], PT2_1[:, :], ALU.subtract).then_inc(L2x_pool_done, 1)
                pool.wait_ge(L2x_vector_done, 226*b + 298)
                pool.tensor_tensor(P2_0[:, :, :], P2_0[:, :, :], st0[:, 16:20].unsqueeze(2).to_broadcast([128, 4, 128]), ALU.mult).then_inc(L2x_pool_done, 1)
                pool.wait_ge(L2x_vector_done, 226*b + 299)
                pool.tensor_tensor(P2_1[:, :, :], P2_1[:, :, :], st1[:, 16:20].unsqueeze(2).to_broadcast([128, 4, 128]), ALU.mult).then_inc(L2x_pool_done, 1)
                pool.wait_ge(L2x_vector_done, 226*b + 311)
                pool.tensor_tensor(P2f_0[:, :], y16_0[:, 0:512], PT2_0[:, :], ALU.add).then_inc(L2x_pool_done, 1)
                pool.wait_ge(L2x_vector_done, 226*b + 312)
                pool.tensor_tensor(P2f_1[:, :], y16_1[:, 0:512], PT2_1[:, :], ALU.add).then_inc(L2x_pool_done, 1)
                pool.wait_ge(L2x_pool_done, 52*b + 19)
                pool.tensor_tensor(P2f_0[:, :], P2f_0[:, :], PT2_0[:, :], ALU.subtract).then_inc(L2x_pool_done, 1)
                pool.wait_ge(L2x_pool_done, 52*b + 20)
                pool.tensor_tensor(P2f_1[:, :], P2f_1[:, :], PT2_1[:, :], ALU.subtract).then_inc(L2x_pool_done, 1)
                pool.wait_ge(L2x_vector_done, 226*b + 323)
                pool.tensor_tensor(P2_0[:, :, :], P2_0[:, :, :], st0[:, 16:20].unsqueeze(2).to_broadcast([128, 4, 128]), ALU.mult).then_inc(L2x_pool_done, 1)
                pool.wait_ge(L2x_vector_done, 226*b + 324)
                pool.tensor_tensor(P2_1[:, :, :], P2_1[:, :, :], st1[:, 16:20].unsqueeze(2).to_broadcast([128, 4, 128]), ALU.mult).then_inc(L2x_pool_done, 1)
                pool.wait_ge(L2x_vector_done, 226*b + 336)
                pool.tensor_tensor(P2f_0[:, :], y16_0[:, 0:512], PT2_0[:, :], ALU.add).then_inc(L2x_pool_done, 1)
                pool.wait_ge(L2x_vector_done, 226*b + 337)
                pool.tensor_tensor(P2f_1[:, :], y16_1[:, 0:512], PT2_1[:, :], ALU.add).then_inc(L2x_pool_done, 1)
                pool.wait_ge(L2x_pool_done, 52*b + 25)
                pool.tensor_tensor(P2f_0[:, :], P2f_0[:, :], PT2_0[:, :], ALU.subtract).then_inc(L2x_pool_done, 1)
                pool.wait_ge(L2x_pool_done, 52*b + 26)
                pool.tensor_tensor(P2f_1[:, :], P2f_1[:, :], PT2_1[:, :], ALU.subtract).then_inc(L2x_pool_done, 1)
                pool.wait_ge(L2x_vector_done, 226*b + 348)
                pool.tensor_tensor(P2_0[:, :, :], P2_0[:, :, :], st0[:, 16:20].unsqueeze(2).to_broadcast([128, 4, 128]), ALU.mult).then_inc(L2x_pool_done, 1)
                pool.wait_ge(L2x_vector_done, 226*b + 349)
                pool.tensor_tensor(P2_1[:, :, :], P2_1[:, :, :], st1[:, 16:20].unsqueeze(2).to_broadcast([128, 4, 128]), ALU.mult).then_inc(L2x_pool_done, 1)
                pool.wait_ge(L2x_vector_done, 226*b + 361)
                pool.tensor_tensor(P2f_0[:, :], y16_0[:, 0:512], PT2_0[:, :], ALU.add).then_inc(L2x_pool_done, 1)
                pool.wait_ge(L2x_vector_done, 226*b + 362)
                pool.tensor_tensor(P2f_1[:, :], y16_1[:, 0:512], PT2_1[:, :], ALU.add).then_inc(L2x_pool_done, 1)
                pool.wait_ge(L2x_pool_done, 52*b + 31)
                pool.tensor_tensor(P2f_0[:, :], P2f_0[:, :], PT2_0[:, :], ALU.subtract).then_inc(L2x_pool_done, 1)
                pool.wait_ge(L2x_pool_done, 52*b + 32)
                pool.tensor_tensor(P2f_1[:, :], P2f_1[:, :], PT2_1[:, :], ALU.subtract).then_inc(L2x_pool_done, 1)
                pool.wait_ge(L2x_vector_done, 226*b + 373)
                pool.tensor_tensor(P2_0[:, :, :], P2_0[:, :, :], st0[:, 16:20].unsqueeze(2).to_broadcast([128, 4, 128]), ALU.mult).then_inc(L2x_pool_done, 1)
                pool.wait_ge(L2x_vector_done, 226*b + 374)
                pool.tensor_tensor(P2_1[:, :, :], P2_1[:, :, :], st1[:, 16:20].unsqueeze(2).to_broadcast([128, 4, 128]), ALU.mult).then_inc(L2x_pool_done, 1)
                pool.wait_ge(L2x_vector_done, 226*b + 386)
                pool.tensor_tensor(P2f_0[:, :], y16_0[:, 0:512], PT2_0[:, :], ALU.add).then_inc(L2x_pool_done, 1)
                pool.wait_ge(L2x_vector_done, 226*b + 387)
                pool.tensor_tensor(P2f_1[:, :], y16_1[:, 0:512], PT2_1[:, :], ALU.add).then_inc(L2x_pool_done, 1)
                pool.wait_ge(L2x_pool_done, 52*b + 37)
                pool.tensor_tensor(P2f_0[:, :], P2f_0[:, :], PT2_0[:, :], ALU.subtract).then_inc(L2x_pool_done, 1)
                pool.wait_ge(L2x_pool_done, 52*b + 38)
                pool.tensor_tensor(P2f_1[:, :], P2f_1[:, :], PT2_1[:, :], ALU.subtract).then_inc(L2x_pool_done, 1)
                pool.wait_ge(L2x_vector_done, 226*b + 398)
                pool.tensor_tensor(P2_0[:, :, :], P2_0[:, :, :], st0[:, 16:20].unsqueeze(2).to_broadcast([128, 4, 128]), ALU.mult).then_inc(L2x_pool_done, 1)
                pool.wait_ge(L2x_vector_done, 226*b + 399)
                pool.tensor_tensor(P2_1[:, :, :], P2_1[:, :, :], st1[:, 16:20].unsqueeze(2).to_broadcast([128, 4, 128]), ALU.mult).then_inc(L2x_pool_done, 1)
                pool.wait_ge(L2x_vector_done, 226*b + 411)
                pool.tensor_tensor(P2f_0[:, :], y16_0[:, 0:512], PT2_0[:, :], ALU.add).then_inc(L2x_pool_done, 1)
                pool.wait_ge(L2x_vector_done, 226*b + 412)
                pool.tensor_tensor(P2f_1[:, :], y16_1[:, 0:512], PT2_1[:, :], ALU.add).then_inc(L2x_pool_done, 1)
                pool.wait_ge(L2x_pool_done, 52*b + 43)
                pool.tensor_tensor(P2f_0[:, :], P2f_0[:, :], PT2_0[:, :], ALU.subtract).then_inc(L2x_pool_done, 1)
                pool.wait_ge(L2x_pool_done, 52*b + 44)
                pool.tensor_tensor(P2f_1[:, :], P2f_1[:, :], PT2_1[:, :], ALU.subtract).then_inc(L2x_pool_done, 1)
                pool.wait_ge(L2x_vector_done, 226*b + 423)
                pool.tensor_tensor(P2_0[:, :, :], P2_0[:, :, :], st0[:, 16:20].unsqueeze(2).to_broadcast([128, 4, 128]), ALU.mult).then_inc(L2x_pool_done, 1)
                pool.wait_ge(L2x_vector_done, 226*b + 424)
                pool.tensor_tensor(P2_1[:, :, :], P2_1[:, :, :], st1[:, 16:20].unsqueeze(2).to_broadcast([128, 4, 128]), ALU.mult).then_inc(L2x_pool_done, 1)
                pool.wait_ge(L2x_vector_done, 226*b + 428)
                pool.tensor_tensor(P2f_0[:, :], y16_0[:, 0:512], PT2_0[:, :], ALU.add).then_inc(L2x_pool_done, 1)
                pool.wait_ge(L2x_pool_done, 52*b + 49)
                pool.tensor_tensor(P2f_0[:, :], P2f_0[:, :], PT2_0[:, :], ALU.subtract).then_inc(L2x_pool_done, 1)
                pool.wait_ge(L2x_vector_done, 226*b + 432)
                pool.tensor_tensor(P2f_1[:, :], y16_1[:, 0:512], PT2_1[:, :], ALU.add).then_inc(L2x_pool_done, 1)
                pool.wait_ge(L2x_pool_done, 52*b + 51)
                pool.tensor_tensor(P2f_1[:, :], P2f_1[:, :], PT2_1[:, :], ALU.subtract).then_inc(L2x_pool_done, 1)
                pool.wait_ge(L2x_vector_done, 226*b + 441)
                pool.tensor_tensor(xsf_0[:, :], y16_0[:, 0:1024], qq_0[:, :], ALU.add).then_inc(L2x_pool_done, 1)
                pool.wait_ge(L2x_vector_done, 226*b + 442)
                pool.tensor_tensor(xsf_1[:, :], y16_1[:, 0:1024], qq_1[:, :], ALU.add).then_inc(L2x_pool_done, 1)
                pool.wait_ge(L2x_pool_done, 52*b + 53)
                pool.tensor_tensor(xsf_0[:, :], xsf_0[:, :], qq_0[:, :], ALU.subtract).then_inc(L2x_pool_done, 1)
                pool.wait_ge(L2x_pool_done, 52*b + 54)
                pool.tensor_tensor(xsf_1[:, :], xsf_1[:, :], qq_1[:, :], ALU.subtract).then_inc(L2x_pool_done, 1)

            pool.sem_inc(L2f_pool_done, 3)
            pool.wait_ge(L2x_matmul_done, 499)
            pool.wait_ge(L2x_pool_done, 206)
            pool.wait_ge(L2x_vector_done, 1122)
            with pool.Fori(0, 4) as b:
                pool.wait_ge(L2f_vector_done, 53*b + 60)
                pool.tensor_tensor(sim_0[:, :, :, :], sim_0[:, :, :, :], v8_0[:, :, :, 0:1].to_broadcast([128, 2, 8, 45]), ALU.subtract).then_inc(L2f_pool_done, 1)
                pool.wait_ge(L2f_vector_done, 53*b + 61)
                pool.tensor_tensor(sim_1[:, :, :, :], sim_1[:, :, :, :], v8_1[:, :, :, 0:1].to_broadcast([128, 2, 8, 45]), ALU.subtract).then_inc(L2f_pool_done, 1)
                pool.wait_ge(L2f_scalar_done, 37*b + 49)
                pool.tensor_tensor(Pra_0[:, :, :], sim_0[:, 0, 0, :].unsqueeze(2).to_broadcast([128, 45, 45]), sim_0[:, 1, 0, :].unsqueeze(1).to_broadcast([128, 45, 45]), ALU.mult).then_inc(L2f_pool_done, 1)
                pool.wait_ge(L2f_scalar_done, 37*b + 50)
                pool.tensor_tensor(Pra_1[:, :, :], sim_1[:, 0, 0, :].unsqueeze(2).to_broadcast([128, 45, 45]), sim_1[:, 1, 0, :].unsqueeze(1).to_broadcast([128, 45, 45]), ALU.mult).then_inc(L2f_pool_done, 1)
                pool.tensor_tensor(Prb_0[:, :, :], sim_0[:, 0, 1, :].unsqueeze(2).to_broadcast([128, 45, 45]), sim_0[:, 1, 1, :].unsqueeze(1).to_broadcast([128, 45, 45]), ALU.mult).then_inc(L2f_pool_done, 1)
                pool.tensor_tensor(Prb_1[:, :, :], sim_1[:, 0, 1, :].unsqueeze(2).to_broadcast([128, 45, 45]), sim_1[:, 1, 1, :].unsqueeze(1).to_broadcast([128, 45, 45]), ALU.mult).then_inc(L2f_pool_done, 1)
                pool.wait_ge(L2f_vector_done, 53*b + 68)
                pool.tensor_tensor(Pra_0[:, :, :], sim_0[:, 0, 2, :].unsqueeze(2).to_broadcast([128, 45, 45]), sim_0[:, 1, 2, :].unsqueeze(1).to_broadcast([128, 45, 45]), ALU.mult).then_inc(L2f_pool_done, 1)
                pool.wait_ge(L2f_vector_done, 53*b + 73)
                pool.tensor_tensor(Pra_1[:, :, :], sim_1[:, 0, 2, :].unsqueeze(2).to_broadcast([128, 45, 45]), sim_1[:, 1, 2, :].unsqueeze(1).to_broadcast([128, 45, 45]), ALU.mult).then_inc(L2f_pool_done, 1)
                pool.wait_ge(L2f_vector_done, 53*b + 75)
                pool.tensor_tensor(Prb_0[:, :, :], sim_0[:, 0, 3, :].unsqueeze(2).to_broadcast([128, 45, 45]), sim_0[:, 1, 3, :].unsqueeze(1).to_broadcast([128, 45, 45]), ALU.mult).then_inc(L2f_pool_done, 1)
                pool.wait_ge(L2f_vector_done, 53*b + 76)
                pool.tensor_tensor(Prb_1[:, :, :], sim_1[:, 0, 3, :].unsqueeze(2).to_broadcast([128, 45, 45]), sim_1[:, 1, 3, :].unsqueeze(1).to_broadcast([128, 45, 45]), ALU.mult).then_inc(L2f_pool_done, 1)
                pool.wait_ge(L2f_vector_done, 53*b + 79)
                pool.tensor_tensor(Pra_0[:, :, :], sim_0[:, 0, 4, :].unsqueeze(2).to_broadcast([128, 45, 45]), sim_0[:, 1, 4, :].unsqueeze(1).to_broadcast([128, 45, 45]), ALU.mult).then_inc(L2f_pool_done, 1)
                pool.wait_ge(L2f_vector_done, 53*b + 80)
                pool.tensor_tensor(Pra_1[:, :, :], sim_1[:, 0, 4, :].unsqueeze(2).to_broadcast([128, 45, 45]), sim_1[:, 1, 4, :].unsqueeze(1).to_broadcast([128, 45, 45]), ALU.mult).then_inc(L2f_pool_done, 1)
                pool.wait_ge(L2f_vector_done, 53*b + 83)
                pool.tensor_tensor(Prb_0[:, :, :], sim_0[:, 0, 5, :].unsqueeze(2).to_broadcast([128, 45, 45]), sim_0[:, 1, 5, :].unsqueeze(1).to_broadcast([128, 45, 45]), ALU.mult).then_inc(L2f_pool_done, 1)
                pool.wait_ge(L2f_vector_done, 53*b + 84)
                pool.tensor_tensor(Prb_1[:, :, :], sim_1[:, 0, 5, :].unsqueeze(2).to_broadcast([128, 45, 45]), sim_1[:, 1, 5, :].unsqueeze(1).to_broadcast([128, 45, 45]), ALU.mult).then_inc(L2f_pool_done, 1)
                pool.wait_ge(L2f_vector_done, 53*b + 87)
                pool.tensor_tensor(Pra_0[:, :, :], sim_0[:, 0, 6, :].unsqueeze(2).to_broadcast([128, 45, 45]), sim_0[:, 1, 6, :].unsqueeze(1).to_broadcast([128, 45, 45]), ALU.mult).then_inc(L2f_pool_done, 1)
                pool.wait_ge(L2f_vector_done, 53*b + 88)
                pool.tensor_tensor(Pra_1[:, :, :], sim_1[:, 0, 6, :].unsqueeze(2).to_broadcast([128, 45, 45]), sim_1[:, 1, 6, :].unsqueeze(1).to_broadcast([128, 45, 45]), ALU.mult).then_inc(L2f_pool_done, 1)
                pool.wait_ge(L2f_vector_done, 53*b + 91)
                pool.tensor_tensor(Prb_0[:, :, :], sim_0[:, 0, 7, :].unsqueeze(2).to_broadcast([128, 45, 45]), sim_0[:, 1, 7, :].unsqueeze(1).to_broadcast([128, 45, 45]), ALU.mult).then_inc(L2f_pool_done, 1)
                pool.wait_ge(L2f_vector_done, 53*b + 92)
                pool.tensor_tensor(Prb_1[:, :, :], sim_1[:, 0, 7, :].unsqueeze(2).to_broadcast([128, 45, 45]), sim_1[:, 1, 7, :].unsqueeze(1).to_broadcast([128, 45, 45]), ALU.mult).then_inc(L2f_pool_done, 1)

            pool.sem_inc(L3a_pool_done, 3)
            pool.wait_ge(L3a_vector_done, 72)
            with pool.Fori(0, 4) as b:
                pool.wait_ge(L3a_vector_done, 74*b + 77)
                pool.tensor_tensor(kR_0[:, 1, :, :], kT3_0[:, 1, :].unsqueeze(1).to_broadcast([128, 16, 128]), mask8[:, :].unsqueeze(2).to_broadcast([128, 16, 128]), ALU.mult).then_inc(L3a_pool_done, 1)
                pool.wait_ge(L3a_vector_done, 74*b + 79)
                pool.tensor_tensor(kR_1[:, 1, :, :], kT3_1[:, 1, :].unsqueeze(1).to_broadcast([128, 16, 128]), mask8[:, :].unsqueeze(2).to_broadcast([128, 16, 128]), ALU.mult).then_inc(L3a_pool_done, 1)
                pool.wait_ge(L3a_vector_done, 74*b + 145)
                pool.sem_inc(pool_waited, 1)
                pool.tensor_tensor(x[:, 2*b+0, :], x[:, 2*b+0, :], un0[:, :], ALU.add)
                pool.wait_ge(L3a_vector_done, 74*b + 146)
                pool.sem_inc(pool_waited, 1)
                pool.tensor_tensor(x[:, 2*b+1, :], x[:, 2*b+1, :], un1[:, :], ALU.add).then_inc(L3a_pool_done, 1)

            pool.sem_inc(L3x_pool_done, 2)
            pool.wait_ge(L3a_vector_done, 301)
            pool.wait_ge(L3a_pool_done, 14)
            pool.wait_ge(L3a_scalar_done, 196)
            pool.wait_ge(L3a_matmul_done, 220)
            with pool.Fori(0, 4) as b:
                pool.wait_ge(L3x_scalar_done, 18*b + 26)
                pool.sem_inc(pool_waited, 1)
                pool.tensor_scalar(ga_0[:, :], ga_0[:, :], 1.0, None, ALU.add).then_inc(L3x_pool_done, 1)
                pool.wait_ge(L3x_scalar_done, 18*b + 32)
                pool.sem_inc(pool_waited, 1)
                pool.tensor_scalar(ga_1[:, :], ga_1[:, :], 1.0, None, ALU.add).then_inc(L3x_pool_done, 1)
                pool.wait_ge(L3x_vector_done, 26*b + 47)
                pool.tensor_tensor(a3_0[:, :], a3_0[:, :], ga_0[:, :], ALU.mult).then_inc(L3x_pool_done, 1)
                pool.wait_ge(L3x_vector_done, 26*b + 48)
                pool.tensor_tensor(a3_1[:, :], a3_1[:, :], ga_1[:, :], ALU.mult).then_inc(L3x_pool_done, 1)

            pool.wait_ge(L3f_vector_done, 57)
            with pool.Fori(0, 4) as b:
                pool.wait_ge(L3f_vector_done, 61*b + 115)
                pool.sem_inc(pool_waited, 1)
                pool.tensor_tensor(x[:, 2*b+0, :], x[:, 2*b+0, :], u0[:, :], ALU.add).then_inc(L3f_pool_done, 1)
                pool.wait_ge(L3f_vector_done, 61*b + 116)
                pool.sem_inc(pool_waited, 1)
                pool.tensor_tensor(x[:, 2*b+1, :], x[:, 2*b+1, :], u1[:, :], ALU.add).then_inc(L3f_pool_done, 1)

        @block.scalar
        def _(act):

            act.preload_act_table_set('natural_log_exp_and_others')

            act.sem_inc(L0a_scalar_done, 6)
            act.wait_ge(L0a_w_loaded, 192)
            act.activation(A[:, :, :], A[:, :, :], ACT.Exp).then_inc(L0a_scalar_done, 1)
            act.wait_ge(L0a_vector_done, 13)
            act.activation(st0[:, 8:9], st0[:, 7:8], ACT.Ln, bias=eps5[:, 0:1]).then_inc(L0a_scalar_done, 1)
            act.wait_ge(L0a_vector_done, 14)
            act.activation(st1[:, 8:9], st1[:, 7:8], ACT.Ln, bias=eps5[:, 0:1]).then_inc(L0a_scalar_done, 1)
            act.wait_ge(L0a_scalar_done, 8)
            act.activation(st0[:, 9:10], st0[:, 8:9], ACT.Exp, scale=-0.5).then_inc(L0a_scalar_done, 1)
            act.wait_ge(L0a_scalar_done, 9)
            act.activation(st1[:, 9:10], st1[:, 8:9], ACT.Exp, scale=-0.5).then_inc(L0a_scalar_done, 1)
            act.wait_ge(L0a_vector_done, 15)
            act.activation(jk0[:, :], u0[:, :], ACT.Square, scale=1.0 / 16.0, accum_out=st0[:, 10:11]).then_inc(L0a_scalar_done, 1)
            act.wait_ge(L0a_vector_done, 16)
            act.activation(jk1[:, :], u1[:, :], ACT.Square, scale=1.0 / 16.0, accum_out=st1[:, 10:11]).then_inc(L0a_scalar_done, 1)
            act.wait_ge(L0a_scalar_done, 12)
            act.activation(st0[:, 11:12], st0[:, 10:11], ACT.Ln, bias=eps5[:, 0:1]).then_inc(L0a_scalar_done, 1)
            act.wait_ge(L0a_scalar_done, 13)
            act.activation(st1[:, 11:12], st1[:, 10:11], ACT.Ln, bias=eps5[:, 0:1]).then_inc(L0a_scalar_done, 1)
            act.wait_ge(L0a_scalar_done, 14)
            act.activation(st0[:, 12:13], st0[:, 11:12], ACT.Exp, scale=-0.5).then_inc(L0a_scalar_done, 1)
            act.wait_ge(L0a_scalar_done, 15)
            act.activation(st1[:, 12:13], st1[:, 11:12], ACT.Exp, scale=-0.5).then_inc(L0a_scalar_done, 1)
            act.wait_ge(L0a_matmul_done, 1)
            act.activation(unT0[:, 0:2, :], ps0[:, 0, 0:256], ACT.Copy)
            act.wait_ge(L0a_matmul_done, 2)
            act.activation(unT1[:, 0:2, :], ps1[:, 0, 0:256], ACT.Copy).then_inc(L0a_scalar_done, 1)
            act.wait_ge(L0a_scalar_done, 18)
            with act.Fori(0, 4) as b:
                act.wait_ge(L0a_vector_done, 20*b + 21)
                act.wait_ge(L0a_scalar_done, 18*b + 3)
                act.activation(st0[:, 8:9], st0[:, 7:8], ACT.Ln, bias=eps5[:, 0:1]).then_inc(L0a_scalar_done, 1)
                act.wait_ge(L0a_vector_done, 20*b + 22)
                act.wait_ge(L0a_scalar_done, 18*b + 4)
                act.activation(st1[:, 8:9], st1[:, 7:8], ACT.Ln, bias=eps5[:, 0:1]).then_inc(L0a_scalar_done, 1)
                act.wait_ge(L0a_scalar_done, 18*b + 19)
                act.activation(st0[:, 9:10], st0[:, 8:9], ACT.Exp, scale=-0.5).then_inc(L0a_scalar_done, 1)
                act.wait_ge(L0a_scalar_done, 18*b + 20)
                act.activation(st1[:, 9:10], st1[:, 8:9], ACT.Exp, scale=-0.5).then_inc(L0a_scalar_done, 1)
                act.wait_ge(L0a_matmul_done, 6*b + 3)
                act.activation(f0[:, :, :], ps0[:, 2, :], ACT.Copy).then_inc(L0a_scalar_done, 1)
                act.activation(zx[:, :, 2*b+0, :], ps0[:, 1, :].rearrange("p (j t) -> p j t", j=4), ACT.Copy)
                act.wait_ge(L0a_matmul_done, 6*b + 4)
                act.activation(f1[:, :, :], ps1[:, 2, :], ACT.Copy).then_inc(L0a_scalar_done, 1)
                act.activation(zx[:, :, 2*b+1, :], ps1[:, 1, :].rearrange("p (j t) -> p j t", j=4), ACT.Copy).then_inc(L0a_scalar_done, 1)
                act.wait_ge(L0a_vector_done, 20*b + 28)
                act.activation(sa0[:, :, :], sa0[:, :, :], ACT.Exp, scale=-1.0).then_inc(L0a_scalar_done, 1)
                act.activation(jk0[:, :], u0[:, :], ACT.Square, scale=1.0 / 16.0, accum_out=st0[:, 10:11]).then_inc(L0a_scalar_done, 1)
                act.wait_ge(L0a_scalar_done, 18*b + 26)
                act.activation(sa0[:, :, :], sa0[:, :, :], ACT.Ln, bias=one[:, 0:1]).then_inc(L0a_scalar_done, 1)
                act.wait_ge(L0a_scalar_done, 18*b + 27)
                act.activation(st0[:, 11:12], st0[:, 10:11], ACT.Ln, bias=eps5[:, 0:1]).then_inc(L0a_scalar_done, 1)
                act.wait_ge(L0a_scalar_done, 18*b + 29)
                act.activation(st0[:, 12:13], st0[:, 11:12], ACT.Exp, scale=-0.5)
                act.wait_ge(L0a_vector_done, 20*b + 29)
                act.activation(sa1[:, :, :], sa1[:, :, :], ACT.Exp, scale=-1.0).then_inc(L0a_scalar_done, 1)
                act.wait_ge(L0a_vector_done, 20*b + 30)
                act.activation(jk1[:, :], u1[:, :], ACT.Square, scale=1.0 / 16.0, accum_out=st1[:, 10:11]).then_inc(L0a_scalar_done, 1)
                act.wait_ge(L0a_scalar_done, 18*b + 30)
                act.activation(sa1[:, :, :], sa1[:, :, :], ACT.Ln, bias=one[:, 0:1]).then_inc(L0a_scalar_done, 1)
                act.wait_ge(L0a_scalar_done, 18*b + 31)
                act.activation(st1[:, 11:12], st1[:, 10:11], ACT.Ln, bias=eps5[:, 0:1]).then_inc(L0a_scalar_done, 1)
                act.wait_ge(L0a_scalar_done, 18*b + 33)
                act.activation(st1[:, 12:13], st1[:, 11:12], ACT.Exp, scale=-0.5).then_inc(L0a_scalar_done, 1)
                act.wait_ge(L0a_matmul_done, 6*b + 7)
                act.activation(unT0[:, 0:2, :], ps0[:, 0, 0:256], ACT.Copy).then_inc(L0a_scalar_done, 1)
                act.wait_ge(L0a_matmul_done, 6*b + 8)
                act.activation(unT1[:, 0:2, :], ps1[:, 0, 0:256], ACT.Copy).then_inc(L0a_scalar_done, 1)
            act.wait_ge(L0a_vector_done, 97)
            act.wait_ge(L0a_matmul_done, 25)
            act.wait_ge(L0a_scalar_done, 89)
            with act.Fori(0, 32) as n:
                act.wait_ge(L0a_scalar_done, 2*n + 89)
                act.wait_ge(L0a_vector_done, 6*n + 95)
                act.sem_inc(act_waited, 1)
                act.activation(dA0[:, :, :], dt[:, 0, :, :], ACT.Exp, scale=A[:, 0, ds(n, 1)]).then_inc(L0a_scalar_done, 1)
                act.wait_ge(L0a_scalar_done, 2*n + 90)
                act.wait_ge(L0a_vector_done, 6*n + 98)
                act.sem_inc(act_waited, 1)
                act.activation(dA1[:, :, :], dt[:, 1, :, :], ACT.Exp, scale=A[:, 1, ds(n, 1)]).then_inc(L0a_scalar_done, 1)
            act.wait_ge(L0a_scalar_done, 154)
            act.wait_ge(L0a_matmul_done, 154)
            act.wait_ge(L0a_vector_done, 291)
            act.wait_ge(L0a_pool_done, 74)
            with act.Fori(0, 4) as b:
                act.wait_ge(L0a_scalar_done, 12*b + 143)
                act.wait_ge(L0a_vector_done, 12*b + 282)
                act.sem_inc(act_waited, 1)
                act.activation(sa0[:, :, :], zx[:, 0:2, 2*b+0, :], ACT.Silu).then_inc(L0a_scalar_done, 1)
                act.wait_ge(L0a_scalar_done, 12*b + 144)
                act.wait_ge(L0a_vector_done, 12*b + 283)
                act.sem_inc(act_waited, 1)
                act.activation(sa1[:, :, :], zx[:, 0:2, 2*b+1, :], ACT.Silu).then_inc(L0a_scalar_done, 1)
                act.wait_ge(L0a_vector_done, 12*b + 296)
                act.activation(jk0[:, :], h0[:, :], ACT.Square, scale=1.0 / 16.0, accum_out=st0[:, 10:11]).then_inc(L0a_scalar_done, 1)
                act.wait_ge(L0a_vector_done, 12*b + 297)
                act.activation(jk1[:, :], h1[:, :], ACT.Square, scale=1.0 / 16.0, accum_out=st1[:, 10:11]).then_inc(L0a_scalar_done, 1)
                act.wait_ge(L0a_scalar_done, 12*b + 157)
                act.activation(st0[:, 11:12], st0[:, 10:11], ACT.Ln, bias=eps5[:, 0:1]).then_inc(L0a_scalar_done, 1)
                act.wait_ge(L0a_scalar_done, 12*b + 158)
                act.activation(st1[:, 11:12], st1[:, 10:11], ACT.Ln, bias=eps5[:, 0:1]).then_inc(L0a_scalar_done, 1)
                act.wait_ge(L0a_scalar_done, 12*b + 159)
                act.activation(st0[:, 12:13], st0[:, 11:12], ACT.Exp, scale=-0.5).then_inc(L0a_scalar_done, 1)
                act.wait_ge(L0a_scalar_done, 12*b + 160)
                act.activation(st1[:, 12:13], st1[:, 11:12], ACT.Exp, scale=-0.5).then_inc(L0a_scalar_done, 1)
                act.wait_ge(L0a_matmul_done, 9*b + 157)
                act.activation(unT0[:, 0:2, :], ps0[:, 0, 0:256], ACT.Copy).then_inc(L0a_scalar_done, 1)
                act.wait_ge(L0a_matmul_done, 9*b + 158)
                act.activation(unT1[:, 0:2, :], ps1[:, 0, 0:256], ACT.Copy).then_inc(L0a_scalar_done, 1)
                act.wait_ge(L0a_matmul_done, 9*b + 160)
                act.activation(tm0[:, :], psf0[:, 512:1280], ACT.Silu).then_inc(L0a_scalar_done, 1)
                act.wait_ge(L0a_matmul_done, 9*b + 161)
                act.activation(tm1[:, :], psf1[:, 512:1280], ACT.Silu).then_inc(L0a_scalar_done, 1)

            act.sem_inc(L0x_scalar_done, 8)
            act.wait_ge(L0x_vector_done, 34)
            act.activation(st0[:, 8:9], st0[:, 7:8], ACT.Ln, bias=eps5[:, 0:1]).then_inc(L0x_scalar_done, 1)
            act.wait_ge(L0x_vector_done, 35)
            act.activation(st1[:, 8:9], st1[:, 7:8], ACT.Ln, bias=eps5[:, 0:1]).then_inc(L0x_scalar_done, 1)
            act.wait_ge(L0x_scalar_done, 9)
            act.activation(st0[:, 9:10], st0[:, 8:9], ACT.Exp, scale=-0.5).then_inc(L0x_scalar_done, 1)
            act.wait_ge(L0x_scalar_done, 10)
            act.activation(st1[:, 9:10], st1[:, 8:9], ACT.Exp, scale=-0.5).then_inc(L0x_scalar_done, 1)
            act.wait_ge(L0a_matmul_done, 182)
            act.wait_ge(L0x_vector_done, 36)
            with act.Fori(0, 4) as b:
                act.wait_ge(L0x_vector_done, 38*b + 42)
                for i in range(2):
                    last = act.activation(S0[:, i, :], ps0[:, 2, 256 * i:256 * i + 256], ACT.Exp, scale=1.0, bias=st0[:, 16 + i:17 + i], accum_out=st0[:, 18 + i:19 + i])
                last.then_inc(L0x_scalar_done, 1)
                act.wait_ge(L0x_vector_done, 38*b + 44)
                for i in range(2):
                    last = act.activation(S1[:, i, :], ps1[:, 2, 256 * i:256 * i + 256], ACT.Exp, scale=1.0, bias=st1[:, 16 + i:17 + i], accum_out=st1[:, 18 + i:19 + i])
                last.then_inc(L0x_scalar_done, 1)
                act.wait_ge(L0x_matmul_done, 14*b + 7)
                act.activation(Pm0[:, :, :], ps0[:, 3, :], ACT.Copy).then_inc(L0x_scalar_done, 1)
                act.wait_ge(L0x_matmul_done, 14*b + 8)
                act.activation(Pm1[:, :, :], ps1[:, 3, :], ACT.Copy).then_inc(L0x_scalar_done, 1)
                act.wait_ge(L0x_vector_done, 38*b + 54)
                act.activation(st0[:, 8:9], st0[:, 7:8], ACT.Ln, bias=eps5[:, 0:1]).then_inc(L0x_scalar_done, 1)
                act.wait_ge(L0x_vector_done, 38*b + 57)
                act.activation(st0[0:64, 13:14], st0[0:64, 12:13], ACT.Ln, bias=eps5[0:64, 0:1]).then_inc(L0x_scalar_done, 1)
                act.wait_ge(L0x_scalar_done, 12*b + 18)
                act.activation(st0[0:64, 14:15], st0[0:64, 13:14], ACT.Exp, scale=-0.5).then_inc(L0x_scalar_done, 1)
                act.wait_ge(L0x_vector_done, 38*b + 60)
                act.activation(st1[:, 8:9], st1[:, 7:8], ACT.Ln, bias=eps5[:, 0:1]).then_inc(L0x_scalar_done, 1)
                act.wait_ge(L0x_vector_done, 38*b + 62)
                act.activation(st1[0:64, 13:14], st1[0:64, 12:13], ACT.Ln, bias=eps5[0:64, 0:1]).then_inc(L0x_scalar_done, 1)
                act.wait_ge(L0x_scalar_done, 12*b + 21)
                act.activation(st1[0:64, 14:15], st1[0:64, 13:14], ACT.Exp, scale=-0.5).then_inc(L0x_scalar_done, 1)
                act.wait_ge(L0x_vector_done, 38*b + 63)
                act.activation(st0[:, 9:10], st0[:, 8:9], ACT.Exp, scale=-0.5).then_inc(L0x_scalar_done, 1)
                act.wait_ge(L0x_vector_done, 38*b + 65)
                act.activation(st1[:, 9:10], st1[:, 8:9], ACT.Exp, scale=-0.5).then_inc(L0x_scalar_done, 1)

            act.sem_inc(L0f_scalar_done, 15)
            act.wait_ge(L0x_scalar_done, 59)
            act.wait_ge(L0f_vector_done, 13)
            act.activation(st0[:, 8:9], st0[:, 7:8], ACT.Ln, bias=eps5[:, 0:1]).then_inc(L0f_scalar_done, 1)
            act.wait_ge(L0x_scalar_done, 60)
            act.wait_ge(L0f_vector_done, 14)
            act.activation(st1[:, 8:9], st1[:, 7:8], ACT.Ln, bias=eps5[:, 0:1]).then_inc(L0f_scalar_done, 1)
            act.wait_ge(L0f_scalar_done, 16)
            act.activation(st0[:, 9:10], st0[:, 8:9], ACT.Exp, scale=-0.5).then_inc(L0f_scalar_done, 1)
            act.wait_ge(L0f_scalar_done, 17)
            act.activation(st1[:, 9:10], st1[:, 8:9], ACT.Exp, scale=-0.5).then_inc(L0f_scalar_done, 1)
            act.wait_ge(L0f_matmul_done, 1)
            act.activation(unT0[:, 0:2, :], ps0[:, 0, 0:256], ACT.Copy)
            act.wait_ge(L0f_matmul_done, 2)
            act.activation(unT1[:, 0:2, :], ps1[:, 0, 0:256], ACT.Copy).then_inc(L0f_scalar_done, 1)
            act.wait_ge(L0f_scalar_done, 20)
            with act.Fori(0, 4) as b:
                act.wait_ge(L0f_vector_done, 18*b + 19)
                act.wait_ge(L0f_scalar_done, 20*b + 3)
                act.activation(st0[:, 8:9], st0[:, 7:8], ACT.Ln, bias=eps5[:, 0:1]).then_inc(L0f_scalar_done, 1)
                act.wait_ge(L0f_vector_done, 18*b + 20)
                act.wait_ge(L0f_scalar_done, 20*b + 4)
                act.activation(st1[:, 8:9], st1[:, 7:8], ACT.Ln, bias=eps5[:, 0:1]).then_inc(L0f_scalar_done, 1)
                act.wait_ge(L0f_scalar_done, 20*b + 21)
                act.activation(st0[:, 9:10], st0[:, 8:9], ACT.Exp, scale=-0.5).then_inc(L0f_scalar_done, 1)
                act.wait_ge(L0f_scalar_done, 20*b + 22)
                act.activation(st1[:, 9:10], st1[:, 8:9], ACT.Exp, scale=-0.5).then_inc(L0f_scalar_done, 1)
                act.wait_ge(L0f_vector_done, 18*b + 27)
                act.activation(acc0_0[:, :], r0_0[:, 0, :], ACT.Relu, scale=mk0_0[:, 0:1])
                act.wait_ge(L0f_vector_done, 18*b + 28)
                act.wait_ge(L0f_pool_done, 15*b + 4)
                act.activation(acc0_1[:, :], r0_1[:, 0, :], ACT.Relu, scale=mk0_1[:, 0:1])
                act.activation(r0_0[:, 1, :], r0_0[:, 1, :], ACT.Relu, scale=mk0_0[:, 1:2]).then_inc(L0f_scalar_done, 1)
                act.activation(r0_1[:, 1, :], r0_1[:, 1, :], ACT.Relu, scale=mk0_1[:, 1:2]).then_inc(L0f_scalar_done, 1)
                act.wait_ge(L0f_vector_done, 18*b + 29)
                act.activation(r0_0[:, 0, :], r0_0[:, 0, :], ACT.Relu, scale=mk0_0[:, 2:3]).then_inc(L0f_scalar_done, 1)
                act.activation(r0_0[:, 1, :], r0_0[:, 1, :], ACT.Relu, scale=mk0_0[:, 3:4]).then_inc(L0f_scalar_done, 1)
                act.wait_ge(L0f_vector_done, 18*b + 30)
                act.activation(r0_1[:, 0, :], r0_1[:, 0, :], ACT.Relu, scale=mk0_1[:, 2:3]).then_inc(L0f_scalar_done, 1)
                act.activation(r0_1[:, 1, :], r0_1[:, 1, :], ACT.Relu, scale=mk0_1[:, 3:4]).then_inc(L0f_scalar_done, 1)
                act.wait_ge(L0f_vector_done, 18*b + 31)
                act.activation(r0_0[:, 0, :], r0_0[:, 0, :], ACT.Relu, scale=mk0_0[:, 4:5]).then_inc(L0f_scalar_done, 1)
                act.activation(r0_0[:, 1, :], r0_0[:, 1, :], ACT.Relu, scale=mk0_0[:, 5:6]).then_inc(L0f_scalar_done, 1)
                act.wait_ge(L0f_vector_done, 18*b + 32)
                act.activation(r0_1[:, 0, :], r0_1[:, 0, :], ACT.Relu, scale=mk0_1[:, 4:5]).then_inc(L0f_scalar_done, 1)
                act.activation(r0_1[:, 1, :], r0_1[:, 1, :], ACT.Relu, scale=mk0_1[:, 5:6]).then_inc(L0f_scalar_done, 1)
                act.wait_ge(L0f_vector_done, 18*b + 33)
                act.activation(r0_0[:, 0, :], r0_0[:, 0, :], ACT.Relu, scale=mk0_0[:, 6:7]).then_inc(L0f_scalar_done, 1)
                act.activation(r0_0[:, 1, :], r0_0[:, 1, :], ACT.Relu, scale=mk0_0[:, 7:8]).then_inc(L0f_scalar_done, 1)
                act.wait_ge(L0f_matmul_done, 12*b + 13)
                act.activation(unT0[:, 0:2, :], ps0[:, 0, 0:256], ACT.Copy).then_inc(L0f_scalar_done, 1)
                act.wait_ge(L0f_matmul_done, 12*b + 14)
                act.activation(unT1[:, 0:2, :], ps1[:, 0, 0:256], ACT.Copy).then_inc(L0f_scalar_done, 1)
                act.wait_ge(L0f_vector_done, 18*b + 34)
                act.activation(r0_1[:, 0, :], r0_1[:, 0, :], ACT.Relu, scale=mk0_1[:, 6:7]).then_inc(L0f_scalar_done, 1)
                act.activation(r0_1[:, 1, :], r0_1[:, 1, :], ACT.Relu, scale=mk0_1[:, 7:8]).then_inc(L0f_scalar_done, 1)

            act.sem_inc(L1a_scalar_done, 6)
            act.wait_ge(L0f_scalar_done, 83)
            act.wait_ge(L1a_vector_done, 5)
            act.activation(st0[:, 8:9], st0[:, 7:8], ACT.Ln, bias=eps5[:, 0:1]).then_inc(L1a_scalar_done, 1)
            act.wait_ge(L0f_scalar_done, 84)
            act.wait_ge(L1a_vector_done, 6)
            act.activation(st1[:, 8:9], st1[:, 7:8], ACT.Ln, bias=eps5[:, 0:1]).then_inc(L1a_scalar_done, 1)
            act.wait_ge(L1a_scalar_done, 7)
            act.activation(st0[:, 9:10], st0[:, 8:9], ACT.Exp, scale=-0.5).then_inc(L1a_scalar_done, 1)
            act.wait_ge(L1a_scalar_done, 8)
            act.activation(st1[:, 9:10], st1[:, 8:9], ACT.Exp, scale=-0.5).then_inc(L1a_scalar_done, 1)
            act.wait_ge(L1a_matmul_done, 1)
            act.activation(unT0[:, 0:2, :], ps0[:, 0, 0:256], ACT.Copy)
            act.wait_ge(L1a_matmul_done, 2)
            act.activation(unT1[:, 0:2, :], ps1[:, 0, 0:256], ACT.Copy).then_inc(L1a_scalar_done, 1)
            act.wait_ge(L1a_scalar_done, 11)
            with act.Fori(0, 4) as b:
                act.wait_ge(L1a_vector_done, 10*b + 11)
                act.wait_ge(L1a_scalar_done, 11*b + 3)
                act.activation(st0[:, 8:9], st0[:, 7:8], ACT.Ln, bias=eps5[:, 0:1]).then_inc(L1a_scalar_done, 1)
                act.wait_ge(L1a_vector_done, 10*b + 12)
                act.wait_ge(L1a_scalar_done, 11*b + 4)
                act.activation(st1[:, 8:9], st1[:, 7:8], ACT.Ln, bias=eps5[:, 0:1]).then_inc(L1a_scalar_done, 1)
                act.wait_ge(L1a_scalar_done, 11*b + 12)
                act.activation(st0[:, 9:10], st0[:, 8:9], ACT.Exp, scale=-0.5).then_inc(L1a_scalar_done, 1)
                act.wait_ge(L1a_scalar_done, 11*b + 13)
                act.activation(st1[:, 9:10], st1[:, 8:9], ACT.Exp, scale=-0.5).then_inc(L1a_scalar_done, 1)
                act.wait_ge(L1a_matmul_done, 12*b + 3)
                act.activation(k1_0[:, :], ps0[:, 1, 256:512], ACT.Copy).then_inc(L1a_scalar_done, 1)
                act.activation(q1_0[:, :], ps0[:, 1, 0:256], ACT.Copy)
                act.wait_ge(L1a_matmul_done, 12*b + 4)
                act.activation(k1_1[:, :], ps1[:, 1, 256:512], ACT.Copy).then_inc(L1a_scalar_done, 1)
                act.activation(q1_1[:, :], ps1[:, 1, 0:256], ACT.Copy).then_inc(L1a_scalar_done, 1)
                act.wait_ge(L1a_matmul_done, 12*b + 9)
                act.activation(vT1_0[:, 0:2, :], ps0[:, 0, 0:256], ACT.Copy).then_inc(L1a_scalar_done, 1)
                act.wait_ge(L1a_matmul_done, 12*b + 10)
                act.activation(vT1_1[:, 0:2, :], ps1[:, 0, 0:256], ACT.Copy).then_inc(L1a_scalar_done, 1)
                act.wait_ge(L1a_matmul_done, 12*b + 13)
                act.activation(unT0[:, 0:2, :], ps0[:, 0, 0:256], ACT.Copy).then_inc(L1a_scalar_done, 1)
                act.wait_ge(L1a_matmul_done, 12*b + 14)
                act.activation(unT1[:, 0:2, :], ps1[:, 0, 0:256], ACT.Copy).then_inc(L1a_scalar_done, 1)

            act.wait_ge(L1x_w_loaded, 112)
            act.activation(dec[:, :], dec[:, :], ACT.Exp, scale=-1.0).then_inc(L1x_scalar_done, 1)
            act.wait_ge(L1x_vector_done, 16)
            act.activation(st0[:, 8:9], st0[:, 7:8], ACT.Ln, bias=eps5[:, 0:1]).then_inc(L1x_scalar_done, 1)
            act.wait_ge(L1x_vector_done, 17)
            act.activation(st1[:, 8:9], st1[:, 7:8], ACT.Ln, bias=eps5[:, 0:1]).then_inc(L1x_scalar_done, 1)
            act.wait_ge(L1x_scalar_done, 2)
            act.activation(st0[:, 9:10], st0[:, 8:9], ACT.Exp, scale=-0.5).then_inc(L1x_scalar_done, 1)
            act.wait_ge(L1x_scalar_done, 3)
            act.activation(st1[:, 9:10], st1[:, 8:9], ACT.Exp, scale=-0.5).then_inc(L1x_scalar_done, 1)
            act.wait_ge(L1x_vector_done, 18)
            with act.Fori(0, 4) as b:
                act.wait_ge(L1x_vector_done, 18*b + 30)
                act.wait_ge(L1x_scalar_done, 8*b + 3)
                act.activation(st0[:, 8:9], st0[:, 7:8], ACT.Ln, bias=eps5[:, 0:1]).then_inc(L1x_scalar_done, 1)
                act.wait_ge(L1x_scalar_done, 8*b + 6)
                act.activation(st0[:, 9:10], st0[:, 8:9], ACT.Exp, scale=-0.5).then_inc(L1x_scalar_done, 1)
                act.wait_ge(L1x_vector_done, 18*b + 32)
                act.activation(st1[:, 8:9], st1[:, 7:8], ACT.Ln, bias=eps5[:, 0:1]).then_inc(L1x_scalar_done, 1)
                act.wait_ge(L1x_scalar_done, 8*b + 8)
                act.activation(st1[:, 9:10], st1[:, 8:9], ACT.Exp, scale=-0.5).then_inc(L1x_scalar_done, 1)
                act.wait_ge(L1x_vector_done, 18*b + 34)
                act.activation(st0[:, 8:9], st0[:, 7:8], ACT.Ln, bias=eps5[:, 0:1]).then_inc(L1x_scalar_done, 1)
                act.wait_ge(L1x_scalar_done, 8*b + 10)
                act.activation(st0[:, 9:10], st0[:, 8:9], ACT.Exp, scale=-0.5).then_inc(L1x_scalar_done, 1)
                act.wait_ge(L1x_vector_done, 18*b + 36)
                act.activation(st1[:, 8:9], st1[:, 7:8], ACT.Ln, bias=eps5[:, 0:1]).then_inc(L1x_scalar_done, 1)
                act.wait_ge(L1x_scalar_done, 8*b + 12)
                act.activation(st1[:, 9:10], st1[:, 8:9], ACT.Exp, scale=-0.5).then_inc(L1x_scalar_done, 1)

            act.sem_inc(L1f_scalar_done, 17)
            act.wait_ge(L1x_scalar_done, 35)
            act.wait_ge(L1f_vector_done, 51)
            act.activation(st0[:, 8:9], st0[:, 7:8], ACT.Ln, bias=eps5[:, 0:1]).then_inc(L1f_scalar_done, 1)
            act.wait_ge(L1x_scalar_done, 37)
            act.wait_ge(L1f_vector_done, 52)
            act.activation(st1[:, 8:9], st1[:, 7:8], ACT.Ln, bias=eps5[:, 0:1]).then_inc(L1f_scalar_done, 1)
            act.wait_ge(L1f_scalar_done, 18)
            act.activation(st0[:, 9:10], st0[:, 8:9], ACT.Exp, scale=-0.5).then_inc(L1f_scalar_done, 1)
            act.wait_ge(L1f_scalar_done, 19)
            act.activation(st1[:, 9:10], st1[:, 8:9], ACT.Exp, scale=-0.5).then_inc(L1f_scalar_done, 1)
            act.wait_ge(L1f_matmul_done, 17)
            act.activation(unT0[:, 0:2, :], ps0[:, 0, 0:256], ACT.Copy)
            act.wait_ge(L1f_matmul_done, 18)
            act.activation(unT1[:, 0:2, :], ps1[:, 0, 0:256], ACT.Copy).then_inc(L1f_scalar_done, 1)
            act.wait_ge(L1f_scalar_done, 22)
            with act.Fori(0, 4) as b:
                act.wait_ge(L1f_vector_done, 56*b + 57)
                act.wait_ge(L1f_scalar_done, 22*b + 3)
                act.activation(st0[:, 8:9], st0[:, 7:8], ACT.Ln, bias=eps5[:, 0:1]).then_inc(L1f_scalar_done, 1)
                act.wait_ge(L1f_vector_done, 56*b + 58)
                act.wait_ge(L1f_scalar_done, 22*b + 4)
                act.activation(st1[:, 8:9], st1[:, 7:8], ACT.Ln, bias=eps5[:, 0:1]).then_inc(L1f_scalar_done, 1)
                act.wait_ge(L1f_scalar_done, 22*b + 23)
                act.activation(st0[:, 9:10], st0[:, 8:9], ACT.Exp, scale=-0.5).then_inc(L1f_scalar_done, 1)
                act.wait_ge(L1f_scalar_done, 22*b + 24)
                act.activation(st1[:, 9:10], st1[:, 8:9], ACT.Exp, scale=-0.5).then_inc(L1f_scalar_done, 1)
                act.wait_ge(L1f_matmul_done, 34*b + 19)
                act.activation(t1_0[:, :], ps0[:, 1, 0:256], ACT.Silu).then_inc(L1f_scalar_done, 1)
                act.wait_ge(L1f_matmul_done, 34*b + 20)
                act.activation(t1_1[:, :], ps1[:, 1, 0:256], ACT.Silu).then_inc(L1f_scalar_done, 1)
                act.wait_ge(L1f_matmul_done, 34*b + 21)
                act.wait_ge(L1f_vector_done, 56*b + 59)
                act.activation(t1_0[:, :], ps0[:, 2, 0:256], ACT.Silu).then_inc(L1f_scalar_done, 1)
                act.wait_ge(L1f_matmul_done, 34*b + 22)
                act.wait_ge(L1f_vector_done, 56*b + 60)
                act.activation(t1_1[:, :], ps1[:, 2, 0:256], ACT.Silu).then_inc(L1f_scalar_done, 1)
                act.wait_ge(L1f_vector_done, 56*b + 61)
                act.wait_ge(L1f_matmul_done, 34*b + 25)
                act.activation(t1_0[:, :], ps0[:, 1, 0:256], ACT.Silu).then_inc(L1f_scalar_done, 1)
                act.wait_ge(L1f_vector_done, 56*b + 65)
                act.wait_ge(L1f_matmul_done, 34*b + 26)
                act.activation(t1_1[:, :], ps1[:, 1, 0:256], ACT.Silu).then_inc(L1f_scalar_done, 1)
                act.wait_ge(L1f_vector_done, 56*b + 68)
                act.wait_ge(L1f_matmul_done, 34*b + 29)
                act.activation(t1_0[:, :], ps0[:, 2, 0:256], ACT.Silu).then_inc(L1f_scalar_done, 1)
                act.wait_ge(L1f_vector_done, 56*b + 70)
                act.wait_ge(L1f_matmul_done, 34*b + 30)
                act.activation(t1_1[:, :], ps1[:, 2, 0:256], ACT.Silu).then_inc(L1f_scalar_done, 1)
                act.wait_ge(L1f_vector_done, 56*b + 71)
                act.wait_ge(L1f_matmul_done, 34*b + 33)
                act.activation(t1_0[:, :], ps0[:, 1, 0:256], ACT.Silu)
                act.wait_ge(L1f_vector_done, 56*b + 72)
                act.wait_ge(L1f_matmul_done, 34*b + 34)
                act.activation(t1_1[:, :], ps1[:, 1, 0:256], ACT.Silu)
                act.activation(pr1_0[:, :], lg1_0[:, :], ACT.Exp, accum_out=st0[:, 17:18]).then_inc(L1f_scalar_done, 1)
                act.activation(pr1_1[:, :], lg1_1[:, :], ACT.Exp, accum_out=st1[:, 17:18]).then_inc(L1f_scalar_done, 1)
                act.wait_ge(L1f_vector_done, 56*b + 92)
                act.activation(t1_0[:, :], ps0[:, 2, 0:256], ACT.Silu).then_inc(L1f_scalar_done, 1)
                act.wait_ge(L1f_vector_done, 56*b + 94)
                act.activation(t1_1[:, :], ps1[:, 2, 0:256], ACT.Silu).then_inc(L1f_scalar_done, 1)
                act.wait_ge(L1f_matmul_done, 34*b + 41)
                act.wait_ge(L1f_vector_done, 56*b + 97)
                act.activation(t1_0[:, :], ps0[:, 1, 0:256], ACT.Silu).then_inc(L1f_scalar_done, 1)
                act.wait_ge(L1f_matmul_done, 34*b + 42)
                act.wait_ge(L1f_vector_done, 56*b + 98)
                act.activation(t1_1[:, :], ps1[:, 1, 0:256], ACT.Silu).then_inc(L1f_scalar_done, 1)
                act.wait_ge(L1f_vector_done, 56*b + 100)
                act.wait_ge(L1f_matmul_done, 34*b + 45)
                act.activation(t1_0[:, :], ps0[:, 2, 0:256], ACT.Silu).then_inc(L1f_scalar_done, 1)
                act.activation(unT0[:, 0:2, :], ps0[:, 0, 0:256], ACT.Copy).then_inc(L1f_scalar_done, 1)
                act.wait_ge(L1f_vector_done, 56*b + 102)
                act.wait_ge(L1f_matmul_done, 34*b + 46)
                act.activation(t1_1[:, :], ps1[:, 2, 0:256], ACT.Silu).then_inc(L1f_scalar_done, 1)
                act.activation(unT1[:, 0:2, :], ps1[:, 0, 0:256], ACT.Copy).then_inc(L1f_scalar_done, 1)

            act.sem_inc(L2a_scalar_done, 21)
            act.wait_ge(L1f_scalar_done, 91)
            act.wait_ge(L2a_vector_done, 42)
            act.activation(st0[:, 8:9], st0[:, 7:8], ACT.Ln, bias=eps5[:, 0:1]).then_inc(L2a_scalar_done, 1)
            act.wait_ge(L1f_scalar_done, 92)
            act.wait_ge(L2a_vector_done, 43)
            act.activation(st1[:, 8:9], st1[:, 7:8], ACT.Ln, bias=eps5[:, 0:1]).then_inc(L2a_scalar_done, 1)
            act.wait_ge(L2a_scalar_done, 22)
            act.activation(st0[:, 9:10], st0[:, 8:9], ACT.Exp, scale=-0.5).then_inc(L2a_scalar_done, 1)
            act.wait_ge(L2a_scalar_done, 23)
            act.activation(st1[:, 9:10], st1[:, 8:9], ACT.Exp, scale=-0.5).then_inc(L2a_scalar_done, 1)
            act.wait_ge(L2a_matmul_done, 1)
            act.activation(unT0[:, 0:2, :], ps0[:, 0, 0:256], ACT.Copy)
            act.wait_ge(L2a_matmul_done, 2)
            act.activation(unT1[:, 0:2, :], ps1[:, 0, 0:256], ACT.Copy).then_inc(L2a_scalar_done, 1)
            act.wait_ge(L2a_scalar_done, 26)
            with act.Fori(0, 4) as b:
                act.wait_ge(L2a_vector_done, 47*b + 48)
                act.wait_ge(L2a_scalar_done, 26*b + 3)
                act.activation(st0[:, 8:9], st0[:, 7:8], ACT.Ln, bias=eps5[:, 0:1]).then_inc(L2a_scalar_done, 1)
                act.wait_ge(L2a_vector_done, 47*b + 49)
                act.wait_ge(L2a_scalar_done, 26*b + 4)
                act.activation(st1[:, 8:9], st1[:, 7:8], ACT.Ln, bias=eps5[:, 0:1]).then_inc(L2a_scalar_done, 1)
                act.wait_ge(L2a_scalar_done, 26*b + 27)
                act.activation(st0[:, 9:10], st0[:, 8:9], ACT.Exp, scale=-0.5).then_inc(L2a_scalar_done, 1)
                act.wait_ge(L2a_scalar_done, 26*b + 28)
                act.activation(st1[:, 9:10], st1[:, 8:9], ACT.Exp, scale=-0.5).then_inc(L2a_scalar_done, 1)
                act.wait_ge(L2a_matmul_done, 29*b + 3)
                act.activation(qT_0[:, :, :], ps0[:, 1, 0:256], ACT.Copy).then_inc(L2a_scalar_done, 1)
                act.wait_ge(L2a_matmul_done, 29*b + 4)
                act.activation(qT_1[:, :, :], ps1[:, 1, 0:256], ACT.Copy).then_inc(L2a_scalar_done, 1)
                act.wait_ge(L2a_matmul_done, 29*b + 5)
                act.activation(v_0[:, :, 0:16], ps0[:, 2, 0:256].rearrange("p (h d) -> p h d", h=16), ACT.Copy)
                act.wait_ge(L2a_matmul_done, 29*b + 6)
                act.activation(v_1[:, :, 0:16], ps1[:, 2, 0:256].rearrange("p (h d) -> p h d", h=16), ACT.Copy)
                act.wait_ge(L2a_vector_done, 47*b + 57)
                for i in range(4):
                    last = act.activation(S_0[:, i, :], S_0[:, i, :], ACT.Exp, scale=0.25, bias=st0[:, 16 + i:17 + i])
                last.then_inc(L2a_scalar_done, 1)
                act.wait_ge(L2a_vector_done, 47*b + 59)
                for i in range(4):
                    last = act.activation(S_1[:, i, :], S_1[:, i, :], ACT.Exp, scale=0.25, bias=st1[:, 16 + i:17 + i])
                last.then_inc(L2a_scalar_done, 1)
                act.wait_ge(L2a_matmul_done, 29*b + 10)
                act.activation(PT_0[:, :, :], ps0[:, 2, :], ACT.Copy).then_inc(L2a_scalar_done, 1)
                act.wait_ge(L2a_matmul_done, 29*b + 11)
                act.activation(PT_1[:, :, :], ps1[:, 2, :], ACT.Copy).then_inc(L2a_scalar_done, 1)
                act.wait_ge(L2a_vector_done, 47*b + 63)
                for i in range(4):
                    last = act.activation(S_0[:, i, :], S_0[:, i, :], ACT.Exp, scale=0.25, bias=st0[:, 16 + i:17 + i])
                last.then_inc(L2a_scalar_done, 1)
                act.wait_ge(L2a_vector_done, 47*b + 67)
                for i in range(4):
                    last = act.activation(S_1[:, i, :], S_1[:, i, :], ACT.Exp, scale=0.25, bias=st1[:, 16 + i:17 + i])
                last.then_inc(L2a_scalar_done, 1)
                act.wait_ge(L2a_matmul_done, 29*b + 14)
                act.activation(PT_0[:, :, :], ps0[:, 2, :], ACT.Copy).then_inc(L2a_scalar_done, 1)
                act.wait_ge(L2a_matmul_done, 29*b + 15)
                act.activation(PT_1[:, :, :], ps1[:, 2, :], ACT.Copy).then_inc(L2a_scalar_done, 1)
                act.wait_ge(L2a_vector_done, 47*b + 71)
                for i in range(4):
                    last = act.activation(S_0[:, i, :], S_0[:, i, :], ACT.Exp, scale=0.25, bias=st0[:, 16 + i:17 + i])
                last.then_inc(L2a_scalar_done, 1)
                act.wait_ge(L2a_vector_done, 47*b + 75)
                for i in range(4):
                    last = act.activation(S_1[:, i, :], S_1[:, i, :], ACT.Exp, scale=0.25, bias=st1[:, 16 + i:17 + i])
                last.then_inc(L2a_scalar_done, 1)
                act.wait_ge(L2a_matmul_done, 29*b + 18)
                act.activation(PT_0[:, :, :], ps0[:, 2, :], ACT.Copy).then_inc(L2a_scalar_done, 1)
                act.wait_ge(L2a_matmul_done, 29*b + 19)
                act.activation(PT_1[:, :, :], ps1[:, 2, :], ACT.Copy).then_inc(L2a_scalar_done, 1)
                act.wait_ge(L2a_vector_done, 47*b + 81)
                for i in range(4):
                    last = act.activation(S_0[:, i, :], S_0[:, i, :], ACT.Exp, scale=0.25, bias=st0[:, 16 + i:17 + i])
                last.then_inc(L2a_scalar_done, 1)
                act.wait_ge(L2a_vector_done, 47*b + 85)
                for i in range(4):
                    last = act.activation(S_1[:, i, :], S_1[:, i, :], ACT.Exp, scale=0.25, bias=st1[:, 16 + i:17 + i])
                last.then_inc(L2a_scalar_done, 1)
                act.wait_ge(L2a_matmul_done, 29*b + 22)
                act.activation(PT_0[:, :, :], ps0[:, 2, :], ACT.Copy).then_inc(L2a_scalar_done, 1)
                act.wait_ge(L2a_matmul_done, 29*b + 23)
                act.activation(PT_1[:, :, :], ps1[:, 2, :], ACT.Copy).then_inc(L2a_scalar_done, 1)
                act.wait_ge(L2a_matmul_done, 29*b + 26)
                act.activation(unT0[:, 0:2, :], ps0[:, 0, 0:256], ACT.Copy).then_inc(L2a_scalar_done, 1)
                act.wait_ge(L2a_matmul_done, 29*b + 27)
                act.activation(unT1[:, 0:2, :], ps1[:, 0, 0:256], ACT.Copy).then_inc(L2a_scalar_done, 1)
                act.wait_ge(L2a_matmul_done, 29*b + 30)
                act.activation(unT0[:, 0:2, :], ps0[:, 0, 0:256], ACT.Copy).then_inc(L2a_scalar_done, 1)
                act.wait_ge(L2a_matmul_done, 29*b + 31)
                act.activation(unT1[:, 0:2, :], ps1[:, 0, 0:256], ACT.Copy).then_inc(L2a_scalar_done, 1)

            act.sem_inc(L2x_scalar_done, 98)
            act.wait_ge(L2a_scalar_done, 107)
            act.wait_ge(L2x_vector_done, 196)
            act.activation(st0[:, 8:9], st0[:, 7:8], ACT.Ln, bias=eps5[:, 0:1]).then_inc(L2x_scalar_done, 1)
            act.wait_ge(L2a_scalar_done, 108)
            act.wait_ge(L2x_vector_done, 197)
            act.activation(st1[:, 8:9], st1[:, 7:8], ACT.Ln, bias=eps5[:, 0:1]).then_inc(L2x_scalar_done, 1)
            act.wait_ge(L2x_scalar_done, 99)
            act.activation(st0[:, 9:10], st0[:, 8:9], ACT.Exp, scale=-0.5).then_inc(L2x_scalar_done, 1)
            act.wait_ge(L2x_scalar_done, 100)
            act.activation(st1[:, 9:10], st1[:, 8:9], ACT.Exp, scale=-0.5).then_inc(L2x_scalar_done, 1)
            act.wait_ge(L2x_vector_done, 202)
            act.activation(st0[:, 8:9], st0[:, 7:8], ACT.Ln, bias=eps5[:, 0:1]).then_inc(L2x_scalar_done, 1)
            act.wait_ge(L2x_vector_done, 203)
            act.activation(st1[:, 8:9], st1[:, 7:8], ACT.Ln, bias=eps5[:, 0:1]).then_inc(L2x_scalar_done, 1)
            act.wait_ge(L2x_scalar_done, 103)
            act.activation(st0[:, 9:10], st0[:, 8:9], ACT.Exp, scale=-0.5).then_inc(L2x_scalar_done, 1)
            act.wait_ge(L2x_scalar_done, 104)
            act.activation(st1[:, 9:10], st1[:, 8:9], ACT.Exp, scale=-0.5).then_inc(L2x_scalar_done, 1)
            act.wait_ge(L2x_matmul_done, 17)
            act.activation(unT0[:, 0:2, :], ps0[:, 0, 0:256], ACT.Copy).then_inc(L2x_scalar_done, 1)
            act.wait_ge(L2x_matmul_done, 18)
            act.activation(unT1[:, 0:2, :], ps1[:, 0, 0:256], ACT.Copy).then_inc(L2x_scalar_done, 1)
            act.wait_ge(L2x_pool_done, 4)
            with act.Fori(0, 4) as b:
                act.wait_ge(L2x_scalar_done, 108*b + 1)
                act.wait_ge(L2x_matmul_done, 124*b + 1)
                act.sem_inc(act_waited, 1)
                act.activation(cx_0[:, :, :], ctxT[:, :, ds(128 * (2*b+0), 128)], ACT.Copy).then_inc(L2x_scalar_done, 1)
                act.wait_ge(L2x_scalar_done, 108*b + 2)
                act.wait_ge(L2x_matmul_done, 124*b + 3)
                act.sem_inc(act_waited, 1)
                act.activation(cx_1[:, :, :], ctxT[:, :, ds(128 * (2*b+1), 128)], ACT.Copy).then_inc(L2x_scalar_done, 1)
                act.wait_ge(L2x_vector_done, 226*b + 221)
                act.wait_ge(L2x_scalar_done, 108*b + 9)
                act.activation(st0[:, 8:9], st0[:, 7:8], ACT.Ln, bias=eps5[:, 0:1]).then_inc(L2x_scalar_done, 1)
                act.wait_ge(L2x_vector_done, 226*b + 222)
                act.wait_ge(L2x_scalar_done, 108*b + 10)
                act.activation(st1[:, 8:9], st1[:, 7:8], ACT.Ln, bias=eps5[:, 0:1]).then_inc(L2x_scalar_done, 1)
                act.wait_ge(L2x_scalar_done, 108*b + 111)
                act.activation(st0[:, 9:10], st0[:, 8:9], ACT.Exp, scale=-0.5).then_inc(L2x_scalar_done, 1)
                act.wait_ge(L2x_scalar_done, 108*b + 112)
                act.activation(st1[:, 9:10], st1[:, 8:9], ACT.Exp, scale=-0.5).then_inc(L2x_scalar_done, 1)
                act.wait_ge(L2x_vector_done, 226*b + 227)
                act.activation(st0[:, 8:9], st0[:, 7:8], ACT.Ln, bias=eps5[:, 0:1]).then_inc(L2x_scalar_done, 1)
                act.wait_ge(L2x_vector_done, 226*b + 228)
                act.activation(st1[:, 8:9], st1[:, 7:8], ACT.Ln, bias=eps5[:, 0:1]).then_inc(L2x_scalar_done, 1)
                act.wait_ge(L2x_scalar_done, 108*b + 115)
                act.activation(st0[:, 9:10], st0[:, 8:9], ACT.Exp, scale=-0.5).then_inc(L2x_scalar_done, 1)
                act.wait_ge(L2x_scalar_done, 108*b + 116)
                act.activation(st1[:, 9:10], st1[:, 8:9], ACT.Exp, scale=-0.5).then_inc(L2x_scalar_done, 1)
                act.wait_ge(L2x_vector_done, 226*b + 235)
                act.activation(vv_0[:, :], vv_0[:, :], ACT.Ln, bias=eps5[:, 0:1]).then_inc(L2x_scalar_done, 1)
                act.wait_ge(L2x_scalar_done, 108*b + 119)
                act.activation(rr_0[:, :], vv_0[:, :], ACT.Exp, scale=-0.5).then_inc(L2x_scalar_done, 1)
                act.wait_ge(L2x_vector_done, 226*b + 238)
                act.activation(vv_1[:, :], vv_1[:, :], ACT.Ln, bias=eps5[:, 0:1]).then_inc(L2x_scalar_done, 1)
                act.wait_ge(L2x_scalar_done, 108*b + 121)
                act.activation(rr_1[:, :], vv_1[:, :], ACT.Exp, scale=-0.5).then_inc(L2x_scalar_done, 1)
                act.wait_ge(L2x_matmul_done, 124*b + 23)
                act.activation(qT2_0[:, :], ps0[:, 3, :], ACT.Identity, scale=nw2[:, 0, 0:1], bias=nw2[:, 0, 1:2])
                act.wait_ge(L2x_vector_done, 226*b + 242)
                act.activation(v2_0[:, :], ps0[:, 2, 256:512], ACT.Copy, scale=wsc[:, 3:4]).then_inc(L2x_scalar_done, 1)
                act.wait_ge(L2x_vector_done, 226*b + 244)
                act.activation(v2_1[:, :], ps1[:, 2, 256:512], ACT.Copy, scale=wsc[:, 3:4]).then_inc(L2x_scalar_done, 1)
                act.wait_ge(L2x_matmul_done, 124*b + 25)
                act.activation(qT2_1[:, :], ps1[:, 3, :], ACT.Identity, scale=nw2[:, 0, 0:1], bias=nw2[:, 0, 1:2])
                act.wait_ge(L2x_matmul_done, 124*b + 26)
                act.activation(kT2_0[:, :], ps0[:, 2, 0:256], ACT.Identity, scale=nw2[:, 2, 0:1], bias=nw2[:, 2, 1:2]).then_inc(L2x_scalar_done, 1)
                act.wait_ge(L2x_matmul_done, 124*b + 27)
                act.activation(kT2_1[:, :], ps1[:, 2, 0:256], ACT.Identity, scale=nw2[:, 2, 0:1], bias=nw2[:, 2, 1:2]).then_inc(L2x_scalar_done, 1)
                act.wait_ge(L2x_vector_done, 226*b + 246)
                for i in range(4):
                    last = act.activation(P2_0[:, i, :], ps0[:, 2, 128 * i:128 * i + 128], ACT.Exp, scale=0.08838834764831845, bias=st0[:, 16 + i:17 + i], accum_out=st0[:, 20 + i:21 + i])
                last.then_inc(L2x_scalar_done, 1)
                act.wait_ge(L2x_vector_done, 226*b + 248)
                for i in range(4):
                    last = act.activation(P2_1[:, i, :], ps1[:, 2, 128 * i:128 * i + 128], ACT.Exp, scale=0.08838834764831845, bias=st1[:, 16 + i:17 + i], accum_out=st1[:, 20 + i:21 + i])
                last.then_inc(L2x_scalar_done, 1)
                act.wait_ge(L2x_matmul_done, 124*b + 32)
                act.activation(PT2_0[:, :], ps0[:, 3, :], ACT.Copy).then_inc(L2x_scalar_done, 1)
                act.wait_ge(L2x_vector_done, 226*b + 253)
                act.activation(vv_0[:, :], vv_0[:, :], ACT.Ln, bias=eps5[:, 0:1]).then_inc(L2x_scalar_done, 1)
                act.wait_ge(L2x_scalar_done, 108*b + 130)
                act.activation(rr_0[:, :], vv_0[:, :], ACT.Exp, scale=-0.5).then_inc(L2x_scalar_done, 1)
                act.wait_ge(L2x_matmul_done, 124*b + 33)
                act.activation(PT2_1[:, :], ps1[:, 3, :], ACT.Copy).then_inc(L2x_scalar_done, 1)
                act.wait_ge(L2x_matmul_done, 124*b + 37)
                act.activation(qT2_0[:, :], ps0[:, 3, :], ACT.Identity, scale=nw2[:, 0, 0:1], bias=nw2[:, 0, 1:2])
                act.wait_ge(L2x_vector_done, 226*b + 261)
                act.activation(vv_1[:, :], vv_1[:, :], ACT.Ln, bias=eps5[:, 0:1]).then_inc(L2x_scalar_done, 1)
                act.wait_ge(L2x_scalar_done, 108*b + 133)
                act.activation(rr_1[:, :], vv_1[:, :], ACT.Exp, scale=-0.5).then_inc(L2x_scalar_done, 1)
                act.wait_ge(L2x_vector_done, 226*b + 264)
                act.activation(v2_0[:, :], ps0[:, 2, 256:512], ACT.Copy, scale=wsc[:, 3:4]).then_inc(L2x_scalar_done, 1)
                act.wait_ge(L2x_matmul_done, 124*b + 39)
                act.activation(kT2_0[:, :], ps0[:, 2, 0:256], ACT.Identity, scale=nw2[:, 2, 0:1], bias=nw2[:, 2, 1:2]).then_inc(L2x_scalar_done, 1)
                act.wait_ge(L2x_vector_done, 226*b + 268)
                act.activation(v2_1[:, :], ps1[:, 2, 256:512], ACT.Copy, scale=wsc[:, 3:4]).then_inc(L2x_scalar_done, 1)
                act.wait_ge(L2x_matmul_done, 124*b + 41)
                act.activation(qT2_1[:, :], ps1[:, 3, :], ACT.Identity, scale=nw2[:, 0, 0:1], bias=nw2[:, 0, 1:2])
                act.wait_ge(L2x_matmul_done, 124*b + 42)
                act.activation(kT2_1[:, :], ps1[:, 2, 0:256], ACT.Identity, scale=nw2[:, 2, 0:1], bias=nw2[:, 2, 1:2]).then_inc(L2x_scalar_done, 1)
                act.wait_ge(L2x_matmul_done, 124*b + 43)
                act.wait_ge(L2x_vector_done, 226*b + 270)
                for i in range(4):
                    last = act.activation(P2_0[:, i, :], ps0[:, 2, 128 * i:128 * i + 128], ACT.Exp, scale=0.08838834764831845, bias=st0[:, 16 + i:17 + i], accum_out=st0[:, 20 + i:21 + i])
                last.then_inc(L2x_scalar_done, 1)
                act.wait_ge(L2x_matmul_done, 124*b + 45)
                act.wait_ge(L2x_vector_done, 226*b + 273)
                for i in range(4):
                    last = act.activation(P2_1[:, i, :], ps1[:, 2, 128 * i:128 * i + 128], ACT.Exp, scale=0.08838834764831845, bias=st1[:, 16 + i:17 + i], accum_out=st1[:, 20 + i:21 + i])
                last.then_inc(L2x_scalar_done, 1)
                act.wait_ge(L2x_matmul_done, 124*b + 47)
                act.activation(PT2_0[:, :], ps0[:, 3, :], ACT.Copy).then_inc(L2x_scalar_done, 1)
                act.wait_ge(L2x_matmul_done, 124*b + 48)
                act.activation(PT2_1[:, :], ps1[:, 3, :], ACT.Copy).then_inc(L2x_scalar_done, 1)
                act.wait_ge(L2x_vector_done, 226*b + 280)
                act.activation(vv_0[:, :], vv_0[:, :], ACT.Ln, bias=eps5[:, 0:1]).then_inc(L2x_scalar_done, 1)
                act.wait_ge(L2x_scalar_done, 108*b + 143)
                act.activation(rr_0[:, :], vv_0[:, :], ACT.Exp, scale=-0.5).then_inc(L2x_scalar_done, 1)
                act.wait_ge(L2x_vector_done, 226*b + 285)
                act.activation(vv_1[:, :], vv_1[:, :], ACT.Ln, bias=eps5[:, 0:1]).then_inc(L2x_scalar_done, 1)
                act.wait_ge(L2x_scalar_done, 108*b + 145)
                act.activation(rr_1[:, :], vv_1[:, :], ACT.Exp, scale=-0.5).then_inc(L2x_scalar_done, 1)
                act.wait_ge(L2x_matmul_done, 124*b + 53)
                act.activation(qT2_0[:, :], ps0[:, 3, :], ACT.Identity, scale=nw2[:, 0, 0:1], bias=nw2[:, 0, 1:2])
                act.wait_ge(L2x_vector_done, 226*b + 291)
                act.activation(v2_0[:, :], ps0[:, 2, 256:512], ACT.Copy, scale=wsc[:, 3:4]).then_inc(L2x_scalar_done, 1)
                act.wait_ge(L2x_vector_done, 226*b + 293)
                act.activation(v2_1[:, :], ps1[:, 2, 256:512], ACT.Copy, scale=wsc[:, 3:4]).then_inc(L2x_scalar_done, 1)
                act.wait_ge(L2x_matmul_done, 124*b + 55)
                act.activation(qT2_1[:, :], ps1[:, 3, :], ACT.Identity, scale=nw2[:, 0, 0:1], bias=nw2[:, 0, 1:2])
                act.wait_ge(L2x_matmul_done, 124*b + 56)
                act.activation(kT2_0[:, :], ps0[:, 2, 0:256], ACT.Identity, scale=nw2[:, 2, 0:1], bias=nw2[:, 2, 1:2]).then_inc(L2x_scalar_done, 1)
                act.wait_ge(L2x_matmul_done, 124*b + 57)
                act.activation(kT2_1[:, :], ps1[:, 2, 0:256], ACT.Identity, scale=nw2[:, 2, 0:1], bias=nw2[:, 2, 1:2]).then_inc(L2x_scalar_done, 1)
                act.wait_ge(L2x_vector_done, 226*b + 295)
                for i in range(4):
                    last = act.activation(P2_0[:, i, :], ps0[:, 2, 128 * i:128 * i + 128], ACT.Exp, scale=0.08838834764831845, bias=st0[:, 16 + i:17 + i], accum_out=st0[:, 20 + i:21 + i])
                last.then_inc(L2x_scalar_done, 1)
                act.wait_ge(L2x_matmul_done, 124*b + 60)
                act.wait_ge(L2x_vector_done, 226*b + 297)
                for i in range(4):
                    last = act.activation(P2_1[:, i, :], ps1[:, 2, 128 * i:128 * i + 128], ACT.Exp, scale=0.08838834764831845, bias=st1[:, 16 + i:17 + i], accum_out=st1[:, 20 + i:21 + i])
                last.then_inc(L2x_scalar_done, 1)
                act.wait_ge(L2x_matmul_done, 124*b + 62)
                act.activation(PT2_0[:, :], ps0[:, 3, :], ACT.Copy).then_inc(L2x_scalar_done, 1)
                act.wait_ge(L2x_matmul_done, 124*b + 63)
                act.activation(PT2_1[:, :], ps1[:, 3, :], ACT.Copy).then_inc(L2x_scalar_done, 1)
                act.wait_ge(L2x_vector_done, 226*b + 305)
                act.activation(vv_0[:, :], vv_0[:, :], ACT.Ln, bias=eps5[:, 0:1]).then_inc(L2x_scalar_done, 1)
                act.wait_ge(L2x_scalar_done, 108*b + 155)
                act.activation(rr_0[:, :], vv_0[:, :], ACT.Exp, scale=-0.5).then_inc(L2x_scalar_done, 1)
                act.wait_ge(L2x_vector_done, 226*b + 310)
                act.activation(vv_1[:, :], vv_1[:, :], ACT.Ln, bias=eps5[:, 0:1]).then_inc(L2x_scalar_done, 1)
                act.wait_ge(L2x_scalar_done, 108*b + 157)
                act.activation(rr_1[:, :], vv_1[:, :], ACT.Exp, scale=-0.5).then_inc(L2x_scalar_done, 1)
                act.wait_ge(L2x_matmul_done, 124*b + 68)
                act.activation(qT2_0[:, :], ps0[:, 3, :], ACT.Identity, scale=nw2[:, 0, 0:1], bias=nw2[:, 0, 1:2])
                act.wait_ge(L2x_vector_done, 226*b + 316)
                act.activation(v2_0[:, :], ps0[:, 2, 256:512], ACT.Copy, scale=wsc[:, 3:4]).then_inc(L2x_scalar_done, 1)
                act.wait_ge(L2x_vector_done, 226*b + 318)
                act.activation(v2_1[:, :], ps1[:, 2, 256:512], ACT.Copy, scale=wsc[:, 3:4]).then_inc(L2x_scalar_done, 1)
                act.wait_ge(L2x_matmul_done, 124*b + 70)
                act.activation(qT2_1[:, :], ps1[:, 3, :], ACT.Identity, scale=nw2[:, 0, 0:1], bias=nw2[:, 0, 1:2])
                act.wait_ge(L2x_matmul_done, 124*b + 71)
                act.activation(kT2_0[:, :], ps0[:, 2, 0:256], ACT.Identity, scale=nw2[:, 2, 0:1], bias=nw2[:, 2, 1:2]).then_inc(L2x_scalar_done, 1)
                act.wait_ge(L2x_matmul_done, 124*b + 72)
                act.activation(kT2_1[:, :], ps1[:, 2, 0:256], ACT.Identity, scale=nw2[:, 2, 0:1], bias=nw2[:, 2, 1:2]).then_inc(L2x_scalar_done, 1)
                act.wait_ge(L2x_vector_done, 226*b + 320)
                for i in range(4):
                    last = act.activation(P2_0[:, i, :], ps0[:, 2, 128 * i:128 * i + 128], ACT.Exp, scale=0.08838834764831845, bias=st0[:, 16 + i:17 + i], accum_out=st0[:, 20 + i:21 + i])
                last.then_inc(L2x_scalar_done, 1)
                act.wait_ge(L2x_matmul_done, 124*b + 75)
                act.wait_ge(L2x_vector_done, 226*b + 322)
                for i in range(4):
                    last = act.activation(P2_1[:, i, :], ps1[:, 2, 128 * i:128 * i + 128], ACT.Exp, scale=0.08838834764831845, bias=st1[:, 16 + i:17 + i], accum_out=st1[:, 20 + i:21 + i])
                last.then_inc(L2x_scalar_done, 1)
                act.wait_ge(L2x_matmul_done, 124*b + 77)
                act.activation(PT2_0[:, :], ps0[:, 3, :], ACT.Copy).then_inc(L2x_scalar_done, 1)
                act.wait_ge(L2x_matmul_done, 124*b + 78)
                act.activation(PT2_1[:, :], ps1[:, 3, :], ACT.Copy).then_inc(L2x_scalar_done, 1)
                act.wait_ge(L2x_vector_done, 226*b + 330)
                act.activation(vv_0[:, :], vv_0[:, :], ACT.Ln, bias=eps5[:, 0:1]).then_inc(L2x_scalar_done, 1)
                act.wait_ge(L2x_scalar_done, 108*b + 167)
                act.activation(rr_0[:, :], vv_0[:, :], ACT.Exp, scale=-0.5).then_inc(L2x_scalar_done, 1)
                act.wait_ge(L2x_vector_done, 226*b + 335)
                act.activation(vv_1[:, :], vv_1[:, :], ACT.Ln, bias=eps5[:, 0:1]).then_inc(L2x_scalar_done, 1)
                act.wait_ge(L2x_scalar_done, 108*b + 169)
                act.activation(rr_1[:, :], vv_1[:, :], ACT.Exp, scale=-0.5).then_inc(L2x_scalar_done, 1)
                act.wait_ge(L2x_matmul_done, 124*b + 83)
                act.activation(qT2_0[:, :], ps0[:, 3, :], ACT.Identity, scale=nw2[:, 1, 0:1], bias=nw2[:, 1, 1:2])
                act.wait_ge(L2x_vector_done, 226*b + 341)
                act.activation(v2_0[:, :], ps0[:, 2, 256:512], ACT.Copy).then_inc(L2x_scalar_done, 1)
                act.wait_ge(L2x_vector_done, 226*b + 343)
                act.activation(v2_1[:, :], ps1[:, 2, 256:512], ACT.Copy).then_inc(L2x_scalar_done, 1)
                act.wait_ge(L2x_matmul_done, 124*b + 85)
                act.activation(qT2_1[:, :], ps1[:, 3, :], ACT.Identity, scale=nw2[:, 1, 0:1], bias=nw2[:, 1, 1:2])
                act.wait_ge(L2x_matmul_done, 124*b + 86)
                act.activation(kT2_0[:, :], ps0[:, 2, 0:256], ACT.Identity, scale=nw2[:, 3, 0:1], bias=nw2[:, 3, 1:2]).then_inc(L2x_scalar_done, 1)
                act.wait_ge(L2x_matmul_done, 124*b + 87)
                act.activation(kT2_1[:, :], ps1[:, 2, 0:256], ACT.Identity, scale=nw2[:, 3, 0:1], bias=nw2[:, 3, 1:2]).then_inc(L2x_scalar_done, 1)
                act.wait_ge(L2x_vector_done, 226*b + 345)
                for i in range(4):
                    last = act.activation(P2_0[:, i, :], ps0[:, 2, 128 * i:128 * i + 128], ACT.Exp, scale=0.08838834764831845, bias=st0[:, 16 + i:17 + i], accum_out=st0[:, 20 + i:21 + i])
                last.then_inc(L2x_scalar_done, 1)
                act.wait_ge(L2x_matmul_done, 124*b + 90)
                act.wait_ge(L2x_vector_done, 226*b + 347)
                for i in range(4):
                    last = act.activation(P2_1[:, i, :], ps1[:, 2, 128 * i:128 * i + 128], ACT.Exp, scale=0.08838834764831845, bias=st1[:, 16 + i:17 + i], accum_out=st1[:, 20 + i:21 + i])
                last.then_inc(L2x_scalar_done, 1)
                act.wait_ge(L2x_matmul_done, 124*b + 92)
                act.activation(PT2_0[:, :], ps0[:, 3, :], ACT.Copy).then_inc(L2x_scalar_done, 1)
                act.wait_ge(L2x_matmul_done, 124*b + 93)
                act.activation(PT2_1[:, :], ps1[:, 3, :], ACT.Copy).then_inc(L2x_scalar_done, 1)
                act.wait_ge(L2x_vector_done, 226*b + 355)
                act.activation(vv_0[:, :], vv_0[:, :], ACT.Ln, bias=eps5[:, 0:1]).then_inc(L2x_scalar_done, 1)
                act.wait_ge(L2x_scalar_done, 108*b + 179)
                act.activation(rr_0[:, :], vv_0[:, :], ACT.Exp, scale=-0.5).then_inc(L2x_scalar_done, 1)
                act.wait_ge(L2x_vector_done, 226*b + 360)
                act.activation(vv_1[:, :], vv_1[:, :], ACT.Ln, bias=eps5[:, 0:1]).then_inc(L2x_scalar_done, 1)
                act.wait_ge(L2x_scalar_done, 108*b + 181)
                act.activation(rr_1[:, :], vv_1[:, :], ACT.Exp, scale=-0.5).then_inc(L2x_scalar_done, 1)
                act.wait_ge(L2x_matmul_done, 124*b + 98)
                act.activation(qT2_0[:, :], ps0[:, 3, :], ACT.Identity, scale=nw2[:, 1, 0:1], bias=nw2[:, 1, 1:2])
                act.wait_ge(L2x_vector_done, 226*b + 366)
                act.activation(v2_0[:, :], ps0[:, 2, 256:512], ACT.Copy).then_inc(L2x_scalar_done, 1)
                act.wait_ge(L2x_vector_done, 226*b + 368)
                act.activation(v2_1[:, :], ps1[:, 2, 256:512], ACT.Copy).then_inc(L2x_scalar_done, 1)
                act.wait_ge(L2x_matmul_done, 124*b + 100)
                act.activation(qT2_1[:, :], ps1[:, 3, :], ACT.Identity, scale=nw2[:, 1, 0:1], bias=nw2[:, 1, 1:2])
                act.wait_ge(L2x_matmul_done, 124*b + 101)
                act.activation(kT2_0[:, :], ps0[:, 2, 0:256], ACT.Identity, scale=nw2[:, 3, 0:1], bias=nw2[:, 3, 1:2]).then_inc(L2x_scalar_done, 1)
                act.wait_ge(L2x_matmul_done, 124*b + 102)
                act.activation(kT2_1[:, :], ps1[:, 2, 0:256], ACT.Identity, scale=nw2[:, 3, 0:1], bias=nw2[:, 3, 1:2]).then_inc(L2x_scalar_done, 1)
                act.wait_ge(L2x_vector_done, 226*b + 370)
                for i in range(4):
                    last = act.activation(P2_0[:, i, :], ps0[:, 2, 128 * i:128 * i + 128], ACT.Exp, scale=0.08838834764831845, bias=st0[:, 16 + i:17 + i], accum_out=st0[:, 20 + i:21 + i])
                last.then_inc(L2x_scalar_done, 1)
                act.wait_ge(L2x_matmul_done, 124*b + 105)
                act.wait_ge(L2x_vector_done, 226*b + 372)
                for i in range(4):
                    last = act.activation(P2_1[:, i, :], ps1[:, 2, 128 * i:128 * i + 128], ACT.Exp, scale=0.08838834764831845, bias=st1[:, 16 + i:17 + i], accum_out=st1[:, 20 + i:21 + i])
                last.then_inc(L2x_scalar_done, 1)
                act.wait_ge(L2x_matmul_done, 124*b + 107)
                act.activation(PT2_0[:, :], ps0[:, 3, :], ACT.Copy).then_inc(L2x_scalar_done, 1)
                act.wait_ge(L2x_matmul_done, 124*b + 108)
                act.activation(PT2_1[:, :], ps1[:, 3, :], ACT.Copy).then_inc(L2x_scalar_done, 1)
                act.wait_ge(L2x_vector_done, 226*b + 380)
                act.activation(vv_0[:, :], vv_0[:, :], ACT.Ln, bias=eps5[:, 0:1]).then_inc(L2x_scalar_done, 1)
                act.wait_ge(L2x_scalar_done, 108*b + 191)
                act.activation(rr_0[:, :], vv_0[:, :], ACT.Exp, scale=-0.5).then_inc(L2x_scalar_done, 1)
                act.wait_ge(L2x_vector_done, 226*b + 385)
                act.activation(vv_1[:, :], vv_1[:, :], ACT.Ln, bias=eps5[:, 0:1]).then_inc(L2x_scalar_done, 1)
                act.wait_ge(L2x_scalar_done, 108*b + 193)
                act.activation(rr_1[:, :], vv_1[:, :], ACT.Exp, scale=-0.5).then_inc(L2x_scalar_done, 1)
                act.wait_ge(L2x_matmul_done, 124*b + 113)
                act.activation(qT2_0[:, :], ps0[:, 3, :], ACT.Identity, scale=nw2[:, 1, 0:1], bias=nw2[:, 1, 1:2])
                act.wait_ge(L2x_vector_done, 226*b + 391)
                act.activation(v2_0[:, :], ps0[:, 2, 256:512], ACT.Copy).then_inc(L2x_scalar_done, 1)
                act.wait_ge(L2x_vector_done, 226*b + 393)
                act.activation(v2_1[:, :], ps1[:, 2, 256:512], ACT.Copy).then_inc(L2x_scalar_done, 1)
                act.wait_ge(L2x_matmul_done, 124*b + 115)
                act.activation(qT2_1[:, :], ps1[:, 3, :], ACT.Identity, scale=nw2[:, 1, 0:1], bias=nw2[:, 1, 1:2])
                act.wait_ge(L2x_matmul_done, 124*b + 116)
                act.activation(kT2_0[:, :], ps0[:, 2, 0:256], ACT.Identity, scale=nw2[:, 3, 0:1], bias=nw2[:, 3, 1:2]).then_inc(L2x_scalar_done, 1)
                act.wait_ge(L2x_matmul_done, 124*b + 117)
                act.activation(kT2_1[:, :], ps1[:, 2, 0:256], ACT.Identity, scale=nw2[:, 3, 0:1], bias=nw2[:, 3, 1:2]).then_inc(L2x_scalar_done, 1)
                act.wait_ge(L2x_vector_done, 226*b + 395)
                for i in range(4):
                    last = act.activation(P2_0[:, i, :], ps0[:, 2, 128 * i:128 * i + 128], ACT.Exp, scale=0.08838834764831845, bias=st0[:, 16 + i:17 + i], accum_out=st0[:, 20 + i:21 + i])
                last.then_inc(L2x_scalar_done, 1)
                act.wait_ge(L2x_matmul_done, 124*b + 120)
                act.wait_ge(L2x_vector_done, 226*b + 397)
                for i in range(4):
                    last = act.activation(P2_1[:, i, :], ps1[:, 2, 128 * i:128 * i + 128], ACT.Exp, scale=0.08838834764831845, bias=st1[:, 16 + i:17 + i], accum_out=st1[:, 20 + i:21 + i])
                last.then_inc(L2x_scalar_done, 1)
                act.wait_ge(L2x_matmul_done, 124*b + 122)
                act.activation(PT2_0[:, :], ps0[:, 3, :], ACT.Copy).then_inc(L2x_scalar_done, 1)
                act.wait_ge(L2x_matmul_done, 124*b + 123)
                act.activation(PT2_1[:, :], ps1[:, 3, :], ACT.Copy).then_inc(L2x_scalar_done, 1)
                act.wait_ge(L2x_vector_done, 226*b + 405)
                act.activation(vv_0[:, :], vv_0[:, :], ACT.Ln, bias=eps5[:, 0:1]).then_inc(L2x_scalar_done, 1)
                act.wait_ge(L2x_scalar_done, 108*b + 203)
                act.activation(rr_0[:, :], vv_0[:, :], ACT.Exp, scale=-0.5).then_inc(L2x_scalar_done, 1)
                act.wait_ge(L2x_vector_done, 226*b + 410)
                act.activation(vv_1[:, :], vv_1[:, :], ACT.Ln, bias=eps5[:, 0:1]).then_inc(L2x_scalar_done, 1)
                act.wait_ge(L2x_scalar_done, 108*b + 205)
                act.activation(rr_1[:, :], vv_1[:, :], ACT.Exp, scale=-0.5).then_inc(L2x_scalar_done, 1)
                act.wait_ge(L2x_matmul_done, 124*b + 128)
                act.activation(qT2_0[:, :], ps0[:, 3, :], ACT.Identity, scale=nw2[:, 1, 0:1], bias=nw2[:, 1, 1:2])
                act.wait_ge(L2x_vector_done, 226*b + 416)
                act.activation(v2_0[:, :], ps0[:, 2, 256:512], ACT.Copy).then_inc(L2x_scalar_done, 1)
                act.wait_ge(L2x_matmul_done, 124*b + 129)
                act.activation(qT2_1[:, :], ps1[:, 3, :], ACT.Identity, scale=nw2[:, 1, 0:1], bias=nw2[:, 1, 1:2])
                act.wait_ge(L2x_vector_done, 226*b + 418)
                act.activation(v2_1[:, :], ps1[:, 2, 256:512], ACT.Copy).then_inc(L2x_scalar_done, 1)
                act.wait_ge(L2x_matmul_done, 124*b + 130)
                act.activation(kT2_0[:, :], ps0[:, 2, 0:256], ACT.Identity, scale=nw2[:, 3, 0:1], bias=nw2[:, 3, 1:2]).then_inc(L2x_scalar_done, 1)
                act.wait_ge(L2x_matmul_done, 124*b + 131)
                act.activation(kT2_1[:, :], ps1[:, 2, 0:256], ACT.Identity, scale=nw2[:, 3, 0:1], bias=nw2[:, 3, 1:2]).then_inc(L2x_scalar_done, 1)
                act.wait_ge(L2x_vector_done, 226*b + 420)
                for i in range(4):
                    last = act.activation(P2_0[:, i, :], ps0[:, 2, 128 * i:128 * i + 128], ACT.Exp, scale=0.08838834764831845, bias=st0[:, 16 + i:17 + i], accum_out=st0[:, 20 + i:21 + i])
                last.then_inc(L2x_scalar_done, 1)
                act.wait_ge(L2x_matmul_done, 124*b + 134)
                act.wait_ge(L2x_vector_done, 226*b + 422)
                for i in range(4):
                    last = act.activation(P2_1[:, i, :], ps1[:, 2, 128 * i:128 * i + 128], ACT.Exp, scale=0.08838834764831845, bias=st1[:, 16 + i:17 + i], accum_out=st1[:, 20 + i:21 + i])
                last.then_inc(L2x_scalar_done, 1)
                act.wait_ge(L2x_matmul_done, 124*b + 135)
                act.activation(PT2_0[:, :], ps0[:, 3, :], ACT.Copy).then_inc(L2x_scalar_done, 1)
                act.wait_ge(L2x_matmul_done, 124*b + 137)
                act.activation(PT2_1[:, :], ps1[:, 3, :], ACT.Copy).then_inc(L2x_scalar_done, 1)
                act.wait_ge(L2x_matmul_done, 124*b + 141)
                act.activation(unT0[:, 0:2, :], ps0[:, 0, 0:256], ACT.Copy).then_inc(L2x_scalar_done, 1)
                act.wait_ge(L2x_matmul_done, 124*b + 142)
                act.activation(unT1[:, 0:2, :], ps1[:, 0, 0:256], ACT.Copy).then_inc(L2x_scalar_done, 1)

            act.sem_inc(L2f_scalar_done, 32)
            act.wait_ge(L2x_scalar_done, 441)
            act.wait_ge(L2f_vector_done, 48)
            act.activation(st0[:, 8:9], st0[:, 7:8], ACT.Ln, bias=eps5[:, 0:1]).then_inc(L2f_scalar_done, 1)
            act.wait_ge(L2x_scalar_done, 442)
            act.wait_ge(L2f_vector_done, 49)
            act.activation(st1[:, 8:9], st1[:, 7:8], ACT.Ln, bias=eps5[:, 0:1]).then_inc(L2f_scalar_done, 1)
            act.wait_ge(L2f_scalar_done, 33)
            act.activation(st0[:, 9:10], st0[:, 8:9], ACT.Exp, scale=-0.5).then_inc(L2f_scalar_done, 1)
            act.wait_ge(L2f_scalar_done, 34)
            act.activation(st1[:, 9:10], st1[:, 8:9], ACT.Exp, scale=-0.5).then_inc(L2f_scalar_done, 1)
            act.wait_ge(L2f_matmul_done, 1)
            act.activation(unT0[:, 0:2, :], ps0[:, 0, 0:256], ACT.Copy)
            act.wait_ge(L2f_matmul_done, 2)
            act.activation(unT1[:, 0:2, :], ps1[:, 0, 0:256], ACT.Copy).then_inc(L2f_scalar_done, 1)
            act.wait_ge(L2x_pool_done, 212)
            act.wait_ge(L2f_scalar_done, 37)
            with act.Fori(0, 4) as b:
                act.wait_ge(L2f_vector_done, 53*b + 54)
                act.wait_ge(L2f_scalar_done, 37*b + 3)
                act.activation(st0[:, 8:9], st0[:, 7:8], ACT.Ln, bias=eps5[:, 0:1]).then_inc(L2f_scalar_done, 1)
                act.wait_ge(L2f_vector_done, 53*b + 55)
                act.wait_ge(L2f_scalar_done, 37*b + 4)
                act.activation(st1[:, 8:9], st1[:, 7:8], ACT.Ln, bias=eps5[:, 0:1]).then_inc(L2f_scalar_done, 1)
                act.wait_ge(L2f_scalar_done, 37*b + 38)
                act.activation(st0[:, 9:10], st0[:, 8:9], ACT.Exp, scale=-0.5).then_inc(L2f_scalar_done, 1)
                act.wait_ge(L2f_scalar_done, 37*b + 39)
                act.activation(st1[:, 9:10], st1[:, 8:9], ACT.Exp, scale=-0.5).then_inc(L2f_scalar_done, 1)
                act.wait_ge(L2f_vector_done, 53*b + 56)
                act.wait_ge(L2f_pool_done, 18*b + 3)
                act.activation(he_0[:, :, :], hb_0[:, :, :], ACT.Silu).then_inc(L2f_scalar_done, 1)
                act.wait_ge(L2f_vector_done, 53*b + 57)
                act.wait_ge(L2f_pool_done, 18*b + 4)
                act.activation(he_1[:, :, :], hb_1[:, :, :], ACT.Silu).then_inc(L2f_scalar_done, 1)
                act.wait_ge(L2f_matmul_done, 29*b + 7)
                act.activation(qc_0[:, :, :], psf0[:, 1024:2048], ACT.Copy).then_inc(L2f_scalar_done, 1)
                act.wait_ge(L2f_matmul_done, 29*b + 8)
                act.activation(qc_1[:, :, :], psf1[:, 1024:2048], ACT.Copy).then_inc(L2f_scalar_done, 1)
                act.wait_ge(L2f_matmul_done, 29*b + 9)
                act.activation(sim_0[:, :, :, :], psf0[:, 0:1024].rearrange('p (q c) -> p q c', q=2)[:, :, 0:360].rearrange('p q (h k) -> p q h k', h=8), ACT.Copy).then_inc(L2f_scalar_done, 1)
                act.wait_ge(L2f_matmul_done, 29*b + 10)
                act.activation(sim_1[:, :, :, :], psf1[:, 0:1024].rearrange('p (q c) -> p q c', q=2)[:, :, 0:360].rearrange('p q (h k) -> p q h k', h=8), ACT.Copy).then_inc(L2f_scalar_done, 1)
                act.wait_ge(L2f_matmul_done, 29*b + 11)
                act.activation(z_0[:, 0:2025], psf0[:, 0:2025], ACT.Copy).then_inc(L2f_scalar_done, 1)
                act.wait_ge(L2f_matmul_done, 29*b + 12)
                act.activation(z_1[:, 0:2025], psf1[:, 0:2025], ACT.Copy)
                act.wait_ge(L2f_pool_done, 18*b + 5)
                act.activation(sim_0[:, :, :, :], sim_0[:, :, :, :], ACT.Exp).then_inc(L2f_scalar_done, 1)
                act.wait_ge(L2f_pool_done, 18*b + 6)
                act.activation(sim_1[:, :, :, :], sim_1[:, :, :, :], ACT.Exp).then_inc(L2f_scalar_done, 1)
                act.wait_ge(L2f_vector_done, 53*b + 62)
                act.activation(v8_0[:, :, :, :], c_0[:, 0:2, :, :], ACT.Exp).then_inc(L2f_scalar_done, 1)
                act.wait_ge(L2f_vector_done, 53*b + 63)
                act.activation(v8_1[:, :, :, :], c_1[:, 0:2, :, :], ACT.Exp).then_inc(L2f_scalar_done, 1)
                act.wait_ge(L2f_vector_done, 53*b + 72)
                act.activation(Qfa_0[:, :], Qfa_0[:, :], ACT.Silu).then_inc(L2f_scalar_done, 1)
                act.wait_ge(L2f_vector_done, 53*b + 74)
                act.activation(Qfa_1[:, :], Qfa_1[:, :], ACT.Silu).then_inc(L2f_scalar_done, 1)
                act.wait_ge(L2f_vector_done, 53*b + 77)
                act.activation(Qfb_0[:, :], Qfb_0[:, :], ACT.Silu).then_inc(L2f_scalar_done, 1)
                act.wait_ge(L2f_vector_done, 53*b + 78)
                act.activation(Qfb_1[:, :], Qfb_1[:, :], ACT.Silu).then_inc(L2f_scalar_done, 1)
                act.wait_ge(L2f_vector_done, 53*b + 81)
                act.activation(Qfa_0[:, :], Qfa_0[:, :], ACT.Silu).then_inc(L2f_scalar_done, 1)
                act.wait_ge(L2f_vector_done, 53*b + 82)
                act.activation(Qfa_1[:, :], Qfa_1[:, :], ACT.Silu).then_inc(L2f_scalar_done, 1)
                act.wait_ge(L2f_vector_done, 53*b + 85)
                act.activation(Qfb_0[:, :], Qfb_0[:, :], ACT.Silu).then_inc(L2f_scalar_done, 1)
                act.wait_ge(L2f_vector_done, 53*b + 86)
                act.activation(Qfb_1[:, :], Qfb_1[:, :], ACT.Silu).then_inc(L2f_scalar_done, 1)
                act.wait_ge(L2f_vector_done, 53*b + 89)
                act.activation(Qfa_0[:, :], Qfa_0[:, :], ACT.Silu).then_inc(L2f_scalar_done, 1)
                act.wait_ge(L2f_vector_done, 53*b + 90)
                act.activation(Qfa_1[:, :], Qfa_1[:, :], ACT.Silu).then_inc(L2f_scalar_done, 1)
                act.wait_ge(L2f_vector_done, 53*b + 93)
                act.activation(Qfb_0[:, :], Qfb_0[:, :], ACT.Silu).then_inc(L2f_scalar_done, 1)
                act.wait_ge(L2f_vector_done, 53*b + 94)
                act.activation(Qfb_1[:, :], Qfb_1[:, :], ACT.Silu).then_inc(L2f_scalar_done, 1)
                act.wait_ge(L2f_vector_done, 53*b + 97)
                act.activation(Qfa_0[:, :], Qfa_0[:, :], ACT.Silu).then_inc(L2f_scalar_done, 1)
                act.wait_ge(L2f_vector_done, 53*b + 98)
                act.activation(Qfa_1[:, :], Qfa_1[:, :], ACT.Silu).then_inc(L2f_scalar_done, 1)
                act.wait_ge(L2f_vector_done, 53*b + 101)
                act.activation(Qfb_0[:, :], Qfb_0[:, :], ACT.Silu).then_inc(L2f_scalar_done, 1)
                act.wait_ge(L2f_vector_done, 53*b + 102)
                act.activation(Qfb_1[:, :], Qfb_1[:, :], ACT.Silu).then_inc(L2f_scalar_done, 1)
                act.wait_ge(L2f_matmul_done, 29*b + 25)
                act.activation(GT_0[:, 0:15, :], psf0[:, 0:1920], ACT.Copy).then_inc(L2f_scalar_done, 1)
                act.wait_ge(L2f_matmul_done, 29*b + 26)
                act.activation(GT_1[:, 0:15, :], psf1[:, 0:1920], ACT.Copy).then_inc(L2f_scalar_done, 1)
                act.activation(GT_0[0:105, 15, :], psf0[0:105, 1920:2048], ACT.Copy).then_inc(L2f_scalar_done, 1)
                act.activation(GT_1[0:105, 15, :], psf1[0:105, 1920:2048], ACT.Copy).then_inc(L2f_scalar_done, 1)
                act.wait_ge(L2f_matmul_done, 29*b + 30)
                act.activation(unT0[:, 0:2, :], ps0[:, 0, 0:256], ACT.Copy).then_inc(L2f_scalar_done, 1)
                act.wait_ge(L2f_matmul_done, 29*b + 31)
                act.activation(unT1[:, 0:2, :], ps1[:, 0, 0:256], ACT.Copy).then_inc(L2f_scalar_done, 1)
            act.preload_act_table_set('natural_log_exp_and_others')

            act.sem_inc(L3a_scalar_done, 35)
            act.wait_ge(L3a_vector_done, 69)
            act.activation(st0[:, 8:9], st0[:, 7:8], ACT.Ln, bias=eps5[:, 0:1]).then_inc(L3a_scalar_done, 1)
            act.wait_ge(L3a_vector_done, 70)
            act.activation(st1[:, 8:9], st1[:, 7:8], ACT.Ln, bias=eps5[:, 0:1]).then_inc(L3a_scalar_done, 1)
            act.wait_ge(L3a_scalar_done, 36)
            act.activation(st0[:, 9:10], st0[:, 8:9], ACT.Exp, scale=-0.5).then_inc(L3a_scalar_done, 1)
            act.wait_ge(L3a_scalar_done, 37)
            act.activation(st1[:, 9:10], st1[:, 8:9], ACT.Exp, scale=-0.5).then_inc(L3a_scalar_done, 1)
            act.wait_ge(L3a_matmul_done, 1)
            act.activation(unT0[:, 0:2, :], ps0[:, 0, 0:256], ACT.Copy)
            act.wait_ge(L3a_matmul_done, 2)
            act.activation(unT1[:, 0:2, :], ps1[:, 0, 0:256], ACT.Copy).then_inc(L3a_scalar_done, 1)
            act.wait_ge(L2f_pool_done, 75)
            act.wait_ge(L3a_scalar_done, 40)
            with act.Fori(0, 4) as b:
                act.wait_ge(L3a_vector_done, 74*b + 75)
                act.wait_ge(L3a_scalar_done, 40*b + 3)
                act.activation(st0[:, 8:9], st0[:, 7:8], ACT.Ln, bias=eps5[:, 0:1]).then_inc(L3a_scalar_done, 1)
                act.wait_ge(L3a_vector_done, 74*b + 76)
                act.wait_ge(L3a_scalar_done, 40*b + 4)
                act.activation(st1[:, 8:9], st1[:, 7:8], ACT.Ln, bias=eps5[:, 0:1]).then_inc(L3a_scalar_done, 1)
                act.wait_ge(L3a_scalar_done, 40*b + 41)
                act.activation(st0[:, 9:10], st0[:, 8:9], ACT.Exp, scale=-0.5).then_inc(L3a_scalar_done, 1)
                act.wait_ge(L3a_scalar_done, 40*b + 42)
                act.activation(st1[:, 9:10], st1[:, 8:9], ACT.Exp, scale=-0.5).then_inc(L3a_scalar_done, 1)
                act.wait_ge(L3a_vector_done, 74*b + 82)
                for i in range(4):
                    last = act.activation(S_0[:, i, :], ps0[:, 1, 128 * i:128 * i + 128], ACT.Exp, scale=0.3535533905932738, bias=st0[:, 16 + i:17 + i])
                last.then_inc(L3a_scalar_done, 1)
                act.wait_ge(L3a_vector_done, 74*b + 84)
                for i in range(4):
                    last = act.activation(S_1[:, i, :], ps1[:, 1, 128 * i:128 * i + 128], ACT.Exp, scale=0.3535533905932738, bias=st1[:, 16 + i:17 + i])
                last.then_inc(L3a_scalar_done, 1)
                act.wait_ge(L3a_matmul_done, 56*b + 8)
                act.activation(PT_0[:, :, :], ps0[:, 2, :], ACT.Copy).then_inc(L3a_scalar_done, 1)
                act.wait_ge(L3a_vector_done, 74*b + 86)
                for i in range(4):
                    last = act.activation(S_0[:, i, :], ps0[:, 1, 128 * i:128 * i + 128], ACT.Exp, scale=0.3535533905932738, bias=st0[:, 16 + i:17 + i])
                last.then_inc(L3a_scalar_done, 1)
                act.wait_ge(L3a_matmul_done, 56*b + 10)
                act.activation(PT_1[:, :, :], ps1[:, 2, :], ACT.Copy).then_inc(L3a_scalar_done, 1)
                act.wait_ge(L3a_vector_done, 74*b + 89)
                for i in range(4):
                    last = act.activation(S_1[:, i, :], ps1[:, 1, 128 * i:128 * i + 128], ACT.Exp, scale=0.3535533905932738, bias=st1[:, 16 + i:17 + i])
                last.then_inc(L3a_scalar_done, 1)
                act.wait_ge(L3a_matmul_done, 56*b + 13)
                act.activation(PT_0[:, :, :], ps0[:, 2, :], ACT.Copy).then_inc(L3a_scalar_done, 1)
                act.wait_ge(L3a_vector_done, 74*b + 93)
                for i in range(4):
                    last = act.activation(S_0[:, i, :], ps0[:, 1, 128 * i:128 * i + 128], ACT.Exp, scale=0.3535533905932738, bias=st0[:, 16 + i:17 + i])
                last.then_inc(L3a_scalar_done, 1)
                act.wait_ge(L3a_matmul_done, 56*b + 16)
                act.activation(PT_1[:, :, :], ps1[:, 2, :], ACT.Copy).then_inc(L3a_scalar_done, 1)
                act.wait_ge(L3a_vector_done, 74*b + 97)
                for i in range(4):
                    last = act.activation(S_1[:, i, :], ps1[:, 1, 128 * i:128 * i + 128], ACT.Exp, scale=0.3535533905932738, bias=st1[:, 16 + i:17 + i])
                last.then_inc(L3a_scalar_done, 1)
                act.wait_ge(L3a_matmul_done, 56*b + 19)
                act.activation(PT_0[:, :, :], ps0[:, 2, :], ACT.Copy).then_inc(L3a_scalar_done, 1)
                act.wait_ge(L3a_vector_done, 74*b + 101)
                for i in range(4):
                    last = act.activation(S_0[:, i, :], ps0[:, 1, 128 * i:128 * i + 128], ACT.Exp, scale=0.3535533905932738, bias=st0[:, 16 + i:17 + i])
                last.then_inc(L3a_scalar_done, 1)
                act.wait_ge(L3a_matmul_done, 56*b + 22)
                act.activation(PT_1[:, :, :], ps1[:, 2, :], ACT.Copy).then_inc(L3a_scalar_done, 1)
                act.wait_ge(L3a_vector_done, 74*b + 105)
                for i in range(4):
                    last = act.activation(S_1[:, i, :], ps1[:, 1, 128 * i:128 * i + 128], ACT.Exp, scale=0.3535533905932738, bias=st1[:, 16 + i:17 + i])
                last.then_inc(L3a_scalar_done, 1)
                act.wait_ge(L3a_matmul_done, 56*b + 25)
                act.activation(PT_0[:, :, :], ps0[:, 2, :], ACT.Copy).then_inc(L3a_scalar_done, 1)
                act.wait_ge(L3a_vector_done, 74*b + 109)
                for i in range(4):
                    last = act.activation(S_0[:, i, :], ps0[:, 1, 128 * i:128 * i + 128], ACT.Exp, scale=0.3535533905932738, bias=st0[:, 16 + i:17 + i])
                last.then_inc(L3a_scalar_done, 1)
                act.wait_ge(L3a_matmul_done, 56*b + 28)
                act.activation(PT_1[:, :, :], ps1[:, 2, :], ACT.Copy).then_inc(L3a_scalar_done, 1)
                act.wait_ge(L3a_vector_done, 74*b + 113)
                for i in range(4):
                    last = act.activation(S_1[:, i, :], ps1[:, 1, 128 * i:128 * i + 128], ACT.Exp, scale=0.3535533905932738, bias=st1[:, 16 + i:17 + i])
                last.then_inc(L3a_scalar_done, 1)
                act.wait_ge(L3a_matmul_done, 56*b + 31)
                act.activation(PT_0[:, :, :], ps0[:, 2, :], ACT.Copy).then_inc(L3a_scalar_done, 1)
                act.wait_ge(L3a_vector_done, 74*b + 117)
                for i in range(4):
                    last = act.activation(S_0[:, i, :], ps0[:, 1, 128 * i:128 * i + 128], ACT.Exp, scale=0.3535533905932738, bias=st0[:, 16 + i:17 + i])
                last.then_inc(L3a_scalar_done, 1)
                act.wait_ge(L3a_matmul_done, 56*b + 34)
                act.activation(PT_1[:, :, :], ps1[:, 2, :], ACT.Copy).then_inc(L3a_scalar_done, 1)
                act.wait_ge(L3a_vector_done, 74*b + 121)
                for i in range(4):
                    last = act.activation(S_1[:, i, :], ps1[:, 1, 128 * i:128 * i + 128], ACT.Exp, scale=0.3535533905932738, bias=st1[:, 16 + i:17 + i])
                last.then_inc(L3a_scalar_done, 1)
                act.wait_ge(L3a_matmul_done, 56*b + 37)
                act.activation(PT_0[:, :, :], ps0[:, 2, :], ACT.Copy).then_inc(L3a_scalar_done, 1)
                act.wait_ge(L3a_vector_done, 74*b + 125)
                for i in range(4):
                    last = act.activation(S_0[:, i, :], ps0[:, 1, 128 * i:128 * i + 128], ACT.Exp, scale=0.3535533905932738, bias=st0[:, 16 + i:17 + i])
                last.then_inc(L3a_scalar_done, 1)
                act.wait_ge(L3a_matmul_done, 56*b + 40)
                act.activation(PT_1[:, :, :], ps1[:, 2, :], ACT.Copy).then_inc(L3a_scalar_done, 1)
                act.wait_ge(L3a_vector_done, 74*b + 129)
                for i in range(4):
                    last = act.activation(S_1[:, i, :], ps1[:, 1, 128 * i:128 * i + 128], ACT.Exp, scale=0.3535533905932738, bias=st1[:, 16 + i:17 + i])
                last.then_inc(L3a_scalar_done, 1)
                act.wait_ge(L3a_matmul_done, 56*b + 43)
                act.activation(PT_0[:, :, :], ps0[:, 2, :], ACT.Copy).then_inc(L3a_scalar_done, 1)
                act.wait_ge(L3a_vector_done, 74*b + 133)
                for i in range(4):
                    last = act.activation(S_0[:, i, :], ps0[:, 1, 128 * i:128 * i + 128], ACT.Exp, scale=0.3535533905932738, bias=st0[:, 16 + i:17 + i])
                last.then_inc(L3a_scalar_done, 1)
                act.wait_ge(L3a_matmul_done, 56*b + 46)
                act.activation(PT_1[:, :, :], ps1[:, 2, :], ACT.Copy).then_inc(L3a_scalar_done, 1)
                act.wait_ge(L3a_vector_done, 74*b + 137)
                for i in range(4):
                    last = act.activation(S_1[:, i, :], ps1[:, 1, 128 * i:128 * i + 128], ACT.Exp, scale=0.3535533905932738, bias=st1[:, 16 + i:17 + i])
                last.then_inc(L3a_scalar_done, 1)
                act.wait_ge(L3a_matmul_done, 56*b + 48)
                act.activation(PT_0[:, :, :], ps0[:, 2, :], ACT.Copy).then_inc(L3a_scalar_done, 1)
                act.wait_ge(L3a_matmul_done, 56*b + 50)
                act.activation(PT_1[:, :, :], ps1[:, 2, :], ACT.Copy).then_inc(L3a_scalar_done, 1)
                act.wait_ge(L3a_matmul_done, 56*b + 53)
                act.activation(unT0[:, 0:2, :], ps0[:, 0, 0:256], ACT.Copy).then_inc(L3a_scalar_done, 1)
                act.wait_ge(L3a_matmul_done, 56*b + 54)
                act.activation(unT1[:, 0:2, :], ps1[:, 0, 0:256], ACT.Copy).then_inc(L3a_scalar_done, 1)
                act.wait_ge(L3a_matmul_done, 56*b + 57)
                act.activation(unT0[:, 0:2, :], ps0[:, 0, 0:256], ACT.Copy).then_inc(L3a_scalar_done, 1)
                act.wait_ge(L3a_matmul_done, 56*b + 58)
                act.activation(unT1[:, 0:2, :], ps1[:, 0, 0:256], ACT.Copy).then_inc(L3a_scalar_done, 1)

            act.sem_inc(L3x_scalar_done, 13)
            act.wait_ge(L3x_vector_done, 21)
            act.activation(st0[:, 8:9], st0[:, 7:8], ACT.Ln, bias=eps5[:, 0:1]).then_inc(L3x_scalar_done, 1)
            act.wait_ge(L3x_vector_done, 22)
            act.activation(st1[:, 8:9], st1[:, 7:8], ACT.Ln, bias=eps5[:, 0:1]).then_inc(L3x_scalar_done, 1)
            act.wait_ge(L3x_scalar_done, 14)
            act.activation(st0[:, 9:10], st0[:, 8:9], ACT.Exp, scale=-0.5).then_inc(L3x_scalar_done, 1)
            act.wait_ge(L3x_scalar_done, 15)
            act.activation(st1[:, 9:10], st1[:, 8:9], ACT.Exp, scale=-0.5).then_inc(L3x_scalar_done, 1)
            act.wait_ge(L3x_matmul_done, 14)
            act.activation(unT0[:, 0:2, :], ps0[:, 0, 0:256], ACT.Copy)
            act.wait_ge(L3x_matmul_done, 15)
            act.activation(unT1[:, 0:2, :], ps1[:, 0, 0:256], ACT.Copy).then_inc(L3x_scalar_done, 1)
            act.wait_ge(L3x_scalar_done, 18)
            with act.Fori(0, 4) as b:
                act.wait_ge(L3x_scalar_done, 18*b + 1)
                act.wait_ge(L3x_matmul_done, 16*b + 1)
                act.sem_inc(act_waited, 1)
                act.activation(cT_0[:, :, :], ctxT[:, :, ds(128 * (2*b+0), 128)], ACT.Copy).then_inc(L3x_scalar_done, 1)
                act.wait_ge(L3x_scalar_done, 18*b + 2)
                act.wait_ge(L3x_matmul_done, 16*b + 2)
                act.sem_inc(act_waited, 1)
                act.activation(cT_1[:, :, :], ctxT[:, :, ds(128 * (2*b+1), 128)], ACT.Copy).then_inc(L3x_scalar_done, 1)
                act.wait_ge(L3x_vector_done, 26*b + 27)
                act.wait_ge(L3x_scalar_done, 18*b + 5)
                act.activation(st0[:, 8:9], st0[:, 7:8], ACT.Ln, bias=eps5[:, 0:1]).then_inc(L3x_scalar_done, 1)
                act.wait_ge(L3x_vector_done, 26*b + 28)
                act.wait_ge(L3x_scalar_done, 18*b + 6)
                act.activation(st1[:, 8:9], st1[:, 7:8], ACT.Ln, bias=eps5[:, 0:1]).then_inc(L3x_scalar_done, 1)
                act.wait_ge(L3x_scalar_done, 18*b + 21)
                act.activation(st0[:, 9:10], st0[:, 8:9], ACT.Exp, scale=-0.5).then_inc(L3x_scalar_done, 1)
                act.wait_ge(L3x_scalar_done, 18*b + 22)
                act.activation(st1[:, 9:10], st1[:, 8:9], ACT.Exp, scale=-0.5).then_inc(L3x_scalar_done, 1)
                act.wait_ge(L3x_vector_done, 26*b + 30)
                act.activation(jk0[:, :], jk0[:, :], ACT.Exp).then_inc(L3x_scalar_done, 1)
                act.wait_ge(L3x_vector_done, 26*b + 31)
                act.activation(ga_0[:, :], ga_0[:, :], ACT.Exp, scale=-1.0).then_inc(L3x_scalar_done, 1)
                act.wait_ge(L3x_vector_done, 26*b + 33)
                act.activation(ks_0[:, :], ks_0[:, :], ACT.Exp).then_inc(L3x_scalar_done, 1)
                act.wait_ge(L3x_vector_done, 26*b + 34)
                act.activation(ks_1[:, :], ks_1[:, :], ACT.Exp).then_inc(L3x_scalar_done, 1)
                act.wait_ge(L3x_vector_done, 26*b + 35)
                act.activation(v3_0[:, :, 0:128], ps0[:, 2, 256:512].rearrange("p (c e) -> p c e", c=2), ACT.Copy).then_inc(L3x_scalar_done, 1)
                act.wait_ge(L3x_matmul_done, 16*b + 20)
                act.activation(unT0[:, 0:2, :], ps0[:, 0, 0:256], ACT.Copy)
                act.wait_ge(L3x_vector_done, 26*b + 37)
                act.activation(jk1[:, :], jk1[:, :], ACT.Exp).then_inc(L3x_scalar_done, 1)
                act.wait_ge(L3x_vector_done, 26*b + 38)
                act.activation(v3_1[:, :, 0:128], ps1[:, 2, 256:512].rearrange("p (c e) -> p c e", c=2), ACT.Copy).then_inc(L3x_scalar_done, 1)
                act.wait_ge(L3x_vector_done, 26*b + 39)
                act.activation(ga_1[:, :], ga_1[:, :], ACT.Exp, scale=-1.0).then_inc(L3x_scalar_done, 1)
                act.wait_ge(L3x_matmul_done, 16*b + 23)
                act.activation(unT1[:, 0:2, :], ps1[:, 0, 0:256], ACT.Copy).then_inc(L3x_scalar_done, 1)
                act.wait_ge(L3x_matmul_done, 16*b + 26)
                act.activation(unT0[:, 0:2, :], ps0[:, 0, 0:256], ACT.Copy).then_inc(L3x_scalar_done, 1)
                act.wait_ge(L3x_matmul_done, 16*b + 27)
                act.activation(unT1[:, 0:2, :], ps1[:, 0, 0:256], ACT.Copy).then_inc(L3x_scalar_done, 1)
                act.wait_ge(L3x_matmul_done, 16*b + 30)
                act.activation(unT0[:, 0:2, :], ps0[:, 0, 0:256], ACT.Copy).then_inc(L3x_scalar_done, 1)
                act.wait_ge(L3x_matmul_done, 16*b + 31)
                act.activation(unT1[:, 0:2, :], ps1[:, 0, 0:256], ACT.Copy)

            act.sem_inc(L3f_scalar_done, 27)
            act.wait_ge(L3f_vector_done, 54)
            act.activation(st0[:, 8:9], st0[:, 7:8], ACT.Ln, bias=eps5[:, 0:1]).then_inc(L3f_scalar_done, 1)
            act.wait_ge(L3f_vector_done, 55)
            act.activation(st1[:, 8:9], st1[:, 7:8], ACT.Ln, bias=eps5[:, 0:1]).then_inc(L3f_scalar_done, 1)
            act.wait_ge(L3f_scalar_done, 28)
            act.activation(st0[:, 9:10], st0[:, 8:9], ACT.Exp, scale=-0.5).then_inc(L3f_scalar_done, 1)
            act.wait_ge(L3f_scalar_done, 29)
            act.activation(st1[:, 9:10], st1[:, 8:9], ACT.Exp, scale=-0.5).then_inc(L3f_scalar_done, 1)
            act.wait_ge(L3f_vector_done, 56)
            act.activation(jk0[:, :], u0[:, :], ACT.Square, scale=1.0 / 16.0, accum_out=st0[:, 10:11]).then_inc(L3f_scalar_done, 1)
            act.wait_ge(L3f_vector_done, 57)
            act.activation(jk1[:, :], u1[:, :], ACT.Square, scale=1.0 / 16.0, accum_out=st1[:, 10:11]).then_inc(L3f_scalar_done, 1)
            act.wait_ge(L3f_scalar_done, 32)
            act.activation(st0[:, 11:12], st0[:, 10:11], ACT.Ln, bias=eps6[:, 0:1]).then_inc(L3f_scalar_done, 1)
            act.wait_ge(L3f_scalar_done, 33)
            act.activation(st1[:, 11:12], st1[:, 10:11], ACT.Ln, bias=eps6[:, 0:1]).then_inc(L3f_scalar_done, 1)
            act.wait_ge(L3f_scalar_done, 34)
            act.activation(st0[:, 12:13], st0[:, 11:12], ACT.Exp, scale=-0.5).then_inc(L3f_scalar_done, 1)
            act.wait_ge(L3f_scalar_done, 35)
            act.activation(st1[:, 12:13], st1[:, 11:12], ACT.Exp, scale=-0.5).then_inc(L3f_scalar_done, 1)
            act.wait_ge(L3f_matmul_done, 1)
            act.activation(unT0[:, 0:2, :], ps0[:, 0, 0:256], ACT.Copy)
            act.wait_ge(L3f_matmul_done, 2)
            act.activation(unT1[:, 0:2, :], ps1[:, 0, 0:256], ACT.Copy).then_inc(L3f_scalar_done, 1)
            act.wait_ge(L3x_pool_done, 18)
            act.wait_ge(L3f_scalar_done, 38)
            with act.Fori(0, 4) as b:
                act.wait_ge(L3f_vector_done, 61*b + 56)
                act.wait_ge(L3f_scalar_done, 44*b + 33)
                act.activation(jk0[:, :], u0[:, :], ACT.Square, scale=1.0 / 16.0, accum_out=st0[:, 10:11]).then_inc(L3f_scalar_done, 1)
                act.wait_ge(L3f_vector_done, 61*b + 57)
                act.wait_ge(L3f_scalar_done, 44*b + 34)
                act.activation(jk1[:, :], u1[:, :], ACT.Square, scale=1.0 / 16.0, accum_out=st1[:, 10:11]).then_inc(L3f_scalar_done, 1)
                act.wait_ge(L3f_scalar_done, 44*b + 39)
                act.activation(st0[:, 11:12], st0[:, 10:11], ACT.Ln, bias=eps6[:, 0:1]).then_inc(L3f_scalar_done, 1)
                act.wait_ge(L3f_scalar_done, 44*b + 40)
                act.activation(st1[:, 11:12], st1[:, 10:11], ACT.Ln, bias=eps6[:, 0:1]).then_inc(L3f_scalar_done, 1)
                act.wait_ge(L3f_scalar_done, 44*b + 41)
                act.wait_ge(L3f_vector_done, 61*b + 58)
                act.activation(st0[:, 12:13], st0[:, 11:12], ACT.Exp, scale=-0.5).then_inc(L3f_scalar_done, 1)
                act.wait_ge(L3f_scalar_done, 44*b + 42)
                act.wait_ge(L3f_vector_done, 61*b + 59)
                act.activation(st1[:, 12:13], st1[:, 11:12], ACT.Exp, scale=-0.5).then_inc(L3f_scalar_done, 1)
                act.wait_ge(L3f_vector_done, 61*b + 62)
                act.activation(st0[:, 8:9], st0[:, 7:8], ACT.Ln, bias=eps5[:, 0:1]).then_inc(L3f_scalar_done, 1)
                act.wait_ge(L3f_matmul_done, 38*b + 3)
                act.activation(qT_0[:, :, :], ps0[:, 1, 0:256], ACT.Copy).then_inc(L3f_scalar_done, 1)
                act.wait_ge(L3f_vector_done, 61*b + 63)
                act.activation(st1[:, 8:9], st1[:, 7:8], ACT.Ln, bias=eps5[:, 0:1]).then_inc(L3f_scalar_done, 1)
                act.wait_ge(L3f_scalar_done, 44*b + 45)
                act.activation(st0[:, 9:10], st0[:, 8:9], ACT.Exp, scale=-0.5)
                act.wait_ge(L3f_scalar_done, 44*b + 47)
                act.activation(st1[:, 9:10], st1[:, 8:9], ACT.Exp, scale=-0.5)
                act.wait_ge(L3f_matmul_done, 38*b + 4)
                act.activation(qT_1[:, :, :], ps1[:, 1, 0:256], ACT.Copy).then_inc(L3f_scalar_done, 1)
                act.wait_ge(L3f_matmul_done, 38*b + 5)
                act.activation(v_0[:, :, 0:16], ps0[:, 2, 0:256].rearrange("p (h d) -> p h d", h=16), ACT.Copy)
                act.wait_ge(L3f_matmul_done, 38*b + 6)
                act.activation(v_1[:, :, 0:16], ps1[:, 2, 0:256].rearrange("p (h d) -> p h d", h=16), ACT.Copy)
                act.wait_ge(L3f_vector_done, 61*b + 69)
                for i in range(4):
                    last = act.activation(S_0[:, i, :], S_0[:, i, :], ACT.Exp, scale=0.25, bias=st0[:, 16 + i:17 + i])
                last.then_inc(L3f_scalar_done, 1)
                act.wait_ge(L3f_vector_done, 61*b + 71)
                for i in range(4):
                    last = act.activation(S_1[:, i, :], S_1[:, i, :], ACT.Exp, scale=0.25, bias=st1[:, 16 + i:17 + i])
                last.then_inc(L3f_scalar_done, 1)
                act.wait_ge(L3f_matmul_done, 38*b + 9)
                act.activation(PT_0[:, :, :], ps0[:, 2, :], ACT.Copy).then_inc(L3f_scalar_done, 1)
                act.wait_ge(L3f_vector_done, 61*b + 74)
                for i in range(4):
                    last = act.activation(S_0[:, i, :], S_0[:, i, :], ACT.Exp, scale=0.25, bias=st0[:, 16 + i:17 + i])
                last.then_inc(L3f_scalar_done, 1)
                act.wait_ge(L3f_matmul_done, 38*b + 10)
                act.activation(PT_1[:, :, :], ps1[:, 2, :], ACT.Copy).then_inc(L3f_scalar_done, 1)
                act.wait_ge(L3f_vector_done, 61*b + 78)
                for i in range(4):
                    last = act.activation(S_1[:, i, :], S_1[:, i, :], ACT.Exp, scale=0.25, bias=st1[:, 16 + i:17 + i])
                last.then_inc(L3f_scalar_done, 1)
                act.wait_ge(L3f_matmul_done, 38*b + 12)
                act.activation(PT_0[:, :, :], ps0[:, 2, :], ACT.Copy).then_inc(L3f_scalar_done, 1)
                act.wait_ge(L3f_vector_done, 61*b + 82)
                for i in range(4):
                    last = act.activation(S_0[:, i, :], S_0[:, i, :], ACT.Exp, scale=0.25, bias=st0[:, 16 + i:17 + i])
                last.then_inc(L3f_scalar_done, 1)
                act.wait_ge(L3f_matmul_done, 38*b + 14)
                act.activation(PT_1[:, :, :], ps1[:, 2, :], ACT.Copy).then_inc(L3f_scalar_done, 1)
                act.wait_ge(L3f_vector_done, 61*b + 86)
                for i in range(4):
                    last = act.activation(S_1[:, i, :], S_1[:, i, :], ACT.Exp, scale=0.25, bias=st1[:, 16 + i:17 + i])
                last.then_inc(L3f_scalar_done, 1)
                act.wait_ge(L3f_matmul_done, 38*b + 16)
                act.activation(PT_0[:, :, :], ps0[:, 2, :], ACT.Copy).then_inc(L3f_scalar_done, 1)
                act.wait_ge(L3f_matmul_done, 38*b + 18)
                act.activation(PT_1[:, :, :], ps1[:, 2, :], ACT.Copy).then_inc(L3f_scalar_done, 1)
                act.wait_ge(L3f_vector_done, 61*b + 91)
                for i in range(4):
                    last = act.activation(S_0[:, i, :], S_0[:, i, :], ACT.Exp, scale=0.25, bias=st0[:, 16 + i:17 + i])
                last.then_inc(L3f_scalar_done, 1)
                act.wait_ge(L3f_vector_done, 61*b + 95)
                for i in range(4):
                    last = act.activation(S_1[:, i, :], S_1[:, i, :], ACT.Exp, scale=0.25, bias=st1[:, 16 + i:17 + i])
                last.then_inc(L3f_scalar_done, 1)
                act.wait_ge(L3f_matmul_done, 38*b + 21)
                act.activation(PT_0[:, :, :], ps0[:, 2, :], ACT.Copy).then_inc(L3f_scalar_done, 1)
                act.wait_ge(L3f_matmul_done, 38*b + 22)
                act.activation(PT_1[:, :, :], ps1[:, 2, :], ACT.Copy).then_inc(L3f_scalar_done, 1)
                act.wait_ge(L3f_matmul_done, 38*b + 25)
                act.activation(unT0[:, 0:2, :], ps0[:, 0, 0:256], ACT.Copy).then_inc(L3f_scalar_done, 1)
                act.wait_ge(L3f_matmul_done, 38*b + 26)
                act.activation(unT1[:, 0:2, :], ps1[:, 0, 0:256], ACT.Copy).then_inc(L3f_scalar_done, 1)
                act.wait_ge(L3f_matmul_done, 38*b + 27)
                act.activation(qT_0[:, :, :], ps0[:, 1, 0:256], ACT.Copy).then_inc(L3f_scalar_done, 1)
                act.wait_ge(L3f_matmul_done, 38*b + 28)
                act.activation(qT_1[:, :, :], ps1[:, 1, 0:256], ACT.Copy).then_inc(L3f_scalar_done, 1)
                act.wait_ge(L3f_matmul_done, 38*b + 30)
                act.activation(unT0[:, 0:2, :], ps0[:, 0, 0:256], ACT.Copy).then_inc(L3f_scalar_done, 1)
                act.wait_ge(L3f_vector_done, 61*b + 103)
                act.activation(md_0[0:16, :], md_0[0:16, :], ACT.Exp, scale=2.0).then_inc(L3f_scalar_done, 1)
                act.wait_ge(L3f_matmul_done, 38*b + 31)
                act.activation(unT1[:, 0:2, :], ps1[:, 0, 0:256], ACT.Copy).then_inc(L3f_scalar_done, 1)
                act.wait_ge(L3f_vector_done, 61*b + 104)
                act.activation(md_1[0:16, :], md_1[0:16, :], ACT.Exp, scale=2.0).then_inc(L3f_scalar_done, 1)
                act.wait_ge(L3f_matmul_done, 38*b + 35)
                act.activation(tt_0[:, :], psf0[:, 0:1024], ACT.Silu).then_inc(L3f_scalar_done, 1)
                act.wait_ge(L3f_matmul_done, 38*b + 36)
                act.activation(tt_1[:, :], psf1[:, 0:1024], ACT.Silu).then_inc(L3f_scalar_done, 1)
                act.wait_ge(L3f_vector_done, 61*b + 117)
                act.activation(jk0[:, :], u0[:, :], ACT.Square, scale=1.0 / 16.0, accum_out=st0[:, 10:11]).then_inc(L3f_scalar_done, 1)
                act.wait_ge(L3f_vector_done, 61*b + 118)
                act.activation(jk1[:, :], u1[:, :], ACT.Square, scale=1.0 / 16.0, accum_out=st1[:, 10:11]).then_inc(L3f_scalar_done, 1)
                act.wait_ge(L3f_scalar_done, 44*b + 75)
                act.activation(st0[:, 11:12], st0[:, 10:11], ACT.Ln, bias=eps6[:, 0:1]).then_inc(L3f_scalar_done, 1)
                act.wait_ge(L3f_scalar_done, 44*b + 76)
                act.activation(st1[:, 11:12], st1[:, 10:11], ACT.Ln, bias=eps6[:, 0:1]).then_inc(L3f_scalar_done, 1)
                act.wait_ge(L3f_scalar_done, 44*b + 77)
                act.activation(st0[:, 12:13], st0[:, 11:12], ACT.Exp, scale=-0.5).then_inc(L3f_scalar_done, 1)
                act.wait_ge(L3f_scalar_done, 44*b + 78)
                act.activation(st1[:, 12:13], st1[:, 11:12], ACT.Exp, scale=-0.5).then_inc(L3f_scalar_done, 1)
                act.wait_ge(L3f_matmul_done, 38*b + 39)
                act.activation(unT0[:, 0:2, :], ps0[:, 0, 0:256], ACT.Copy).then_inc(L3f_scalar_done, 1)
                act.wait_ge(L3f_matmul_done, 38*b + 40)
                act.activation(unT1[:, 0:2, :], ps1[:, 0, 0:256], ACT.Copy).then_inc(L3f_scalar_done, 1)

        @block.vector
        def _(dve):

            dve.sem_inc(L0a_vector_done, 10)
            dve.wait_ge(L0a_scalar_done, 7)
            dve.tensor_scalar(A[:, :, :], A[:, :, :], -1.0, None, ALU.mult)
            dve.wait_ge(setup_pool_done, 7)
            dve.tensor_copy(selC[:, :, :].rearrange('p n (g r) -> p n g r', g=4), idb4[:, :, :].rearrange('p g n -> p n g').unsqueeze(3).to_broadcast([128, 32, 4, 32]))
            dve.wait_ge(x_loaded, 16)
            dve.bn_stats(st0[:, 0:6], x[:, 0, :]).then_inc(L0a_vector_done, 1)
            dve.bn_stats(st1[:, 0:6], x[:, 1, :]).then_inc(L0a_vector_done, 1)
            dve.wait_ge(L0a_vector_done, 11)
            dve.bn_aggr(st0[:, 6:8], st0[:, 0:6]).then_inc(L0a_vector_done, 1)
            dve.wait_ge(L0a_vector_done, 12)
            dve.bn_aggr(st1[:, 6:8], st1[:, 0:6]).then_inc(L0a_vector_done, 1)
            dve.wait_ge(L0a_scalar_done, 10)
            dve.tensor_scalar(u0[:, :], x[:, 0, :], st0[:, 6:7], st0[:, 9:10], ALU.subtract, ALU.mult).then_inc(L0a_vector_done, 1)
            dve.wait_ge(L0a_scalar_done, 11)
            dve.tensor_scalar(u1[:, :], x[:, 1, :], st1[:, 6:7], st1[:, 9:10], ALU.subtract, ALU.mult).then_inc(L0a_vector_done, 1)
            dve.wait_ge(L0a_w_loaded, 192)
            dve.wait_ge(L0a_scalar_done, 16)
            dve.scalar_tensor_tensor(un0[:, :], u0[:, :], st0[:, 12:13], n1[:, :], ALU.mult, ALU.mult).then_inc(L0a_vector_done, 1)
            dve.wait_ge(L0a_scalar_done, 17)
            dve.scalar_tensor_tensor(un1[:, :], u1[:, :], st1[:, 12:13], n1[:, :], ALU.mult, ALU.mult).then_inc(L0a_vector_done, 1)
            dve.wait_ge(ctx_loaded, 32)
            dve.wait_ge(L0a_matmul_done, 2)
            with dve.Fori(0, 4) as b:
                dve.wait_ge(L0a_vector_done, 20*b + 1)
                dve.sem_inc(dve_waited, 1)
                dve.bn_stats(st0[:, 0:6], x_next[:, 2*b+0, :]).then_inc(L0a_vector_done, 1)
                dve.wait_ge(L0a_vector_done, 20*b + 2)
                dve.sem_inc(dve_waited, 1)
                dve.bn_stats(st1[:, 0:6], x_next[:, 2*b+1, :]).then_inc(L0a_vector_done, 1)
                dve.wait_ge(L0a_vector_done, 20*b + 19)
                dve.wait_ge(L0a_scalar_done, 18*b + 1)
                dve.sem_inc(dve_waited, 1)
                dve.bn_aggr(st0[:, 6:8], st0[:, 0:6]).then_inc(L0a_vector_done, 1)
                dve.wait_ge(L0a_vector_done, 20*b + 20)
                dve.wait_ge(L0a_scalar_done, 18*b + 2)
                dve.sem_inc(dve_waited, 1)
                dve.bn_aggr(st1[:, 6:8], st1[:, 0:6]).then_inc(L0a_vector_done, 1)
                dve.wait_ge(L0a_pool_done, 2*b + 3)
                dve.wait_ge(L0a_scalar_done, 18*b + 21)
                dve.tensor_scalar(u0[:, :], x_next[:, 2*b+0, :], st0[:, 6:7], st0[:, 9:10], ALU.subtract, ALU.mult).then_inc(L0a_vector_done, 1)
                dve.wait_ge(L0a_scalar_done, 18*b + 23)
                dve.sem_inc(dve_waited, 1)
                dve.tensor_copy(s3[:, 0, :, 2*b+0, :], f0[:, 0:3, :]).then_inc(L0a_vector_done, 1)
                dve.wait_ge(L0a_vector_done, 20*b + 24)
                dve.tensor_tensor(r0[:, :, :], f0[:, 0:3, :], s3[:, 0, :, 2*b+0, :], ALU.subtract).then_inc(L0a_vector_done, 1)
                dve.wait_ge(L0a_vector_done, 20*b + 25)
                dve.sem_inc(dve_waited, 1)
                dve.tensor_copy(s3[:, 1, :, 2*b+0, :], r0[:, :, :])
                dve.wait_ge(L0a_matmul_done, 6*b + 5)
                for j in range(2):
                    dve.tensor_scalar(sp0[:, j, :], ps0[:, 3, 128 * j:128 * j + 128], b_dt[:, j:j + 1], None, ALU.add)
                dve.wait_ge(L0a_scalar_done, 18*b + 24)
                dve.sem_inc(dve_waited, 1)
                dve.tensor_copy(s3[:, 0, :, 2*b+1, :], f1[:, 0:3, :]).then_inc(L0a_vector_done, 1)
                dve.wait_ge(L0a_matmul_done, 6*b + 6)
                for j in range(2):
                    dve.tensor_scalar(sp1[:, j, :], ps1[:, 3, 128 * j:128 * j + 128], b_dt[:, j:j + 1], None, ALU.add)
                dve.wait_ge(L0a_vector_done, 20*b + 26)
                dve.tensor_tensor(r1[:, :, :], f1[:, 0:3, :], s3[:, 0, :, 2*b+1, :], ALU.subtract).then_inc(L0a_vector_done, 1)
                dve.scalar_tensor_tensor(sa0[:, :, :], sp0[:, :, :], -1.0, sp0[:, :, :], ALU.mult, ALU.max).then_inc(L0a_vector_done, 1)
                dve.wait_ge(L0a_vector_done, 20*b + 27)
                dve.sem_inc(dve_waited, 1)
                dve.tensor_copy(s3[:, 1, :, 2*b+1, :], r1[:, :, :])
                dve.scalar_tensor_tensor(sa1[:, :, :], sp1[:, :, :], -1.0, sp1[:, :, :], ALU.mult, ALU.max).then_inc(L0a_vector_done, 1)
                dve.wait_ge(L0a_pool_done, 2*b + 4)
                dve.tensor_scalar(u1[:, :], x_next[:, 2*b+1, :], st1[:, 6:7], st1[:, 9:10], ALU.subtract, ALU.mult).then_inc(L0a_vector_done, 1)
                dve.wait_ge(L0a_vector_done, 20*b + 28)
                dve.tensor_scalar(sp0[:, :, :], sp0[:, :, :], 0.0, None, ALU.max).then_inc(L0a_vector_done, 1)
                dve.wait_ge(L0a_vector_done, 20*b + 29)
                dve.tensor_scalar(sp1[:, :, :], sp1[:, :, :], 0.0, None, ALU.max).then_inc(L0a_vector_done, 1)
                dve.tensor_tensor(r0[:, :, :], r0[:, :, :], s3[:, 1, :, 2*b+0, :], ALU.subtract).then_inc(L0a_vector_done, 1)
                dve.tensor_tensor(r1[:, :, :], r1[:, :, :], s3[:, 1, :, 2*b+1, :], ALU.subtract).then_inc(L0a_vector_done, 1)
                dve.wait_ge(L0a_scalar_done, 18*b + 28)
                dve.wait_ge(L0a_vector_done, 20*b + 31)
                dve.tensor_tensor(dt[:, :, 2*b+0, :], sp0[:, :, :], sa0[:, :, :], ALU.add)
                dve.wait_ge(L0a_vector_done, 20*b + 32)
                dve.wait_ge(L0a_scalar_done, 18*b + 32)
                dve.tensor_tensor(dt[:, :, 2*b+1, :], sp1[:, :, :], sa1[:, :, :], ALU.add).then_inc(L0a_vector_done, 1)
                dve.wait_ge(L0a_vector_done, 20*b + 33)
                dve.sem_inc(dve_waited, 1)
                dve.tensor_copy(s3[:, 2, :, 2*b+0, :], r0[:, :, :])
                dve.wait_ge(L0a_vector_done, 20*b + 34)
                dve.sem_inc(dve_waited, 1)
                dve.tensor_copy(s3[:, 2, :, 2*b+1, :], r1[:, :, :]).then_inc(L0a_vector_done, 1)
                dve.scalar_tensor_tensor(un0[:, :], u0[:, :], st0[:, 12:13], n1[:, :], ALU.mult, ALU.mult).then_inc(L0a_vector_done, 1)
                dve.wait_ge(L0a_scalar_done, 18*b + 34)
                dve.scalar_tensor_tensor(un1[:, :], u1[:, :], st1[:, 12:13], n1[:, :], ALU.mult, ALU.mult).then_inc(L0a_vector_done, 1)
            dve.wait_ge(L0a_scalar_done, 79)
            dve.wait_ge(L0a_vector_done, 95)
            dve.tensor_tensor(dtx[:, :, :, :], dt[:, :, :, :], zx[:, 2:4, :, :], ALU.mult).then_inc(L0a_vector_done, 1)
            dve.wait_ge(L0a_matmul_done, 26)
            dve.wait_ge(L0a_scalar_done, 90)
            dve.wait_ge(L0a_vector_done, 99)
            with dve.Fori(0, 32) as n:
                dve.wait_ge(L0a_scalar_done, 2*n + 91)
                dve.memset(dA0[:, :, 0:1], 0.0)
                dve.wait_ge(L0a_matmul_done, 4*n + 27)
                dve.tensor_tensor(us0[:, :, :], ps0[:, 0:2, :].rearrange('p h (b t) -> p (h b) t', t=128), dtx[:, 0, :, :], ALU.mult).then_inc(L0a_vector_done, 1)
                dve.wait_ge(L0a_scalar_done, 2*n + 92)
                dve.memset(dA1[:, :, 0:1], 0.0)
                dve.wait_ge(L0a_vector_done, 6*n + 100)
                dve.tensor_tensor_scan(hsf0[:, :], dAf0[:, :], usf0[:, :], 0.0, ALU.mult, ALU.add).then_inc(L0a_vector_done, 1)
                dve.wait_ge(L0a_matmul_done, 4*n + 28)
                dve.tensor_tensor(us1[:, :, :], ps1[:, 0:2, :].rearrange('p h (b t) -> p (h b) t', t=128), dtx[:, 1, :, :], ALU.mult).then_inc(L0a_vector_done, 1)
                dve.wait_ge(L0a_matmul_done, 4*n + 29)
                dve.wait_ge(L0a_vector_done, 6*n + 101)
                dve.wait_ge(L0a_pool_done, 2*n + 9)
                dve.tensor_tensor(hc0[:, :, :], ps0[:, 2:4, :].rearrange('p h (b t) -> p (h b) t', t=128), hs0[:, :, :], ALU.mult).then_inc(L0a_vector_done, 1)
                dve.wait_ge(L0a_vector_done, 6*n + 102)
                dve.tensor_tensor_scan(hsf1[:, :], dAf1[:, :], usf1[:, :], 0.0, ALU.mult, ALU.add).then_inc(L0a_vector_done, 1)
                dve.wait_ge(L0a_matmul_done, 4*n + 30)
                dve.wait_ge(L0a_vector_done, 6*n + 104)
                dve.wait_ge(L0a_pool_done, 2*n + 10)
                dve.tensor_tensor(hc1[:, :, :], ps1[:, 2:4, :].rearrange('p h (b t) -> p (h b) t', t=128), hs1[:, :, :], ALU.mult).then_inc(L0a_vector_done, 1)
            dve.wait_ge(L0a_w_loaded, 192)
            dve.wait_ge(L0a_scalar_done, 154)
            dve.wait_ge(L0a_matmul_done, 154)
            dve.wait_ge(L0a_vector_done, 291)
            dve.wait_ge(L0a_pool_done, 74)
            with dve.Fori(0, 4) as b:
                dve.wait_ge(L0a_vector_done, 12*b + 282)
                dve.wait_ge(L0a_matmul_done, 9*b + 146)
                for j in range(2):
                    last = dve.scalar_tensor_tensor(sp0[:, j, :], zx[:, 2 + j, 2*b+0, :], Dp[:, j:j + 1], y[:, j, 2*b+0, :], ALU.mult, ALU.add)
                last.then_inc(L0a_vector_done, 1)
                dve.wait_ge(L0a_vector_done, 12*b + 283)
                dve.wait_ge(L0a_matmul_done, 9*b + 147)
                for j in range(2):
                    last = dve.scalar_tensor_tensor(sp1[:, j, :], zx[:, 2 + j, 2*b+1, :], Dp[:, j:j + 1], y[:, j, 2*b+1, :], ALU.mult, ALU.add)
                last.then_inc(L0a_vector_done, 1)
                dve.wait_ge(L0a_scalar_done, 12*b + 155)
                dve.wait_ge(L0a_vector_done, 12*b + 292)
                dve.tensor_tensor(sp0[:, :, :], sp0[:, :, :], sa0[:, :, :], ALU.mult).then_inc(L0a_vector_done, 1)
                dve.wait_ge(L0a_vector_done, 12*b + 293)
                dve.wait_ge(L0a_scalar_done, 12*b + 156)
                dve.tensor_tensor(sp1[:, :, :], sp1[:, :, :], sa1[:, :, :], ALU.mult).then_inc(L0a_vector_done, 1)
                dve.wait_ge(L0a_matmul_done, 9*b + 155)
                dve.wait_ge(L0a_pool_done, 2*b + 73)
                dve.tensor_tensor(h0[:, :], ps0[:, 0, 0:256], uall[:, 2*b+0, :], ALU.add).then_inc(L0a_vector_done, 1)
                dve.wait_ge(L0a_matmul_done, 9*b + 156)
                dve.wait_ge(L0a_pool_done, 2*b + 74)
                dve.tensor_tensor(h1[:, :], ps1[:, 0, 0:256], uall[:, 2*b+1, :], ALU.add).then_inc(L0a_vector_done, 1)
                dve.wait_ge(L0a_scalar_done, 12*b + 161)
                dve.scalar_tensor_tensor(un0[:, :], h0[:, :], st0[:, 12:13], n2[:, :], ALU.mult, ALU.mult).then_inc(L0a_vector_done, 1)
                dve.wait_ge(L0a_scalar_done, 12*b + 162)
                dve.scalar_tensor_tensor(un1[:, :], h1[:, :], st1[:, 12:13], n2[:, :], ALU.mult, ALU.mult).then_inc(L0a_vector_done, 1)
                dve.wait_ge(L0a_scalar_done, 12*b + 165)
                dve.tensor_tensor(m0[:, :], tm0[:, :], psf0[:, 1280:2048], ALU.mult).then_inc(L0a_vector_done, 1)
                dve.wait_ge(L0a_scalar_done, 12*b + 166)
                dve.tensor_tensor(m1[:, :], tm1[:, :], psf1[:, 1280:2048], ALU.mult).then_inc(L0a_vector_done, 1)
                dve.wait_ge(L0a_matmul_done, 9*b + 162)
                dve.tensor_tensor(h0[:, :], h0[:, :], ps0[:, 0, 0:256], ALU.add).then_inc(L0a_vector_done, 1)
                dve.wait_ge(L0a_matmul_done, 9*b + 163)
                dve.tensor_tensor(h1[:, :], h1[:, :], ps1[:, 0, 0:256], ALU.add).then_inc(L0a_vector_done, 1)

            dve.sem_inc(L0x_vector_done, 31)
            dve.wait_ge(L0a_pool_done, 82)
            dve.bn_stats(st0[:, 0:6], x[:, 0, :]).then_inc(L0x_vector_done, 1)
            dve.bn_stats(st1[:, 0:6], x[:, 1, :]).then_inc(L0x_vector_done, 1)
            dve.wait_ge(L0x_vector_done, 32)
            dve.bn_aggr(st0[:, 6:8], st0[:, 0:6]).then_inc(L0x_vector_done, 1)
            dve.wait_ge(L0x_vector_done, 33)
            dve.bn_aggr(st1[:, 6:8], st1[:, 0:6]).then_inc(L0x_vector_done, 1)
            dve.wait_ge(L0x_scalar_done, 11)
            dve.tensor_scalar(u0[:, :], x[:, 0, :], st0[:, 6:7], st0[:, 9:10], ALU.subtract, ALU.mult)
            dve.wait_ge(L0x_scalar_done, 12)
            dve.tensor_scalar(u1[:, :], x[:, 1, :], st1[:, 6:7], st1[:, 9:10], ALU.subtract, ALU.mult).then_inc(L0x_vector_done, 1)
            dve.wait_ge(L0x_w_loaded, 160)
            dve.wait_ge(L0a_matmul_done, 190)
            dve.wait_ge(L0x_vector_done, 36)
            with dve.Fori(0, 4) as b:
                dve.wait_ge(L0x_matmul_done, 14*b + 1)
                dve.tensor_scalar(phT0[0:64, :], ps0[0:64, 1, 0:256], b_ph[0:64, 0:1], None, ALU.add)
                dve.wait_ge(L0x_matmul_done, 14*b + 2)
                dve.tensor_scalar(phT1[0:64, :], ps1[0:64, 1, 0:256], b_ph[0:64, 0:1], None, ALU.add)
                dve.wait_ge(L0x_matmul_done, 14*b + 3)
                dve.tensor_scalar(thT0[0:64, :], ps0[0:64, 0, 0:256], b_th[0:64, 0:1], None, ALU.add).then_inc(L0x_vector_done, 1)
                dve.wait_ge(L0x_matmul_done, 14*b + 4)
                dve.tensor_scalar(thT1[0:64, :], ps1[0:64, 0, 0:256], b_th[0:64, 0:1], None, ALU.add).then_inc(L0x_vector_done, 1)
                dve.tensor_tensor(g_0[:, :, :], ps0[:, 0, 256:384].rearrange('p (k l) -> p k l', k=2), b_g[:, None, :].to_broadcast([128, 2, 64]), ALU.add).then_inc(L0x_vector_done, 1)
                dve.tensor_tensor(g_1[:, :, :], ps1[:, 0, 256:384].rearrange('p (k l) -> p k l', k=2), b_g[:, None, :].to_broadcast([128, 2, 64]), ALU.add).then_inc(L0x_vector_done, 1)
                dve.wait_ge(L0x_matmul_done, 14*b + 5)
                dve.wait_ge(L0x_pool_done, 4*b + 1)
                dve.tensor_reduce(st0[:, 16:18], ps0[:, 2, :].rearrange("p (t s) -> p t s", t=2), AX.X, ALU.max).then_inc(L0x_vector_done, 1)
                dve.wait_ge(L0x_vector_done, 38*b + 41)
                dve.tensor_scalar(st0[:, 16:18], st0[:, 16:18], -1.0, None, ALU.mult).then_inc(L0x_vector_done, 1)
                dve.wait_ge(L0x_matmul_done, 14*b + 6)
                dve.wait_ge(L0x_pool_done, 4*b + 2)
                dve.tensor_reduce(st1[:, 16:18], ps1[:, 2, :].rearrange("p (t s) -> p t s", t=2), AX.X, ALU.max).then_inc(L0x_vector_done, 1)
                dve.wait_ge(L0x_vector_done, 38*b + 43)
                dve.tensor_scalar(st1[:, 16:18], st1[:, 16:18], -1.0, None, ALU.mult).then_inc(L0x_vector_done, 1)
                dve.wait_ge(L0x_scalar_done, 12*b + 13)
                dve.reciprocal(st0[:, 16:18], st0[:, 18:20]).then_inc(L0x_vector_done, 1)
                dve.wait_ge(L0x_scalar_done, 12*b + 14)
                dve.reciprocal(st1[:, 16:18], st1[:, 18:20]).then_inc(L0x_vector_done, 1)
                dve.wait_ge(L0x_matmul_done, 14*b + 9)
                dve.bn_stats(st0[0:64, 0:6], ps0[0:64, 1, 0:256]).then_inc(L0x_vector_done, 1)
                dve.wait_ge(L0x_vector_done, 38*b + 47)
                dve.sem_inc(dve_waited, 1)
                dve.bn_aggr(st0[0:64, 6:8], st0[0:64, 0:6]).then_inc(L0x_vector_done, 1)
                dve.wait_ge(L0x_vector_done, 38*b + 48)
                dve.tensor_tensor(st0[0:64, 8:9], st0[0:64, 6:7], st0[0:64, 6:7], ALU.mult).then_inc(L0x_vector_done, 1)
                dve.bn_stats(st0[:, 0:6], x_next[:, 2*b+0, :])
                dve.wait_ge(L0x_vector_done, 38*b + 49)
                dve.tensor_tensor(st0[0:64, 7:8], st0[0:64, 7:8], st0[0:64, 8:9], ALU.add).then_inc(L0x_vector_done, 1)
                dve.wait_ge(L0x_matmul_done, 14*b + 10)
                dve.bn_stats(st1[0:64, 0:6], ps1[0:64, 1, 0:256]).then_inc(L0x_vector_done, 1)
                dve.wait_ge(L0x_matmul_done, 14*b + 11)
                dve.tensor_scalar(st0[0:64, 9:11], ps0[0:64, 1, 256:258], 1.0 / 64, None, ALU.mult).then_inc(L0x_vector_done, 1)
                dve.wait_ge(L0x_vector_done, 38*b + 51)
                dve.sem_inc(dve_waited, 1)
                dve.bn_aggr(st1[0:64, 6:8], st1[0:64, 0:6]).then_inc(L0x_vector_done, 1)
                dve.bn_aggr(st0[:, 6:8], st0[:, 0:6]).then_inc(L0x_vector_done, 1)
                dve.wait_ge(L0x_vector_done, 38*b + 52)
                dve.tensor_tensor(st0[0:64, 11:12], st0[0:64, 9:10], st0[0:64, 9:10], ALU.mult).then_inc(L0x_vector_done, 1)
                dve.wait_ge(L0x_vector_done, 38*b + 53)
                dve.tensor_tensor(st1[0:64, 8:9], st1[0:64, 6:7], st1[0:64, 6:7], ALU.mult).then_inc(L0x_vector_done, 1)
                dve.bn_stats(st1[:, 0:6], x_next[:, 2*b+1, :])
                dve.wait_ge(L0x_vector_done, 38*b + 55)
                dve.tensor_tensor(st0[0:64, 12:13], st0[0:64, 10:11], st0[0:64, 11:12], ALU.subtract).then_inc(L0x_vector_done, 1)
                dve.wait_ge(L0x_vector_done, 38*b + 56)
                dve.tensor_tensor(st1[0:64, 7:8], st1[0:64, 7:8], st1[0:64, 8:9], ALU.add).then_inc(L0x_vector_done, 1)
                dve.wait_ge(L0x_matmul_done, 14*b + 12)
                dve.tensor_scalar(st1[0:64, 9:11], ps1[0:64, 1, 256:258], 1.0 / 64, None, ALU.mult).then_inc(L0x_vector_done, 1)
                dve.bn_aggr(st1[:, 6:8], st1[:, 0:6]).then_inc(L0x_vector_done, 1)
                dve.wait_ge(L0x_vector_done, 38*b + 59)
                dve.tensor_tensor(st1[0:64, 11:12], st1[0:64, 9:10], st1[0:64, 9:10], ALU.mult).then_inc(L0x_vector_done, 1)
                dve.wait_ge(L0x_vector_done, 38*b + 61)
                dve.tensor_tensor(st1[0:64, 12:13], st1[0:64, 10:11], st1[0:64, 11:12], ALU.subtract).then_inc(L0x_vector_done, 1)
                dve.wait_ge(L0x_scalar_done, 12*b + 19)
                dve.tensor_scalar(t_0[0:64, :], ps0[0:64, 1, 0:256], st0[0:64, 9:10], st0[0:64, 14:15], ALU.subtract, ALU.mult).then_inc(L0x_vector_done, 1)
                dve.wait_ge(L0x_vector_done, 38*b + 63)
                dve.tensor_tensor(t_0[0:64, :], t_0[0:64, :], gam0[0:64, :], ALU.mult).then_inc(L0x_vector_done, 1)
                dve.wait_ge(L0x_scalar_done, 12*b + 22)
                dve.tensor_scalar(t_1[0:64, :], ps1[0:64, 1, 0:256], st1[0:64, 9:10], st1[0:64, 14:15], ALU.subtract, ALU.mult).then_inc(L0x_vector_done, 1)
                dve.wait_ge(L0x_vector_done, 38*b + 64)
                dve.tensor_tensor(t_0[0:64, :], t_0[0:64, :], bet0[0:64, :], ALU.add).then_inc(L0x_vector_done, 1)
                dve.wait_ge(L0x_vector_done, 38*b + 65)
                dve.tensor_tensor(t_1[0:64, :], t_1[0:64, :], gam0[0:64, :], ALU.mult).then_inc(L0x_vector_done, 1)
                dve.wait_ge(L0x_vector_done, 38*b + 66)
                dve.tensor_scalar(t_0[0:64, :], t_0[0:64, :], 0.0, None, ALU.max).then_inc(L0x_vector_done, 1)
                dve.wait_ge(L0x_vector_done, 38*b + 67)
                dve.tensor_tensor(t_1[0:64, :], t_1[0:64, :], bet0[0:64, :], ALU.add).then_inc(L0x_vector_done, 1)
                dve.wait_ge(L0x_vector_done, 38*b + 69)
                dve.tensor_scalar(t_1[0:64, :], t_1[0:64, :], 0.0, None, ALU.max).then_inc(L0x_vector_done, 1)
                dve.wait_ge(L0x_matmul_done, 14*b + 13)
                dve.scalar_tensor_tensor(u0[:, :], ps0[:, 3, 0:256], b_xo[:, 0:1], ctx[:, 2*b+0, :], ALU.add, ALU.add).then_inc(L0x_vector_done, 1)
                dve.wait_ge(L0x_matmul_done, 14*b + 14)
                dve.scalar_tensor_tensor(u1[:, :], ps1[:, 3, 0:256], b_xo[:, 0:1], ctx[:, 2*b+1, :], ALU.add, ALU.add).then_inc(L0x_vector_done, 1)
                dve.wait_ge(L0x_scalar_done, 12*b + 23)
                dve.wait_ge(L0x_pool_done, 4*b + 7)
                dve.tensor_scalar(u0[:, :], x_next[:, 2*b+0, :], st0[:, 6:7], st0[:, 9:10], ALU.subtract, ALU.mult).then_inc(L0x_vector_done, 1)
                dve.wait_ge(L0x_scalar_done, 12*b + 24)
                dve.wait_ge(L0x_pool_done, 4*b + 8)
                dve.tensor_scalar(u1[:, :], x_next[:, 2*b+1, :], st1[:, 6:7], st1[:, 9:10], ALU.subtract, ALU.mult).then_inc(L0x_vector_done, 1)

            dve.sem_inc(L0f_vector_done, 10)
            dve.wait_ge(L0x_vector_done, 168)
            dve.wait_ge(L0x_pool_done, 20)
            dve.bn_stats(st0[:, 0:6], x[:, 0, :]).then_inc(L0f_vector_done, 1)
            dve.wait_ge(L0x_vector_done, 174)
            dve.bn_stats(st1[:, 0:6], x[:, 1, :]).then_inc(L0f_vector_done, 1)
            dve.wait_ge(L0x_scalar_done, 53)
            dve.wait_ge(L0f_vector_done, 11)
            dve.bn_aggr(st0[:, 6:8], st0[:, 0:6]).then_inc(L0f_vector_done, 1)
            dve.wait_ge(L0x_scalar_done, 56)
            dve.wait_ge(L0f_vector_done, 12)
            dve.bn_aggr(st1[:, 6:8], st1[:, 0:6]).then_inc(L0f_vector_done, 1)
            dve.wait_ge(L0f_scalar_done, 18)
            dve.tensor_scalar(u0[:, :], x[:, 0, :], st0[:, 6:7], st0[:, 9:10], ALU.subtract, ALU.mult).then_inc(L0f_vector_done, 1)
            dve.wait_ge(L0f_scalar_done, 19)
            dve.tensor_scalar(u1[:, :], x[:, 1, :], st1[:, 6:7], st1[:, 9:10], ALU.subtract, ALU.mult).then_inc(L0f_vector_done, 1)
            dve.wait_ge(L0f_w_loaded, 64)
            dve.wait_ge(L0f_scalar_done, 20)
            with dve.Fori(0, 4) as b:
                dve.wait_ge(L0f_vector_done, 18*b + 1)
                dve.sem_inc(dve_waited, 1)
                dve.bn_stats(st0[:, 0:6], x_next[:, 2*b+0, :]).then_inc(L0f_vector_done, 1)
                dve.wait_ge(L0f_vector_done, 18*b + 2)
                dve.sem_inc(dve_waited, 1)
                dve.bn_stats(st1[:, 0:6], x_next[:, 2*b+1, :]).then_inc(L0f_vector_done, 1)
                dve.wait_ge(L0f_vector_done, 18*b + 17)
                dve.wait_ge(L0f_scalar_done, 20*b + 1)
                dve.sem_inc(dve_waited, 1)
                dve.bn_aggr(st0[:, 6:8], st0[:, 0:6]).then_inc(L0f_vector_done, 1)
                dve.wait_ge(L0f_vector_done, 18*b + 18)
                dve.wait_ge(L0f_scalar_done, 20*b + 2)
                dve.sem_inc(dve_waited, 1)
                dve.bn_aggr(st1[:, 6:8], st1[:, 0:6]).then_inc(L0f_vector_done, 1)
                dve.wait_ge(L0f_scalar_done, 20*b + 23)
                dve.wait_ge(L0f_matmul_done, 12*b + 1)
                dve.tensor_scalar(u0[:, :], x_next[:, 2*b+0, :], st0[:, 6:7], st0[:, 9:10], ALU.subtract, ALU.mult)
                dve.wait_ge(L0f_scalar_done, 20*b + 24)
                dve.wait_ge(L0f_matmul_done, 12*b + 2)
                dve.tensor_scalar(u1[:, :], x_next[:, 2*b+1, :], st1[:, 6:7], st1[:, 9:10], ALU.subtract, ALU.mult)
                dve.wait_ge(L0f_matmul_done, 12*b + 3)
                dve.wait_ge(L0f_pool_done, 15*b + 1)
                dve.tensor_tensor(r0_0[:, :, :], ps0[:, 1, :].rearrange('p (e o) -> p e o', e=2), b_e0[:, 0:512].rearrange('p (e o) -> p e o', e=2), ALU.add).then_inc(L0f_vector_done, 1)
                dve.wait_ge(L0f_matmul_done, 12*b + 4)
                dve.wait_ge(L0f_pool_done, 15*b + 3)
                dve.tensor_tensor(r0_1[:, :, :], ps1[:, 1, :].rearrange('p (e o) -> p e o', e=2), b_e0[:, 0:512].rearrange('p (e o) -> p e o', e=2), ALU.add).then_inc(L0f_vector_done, 1)
                dve.wait_ge(L0f_matmul_done, 12*b + 5)
                dve.tensor_tensor(lg0_0[:, :], ps0[:, 0, 256:264], b_gt0[:, :], ALU.add).then_inc(L0f_vector_done, 1)
                dve.wait_ge(L0f_matmul_done, 12*b + 6)
                dve.tensor_tensor(lg0_1[:, :], ps1[:, 0, 256:264], b_gt0[:, :], ALU.add).then_inc(L0f_vector_done, 1)
                dve.wait_ge(L0f_vector_done, 18*b + 23)
                dve.sem_inc(dve_waited, 1)
                dve.max(st0[:, 16:24], lg0_0[:, :]).then_inc(L0f_vector_done, 1)
                dve.wait_ge(L0f_vector_done, 18*b + 24)
                dve.sem_inc(dve_waited, 1)
                dve.max(st1[:, 16:24], lg0_1[:, :]).then_inc(L0f_vector_done, 1)
                dve.wait_ge(L0f_vector_done, 18*b + 25)
                dve.tensor_scalar(mk0_0[:, :], lg0_0[:, :], st0[:, 17:18], 0.5, ALU.is_ge, ALU.mult).then_inc(L0f_vector_done, 1)
                dve.wait_ge(L0f_vector_done, 18*b + 26)
                dve.tensor_scalar(mk0_1[:, :], lg0_1[:, :], st1[:, 17:18], 0.5, ALU.is_ge, ALU.mult).then_inc(L0f_vector_done, 1)
                dve.wait_ge(L0f_matmul_done, 12*b + 7)
                dve.wait_ge(L0f_pool_done, 15*b + 5)
                dve.tensor_tensor(r0_0[:, :, :], ps0[:, 2, :].rearrange('p (e o) -> p e o', e=2), b_e0[:, 512:1024].rearrange('p (e o) -> p e o', e=2), ALU.add).then_inc(L0f_vector_done, 1)
                dve.wait_ge(L0f_matmul_done, 12*b + 8)
                dve.wait_ge(L0f_pool_done, 15*b + 6)
                dve.tensor_tensor(r0_1[:, :, :], ps1[:, 2, :].rearrange('p (e o) -> p e o', e=2), b_e0[:, 512:1024].rearrange('p (e o) -> p e o', e=2), ALU.add).then_inc(L0f_vector_done, 1)
                dve.wait_ge(L0f_matmul_done, 12*b + 9)
                dve.wait_ge(L0f_pool_done, 15*b + 8)
                dve.tensor_tensor(r0_0[:, :, :], ps0[:, 3, :].rearrange('p (e o) -> p e o', e=2), b_e0[:, 1024:1536].rearrange('p (e o) -> p e o', e=2), ALU.add).then_inc(L0f_vector_done, 1)
                dve.wait_ge(L0f_matmul_done, 12*b + 10)
                dve.wait_ge(L0f_pool_done, 15*b + 10)
                dve.tensor_tensor(r0_1[:, :, :], ps1[:, 3, :].rearrange('p (e o) -> p e o', e=2), b_e0[:, 1024:1536].rearrange('p (e o) -> p e o', e=2), ALU.add).then_inc(L0f_vector_done, 1)
                dve.wait_ge(L0f_matmul_done, 12*b + 11)
                dve.wait_ge(L0f_pool_done, 15*b + 12)
                dve.tensor_tensor(r0_0[:, :, :], ps0[:, 1, :].rearrange('p (e o) -> p e o', e=2), b_e0[:, 1536:2048].rearrange('p (e o) -> p e o', e=2), ALU.add).then_inc(L0f_vector_done, 1)
                dve.wait_ge(L0f_matmul_done, 12*b + 12)
                dve.wait_ge(L0f_pool_done, 15*b + 14)
                dve.tensor_tensor(r0_1[:, :, :], ps1[:, 1, :].rearrange('p (e o) -> p e o', e=2), b_e0[:, 1536:2048].rearrange('p (e o) -> p e o', e=2), ALU.add).then_inc(L0f_vector_done, 1)

            dve.sem_inc(L1a_vector_done, 2)
            dve.wait_ge(L0f_vector_done, 73)
            dve.wait_ge(L0f_pool_done, 64)
            dve.bn_stats(st0[:, 0:6], x[:, 0, :]).then_inc(L1a_vector_done, 1)
            dve.wait_ge(L0f_vector_done, 74)
            dve.bn_stats(st1[:, 0:6], x[:, 1, :]).then_inc(L1a_vector_done, 1)
            dve.wait_ge(L0f_scalar_done, 81)
            dve.wait_ge(L1a_vector_done, 3)
            dve.bn_aggr(st0[:, 6:8], st0[:, 0:6]).then_inc(L1a_vector_done, 1)
            dve.wait_ge(L0f_scalar_done, 82)
            dve.wait_ge(L1a_vector_done, 4)
            dve.bn_aggr(st1[:, 6:8], st1[:, 0:6]).then_inc(L1a_vector_done, 1)
            dve.wait_ge(L0f_matmul_done, 49)
            dve.wait_ge(L1a_scalar_done, 9)
            dve.tensor_scalar(u0[:, :], x[:, 0, :], st0[:, 6:7], st0[:, 9:10], ALU.subtract, ALU.mult).then_inc(L1a_vector_done, 1)
            dve.wait_ge(L0f_matmul_done, 50)
            dve.wait_ge(L1a_scalar_done, 10)
            dve.tensor_scalar(u1[:, :], x[:, 1, :], st1[:, 6:7], st1[:, 9:10], ALU.subtract, ALU.mult).then_inc(L1a_vector_done, 1)
            dve.wait_ge(L1a_matmul_done, 2)
            with dve.Fori(0, 4) as b:
                dve.wait_ge(L1a_vector_done, 10*b + 1)
                dve.sem_inc(dve_waited, 1)
                dve.bn_stats(st0[:, 0:6], x_next[:, 2*b+0, :]).then_inc(L1a_vector_done, 1)
                dve.wait_ge(L1a_vector_done, 10*b + 2)
                dve.sem_inc(dve_waited, 1)
                dve.bn_stats(st1[:, 0:6], x_next[:, 2*b+1, :]).then_inc(L1a_vector_done, 1)
                dve.wait_ge(L1a_vector_done, 10*b + 9)
                dve.wait_ge(L1a_scalar_done, 11*b + 1)
                dve.sem_inc(dve_waited, 1)
                dve.bn_aggr(st0[:, 6:8], st0[:, 0:6]).then_inc(L1a_vector_done, 1)
                dve.wait_ge(L1a_vector_done, 10*b + 10)
                dve.wait_ge(L1a_scalar_done, 11*b + 2)
                dve.sem_inc(dve_waited, 1)
                dve.bn_aggr(st1[:, 6:8], st1[:, 0:6]).then_inc(L1a_vector_done, 1)
                dve.wait_ge(L1a_scalar_done, 11*b + 14)
                dve.wait_ge(L1a_matmul_done, 12*b + 1)
                dve.tensor_scalar(u0[:, :], x_next[:, 2*b+0, :], st0[:, 6:7], st0[:, 9:10], ALU.subtract, ALU.mult)
                dve.wait_ge(L1a_scalar_done, 11*b + 15)
                dve.wait_ge(L1a_matmul_done, 12*b + 2)
                dve.tensor_scalar(u1[:, :], x_next[:, 2*b+1, :], st1[:, 6:7], st1[:, 9:10], ALU.subtract, ALU.mult)
                dve.wait_ge(L1a_scalar_done, 11*b + 16)
                dve.wait_ge(L1a_matmul_done, 12*b + 5)
                dve.tensor_tensor(kv1_0[:, :], k1_0[:, :], ps0[:, 2, 0:256], ALU.mult).then_inc(L1a_vector_done, 1)
                dve.wait_ge(L1a_scalar_done, 11*b + 17)
                dve.wait_ge(L1a_matmul_done, 12*b + 6)
                dve.tensor_tensor(kv1_1[:, :], k1_1[:, :], ps1[:, 2, 0:256], ALU.mult).then_inc(L1a_vector_done, 1)
                dve.wait_ge(L1a_matmul_done, 12*b + 7)
                dve.scalar_tensor_tensor(kv1_0[:, :], ps0[:, 3, 0:256], 16.0 / 128, q1_0[:, :], ALU.mult, ALU.mult).then_inc(L1a_vector_done, 1)
                dve.wait_ge(L1a_scalar_done, 11*b + 18)
                dve.wait_ge(L1a_matmul_done, 12*b + 8)
                dve.scalar_tensor_tensor(kv1_1[:, :], ps1[:, 3, 0:256], 16.0 / 128, q1_1[:, :], ALU.mult, ALU.mult).then_inc(L1a_vector_done, 1)
                dve.wait_ge(L1a_matmul_done, 12*b + 11)
                dve.tensor_tensor(x[:, 2*b+0, :], ps0[:, 2, 0:256], x[:, 2*b+0, :], ALU.add).then_inc(L1a_vector_done, 1)
                dve.wait_ge(L1a_matmul_done, 12*b + 12)
                dve.tensor_tensor(x[:, 2*b+1, :], ps1[:, 2, 0:256], x[:, 2*b+1, :], ALU.add).then_inc(L1a_vector_done, 1)

            dve.sem_inc(L1x_vector_done, 11)
            dve.wait_ge(L1x_scalar_done, 1)
            dve.tensor_scalar(dec[:, :], dec[:, :], 1.0, None, ALU.add).then_inc(L1x_vector_done, 1)
            dve.wait_ge(L1x_vector_done, 12)
            dve.reciprocal(dec[:, :], dec[:, :]).then_inc(L1x_vector_done, 1)
            dve.wait_ge(L1x_vector_done, 13)
            dve.tensor_scalar(Kt[:, :], ones[:, :], dec[:, 0:1], None, ALU.mult)
            dve.bn_stats(st0[:, 0:6], x[:, 0, :]).then_inc(L1x_vector_done, 1)
            dve.bn_stats(st1[:, 0:6], x[:, 1, :]).then_inc(L1x_vector_done, 1)
            dve.wait_ge(L1x_vector_done, 14)
            dve.bn_aggr(st0[:, 6:8], st0[:, 0:6]).then_inc(L1x_vector_done, 1)
            dve.wait_ge(L1x_vector_done, 15)
            dve.bn_aggr(st1[:, 6:8], st1[:, 0:6]).then_inc(L1x_vector_done, 1)
            dve.wait_ge(L1a_matmul_done, 49)
            dve.wait_ge(L1x_scalar_done, 4)
            dve.tensor_scalar(u0[:, :], x[:, 0, :], st0[:, 6:7], st0[:, 9:10], ALU.subtract, ALU.mult)
            dve.wait_ge(L1a_matmul_done, 50)
            dve.wait_ge(L1x_scalar_done, 5)
            dve.tensor_scalar(u1[:, :], x[:, 1, :], st1[:, 6:7], st1[:, 9:10], ALU.subtract, ALU.mult).then_inc(L1x_vector_done, 1)
            dve.wait_ge(L1x_vector_done, 18)
            with dve.Fori(0, 4) as b:
                dve.wait_ge(L1x_matmul_done, 4*b + 1)
                dve.wait_ge(L1x_vector_done, 18*b + 3)
                for j in range(2):
                    last = dve.tensor_scalar(xi_0[:, j, :], ps0[:, 0, 128 * j:128 * j + 128], b_i1[:, j:j + 1], None, ALU.add)
                last.then_inc(L1x_vector_done, 1)
                dve.wait_ge(L1x_matmul_done, 4*b + 2)
                dve.wait_ge(L1x_vector_done, 18*b + 4)
                for j in range(2):
                    last = dve.tensor_scalar(xi_1[:, j, :], ps1[:, 0, 128 * j:128 * j + 128], b_i1[:, j:j + 1], None, ALU.add)
                last.then_inc(L1x_vector_done, 1)
                dve.wait_ge(L1x_vector_done, 18*b + 19)
                for j in range(2):
                    last = dve.tensor_tensor_scan(ss_0[:, j, :], Kt[:, :], xi_0[:, j, :], 0.0, ALU.mult, ALU.add)
                last.then_inc(L1x_vector_done, 1)
                dve.wait_ge(L1x_vector_done, 18*b + 20)
                for j in range(2):
                    last = dve.tensor_tensor_scan(ss_1[:, j, :], Kt[:, :], xi_1[:, j, :], 0.0, ALU.mult, ALU.add)
                last.then_inc(L1x_vector_done, 1)
                dve.wait_ge(L1x_vector_done, 18*b + 21)
                dve.tensor_reduce(st0[:, 16:18], ss_0[:, :, :], AX.X, ALU.add).then_inc(L1x_vector_done, 1)
                dve.wait_ge(L1x_vector_done, 18*b + 22)
                dve.tensor_reduce(st1[:, 16:18], ss_1[:, :, :], AX.X, ALU.add).then_inc(L1x_vector_done, 1)
                dve.wait_ge(L1x_vector_done, 18*b + 23)
                for j in range(2):
                    last = dve.tensor_scalar(mn_0[:, j, :], ones[:, :], st0[:, 16 + j:17 + j], 1.0 / 128, ALU.mult, ALU.mult)
                last.then_inc(L1x_vector_done, 1)
                dve.wait_ge(L1x_vector_done, 18*b + 24)
                for j in range(2):
                    last = dve.tensor_scalar(mn_1[:, j, :], ones[:, :], st1[:, 16 + j:17 + j], 1.0 / 128, ALU.mult, ALU.mult)
                last.then_inc(L1x_vector_done, 1)
                dve.wait_ge(L1x_matmul_done, 4*b + 3)
                dve.tensor_tensor(u0[:, :], ps0[:, 1, 0:256], u0[:, :], ALU.add).then_inc(L1x_vector_done, 1)
                dve.wait_ge(L1x_matmul_done, 4*b + 4)
                dve.tensor_tensor(u1[:, :], ps1[:, 1, 0:256], u1[:, :], ALU.add).then_inc(L1x_vector_done, 1)
                dve.wait_ge(L1x_pool_done, 7*b + 1)
                dve.bn_stats(st0[:, 0:6], u0[:, :]).then_inc(L1x_vector_done, 1)
                dve.wait_ge(L1x_vector_done, 18*b + 29)
                dve.wait_ge(L1x_scalar_done, 8*b + 2)
                dve.sem_inc(dve_waited, 1)
                dve.bn_aggr(st0[:, 6:8], st0[:, 0:6]).then_inc(L1x_vector_done, 1)
                dve.wait_ge(L1x_vector_done, 18*b + 30)
                dve.sem_inc(dve_waited, 1)
                dve.bn_stats(st0[:, 0:6], x_next[:, 2*b+0, :])
                dve.wait_ge(L1x_pool_done, 7*b + 2)
                dve.bn_stats(st1[:, 0:6], u1[:, :]).then_inc(L1x_vector_done, 1)
                dve.wait_ge(L1x_vector_done, 18*b + 31)
                dve.wait_ge(L1x_scalar_done, 8*b + 4)
                dve.sem_inc(dve_waited, 1)
                dve.bn_aggr(st1[:, 6:8], st1[:, 0:6]).then_inc(L1x_vector_done, 1)
                dve.wait_ge(L1x_scalar_done, 8*b + 7)
                dve.tensor_scalar(un0[:, :], u0[:, :], st0[:, 6:7], st0[:, 9:10], ALU.subtract, ALU.mult).then_inc(L1x_vector_done, 1)
                dve.wait_ge(L1x_vector_done, 18*b + 32)
                dve.sem_inc(dve_waited, 1)
                dve.bn_stats(st1[:, 0:6], x_next[:, 2*b+1, :])
                dve.wait_ge(L1x_vector_done, 18*b + 33)
                dve.sem_inc(dve_waited, 1)
                dve.bn_aggr(st0[:, 6:8], st0[:, 0:6]).then_inc(L1x_vector_done, 1)
                dve.wait_ge(L1x_scalar_done, 8*b + 9)
                dve.tensor_scalar(un1[:, :], u1[:, :], st1[:, 6:7], st1[:, 9:10], ALU.subtract, ALU.mult).then_inc(L1x_vector_done, 1)
                dve.wait_ge(L1x_vector_done, 18*b + 35)
                dve.sem_inc(dve_waited, 1)
                dve.bn_aggr(st1[:, 6:8], st1[:, 0:6]).then_inc(L1x_vector_done, 1)
                dve.wait_ge(L1x_scalar_done, 8*b + 11)
                dve.tensor_scalar(u0[:, :], x_next[:, 2*b+0, :], st0[:, 6:7], st0[:, 9:10], ALU.subtract, ALU.mult)
                dve.wait_ge(L1x_scalar_done, 8*b + 13)
                dve.tensor_scalar(u1[:, :], x_next[:, 2*b+1, :], st1[:, 6:7], st1[:, 9:10], ALU.subtract, ALU.mult)

            dve.sem_inc(L1f_vector_done, 48)
            dve.wait_ge(L1x_vector_done, 75)
            dve.memset(lg1_0[:, 7:8], -1e30)
            dve.memset(bp1_0[:, 7:8], -1e30)
            dve.memset(wv1_0[:, 0:1], 1.0)
            dve.wait_ge(L1x_vector_done, 78)
            dve.memset(lg1_1[:, 7:8], -1e30)
            dve.memset(bp1_1[:, 7:8], -1e30)
            dve.memset(wv1_1[:, 0:1], 1.0)
            dve.wait_ge(L1x_vector_done, 88)
            dve.wait_ge(L1x_pool_done, 28)
            dve.bn_stats(st0[:, 0:6], x[:, 0, :]).then_inc(L1f_vector_done, 1)
            dve.wait_ge(L1x_vector_done, 90)
            dve.bn_stats(st1[:, 0:6], x[:, 1, :]).then_inc(L1f_vector_done, 1)
            dve.wait_ge(L1x_scalar_done, 34)
            dve.wait_ge(L1f_vector_done, 49)
            dve.bn_aggr(st0[:, 6:8], st0[:, 0:6]).then_inc(L1f_vector_done, 1)
            dve.wait_ge(L1x_scalar_done, 36)
            dve.wait_ge(L1f_vector_done, 50)
            dve.bn_aggr(st1[:, 6:8], st1[:, 0:6]).then_inc(L1f_vector_done, 1)
            dve.wait_ge(L1f_scalar_done, 20)
            dve.tensor_scalar(u0[:, :], x[:, 0, :], st0[:, 6:7], st0[:, 9:10], ALU.subtract, ALU.mult).then_inc(L1f_vector_done, 1)
            dve.wait_ge(L1f_scalar_done, 21)
            dve.tensor_scalar(u1[:, :], x[:, 1, :], st1[:, 6:7], st1[:, 9:10], ALU.subtract, ALU.mult).then_inc(L1f_vector_done, 1)
            dve.wait_ge(L1f_w_loaded, 80)
            dve.wait_ge(L1f_scalar_done, 22)
            with dve.Fori(0, 4) as b:
                dve.wait_ge(L1f_vector_done, 56*b + 1)
                dve.sem_inc(dve_waited, 1)
                dve.bn_stats(st0[:, 0:6], x_next[:, 2*b+0, :]).then_inc(L1f_vector_done, 1)
                dve.wait_ge(L1f_vector_done, 56*b + 2)
                dve.sem_inc(dve_waited, 1)
                dve.bn_stats(st1[:, 0:6], x_next[:, 2*b+1, :]).then_inc(L1f_vector_done, 1)
                dve.wait_ge(L1f_vector_done, 56*b + 55)
                dve.wait_ge(L1f_scalar_done, 22*b + 1)
                dve.sem_inc(dve_waited, 1)
                dve.bn_aggr(st0[:, 6:8], st0[:, 0:6]).then_inc(L1f_vector_done, 1)
                dve.wait_ge(L1f_vector_done, 56*b + 56)
                dve.wait_ge(L1f_scalar_done, 22*b + 2)
                dve.sem_inc(dve_waited, 1)
                dve.bn_aggr(st1[:, 6:8], st1[:, 0:6]).then_inc(L1f_vector_done, 1)
                dve.wait_ge(L1f_scalar_done, 22*b + 25)
                dve.wait_ge(L1f_matmul_done, 34*b + 1)
                dve.tensor_scalar(u0[:, :], x_next[:, 2*b+0, :], st0[:, 6:7], st0[:, 9:10], ALU.subtract, ALU.mult)
                dve.wait_ge(L1f_scalar_done, 22*b + 26)
                dve.wait_ge(L1f_matmul_done, 34*b + 2)
                dve.tensor_scalar(u1[:, :], x_next[:, 2*b+1, :], st1[:, 6:7], st1[:, 9:10], ALU.subtract, ALU.mult)
                dve.wait_ge(L1f_scalar_done, 22*b + 27)
                dve.tensor_tensor(m1_0[:, 0, :], t1_0[:, :], ps0[:, 1, 256:512], ALU.mult).then_inc(L1f_vector_done, 1)
                dve.wait_ge(L1f_scalar_done, 22*b + 28)
                dve.tensor_tensor(m1_1[:, 0, :], t1_1[:, :], ps1[:, 1, 256:512], ALU.mult).then_inc(L1f_vector_done, 1)
                dve.wait_ge(L1f_scalar_done, 22*b + 29)
                dve.tensor_tensor(m1_0[:, 1, :], t1_0[:, :], ps0[:, 2, 256:512], ALU.mult).then_inc(L1f_vector_done, 1)
                dve.wait_ge(L1f_matmul_done, 34*b + 23)
                dve.tensor_tensor(lg1_0[:, 0:7], ps0[:, 0, 256:263], b_gt1[:, :], ALU.add).then_inc(L1f_vector_done, 1)
                dve.wait_ge(L1f_vector_done, 56*b + 62)
                dve.tensor_reduce(st0[:, 16:17], lg1_0[:, 0:7], AX.X, ALU.max).then_inc(L1f_vector_done, 1)
                dve.wait_ge(L1f_matmul_done, 34*b + 24)
                dve.tensor_tensor(lg1_1[:, 0:7], ps1[:, 0, 256:263], b_gt1[:, :], ALU.add).then_inc(L1f_vector_done, 1)
                dve.wait_ge(L1f_vector_done, 56*b + 63)
                dve.tensor_scalar(lg1_0[:, 0:7], lg1_0[:, 0:7], st0[:, 16:17], None, ALU.subtract)
                dve.wait_ge(L1f_scalar_done, 22*b + 30)
                dve.tensor_tensor(m1_1[:, 1, :], t1_1[:, :], ps1[:, 2, 256:512], ALU.mult).then_inc(L1f_vector_done, 1)
                dve.wait_ge(L1f_vector_done, 56*b + 64)
                dve.tensor_reduce(st1[:, 16:17], lg1_1[:, 0:7], AX.X, ALU.max).then_inc(L1f_vector_done, 1)
                dve.wait_ge(L1f_vector_done, 56*b + 66)
                dve.tensor_scalar(lg1_1[:, 0:7], lg1_1[:, 0:7], st1[:, 16:17], None, ALU.subtract)
                dve.wait_ge(L1f_matmul_done, 34*b + 27)
                dve.wait_ge(L1f_pool_done, 2*b + 1)
                dve.tensor_copy(acc1_0[:, :], ps0[:, 3, 0:256]).then_inc(L1f_vector_done, 1)
                dve.wait_ge(L1f_scalar_done, 22*b + 31)
                dve.tensor_tensor(m1_0[:, 0, :], t1_0[:, :], ps0[:, 1, 256:512], ALU.mult).then_inc(L1f_vector_done, 1)
                dve.wait_ge(L1f_matmul_done, 34*b + 28)
                dve.wait_ge(L1f_pool_done, 2*b + 2)
                dve.tensor_copy(acc1_1[:, :], ps1[:, 3, 0:256]).then_inc(L1f_vector_done, 1)
                dve.wait_ge(L1f_scalar_done, 22*b + 32)
                dve.tensor_tensor(m1_1[:, 0, :], t1_1[:, :], ps1[:, 1, 256:512], ALU.mult).then_inc(L1f_vector_done, 1)
                dve.wait_ge(L1f_scalar_done, 22*b + 33)
                dve.wait_ge(L1f_matmul_done, 34*b + 31)
                dve.tensor_tensor(m1_0[:, 1, :], t1_0[:, :], ps0[:, 2, 256:512], ALU.mult).then_inc(L1f_vector_done, 1)
                dve.wait_ge(L1f_scalar_done, 22*b + 34)
                dve.wait_ge(L1f_matmul_done, 34*b + 32)
                dve.tensor_tensor(m1_1[:, 1, :], t1_1[:, :], ps1[:, 2, 256:512], ALU.mult).then_inc(L1f_vector_done, 1)
                dve.wait_ge(L1f_scalar_done, 22*b + 35)
                dve.reciprocal(st0[:, 18:19], st0[:, 17:18]).then_inc(L1f_vector_done, 1)
                dve.wait_ge(L1f_vector_done, 56*b + 73)
                dve.tensor_scalar(pr1_0[:, :], pr1_0[:, :], st0[:, 18:19], None, ALU.mult).then_inc(L1f_vector_done, 1)
                dve.wait_ge(L1f_scalar_done, 22*b + 36)
                dve.reciprocal(st1[:, 18:19], st1[:, 17:18]).then_inc(L1f_vector_done, 1)
                dve.wait_ge(L1f_vector_done, 56*b + 74)
                dve.tensor_tensor(bp1_0[:, 0:7], pr1_0[:, 0:7], bi1[:, :], ALU.add).then_inc(L1f_vector_done, 1)
                dve.wait_ge(L1f_vector_done, 56*b + 75)
                dve.tensor_scalar(pr1_1[:, :], pr1_1[:, :], st1[:, 18:19], None, ALU.mult).then_inc(L1f_vector_done, 1)
                dve.wait_ge(L1f_vector_done, 56*b + 76)
                dve.sem_inc(dve_waited, 1)
                dve.max(st0[:, 24:32], bp1_0[:, :]).then_inc(L1f_vector_done, 1)
                dve.wait_ge(L1f_vector_done, 56*b + 77)
                dve.tensor_tensor(bp1_1[:, 0:7], pr1_1[:, 0:7], bi1[:, :], ALU.add).then_inc(L1f_vector_done, 1)
                dve.wait_ge(L1f_vector_done, 56*b + 78)
                dve.scalar_tensor_tensor(wv1_0[:, 1:8], bp1_0[:, 0:7], st0[:, 26:27], pr1_0[:, 0:7], ALU.is_ge, ALU.mult).then_inc(L1f_vector_done, 1)
                dve.wait_ge(L1f_vector_done, 56*b + 79)
                dve.sem_inc(dve_waited, 1)
                dve.max(st1[:, 24:32], bp1_1[:, :]).then_inc(L1f_vector_done, 1)
                dve.wait_ge(L1f_vector_done, 56*b + 80)
                dve.tensor_reduce(st0[:, 19:20], wv1_0[:, 1:8], AX.X, ALU.add).then_inc(L1f_vector_done, 1)
                dve.wait_ge(L1f_vector_done, 56*b + 81)
                dve.scalar_tensor_tensor(wv1_1[:, 1:8], bp1_1[:, 0:7], st1[:, 26:27], pr1_1[:, 0:7], ALU.is_ge, ALU.mult).then_inc(L1f_vector_done, 1)
                dve.wait_ge(L1f_vector_done, 56*b + 82)
                dve.reciprocal(st0[:, 20:21], st0[:, 19:20]).then_inc(L1f_vector_done, 1)
                dve.wait_ge(L1f_vector_done, 56*b + 83)
                dve.tensor_reduce(st1[:, 19:20], wv1_1[:, 1:8], AX.X, ALU.add).then_inc(L1f_vector_done, 1)
                dve.wait_ge(L1f_vector_done, 56*b + 84)
                dve.tensor_scalar(wv1_0[:, 1:8], wv1_0[:, 1:8], st0[:, 20:21], None, ALU.mult).then_inc(L1f_vector_done, 1)
                dve.wait_ge(L1f_vector_done, 56*b + 85)
                dve.reciprocal(st1[:, 20:21], st1[:, 19:20]).then_inc(L1f_vector_done, 1)
                dve.wait_ge(L1f_vector_done, 56*b + 86)
                dve.scalar_tensor_tensor(acc1_0[:, :], ps0[:, 3, 256:512], wv1_0[:, 1:2], acc1_0[:, :], ALU.mult, ALU.add).then_inc(L1f_vector_done, 1)
                dve.wait_ge(L1f_vector_done, 56*b + 87)
                dve.tensor_scalar(wv1_1[:, 1:8], wv1_1[:, 1:8], st1[:, 20:21], None, ALU.mult).then_inc(L1f_vector_done, 1)
                dve.wait_ge(L1f_vector_done, 56*b + 89)
                dve.scalar_tensor_tensor(acc1_1[:, :], ps1[:, 3, 256:512], wv1_1[:, 1:2], acc1_1[:, :], ALU.mult, ALU.add).then_inc(L1f_vector_done, 1)
                dve.wait_ge(L1f_matmul_done, 34*b + 37)
                dve.scalar_tensor_tensor(acc1_0[:, :], ps0[:, 3, 0:256], wv1_0[:, 2:3], acc1_0[:, :], ALU.mult, ALU.add).then_inc(L1f_vector_done, 1)
                dve.tensor_tensor(m1_0[:, 0, :], t1_0[:, :], ps0[:, 1, 256:512], ALU.mult).then_inc(L1f_vector_done, 1)
                dve.wait_ge(L1f_matmul_done, 34*b + 38)
                dve.scalar_tensor_tensor(acc1_1[:, :], ps1[:, 3, 0:256], wv1_1[:, 2:3], acc1_1[:, :], ALU.mult, ALU.add).then_inc(L1f_vector_done, 1)
                dve.tensor_tensor(m1_1[:, 0, :], t1_1[:, :], ps1[:, 1, 256:512], ALU.mult).then_inc(L1f_vector_done, 1)
                dve.wait_ge(L1f_matmul_done, 34*b + 39)
                dve.scalar_tensor_tensor(acc1_0[:, :], ps0[:, 3, 256:512], wv1_0[:, 3:4], acc1_0[:, :], ALU.mult, ALU.add).then_inc(L1f_vector_done, 1)
                dve.wait_ge(L1f_matmul_done, 34*b + 40)
                dve.scalar_tensor_tensor(acc1_1[:, :], ps1[:, 3, 256:512], wv1_1[:, 3:4], acc1_1[:, :], ALU.mult, ALU.add).then_inc(L1f_vector_done, 1)
                dve.wait_ge(L1f_scalar_done, 22*b + 37)
                dve.tensor_tensor(m1_0[:, 1, :], t1_0[:, :], ps0[:, 2, 256:512], ALU.mult).then_inc(L1f_vector_done, 1)
                dve.wait_ge(L1f_scalar_done, 22*b + 38)
                dve.tensor_tensor(m1_1[:, 1, :], t1_1[:, :], ps1[:, 2, 256:512], ALU.mult).then_inc(L1f_vector_done, 1)
                dve.wait_ge(L1f_matmul_done, 34*b + 43)
                dve.scalar_tensor_tensor(acc1_0[:, :], ps0[:, 3, 0:256], wv1_0[:, 4:5], acc1_0[:, :], ALU.mult, ALU.add).then_inc(L1f_vector_done, 1)
                dve.wait_ge(L1f_scalar_done, 22*b + 39)
                dve.tensor_tensor(m1_0[:, 0, :], t1_0[:, :], ps0[:, 1, 256:512], ALU.mult).then_inc(L1f_vector_done, 1)
                dve.wait_ge(L1f_matmul_done, 34*b + 44)
                dve.scalar_tensor_tensor(acc1_1[:, :], ps1[:, 3, 0:256], wv1_1[:, 4:5], acc1_1[:, :], ALU.mult, ALU.add).then_inc(L1f_vector_done, 1)
                dve.wait_ge(L1f_scalar_done, 22*b + 40)
                dve.tensor_tensor(m1_1[:, 0, :], t1_1[:, :], ps1[:, 1, 256:512], ALU.mult).then_inc(L1f_vector_done, 1)
                dve.wait_ge(L1f_matmul_done, 34*b + 47)
                dve.scalar_tensor_tensor(acc1_0[:, :], ps0[:, 3, 256:512], wv1_0[:, 5:6], acc1_0[:, :], ALU.mult, ALU.add).then_inc(L1f_vector_done, 1)
                dve.wait_ge(L1f_scalar_done, 22*b + 41)
                dve.tensor_tensor(m1_0[:, 1, :], t1_0[:, :], ps0[:, 2, 256:512], ALU.mult).then_inc(L1f_vector_done, 1)
                dve.wait_ge(L1f_matmul_done, 34*b + 48)
                dve.scalar_tensor_tensor(acc1_1[:, :], ps1[:, 3, 256:512], wv1_1[:, 5:6], acc1_1[:, :], ALU.mult, ALU.add).then_inc(L1f_vector_done, 1)
                dve.wait_ge(L1f_scalar_done, 22*b + 43)
                dve.tensor_tensor(m1_1[:, 1, :], t1_1[:, :], ps1[:, 2, 256:512], ALU.mult).then_inc(L1f_vector_done, 1)
                dve.wait_ge(L1f_matmul_done, 34*b + 49)
                dve.scalar_tensor_tensor(acc1_0[:, :], ps0[:, 3, 0:256], wv1_0[:, 6:7], acc1_0[:, :], ALU.mult, ALU.add).then_inc(L1f_vector_done, 1)
                dve.wait_ge(L1f_matmul_done, 34*b + 50)
                dve.scalar_tensor_tensor(acc1_1[:, :], ps1[:, 3, 0:256], wv1_1[:, 6:7], acc1_1[:, :], ALU.mult, ALU.add).then_inc(L1f_vector_done, 1)
                dve.wait_ge(L1f_matmul_done, 34*b + 51)
                dve.scalar_tensor_tensor(acc1_0[:, :], ps0[:, 3, 256:512], wv1_0[:, 7:8], acc1_0[:, :], ALU.mult, ALU.add).then_inc(L1f_vector_done, 1)
                dve.wait_ge(L1f_matmul_done, 34*b + 52)
                dve.scalar_tensor_tensor(acc1_1[:, :], ps1[:, 3, 256:512], wv1_1[:, 7:8], acc1_1[:, :], ALU.mult, ALU.add).then_inc(L1f_vector_done, 1)

            dve.sem_inc(L2a_vector_done, 39)
            dve.memset(v_0[:, :, 16:17], 1.0)
            dve.memset(v_1[:, :, 16:17], 1.0)
            dve.wait_ge(L1f_vector_done, 225)
            dve.wait_ge(L1f_pool_done, 10)
            dve.bn_stats(st0[:, 0:6], x[:, 0, :]).then_inc(L2a_vector_done, 1)
            dve.wait_ge(L1f_vector_done, 226)
            dve.bn_stats(st1[:, 0:6], x[:, 1, :]).then_inc(L2a_vector_done, 1)
            dve.wait_ge(L1f_scalar_done, 89)
            dve.wait_ge(L2a_vector_done, 40)
            dve.bn_aggr(st0[:, 6:8], st0[:, 0:6]).then_inc(L2a_vector_done, 1)
            dve.wait_ge(L1f_scalar_done, 90)
            dve.wait_ge(L2a_vector_done, 41)
            dve.bn_aggr(st1[:, 6:8], st1[:, 0:6]).then_inc(L2a_vector_done, 1)
            dve.wait_ge(L1f_matmul_done, 137)
            dve.wait_ge(L2a_scalar_done, 24)
            dve.tensor_scalar(u0[:, :], x[:, 0, :], st0[:, 6:7], st0[:, 9:10], ALU.subtract, ALU.mult).then_inc(L2a_vector_done, 1)
            dve.wait_ge(L1f_matmul_done, 138)
            dve.wait_ge(L2a_scalar_done, 25)
            dve.tensor_scalar(u1[:, :], x[:, 1, :], st1[:, 6:7], st1[:, 9:10], ALU.subtract, ALU.mult).then_inc(L2a_vector_done, 1)
            dve.wait_ge(L2a_matmul_done, 2)
            with dve.Fori(0, 4) as b:
                dve.wait_ge(L2a_vector_done, 47*b + 1)
                dve.sem_inc(dve_waited, 1)
                dve.bn_stats(st0[:, 0:6], x_next[:, 2*b+0, :]).then_inc(L2a_vector_done, 1)
                dve.wait_ge(L2a_vector_done, 47*b + 2)
                dve.sem_inc(dve_waited, 1)
                dve.bn_stats(st1[:, 0:6], x_next[:, 2*b+1, :]).then_inc(L2a_vector_done, 1)
                dve.wait_ge(L2a_vector_done, 47*b + 46)
                dve.wait_ge(L2a_scalar_done, 26*b + 1)
                dve.sem_inc(dve_waited, 1)
                dve.bn_aggr(st0[:, 6:8], st0[:, 0:6]).then_inc(L2a_vector_done, 1)
                dve.wait_ge(L2a_vector_done, 47*b + 47)
                dve.wait_ge(L2a_scalar_done, 26*b + 2)
                dve.sem_inc(dve_waited, 1)
                dve.bn_aggr(st1[:, 6:8], st1[:, 0:6]).then_inc(L2a_vector_done, 1)
                dve.wait_ge(L2a_scalar_done, 26*b + 29)
                dve.wait_ge(L2a_matmul_done, 29*b + 1)
                dve.tensor_scalar(u0[:, :], x_next[:, 2*b+0, :], st0[:, 6:7], st0[:, 9:10], ALU.subtract, ALU.mult)
                dve.wait_ge(L2a_scalar_done, 26*b + 30)
                dve.wait_ge(L2a_matmul_done, 29*b + 2)
                dve.tensor_scalar(u1[:, :], x_next[:, 2*b+1, :], st1[:, 6:7], st1[:, 9:10], ALU.subtract, ALU.mult)
                dve.wait_ge(L2a_scalar_done, 26*b + 31)
                dve.tensor_tensor(kM_0[:, 0, :, :], ps0[:, 1, 256:384].unsqueeze(1).to_broadcast([128, 8, 128]), mask16[:, :].unsqueeze(2).to_broadcast([128, 8, 128]), ALU.mult).then_inc(L2a_vector_done, 1)
                dve.tensor_tensor(kM_0[:, 1, :, :], ps0[:, 1, 384:512].unsqueeze(1).to_broadcast([128, 8, 128]), mask16[:, :].unsqueeze(2).to_broadcast([128, 8, 128]), ALU.mult).then_inc(L2a_vector_done, 1)
                dve.wait_ge(L2a_scalar_done, 26*b + 32)
                dve.tensor_tensor(kM_1[:, 0, :, :], ps1[:, 1, 256:384].unsqueeze(1).to_broadcast([128, 8, 128]), mask16[:, :].unsqueeze(2).to_broadcast([128, 8, 128]), ALU.mult).then_inc(L2a_vector_done, 1)
                dve.tensor_tensor(kM_1[:, 1, :, :], ps1[:, 1, 384:512].unsqueeze(1).to_broadcast([128, 8, 128]), mask16[:, :].unsqueeze(2).to_broadcast([128, 8, 128]), ALU.mult).then_inc(L2a_vector_done, 1)
                dve.wait_ge(L2a_matmul_done, 29*b + 7)
                dve.scalar_tensor_tensor(S_0[:, 0, :], alibi[:, :], 0.015625, ps0[:, 1, 0:128], ALU.mult, ALU.add)
                dve.scalar_tensor_tensor(S_0[:, 1, :], alibi[:, :], 0.25, ps0[:, 1, 128:256], ALU.mult, ALU.add)
                dve.scalar_tensor_tensor(S_0[:, 2, :], alibi[:, :], 0.6299605249474366, ps0[:, 1, 256:384], ALU.mult, ALU.add)
                dve.scalar_tensor_tensor(S_0[:, 3, :], alibi[:, :], 1.0, ps0[:, 1, 384:512], ALU.mult, ALU.add).then_inc(L2a_vector_done, 1)
                dve.wait_ge(L2a_vector_done, 47*b + 54)
                dve.tensor_reduce(st0[:, 16:20], S_0[:, :, :], AX.X, ALU.max).then_inc(L2a_vector_done, 1)
                dve.wait_ge(L2a_matmul_done, 29*b + 8)
                dve.scalar_tensor_tensor(S_1[:, 0, :], alibi[:, :], 0.015625, ps1[:, 1, 0:128], ALU.mult, ALU.add)
                dve.scalar_tensor_tensor(S_1[:, 1, :], alibi[:, :], 0.25, ps1[:, 1, 128:256], ALU.mult, ALU.add)
                dve.scalar_tensor_tensor(S_1[:, 2, :], alibi[:, :], 0.6299605249474366, ps1[:, 1, 256:384], ALU.mult, ALU.add)
                dve.scalar_tensor_tensor(S_1[:, 3, :], alibi[:, :], 1.0, ps1[:, 1, 384:512], ALU.mult, ALU.add).then_inc(L2a_vector_done, 1)
                dve.wait_ge(L2a_vector_done, 47*b + 55)
                dve.tensor_scalar(st0[:, 16:20], st0[:, 16:20], -0.25, None, ALU.mult).then_inc(L2a_vector_done, 1)
                dve.wait_ge(L2a_vector_done, 47*b + 56)
                dve.tensor_reduce(st1[:, 16:20], S_1[:, :, :], AX.X, ALU.max).then_inc(L2a_vector_done, 1)
                dve.wait_ge(L2a_vector_done, 47*b + 58)
                dve.tensor_scalar(st1[:, 16:20], st1[:, 16:20], -0.25, None, ALU.mult).then_inc(L2a_vector_done, 1)
                dve.wait_ge(L2a_matmul_done, 29*b + 10)
                dve.scalar_tensor_tensor(S_0[:, 0, :], alibi[:, :], 1.3195079107728942, ps0[:, 1, 0:128], ALU.mult, ALU.add)
                dve.scalar_tensor_tensor(S_0[:, 1, :], alibi[:, :], 1.5874010519681996, ps0[:, 1, 128:256], ALU.mult, ALU.add)
                dve.scalar_tensor_tensor(S_0[:, 2, :], alibi[:, :], 1.8114473285278134, ps0[:, 1, 256:384], ALU.mult, ALU.add)
                dve.scalar_tensor_tensor(S_0[:, 3, :], alibi[:, :], 2.0, ps0[:, 1, 384:512], ALU.mult, ALU.add).then_inc(L2a_vector_done, 1)
                dve.wait_ge(L2a_vector_done, 47*b + 60)
                dve.tensor_reduce(st0[:, 16:20], S_0[:, :, :], AX.X, ALU.max).then_inc(L2a_vector_done, 1)
                dve.wait_ge(L2a_matmul_done, 29*b + 11)
                dve.scalar_tensor_tensor(S_1[:, 0, :], alibi[:, :], 1.3195079107728942, ps1[:, 1, 0:128], ALU.mult, ALU.add)
                dve.scalar_tensor_tensor(S_1[:, 1, :], alibi[:, :], 1.5874010519681996, ps1[:, 1, 128:256], ALU.mult, ALU.add)
                dve.scalar_tensor_tensor(S_1[:, 2, :], alibi[:, :], 1.8114473285278134, ps1[:, 1, 256:384], ALU.mult, ALU.add)
                dve.scalar_tensor_tensor(S_1[:, 3, :], alibi[:, :], 2.0, ps1[:, 1, 384:512], ALU.mult, ALU.add).then_inc(L2a_vector_done, 1)
                dve.wait_ge(L2a_vector_done, 47*b + 61)
                dve.tensor_scalar(st0[:, 16:20], st0[:, 16:20], -0.25, None, ALU.mult).then_inc(L2a_vector_done, 1)
                dve.wait_ge(L2a_vector_done, 47*b + 62)
                dve.tensor_reduce(st1[:, 16:20], S_1[:, :, :], AX.X, ALU.max).then_inc(L2a_vector_done, 1)
                dve.wait_ge(L2a_matmul_done, 29*b + 12)
                dve.reciprocal(st0[:, 20:24], ps0[:, 3, 0:68].rearrange('p (h e) -> p h e', h=4)[:, :, 16]).then_inc(L2a_vector_done, 1)
                dve.wait_ge(L2a_matmul_done, 29*b + 13)
                dve.reciprocal(st1[:, 20:24], ps1[:, 3, 0:68].rearrange('p (h e) -> p h e', h=4)[:, :, 16]).then_inc(L2a_vector_done, 1)
                dve.wait_ge(L2a_vector_done, 47*b + 64)
                dve.tensor_scalar(st1[:, 16:20], st1[:, 16:20], -0.25, None, ALU.mult).then_inc(L2a_vector_done, 1)
                dve.wait_ge(L2a_vector_done, 47*b + 65)
                dve.tensor_tensor(ao_0[:, 0:64].rearrange('p (h d) -> p h d', h=4), ps0[:, 3, 0:68].rearrange('p (h e) -> p h e', h=4)[:, :, 0:16], st0[:, 20:24].unsqueeze(2).to_broadcast([128, 4, 16]), ALU.mult)
                dve.wait_ge(L2a_vector_done, 47*b + 66)
                dve.tensor_tensor(ao_1[:, 0:64].rearrange('p (h d) -> p h d', h=4), ps1[:, 3, 0:68].rearrange('p (h e) -> p h e', h=4)[:, :, 0:16], st1[:, 20:24].unsqueeze(2).to_broadcast([128, 4, 16]), ALU.mult)
                dve.wait_ge(L2a_matmul_done, 29*b + 14)
                dve.scalar_tensor_tensor(S_0[:, 0, :], alibi[:, :], 2.160119477784612, ps0[:, 1, 0:128], ALU.mult, ALU.add)
                dve.scalar_tensor_tensor(S_0[:, 1, :], alibi[:, :], 2.2973967099940698, ps0[:, 1, 128:256], ALU.mult, ALU.add)
                dve.scalar_tensor_tensor(S_0[:, 2, :], alibi[:, :], 2.4161788888088944, ps0[:, 1, 256:384], ALU.mult, ALU.add)
                dve.scalar_tensor_tensor(S_0[:, 3, :], alibi[:, :], 2.5198420997897464, ps0[:, 1, 384:512], ALU.mult, ALU.add).then_inc(L2a_vector_done, 1)
                dve.wait_ge(L2a_vector_done, 47*b + 68)
                dve.tensor_reduce(st0[:, 16:20], S_0[:, :, :], AX.X, ALU.max).then_inc(L2a_vector_done, 1)
                dve.wait_ge(L2a_matmul_done, 29*b + 15)
                dve.scalar_tensor_tensor(S_1[:, 0, :], alibi[:, :], 2.160119477784612, ps1[:, 1, 0:128], ALU.mult, ALU.add)
                dve.scalar_tensor_tensor(S_1[:, 1, :], alibi[:, :], 2.2973967099940698, ps1[:, 1, 128:256], ALU.mult, ALU.add)
                dve.scalar_tensor_tensor(S_1[:, 2, :], alibi[:, :], 2.4161788888088944, ps1[:, 1, 256:384], ALU.mult, ALU.add)
                dve.scalar_tensor_tensor(S_1[:, 3, :], alibi[:, :], 2.5198420997897464, ps1[:, 1, 384:512], ALU.mult, ALU.add).then_inc(L2a_vector_done, 1)
                dve.wait_ge(L2a_vector_done, 47*b + 69)
                dve.tensor_scalar(st0[:, 16:20], st0[:, 16:20], -0.25, None, ALU.mult).then_inc(L2a_vector_done, 1)
                dve.wait_ge(L2a_vector_done, 47*b + 70)
                dve.tensor_reduce(st1[:, 16:20], S_1[:, :, :], AX.X, ALU.max).then_inc(L2a_vector_done, 1)
                dve.wait_ge(L2a_matmul_done, 29*b + 16)
                dve.reciprocal(st0[:, 20:24], ps0[:, 3, 0:68].rearrange('p (h e) -> p h e', h=4)[:, :, 16]).then_inc(L2a_vector_done, 1)
                dve.wait_ge(L2a_matmul_done, 29*b + 17)
                dve.reciprocal(st1[:, 20:24], ps1[:, 3, 0:68].rearrange('p (h e) -> p h e', h=4)[:, :, 16]).then_inc(L2a_vector_done, 1)
                dve.wait_ge(L2a_vector_done, 47*b + 72)
                dve.tensor_scalar(st1[:, 16:20], st1[:, 16:20], -0.25, None, ALU.mult).then_inc(L2a_vector_done, 1)
                dve.wait_ge(L2a_vector_done, 47*b + 73)
                dve.tensor_tensor(ao_0[:, 64:128].rearrange('p (h d) -> p h d', h=4), ps0[:, 3, 0:68].rearrange('p (h e) -> p h e', h=4)[:, :, 0:16], st0[:, 20:24].unsqueeze(2).to_broadcast([128, 4, 16]), ALU.mult).then_inc(L2a_vector_done, 1)
                dve.wait_ge(L2a_vector_done, 47*b + 74)
                dve.tensor_tensor(ao_1[:, 64:128].rearrange('p (h d) -> p h d', h=4), ps1[:, 3, 0:68].rearrange('p (h e) -> p h e', h=4)[:, :, 0:16], st1[:, 20:24].unsqueeze(2).to_broadcast([128, 4, 16]), ALU.mult).then_inc(L2a_vector_done, 1)
                dve.wait_ge(L2a_matmul_done, 29*b + 18)
                dve.scalar_tensor_tensor(S_0[:, 0, :], alibi[:, :], 2.611023395419619, ps0[:, 1, 0:128], ALU.mult, ALU.add)
                dve.scalar_tensor_tensor(S_0[:, 1, :], alibi[:, :], 2.6918003852647123, ps0[:, 1, 128:256], ALU.mult, ALU.add)
                dve.scalar_tensor_tensor(S_0[:, 2, :], alibi[:, :], 2.763825759935552, ps0[:, 1, 256:384], ALU.mult, ALU.add)
                dve.scalar_tensor_tensor(S_0[:, 3, :], alibi[:, :], 2.8284271247461903, ps0[:, 1, 384:512], ALU.mult, ALU.add).then_inc(L2a_vector_done, 1)
                dve.wait_ge(L2a_vector_done, 47*b + 78)
                dve.tensor_reduce(st0[:, 16:20], S_0[:, :, :], AX.X, ALU.max).then_inc(L2a_vector_done, 1)
                dve.wait_ge(L2a_matmul_done, 29*b + 19)
                dve.scalar_tensor_tensor(S_1[:, 0, :], alibi[:, :], 2.611023395419619, ps1[:, 1, 0:128], ALU.mult, ALU.add)
                dve.scalar_tensor_tensor(S_1[:, 1, :], alibi[:, :], 2.6918003852647123, ps1[:, 1, 128:256], ALU.mult, ALU.add)
                dve.scalar_tensor_tensor(S_1[:, 2, :], alibi[:, :], 2.763825759935552, ps1[:, 1, 256:384], ALU.mult, ALU.add)
                dve.scalar_tensor_tensor(S_1[:, 3, :], alibi[:, :], 2.8284271247461903, ps1[:, 1, 384:512], ALU.mult, ALU.add).then_inc(L2a_vector_done, 1)
                dve.wait_ge(L2a_vector_done, 47*b + 79)
                dve.tensor_scalar(st0[:, 16:20], st0[:, 16:20], -0.25, None, ALU.mult).then_inc(L2a_vector_done, 1)
                dve.wait_ge(L2a_matmul_done, 29*b + 20)
                dve.reciprocal(st0[:, 20:24], ps0[:, 3, 0:68].rearrange('p (h e) -> p h e', h=4)[:, :, 16]).then_inc(L2a_vector_done, 1)
                dve.wait_ge(L2a_vector_done, 47*b + 80)
                dve.tensor_reduce(st1[:, 16:20], S_1[:, :, :], AX.X, ALU.max).then_inc(L2a_vector_done, 1)
                dve.wait_ge(L2a_matmul_done, 29*b + 21)
                dve.reciprocal(st1[:, 20:24], ps1[:, 3, 0:68].rearrange('p (h e) -> p h e', h=4)[:, :, 16]).then_inc(L2a_vector_done, 1)
                dve.wait_ge(L2a_vector_done, 47*b + 82)
                dve.tensor_tensor(ao_0[:, 128:192].rearrange('p (h d) -> p h d', h=4), ps0[:, 3, 0:68].rearrange('p (h e) -> p h e', h=4)[:, :, 0:16], st0[:, 20:24].unsqueeze(2).to_broadcast([128, 4, 16]), ALU.mult)
                dve.wait_ge(L2a_vector_done, 47*b + 83)
                dve.tensor_scalar(st1[:, 16:20], st1[:, 16:20], -0.25, None, ALU.mult).then_inc(L2a_vector_done, 1)
                dve.wait_ge(L2a_vector_done, 47*b + 84)
                dve.tensor_tensor(ao_1[:, 128:192].rearrange('p (h d) -> p h d', h=4), ps1[:, 3, 0:68].rearrange('p (h e) -> p h e', h=4)[:, :, 0:16], st1[:, 20:24].unsqueeze(2).to_broadcast([128, 4, 16]), ALU.mult).then_inc(L2a_vector_done, 1)
                dve.wait_ge(L2a_matmul_done, 29*b + 24)
                dve.reciprocal(st0[:, 20:24], ps0[:, 3, 0:68].rearrange('p (h e) -> p h e', h=4)[:, :, 16]).then_inc(L2a_vector_done, 1)
                dve.wait_ge(L2a_vector_done, 47*b + 87)
                dve.tensor_tensor(ao_0[:, 192:256].rearrange('p (h d) -> p h d', h=4), ps0[:, 3, 0:68].rearrange('p (h e) -> p h e', h=4)[:, :, 0:16], st0[:, 20:24].unsqueeze(2).to_broadcast([128, 4, 16]), ALU.mult).then_inc(L2a_vector_done, 1)
                dve.wait_ge(L2a_matmul_done, 29*b + 25)
                dve.reciprocal(st1[:, 20:24], ps1[:, 3, 0:68].rearrange('p (h e) -> p h e', h=4)[:, :, 16]).then_inc(L2a_vector_done, 1)
                dve.wait_ge(L2a_vector_done, 47*b + 89)
                dve.tensor_tensor(ao_1[:, 192:256].rearrange('p (h d) -> p h d', h=4), ps1[:, 3, 0:68].rearrange('p (h e) -> p h e', h=4)[:, :, 0:16], st1[:, 20:24].unsqueeze(2).to_broadcast([128, 4, 16]), ALU.mult).then_inc(L2a_vector_done, 1)
                dve.wait_ge(L2a_matmul_done, 29*b + 28)
                dve.tensor_tensor(x[:, 2*b+0, :], ps0[:, 1, 0:256], x[:, 2*b+0, :], ALU.add).then_inc(L2a_vector_done, 1)
                dve.wait_ge(L2a_matmul_done, 29*b + 29)
                dve.tensor_tensor(x[:, 2*b+1, :], ps1[:, 1, 0:256], x[:, 2*b+1, :], ALU.add).then_inc(L2a_vector_done, 1)

            dve.sem_inc(L2x_vector_done, 191)
            dve.wait_ge(L2x_w_loaded, 176)
            dve.reciprocal(inrc[:, :, :], insc[:, :, :])
            dve.wait_ge(L2x_w_loaded, 176)
            dve.reciprocal(smr[:, :], smo[:, :])
            dve.wait_ge(L2x_w_loaded, 176)
            dve.tensor_tensor(wps[:, :], wsc[:, 4:5], wsc[:, 5:6], ALU.mult)
            dve.memset(srow[:, :, :], 1.0).then_inc(L2x_vector_done, 1)
            dve.wait_ge(L2x_vector_done, 192)
            dve.tensor_scalar(srow[:, 0, 0:4], srow[:, 0, 0:4], wsc[:, 0:1], None, ALU.mult)
            dve.tensor_scalar(srow[:, 1, 0:4], srow[:, 1, 0:4], wsc[:, 1:2], None, ALU.mult)
            dve.tensor_scalar(srow[:, 0, 4:6], srow[:, 0, 4:6], wsc[:, 2:3], None, ALU.mult).then_inc(L2x_vector_done, 1)
            dve.wait_ge(L2x_vector_done, 193)
            dve.tensor_tensor(ssq[:, :, :], srow[:, :, :], srow[:, :, :], ALU.mult)
            dve.bn_stats(st0[:, 0:6], x[:, 0, :]).then_inc(L2x_vector_done, 1)
            dve.bn_stats(st1[:, 0:6], x[:, 1, :]).then_inc(L2x_vector_done, 1)
            dve.wait_ge(L2a_scalar_done, 105)
            dve.wait_ge(L2x_vector_done, 194)
            dve.bn_aggr(st0[:, 6:8], st0[:, 0:6]).then_inc(L2x_vector_done, 1)
            dve.wait_ge(L2a_scalar_done, 106)
            dve.wait_ge(L2x_vector_done, 195)
            dve.bn_aggr(st1[:, 6:8], st1[:, 0:6]).then_inc(L2x_vector_done, 1)
            dve.wait_ge(L2a_matmul_done, 117)
            dve.wait_ge(L2x_scalar_done, 101)
            dve.tensor_scalar(u0[:, :], x[:, 0, :], st0[:, 6:7], st0[:, 9:10], ALU.subtract, ALU.mult).then_inc(L2x_vector_done, 1)
            dve.wait_ge(L2a_matmul_done, 118)
            dve.wait_ge(L2x_scalar_done, 102)
            dve.tensor_scalar(u1[:, :], x[:, 1, :], st1[:, 6:7], st1[:, 9:10], ALU.subtract, ALU.mult).then_inc(L2x_vector_done, 1)
            dve.wait_ge(L2x_vector_done, 198)
            dve.bn_stats(st0[:, 0:6], u0[:, :]).then_inc(L2x_vector_done, 1)
            dve.wait_ge(L2x_vector_done, 199)
            dve.bn_stats(st1[:, 0:6], u1[:, :]).then_inc(L2x_vector_done, 1)
            dve.wait_ge(L2x_vector_done, 200)
            dve.bn_aggr(st0[:, 6:8], st0[:, 0:6]).then_inc(L2x_vector_done, 1)
            dve.wait_ge(L2x_vector_done, 201)
            dve.bn_aggr(st1[:, 6:8], st1[:, 0:6]).then_inc(L2x_vector_done, 1)
            dve.wait_ge(L2x_scalar_done, 105)
            dve.tensor_scalar(un0[:, :], u0[:, :], st0[:, 6:7], st0[:, 9:10], ALU.subtract, ALU.mult).then_inc(L2x_vector_done, 1)
            dve.wait_ge(L2x_scalar_done, 106)
            dve.tensor_scalar(un1[:, :], u1[:, :], st1[:, 6:7], st1[:, 9:10], ALU.subtract, ALU.mult).then_inc(L2x_vector_done, 1)
            dve.wait_ge(L2x_vector_done, 204)
            dve.tensor_tensor(un0[:, :], un0[:, :], lnb2[:, 0, :], ALU.mult).then_inc(L2x_vector_done, 1)
            dve.wait_ge(L2x_vector_done, 205)
            dve.tensor_tensor(un1[:, :], un1[:, :], lnb2[:, 0, :], ALU.mult).then_inc(L2x_vector_done, 1)
            dve.wait_ge(L2x_vector_done, 206)
            dve.tensor_tensor(un0[:, :], un0[:, :], lnb2[:, 1, :], ALU.add).then_inc(L2x_vector_done, 1)
            dve.wait_ge(L2x_vector_done, 207)
            dve.tensor_tensor(un1[:, :], un1[:, :], lnb2[:, 1, :], ALU.add).then_inc(L2x_vector_done, 1)
            dve.wait_ge(L2x_scalar_done, 107)
            dve.tensor_tensor(xs_0[:, :, :, :], unT0[:, :, :].unsqueeze(1).to_broadcast([128, 4, 2, 128]), inrc[:, :, :].unsqueeze(3).to_broadcast([128, 4, 2, 128]), ALU.mult).then_inc(L2x_vector_done, 1)
            dve.wait_ge(L2x_scalar_done, 108)
            dve.tensor_tensor(xs_1[:, :, :, :], unT1[:, :, :].unsqueeze(1).to_broadcast([128, 4, 2, 128]), inrc[:, :, :].unsqueeze(3).to_broadcast([128, 4, 2, 128]), ALU.mult).then_inc(L2x_vector_done, 1)
            dve.wait_ge(L2x_vector_done, 210)
            dve.tensor_scalar(y16_0[:, :], xsf_0[:, :], 448.0, -448.0, ALU.min, ALU.max).then_inc(L2x_vector_done, 1)
            dve.wait_ge(L2x_vector_done, 211)
            dve.tensor_scalar(y16_1[:, :], xsf_1[:, :], 448.0, -448.0, ALU.min, ALU.max).then_inc(L2x_vector_done, 1)
            dve.wait_ge(L2x_vector_done, 212)
            dve.tensor_scalar(e16_0[:, 0:1024], y16u_0[:, 0:1024], 0x7F80, None, ALU.bitwise_and).then_inc(L2x_vector_done, 1)
            dve.wait_ge(L2x_vector_done, 213)
            dve.tensor_scalar(e16_1[:, 0:1024], y16u_1[:, 0:1024], 0x7F80, None, ALU.bitwise_and).then_inc(L2x_vector_done, 1)
            dve.wait_ge(L2x_vector_done, 214)
            dve.tensor_scalar(qq_0[:, :], e16b_0[:, 0:1024], 2.0 ** -6, 1.5 * 2.0 ** 20, ALU.max, ALU.mult).then_inc(L2x_vector_done, 1)
            dve.wait_ge(L2x_vector_done, 215)
            dve.tensor_scalar(qq_1[:, :], e16b_1[:, 0:1024], 2.0 ** -6, 1.5 * 2.0 ** 20, ALU.max, ALU.mult).then_inc(L2x_vector_done, 1)
            dve.wait_ge(L2x_pool_done, 3)
            dve.tensor_tensor(xs_0[:, :, :, :], xs_0[:, :, :, :], insc[:, :, :].unsqueeze(3).to_broadcast([128, 4, 2, 128]), ALU.mult)
            dve.wait_ge(L2x_pool_done, 4)
            dve.tensor_tensor(xs_1[:, :, :, :], xs_1[:, :, :, :], insc[:, :, :].unsqueeze(3).to_broadcast([128, 4, 2, 128]), ALU.mult).then_inc(L2x_vector_done, 1)
            dve.wait_ge(L2x_vector_done, 218)
            with dve.Fori(0, 4) as b:
                dve.wait_ge(L2x_vector_done, 226*b + 1)
                dve.sem_inc(dve_waited, 1)
                dve.bn_stats(st0[:, 0:6], x_next[:, 2*b+0, :]).then_inc(L2x_vector_done, 1)
                dve.wait_ge(L2x_vector_done, 226*b + 2)
                dve.sem_inc(dve_waited, 1)
                dve.bn_stats(st1[:, 0:6], x_next[:, 2*b+1, :]).then_inc(L2x_vector_done, 1)
                dve.wait_ge(L2x_vector_done, 226*b + 219)
                dve.wait_ge(L2x_scalar_done, 108*b + 7)
                dve.sem_inc(dve_waited, 1)
                dve.bn_aggr(st0[:, 6:8], st0[:, 0:6]).then_inc(L2x_vector_done, 1)
                dve.wait_ge(L2x_vector_done, 226*b + 220)
                dve.wait_ge(L2x_scalar_done, 108*b + 8)
                dve.sem_inc(dve_waited, 1)
                dve.bn_aggr(st1[:, 6:8], st1[:, 0:6]).then_inc(L2x_vector_done, 1)
                dve.wait_ge(L2x_scalar_done, 108*b + 113)
                dve.tensor_scalar(u0[:, :], x_next[:, 2*b+0, :], st0[:, 6:7], st0[:, 9:10], ALU.subtract, ALU.mult).then_inc(L2x_vector_done, 1)
                dve.wait_ge(L2x_matmul_done, 124*b + 19)
                for i in range(4):
                    dve.bn_stats(s6_0[:, i, :], ps0[:, 1, 128 * i:128 * i + 128])
                dve.wait_ge(L2x_scalar_done, 108*b + 114)
                dve.tensor_scalar(u1[:, :], x_next[:, 2*b+1, :], st1[:, 6:7], st1[:, 9:10], ALU.subtract, ALU.mult).then_inc(L2x_vector_done, 1)
                dve.wait_ge(L2x_vector_done, 226*b + 223)
                dve.bn_stats(st0[:, 0:6], u0[:, :]).then_inc(L2x_vector_done, 1)
                dve.wait_ge(L2x_vector_done, 226*b + 224)
                dve.bn_stats(st1[:, 0:6], u1[:, :]).then_inc(L2x_vector_done, 1)
                dve.wait_ge(L2x_vector_done, 226*b + 225)
                dve.sem_inc(dve_waited, 1)
                dve.bn_aggr(st0[:, 6:8], st0[:, 0:6]).then_inc(L2x_vector_done, 1)
                dve.wait_ge(L2x_vector_done, 226*b + 226)
                dve.sem_inc(dve_waited, 1)
                dve.bn_aggr(st1[:, 6:8], st1[:, 0:6]).then_inc(L2x_vector_done, 1)
                dve.wait_ge(L2x_scalar_done, 108*b + 117)
                dve.tensor_scalar(un0[:, :], u0[:, :], st0[:, 6:7], st0[:, 9:10], ALU.subtract, ALU.mult).then_inc(L2x_vector_done, 1)
                dve.wait_ge(L2x_matmul_done, 124*b + 20)
                for i in range(4):
                    dve.bn_stats(s6_1[:, i, :], ps1[:, 1, 128 * i:128 * i + 128])
                dve.wait_ge(L2x_scalar_done, 108*b + 118)
                dve.tensor_scalar(un1[:, :], u1[:, :], st1[:, 6:7], st1[:, 9:10], ALU.subtract, ALU.mult).then_inc(L2x_vector_done, 1)
                dve.wait_ge(L2x_vector_done, 226*b + 229)
                dve.tensor_tensor(un0[:, :], un0[:, :], lnb2[:, 0, :], ALU.mult).then_inc(L2x_vector_done, 1)
                dve.wait_ge(L2x_vector_done, 226*b + 230)
                dve.tensor_tensor(un1[:, :], un1[:, :], lnb2[:, 0, :], ALU.mult).then_inc(L2x_vector_done, 1)
                dve.wait_ge(L2x_vector_done, 226*b + 231)
                dve.tensor_tensor(un0[:, :], un0[:, :], lnb2[:, 1, :], ALU.add)
                dve.wait_ge(L2x_vector_done, 226*b + 232)
                dve.tensor_tensor(un1[:, :], un1[:, :], lnb2[:, 1, :], ALU.add)
                dve.wait_ge(L2x_matmul_done, 124*b + 21)
                for i in range(2):
                    last = dve.bn_stats(s6_0[:, 4 + i, :], ps0[:, 2, 128 * i:128 * i + 128])
                last.then_inc(L2x_vector_done, 1)
                dve.wait_ge(L2x_vector_done, 226*b + 233)
                dve.sem_inc(dve_waited, 1)
                for i in range(6):
                    last = dve.bn_aggr(mv_0[:, i, :], s6_0[:, i, :])
                last.then_inc(L2x_vector_done, 1)
                dve.wait_ge(L2x_vector_done, 226*b + 234)
                dve.tensor_tensor(vv_0[:, :], mv_0[:, :, 1], ssq[:, 0, :], ALU.mult).then_inc(L2x_vector_done, 1)
                dve.wait_ge(L2x_matmul_done, 124*b + 22)
                for i in range(2):
                    last = dve.bn_stats(s6_1[:, 4 + i, :], ps1[:, 2, 128 * i:128 * i + 128])
                last.then_inc(L2x_vector_done, 1)
                dve.wait_ge(L2x_vector_done, 226*b + 236)
                dve.sem_inc(dve_waited, 1)
                for i in range(6):
                    last = dve.bn_aggr(mv_1[:, i, :], s6_1[:, i, :])
                last.then_inc(L2x_vector_done, 1)
                dve.wait_ge(L2x_vector_done, 226*b + 237)
                dve.tensor_tensor(vv_1[:, :], mv_1[:, :, 1], ssq[:, 0, :], ALU.mult).then_inc(L2x_vector_done, 1)
                dve.wait_ge(L2x_scalar_done, 108*b + 120)
                dve.tensor_tensor(rr_0[:, :], rr_0[:, :], srow[:, 0, :], ALU.mult).then_inc(L2x_vector_done, 1)
                dve.wait_ge(L2x_vector_done, 226*b + 239)
                dve.wait_ge(L2x_pool_done, 52*b + 3)
                for i in range(4):
                    last = dve.tensor_scalar(qk_0[:, i, :], ps0[:, 1, 128 * i:128 * i + 128], mv_0[:, i, 0:1], rr_0[:, i:i + 1], ALU.subtract, ALU.mult)
                last.then_inc(L2x_vector_done, 1)
                dve.wait_ge(L2x_scalar_done, 108*b + 122)
                dve.tensor_tensor(rr_1[:, :], rr_1[:, :], srow[:, 0, :], ALU.mult).then_inc(L2x_vector_done, 1)
                for i in range(2):
                    last = dve.tensor_scalar(qk_0[:, 4 + i, :], ps0[:, 2, 128 * i:128 * i + 128], mv_0[:, 4 + i, 0:1], rr_0[:, 4 + i:5 + i], ALU.subtract, ALU.mult)
                last.then_inc(L2x_vector_done, 1)
                dve.wait_ge(L2x_vector_done, 226*b + 241)
                dve.wait_ge(L2x_pool_done, 52*b + 4)
                for i in range(4):
                    last = dve.tensor_scalar(qk_1[:, i, :], ps1[:, 1, 128 * i:128 * i + 128], mv_1[:, i, 0:1], rr_1[:, i:i + 1], ALU.subtract, ALU.mult)
                last.then_inc(L2x_vector_done, 1)
                for i in range(2):
                    last = dve.tensor_scalar(qk_1[:, 4 + i, :], ps1[:, 2, 128 * i:128 * i + 128], mv_1[:, 4 + i, 0:1], rr_1[:, 4 + i:5 + i], ALU.subtract, ALU.mult)
                last.then_inc(L2x_vector_done, 1)
                dve.wait_ge(L2x_matmul_done, 124*b + 24)
                for i in range(4):
                    dve.bn_stats(s6_0[:, i, :], ps0[:, 1, 128 * i:128 * i + 128])
                dve.wait_ge(L2x_matmul_done, 124*b + 28)
                for i in range(4):
                    dve.bn_stats(s6_1[:, i, :], ps1[:, 1, 128 * i:128 * i + 128])
                dve.wait_ge(L2x_matmul_done, 124*b + 29)
                dve.tensor_reduce(st0[:, 16:20], ps0[:, 2, :].rearrange("p (h s) -> p h s", h=4), AX.X, ALU.max).then_inc(L2x_vector_done, 1)
                dve.wait_ge(L2x_vector_done, 226*b + 245)
                dve.tensor_scalar(st0[:, 16:20], st0[:, 16:20], -0.08838834764831845, None, ALU.mult).then_inc(L2x_vector_done, 1)
                dve.wait_ge(L2x_matmul_done, 124*b + 30)
                dve.tensor_reduce(st1[:, 16:20], ps1[:, 2, :].rearrange("p (h s) -> p h s", h=4), AX.X, ALU.max).then_inc(L2x_vector_done, 1)
                dve.wait_ge(L2x_vector_done, 226*b + 247)
                dve.tensor_scalar(st1[:, 16:20], st1[:, 16:20], -0.08838834764831845, None, ALU.mult).then_inc(L2x_vector_done, 1)
                dve.wait_ge(L2x_scalar_done, 108*b + 127)
                dve.reciprocal(st0[:, 16:20], st0[:, 20:24]).then_inc(L2x_vector_done, 1)
                dve.wait_ge(L2x_scalar_done, 108*b + 128)
                dve.reciprocal(st1[:, 16:20], st1[:, 20:24]).then_inc(L2x_vector_done, 1)
                dve.wait_ge(L2x_matmul_done, 124*b + 31)
                for i in range(2):
                    last = dve.bn_stats(s6_0[:, 4 + i, :], ps0[:, 2, 128 * i:128 * i + 128])
                last.then_inc(L2x_vector_done, 1)
                dve.wait_ge(L2x_vector_done, 226*b + 251)
                dve.sem_inc(dve_waited, 1)
                for i in range(6):
                    last = dve.bn_aggr(mv_0[:, i, :], s6_0[:, i, :])
                last.then_inc(L2x_vector_done, 1)
                dve.wait_ge(L2x_vector_done, 226*b + 252)
                dve.tensor_tensor(vv_0[:, :], mv_0[:, :, 1], ssq[:, 0, :], ALU.mult).then_inc(L2x_vector_done, 1)
                dve.wait_ge(L2x_scalar_done, 108*b + 131)
                dve.tensor_tensor(rr_0[:, :], rr_0[:, :], srow[:, 0, :], ALU.mult).then_inc(L2x_vector_done, 1)
                dve.wait_ge(L2x_vector_done, 226*b + 254)
                for i in range(4):
                    dve.tensor_scalar(qk_0[:, i, :], ps0[:, 1, 128 * i:128 * i + 128], mv_0[:, i, 0:1], rr_0[:, i:i + 1], ALU.subtract, ALU.mult)
                dve.wait_ge(L2x_matmul_done, 124*b + 34)
                dve.tensor_tensor(P2_0[:, :, :], ps0[:, 3, :].rearrange('p (h t) -> p h t', h=4), smr[:, 0:4].unsqueeze(2).to_broadcast([128, 4, 128]), ALU.mult).then_inc(L2x_vector_done, 1)
                dve.wait_ge(L2x_matmul_done, 124*b + 35)
                for i in range(2):
                    last = dve.bn_stats(s6_1[:, 4 + i, :], ps1[:, 2, 128 * i:128 * i + 128])
                last.then_inc(L2x_vector_done, 1)
                dve.wait_ge(L2x_vector_done, 226*b + 255)
                dve.tensor_scalar(y16_0[:, 0:512], P2f_0[:, :], 448.0, -448.0, ALU.min, ALU.max).then_inc(L2x_vector_done, 1)
                dve.wait_ge(L2x_vector_done, 226*b + 256)
                dve.sem_inc(dve_waited, 1)
                for i in range(6):
                    dve.bn_aggr(mv_1[:, i, :], s6_1[:, i, :])
                dve.wait_ge(L2x_matmul_done, 124*b + 36)
                dve.tensor_tensor(P2_1[:, :, :], ps1[:, 3, :].rearrange('p (h t) -> p h t', h=4), smr[:, 0:4].unsqueeze(2).to_broadcast([128, 4, 128]), ALU.mult).then_inc(L2x_vector_done, 1)
                dve.wait_ge(L2x_vector_done, 226*b + 257)
                dve.tensor_scalar(e16_0[:, 0:512], y16u_0[:, 0:512], 0x7F80, None, ALU.bitwise_and).then_inc(L2x_vector_done, 1)
                dve.wait_ge(L2x_vector_done, 226*b + 258)
                dve.tensor_scalar(y16_1[:, 0:512], P2f_1[:, :], 448.0, -448.0, ALU.min, ALU.max).then_inc(L2x_vector_done, 1)
                dve.tensor_tensor(vv_1[:, :], mv_1[:, :, 1], ssq[:, 0, :], ALU.mult).then_inc(L2x_vector_done, 1)
                dve.wait_ge(L2x_vector_done, 226*b + 259)
                dve.tensor_scalar(PT2_0[:, :], e16b_0[:, 0:512], 2.0 ** -6, 1.5 * 2.0 ** 20, ALU.max, ALU.mult).then_inc(L2x_vector_done, 1)
                dve.wait_ge(L2x_vector_done, 226*b + 260)
                dve.tensor_scalar(e16_1[:, 0:512], y16u_1[:, 0:512], 0x7F80, None, ALU.bitwise_and).then_inc(L2x_vector_done, 1)
                for i in range(2):
                    last = dve.tensor_scalar(qk_0[:, 4 + i, :], ps0[:, 2, 128 * i:128 * i + 128], mv_0[:, 4 + i, 0:1], rr_0[:, 4 + i:5 + i], ALU.subtract, ALU.mult)
                last.then_inc(L2x_vector_done, 1)
                dve.wait_ge(L2x_vector_done, 226*b + 263)
                dve.tensor_scalar(PT2_1[:, :], e16b_1[:, 0:512], 2.0 ** -6, 1.5 * 2.0 ** 20, ALU.max, ALU.mult).then_inc(L2x_vector_done, 1)
                dve.wait_ge(L2x_scalar_done, 108*b + 134)
                dve.tensor_tensor(rr_1[:, :], rr_1[:, :], srow[:, 0, :], ALU.mult).then_inc(L2x_vector_done, 1)
                dve.wait_ge(L2x_matmul_done, 124*b + 38)
                for i in range(4):
                    dve.bn_stats(s6_0[:, i, :], ps0[:, 1, 128 * i:128 * i + 128])
                dve.wait_ge(L2x_vector_done, 226*b + 266)
                for i in range(4):
                    last = dve.tensor_scalar(qk_1[:, i, :], ps1[:, 1, 128 * i:128 * i + 128], mv_1[:, i, 0:1], rr_1[:, i:i + 1], ALU.subtract, ALU.mult)
                last.then_inc(L2x_vector_done, 1)
                for i in range(2):
                    last = dve.tensor_scalar(qk_1[:, 4 + i, :], ps1[:, 2, 128 * i:128 * i + 128], mv_1[:, 4 + i, 0:1], rr_1[:, 4 + i:5 + i], ALU.subtract, ALU.mult)
                last.then_inc(L2x_vector_done, 1)
                dve.wait_ge(L2x_matmul_done, 124*b + 40)
                dve.tensor_reduce(st0[:, 16:20], ps0[:, 2, :].rearrange("p (h s) -> p h s", h=4), AX.X, ALU.max).then_inc(L2x_vector_done, 1)
                dve.wait_ge(L2x_vector_done, 226*b + 269)
                dve.tensor_scalar(st0[:, 16:20], st0[:, 16:20], -0.08838834764831845, None, ALU.mult).then_inc(L2x_vector_done, 1)
                dve.wait_ge(L2x_matmul_done, 124*b + 44)
                dve.tensor_reduce(st1[:, 16:20], ps1[:, 2, :].rearrange("p (h s) -> p h s", h=4), AX.X, ALU.max).then_inc(L2x_vector_done, 1)
                dve.wait_ge(L2x_scalar_done, 108*b + 139)
                dve.reciprocal(st0[:, 16:20], st0[:, 20:24]).then_inc(L2x_vector_done, 1)
                dve.wait_ge(L2x_vector_done, 226*b + 271)
                dve.tensor_scalar(st1[:, 16:20], st1[:, 16:20], -0.08838834764831845, None, ALU.mult).then_inc(L2x_vector_done, 1)
                dve.wait_ge(L2x_scalar_done, 108*b + 140)
                dve.reciprocal(st1[:, 16:20], st1[:, 20:24]).then_inc(L2x_vector_done, 1)
                dve.wait_ge(L2x_matmul_done, 124*b + 46)
                for i in range(4):
                    dve.bn_stats(s6_1[:, i, :], ps1[:, 1, 128 * i:128 * i + 128])
                dve.wait_ge(L2x_matmul_done, 124*b + 49)
                dve.tensor_tensor(P2_0[:, :, :], ps0[:, 3, :].rearrange('p (h t) -> p h t', h=4), smr[:, 4:8].unsqueeze(2).to_broadcast([128, 4, 128]), ALU.mult).then_inc(L2x_vector_done, 1)
                dve.wait_ge(L2x_vector_done, 226*b + 275)
                dve.tensor_scalar(y16_0[:, 0:512], P2f_0[:, :], 448.0, -448.0, ALU.min, ALU.max).then_inc(L2x_vector_done, 1)
                dve.wait_ge(L2x_matmul_done, 124*b + 50)
                for i in range(2):
                    last = dve.bn_stats(s6_0[:, 4 + i, :], ps0[:, 2, 128 * i:128 * i + 128])
                last.then_inc(L2x_vector_done, 1)
                dve.wait_ge(L2x_vector_done, 226*b + 276)
                dve.tensor_scalar(e16_0[:, 0:512], y16u_0[:, 0:512], 0x7F80, None, ALU.bitwise_and)
                dve.wait_ge(L2x_vector_done, 226*b + 277)
                dve.sem_inc(dve_waited, 1)
                for i in range(6):
                    last = dve.bn_aggr(mv_0[:, i, :], s6_0[:, i, :])
                last.then_inc(L2x_vector_done, 1)
                dve.wait_ge(L2x_matmul_done, 124*b + 51)
                dve.tensor_tensor(P2_1[:, :, :], ps1[:, 3, :].rearrange('p (h t) -> p h t', h=4), smr[:, 4:8].unsqueeze(2).to_broadcast([128, 4, 128]), ALU.mult).then_inc(L2x_vector_done, 1)
                dve.wait_ge(L2x_vector_done, 226*b + 278)
                dve.tensor_tensor(vv_0[:, :], mv_0[:, :, 1], ssq[:, 0, :], ALU.mult).then_inc(L2x_vector_done, 1)
                dve.wait_ge(L2x_matmul_done, 124*b + 52)
                for i in range(2):
                    last = dve.bn_stats(s6_1[:, 4 + i, :], ps1[:, 2, 128 * i:128 * i + 128])
                last.then_inc(L2x_vector_done, 1)
                dve.wait_ge(L2x_vector_done, 226*b + 279)
                dve.tensor_scalar(y16_1[:, 0:512], P2f_1[:, :], 448.0, -448.0, ALU.min, ALU.max).then_inc(L2x_vector_done, 1)
                dve.wait_ge(L2x_vector_done, 226*b + 281)
                dve.sem_inc(dve_waited, 1)
                for i in range(6):
                    last = dve.bn_aggr(mv_1[:, i, :], s6_1[:, i, :])
                last.then_inc(L2x_vector_done, 1)
                dve.wait_ge(L2x_vector_done, 226*b + 282)
                dve.tensor_scalar(e16_1[:, 0:512], y16u_1[:, 0:512], 0x7F80, None, ALU.bitwise_and).then_inc(L2x_vector_done, 1)
                dve.wait_ge(L2x_vector_done, 226*b + 283)
                dve.tensor_tensor(vv_1[:, :], mv_1[:, :, 1], ssq[:, 0, :], ALU.mult).then_inc(L2x_vector_done, 1)
                dve.tensor_scalar(PT2_0[:, :], e16b_0[:, 0:512], 2.0 ** -6, 1.5 * 2.0 ** 20, ALU.max, ALU.mult).then_inc(L2x_vector_done, 1)
                dve.wait_ge(L2x_vector_done, 226*b + 284)
                dve.tensor_scalar(PT2_1[:, :], e16b_1[:, 0:512], 2.0 ** -6, 1.5 * 2.0 ** 20, ALU.max, ALU.mult).then_inc(L2x_vector_done, 1)
                dve.wait_ge(L2x_scalar_done, 108*b + 144)
                dve.tensor_tensor(rr_0[:, :], rr_0[:, :], srow[:, 0, :], ALU.mult).then_inc(L2x_vector_done, 1)
                dve.wait_ge(L2x_vector_done, 226*b + 288)
                for i in range(4):
                    last = dve.tensor_scalar(qk_0[:, i, :], ps0[:, 1, 128 * i:128 * i + 128], mv_0[:, i, 0:1], rr_0[:, i:i + 1], ALU.subtract, ALU.mult)
                last.then_inc(L2x_vector_done, 1)
                dve.wait_ge(L2x_scalar_done, 108*b + 146)
                dve.tensor_tensor(rr_1[:, :], rr_1[:, :], srow[:, 0, :], ALU.mult).then_inc(L2x_vector_done, 1)
                for i in range(2):
                    last = dve.tensor_scalar(qk_0[:, 4 + i, :], ps0[:, 2, 128 * i:128 * i + 128], mv_0[:, 4 + i, 0:1], rr_0[:, 4 + i:5 + i], ALU.subtract, ALU.mult)
                last.then_inc(L2x_vector_done, 1)
                dve.wait_ge(L2x_vector_done, 226*b + 290)
                for i in range(4):
                    last = dve.tensor_scalar(qk_1[:, i, :], ps1[:, 1, 128 * i:128 * i + 128], mv_1[:, i, 0:1], rr_1[:, i:i + 1], ALU.subtract, ALU.mult)
                last.then_inc(L2x_vector_done, 1)
                for i in range(2):
                    last = dve.tensor_scalar(qk_1[:, 4 + i, :], ps1[:, 2, 128 * i:128 * i + 128], mv_1[:, 4 + i, 0:1], rr_1[:, 4 + i:5 + i], ALU.subtract, ALU.mult)
                last.then_inc(L2x_vector_done, 1)
                dve.wait_ge(L2x_matmul_done, 124*b + 54)
                for i in range(4):
                    dve.bn_stats(s6_0[:, i, :], ps0[:, 1, 128 * i:128 * i + 128])
                dve.wait_ge(L2x_matmul_done, 124*b + 58)
                dve.tensor_reduce(st0[:, 16:20], ps0[:, 2, :].rearrange("p (h s) -> p h s", h=4), AX.X, ALU.max).then_inc(L2x_vector_done, 1)
                dve.wait_ge(L2x_vector_done, 226*b + 294)
                dve.tensor_scalar(st0[:, 16:20], st0[:, 16:20], -0.08838834764831845, None, ALU.mult).then_inc(L2x_vector_done, 1)
                dve.wait_ge(L2x_matmul_done, 124*b + 59)
                dve.tensor_reduce(st1[:, 16:20], ps1[:, 2, :].rearrange("p (h s) -> p h s", h=4), AX.X, ALU.max).then_inc(L2x_vector_done, 1)
                dve.wait_ge(L2x_vector_done, 226*b + 296)
                dve.tensor_scalar(st1[:, 16:20], st1[:, 16:20], -0.08838834764831845, None, ALU.mult).then_inc(L2x_vector_done, 1)
                dve.wait_ge(L2x_scalar_done, 108*b + 151)
                dve.reciprocal(st0[:, 16:20], st0[:, 20:24]).then_inc(L2x_vector_done, 1)
                dve.wait_ge(L2x_scalar_done, 108*b + 152)
                dve.reciprocal(st1[:, 16:20], st1[:, 20:24]).then_inc(L2x_vector_done, 1)
                dve.wait_ge(L2x_matmul_done, 124*b + 61)
                for i in range(4):
                    dve.bn_stats(s6_1[:, i, :], ps1[:, 1, 128 * i:128 * i + 128])
                dve.wait_ge(L2x_matmul_done, 124*b + 64)
                dve.tensor_tensor(P2_0[:, :, :], ps0[:, 3, :].rearrange('p (h t) -> p h t', h=4), smr[:, 8:12].unsqueeze(2).to_broadcast([128, 4, 128]), ALU.mult).then_inc(L2x_vector_done, 1)
                dve.wait_ge(L2x_vector_done, 226*b + 300)
                dve.tensor_scalar(y16_0[:, 0:512], P2f_0[:, :], 448.0, -448.0, ALU.min, ALU.max).then_inc(L2x_vector_done, 1)
                dve.wait_ge(L2x_matmul_done, 124*b + 65)
                for i in range(2):
                    last = dve.bn_stats(s6_0[:, 4 + i, :], ps0[:, 2, 128 * i:128 * i + 128])
                last.then_inc(L2x_vector_done, 1)
                dve.wait_ge(L2x_vector_done, 226*b + 301)
                dve.tensor_scalar(e16_0[:, 0:512], y16u_0[:, 0:512], 0x7F80, None, ALU.bitwise_and)
                dve.wait_ge(L2x_vector_done, 226*b + 302)
                dve.sem_inc(dve_waited, 1)
                for i in range(6):
                    last = dve.bn_aggr(mv_0[:, i, :], s6_0[:, i, :])
                last.then_inc(L2x_vector_done, 1)
                dve.wait_ge(L2x_matmul_done, 124*b + 66)
                dve.tensor_tensor(P2_1[:, :, :], ps1[:, 3, :].rearrange('p (h t) -> p h t', h=4), smr[:, 8:12].unsqueeze(2).to_broadcast([128, 4, 128]), ALU.mult).then_inc(L2x_vector_done, 1)
                dve.wait_ge(L2x_vector_done, 226*b + 303)
                dve.tensor_tensor(vv_0[:, :], mv_0[:, :, 1], ssq[:, 0, :], ALU.mult).then_inc(L2x_vector_done, 1)
                dve.wait_ge(L2x_matmul_done, 124*b + 67)
                for i in range(2):
                    last = dve.bn_stats(s6_1[:, 4 + i, :], ps1[:, 2, 128 * i:128 * i + 128])
                last.then_inc(L2x_vector_done, 1)
                dve.wait_ge(L2x_vector_done, 226*b + 304)
                dve.tensor_scalar(y16_1[:, 0:512], P2f_1[:, :], 448.0, -448.0, ALU.min, ALU.max).then_inc(L2x_vector_done, 1)
                dve.wait_ge(L2x_vector_done, 226*b + 306)
                dve.sem_inc(dve_waited, 1)
                for i in range(6):
                    last = dve.bn_aggr(mv_1[:, i, :], s6_1[:, i, :])
                last.then_inc(L2x_vector_done, 1)
                dve.wait_ge(L2x_vector_done, 226*b + 307)
                dve.tensor_scalar(e16_1[:, 0:512], y16u_1[:, 0:512], 0x7F80, None, ALU.bitwise_and).then_inc(L2x_vector_done, 1)
                dve.wait_ge(L2x_vector_done, 226*b + 308)
                dve.tensor_tensor(vv_1[:, :], mv_1[:, :, 1], ssq[:, 0, :], ALU.mult).then_inc(L2x_vector_done, 1)
                dve.tensor_scalar(PT2_0[:, :], e16b_0[:, 0:512], 2.0 ** -6, 1.5 * 2.0 ** 20, ALU.max, ALU.mult).then_inc(L2x_vector_done, 1)
                dve.wait_ge(L2x_vector_done, 226*b + 309)
                dve.tensor_scalar(PT2_1[:, :], e16b_1[:, 0:512], 2.0 ** -6, 1.5 * 2.0 ** 20, ALU.max, ALU.mult).then_inc(L2x_vector_done, 1)
                dve.wait_ge(L2x_scalar_done, 108*b + 156)
                dve.tensor_tensor(rr_0[:, :], rr_0[:, :], srow[:, 0, :], ALU.mult).then_inc(L2x_vector_done, 1)
                dve.wait_ge(L2x_vector_done, 226*b + 313)
                for i in range(4):
                    last = dve.tensor_scalar(qk_0[:, i, :], ps0[:, 1, 128 * i:128 * i + 128], mv_0[:, i, 0:1], rr_0[:, i:i + 1], ALU.subtract, ALU.mult)
                last.then_inc(L2x_vector_done, 1)
                dve.wait_ge(L2x_scalar_done, 108*b + 158)
                dve.tensor_tensor(rr_1[:, :], rr_1[:, :], srow[:, 0, :], ALU.mult).then_inc(L2x_vector_done, 1)
                for i in range(2):
                    last = dve.tensor_scalar(qk_0[:, 4 + i, :], ps0[:, 2, 128 * i:128 * i + 128], mv_0[:, 4 + i, 0:1], rr_0[:, 4 + i:5 + i], ALU.subtract, ALU.mult)
                last.then_inc(L2x_vector_done, 1)
                dve.wait_ge(L2x_vector_done, 226*b + 315)
                for i in range(4):
                    last = dve.tensor_scalar(qk_1[:, i, :], ps1[:, 1, 128 * i:128 * i + 128], mv_1[:, i, 0:1], rr_1[:, i:i + 1], ALU.subtract, ALU.mult)
                last.then_inc(L2x_vector_done, 1)
                for i in range(2):
                    last = dve.tensor_scalar(qk_1[:, 4 + i, :], ps1[:, 2, 128 * i:128 * i + 128], mv_1[:, 4 + i, 0:1], rr_1[:, 4 + i:5 + i], ALU.subtract, ALU.mult)
                last.then_inc(L2x_vector_done, 1)
                dve.wait_ge(L2x_matmul_done, 124*b + 69)
                for i in range(4):
                    dve.bn_stats(s6_0[:, i, :], ps0[:, 1, 128 * i:128 * i + 128])
                dve.wait_ge(L2x_matmul_done, 124*b + 73)
                dve.tensor_reduce(st0[:, 16:20], ps0[:, 2, :].rearrange("p (h s) -> p h s", h=4), AX.X, ALU.max).then_inc(L2x_vector_done, 1)
                dve.wait_ge(L2x_vector_done, 226*b + 319)
                dve.tensor_scalar(st0[:, 16:20], st0[:, 16:20], -0.08838834764831845, None, ALU.mult).then_inc(L2x_vector_done, 1)
                dve.wait_ge(L2x_matmul_done, 124*b + 74)
                dve.tensor_reduce(st1[:, 16:20], ps1[:, 2, :].rearrange("p (h s) -> p h s", h=4), AX.X, ALU.max).then_inc(L2x_vector_done, 1)
                dve.wait_ge(L2x_vector_done, 226*b + 321)
                dve.tensor_scalar(st1[:, 16:20], st1[:, 16:20], -0.08838834764831845, None, ALU.mult).then_inc(L2x_vector_done, 1)
                dve.wait_ge(L2x_scalar_done, 108*b + 163)
                dve.reciprocal(st0[:, 16:20], st0[:, 20:24]).then_inc(L2x_vector_done, 1)
                dve.wait_ge(L2x_scalar_done, 108*b + 164)
                dve.reciprocal(st1[:, 16:20], st1[:, 20:24]).then_inc(L2x_vector_done, 1)
                dve.wait_ge(L2x_matmul_done, 124*b + 76)
                for i in range(4):
                    dve.bn_stats(s6_1[:, i, :], ps1[:, 1, 128 * i:128 * i + 128])
                dve.wait_ge(L2x_matmul_done, 124*b + 79)
                dve.tensor_tensor(P2_0[:, :, :], ps0[:, 3, :].rearrange('p (h t) -> p h t', h=4), smr[:, 12:16].unsqueeze(2).to_broadcast([128, 4, 128]), ALU.mult).then_inc(L2x_vector_done, 1)
                dve.wait_ge(L2x_vector_done, 226*b + 325)
                dve.tensor_scalar(y16_0[:, 0:512], P2f_0[:, :], 448.0, -448.0, ALU.min, ALU.max).then_inc(L2x_vector_done, 1)
                dve.wait_ge(L2x_matmul_done, 124*b + 80)
                for i in range(2):
                    last = dve.bn_stats(s6_0[:, 4 + i, :], ps0[:, 2, 128 * i:128 * i + 128])
                last.then_inc(L2x_vector_done, 1)
                dve.wait_ge(L2x_vector_done, 226*b + 326)
                dve.tensor_scalar(e16_0[:, 0:512], y16u_0[:, 0:512], 0x7F80, None, ALU.bitwise_and)
                dve.wait_ge(L2x_vector_done, 226*b + 327)
                dve.sem_inc(dve_waited, 1)
                for i in range(6):
                    last = dve.bn_aggr(mv_0[:, i, :], s6_0[:, i, :])
                last.then_inc(L2x_vector_done, 1)
                dve.wait_ge(L2x_matmul_done, 124*b + 81)
                dve.tensor_tensor(P2_1[:, :, :], ps1[:, 3, :].rearrange('p (h t) -> p h t', h=4), smr[:, 12:16].unsqueeze(2).to_broadcast([128, 4, 128]), ALU.mult).then_inc(L2x_vector_done, 1)
                dve.wait_ge(L2x_vector_done, 226*b + 328)
                dve.tensor_tensor(vv_0[:, :], mv_0[:, :, 1], ssq[:, 1, :], ALU.mult).then_inc(L2x_vector_done, 1)
                dve.wait_ge(L2x_matmul_done, 124*b + 82)
                for i in range(2):
                    last = dve.bn_stats(s6_1[:, 4 + i, :], ps1[:, 2, 128 * i:128 * i + 128])
                last.then_inc(L2x_vector_done, 1)
                dve.wait_ge(L2x_vector_done, 226*b + 329)
                dve.tensor_scalar(y16_1[:, 0:512], P2f_1[:, :], 448.0, -448.0, ALU.min, ALU.max).then_inc(L2x_vector_done, 1)
                dve.wait_ge(L2x_vector_done, 226*b + 331)
                dve.sem_inc(dve_waited, 1)
                for i in range(6):
                    last = dve.bn_aggr(mv_1[:, i, :], s6_1[:, i, :])
                last.then_inc(L2x_vector_done, 1)
                dve.wait_ge(L2x_vector_done, 226*b + 332)
                dve.tensor_scalar(e16_1[:, 0:512], y16u_1[:, 0:512], 0x7F80, None, ALU.bitwise_and).then_inc(L2x_vector_done, 1)
                dve.wait_ge(L2x_vector_done, 226*b + 333)
                dve.tensor_tensor(vv_1[:, :], mv_1[:, :, 1], ssq[:, 1, :], ALU.mult).then_inc(L2x_vector_done, 1)
                dve.tensor_scalar(PT2_0[:, :], e16b_0[:, 0:512], 2.0 ** -6, 1.5 * 2.0 ** 20, ALU.max, ALU.mult).then_inc(L2x_vector_done, 1)
                dve.wait_ge(L2x_vector_done, 226*b + 334)
                dve.tensor_scalar(PT2_1[:, :], e16b_1[:, 0:512], 2.0 ** -6, 1.5 * 2.0 ** 20, ALU.max, ALU.mult).then_inc(L2x_vector_done, 1)
                dve.wait_ge(L2x_scalar_done, 108*b + 168)
                dve.tensor_tensor(rr_0[:, :], rr_0[:, :], srow[:, 1, :], ALU.mult).then_inc(L2x_vector_done, 1)
                dve.wait_ge(L2x_vector_done, 226*b + 338)
                for i in range(4):
                    last = dve.tensor_scalar(qk_0[:, i, :], ps0[:, 1, 128 * i:128 * i + 128], mv_0[:, i, 0:1], rr_0[:, i:i + 1], ALU.subtract, ALU.mult)
                last.then_inc(L2x_vector_done, 1)
                dve.wait_ge(L2x_scalar_done, 108*b + 170)
                dve.tensor_tensor(rr_1[:, :], rr_1[:, :], srow[:, 1, :], ALU.mult).then_inc(L2x_vector_done, 1)
                for i in range(2):
                    last = dve.tensor_scalar(qk_0[:, 4 + i, :], ps0[:, 2, 128 * i:128 * i + 128], mv_0[:, 4 + i, 0:1], rr_0[:, 4 + i:5 + i], ALU.subtract, ALU.mult)
                last.then_inc(L2x_vector_done, 1)
                dve.wait_ge(L2x_vector_done, 226*b + 340)
                for i in range(4):
                    last = dve.tensor_scalar(qk_1[:, i, :], ps1[:, 1, 128 * i:128 * i + 128], mv_1[:, i, 0:1], rr_1[:, i:i + 1], ALU.subtract, ALU.mult)
                last.then_inc(L2x_vector_done, 1)
                for i in range(2):
                    last = dve.tensor_scalar(qk_1[:, 4 + i, :], ps1[:, 2, 128 * i:128 * i + 128], mv_1[:, 4 + i, 0:1], rr_1[:, 4 + i:5 + i], ALU.subtract, ALU.mult)
                last.then_inc(L2x_vector_done, 1)
                dve.wait_ge(L2x_matmul_done, 124*b + 84)
                for i in range(4):
                    dve.bn_stats(s6_0[:, i, :], ps0[:, 1, 128 * i:128 * i + 128])
                dve.wait_ge(L2x_matmul_done, 124*b + 88)
                dve.tensor_reduce(st0[:, 16:20], ps0[:, 2, :].rearrange("p (h s) -> p h s", h=4), AX.X, ALU.max).then_inc(L2x_vector_done, 1)
                dve.wait_ge(L2x_vector_done, 226*b + 344)
                dve.tensor_scalar(st0[:, 16:20], st0[:, 16:20], -0.08838834764831845, None, ALU.mult).then_inc(L2x_vector_done, 1)
                dve.wait_ge(L2x_matmul_done, 124*b + 89)
                dve.tensor_reduce(st1[:, 16:20], ps1[:, 2, :].rearrange("p (h s) -> p h s", h=4), AX.X, ALU.max).then_inc(L2x_vector_done, 1)
                dve.wait_ge(L2x_vector_done, 226*b + 346)
                dve.tensor_scalar(st1[:, 16:20], st1[:, 16:20], -0.08838834764831845, None, ALU.mult).then_inc(L2x_vector_done, 1)
                dve.wait_ge(L2x_scalar_done, 108*b + 175)
                dve.reciprocal(st0[:, 16:20], st0[:, 20:24]).then_inc(L2x_vector_done, 1)
                dve.wait_ge(L2x_scalar_done, 108*b + 176)
                dve.reciprocal(st1[:, 16:20], st1[:, 20:24]).then_inc(L2x_vector_done, 1)
                dve.wait_ge(L2x_matmul_done, 124*b + 91)
                for i in range(4):
                    dve.bn_stats(s6_1[:, i, :], ps1[:, 1, 128 * i:128 * i + 128])
                dve.wait_ge(L2x_matmul_done, 124*b + 94)
                dve.tensor_tensor(P2_0[:, :, :], ps0[:, 3, :].rearrange('p (h t) -> p h t', h=4), smr[:, 16:20].unsqueeze(2).to_broadcast([128, 4, 128]), ALU.mult).then_inc(L2x_vector_done, 1)
                dve.wait_ge(L2x_vector_done, 226*b + 350)
                dve.tensor_scalar(y16_0[:, 0:512], P2f_0[:, :], 448.0, -448.0, ALU.min, ALU.max).then_inc(L2x_vector_done, 1)
                dve.wait_ge(L2x_matmul_done, 124*b + 95)
                for i in range(2):
                    last = dve.bn_stats(s6_0[:, 4 + i, :], ps0[:, 2, 128 * i:128 * i + 128])
                last.then_inc(L2x_vector_done, 1)
                dve.wait_ge(L2x_vector_done, 226*b + 351)
                dve.tensor_scalar(e16_0[:, 0:512], y16u_0[:, 0:512], 0x7F80, None, ALU.bitwise_and)
                dve.wait_ge(L2x_vector_done, 226*b + 352)
                dve.sem_inc(dve_waited, 1)
                for i in range(6):
                    last = dve.bn_aggr(mv_0[:, i, :], s6_0[:, i, :])
                last.then_inc(L2x_vector_done, 1)
                dve.wait_ge(L2x_matmul_done, 124*b + 96)
                dve.tensor_tensor(P2_1[:, :, :], ps1[:, 3, :].rearrange('p (h t) -> p h t', h=4), smr[:, 16:20].unsqueeze(2).to_broadcast([128, 4, 128]), ALU.mult).then_inc(L2x_vector_done, 1)
                dve.wait_ge(L2x_vector_done, 226*b + 353)
                dve.tensor_tensor(vv_0[:, :], mv_0[:, :, 1], ssq[:, 1, :], ALU.mult).then_inc(L2x_vector_done, 1)
                dve.wait_ge(L2x_matmul_done, 124*b + 97)
                for i in range(2):
                    last = dve.bn_stats(s6_1[:, 4 + i, :], ps1[:, 2, 128 * i:128 * i + 128])
                last.then_inc(L2x_vector_done, 1)
                dve.wait_ge(L2x_vector_done, 226*b + 354)
                dve.tensor_scalar(y16_1[:, 0:512], P2f_1[:, :], 448.0, -448.0, ALU.min, ALU.max).then_inc(L2x_vector_done, 1)
                dve.wait_ge(L2x_vector_done, 226*b + 356)
                dve.sem_inc(dve_waited, 1)
                for i in range(6):
                    last = dve.bn_aggr(mv_1[:, i, :], s6_1[:, i, :])
                last.then_inc(L2x_vector_done, 1)
                dve.wait_ge(L2x_vector_done, 226*b + 357)
                dve.tensor_scalar(e16_1[:, 0:512], y16u_1[:, 0:512], 0x7F80, None, ALU.bitwise_and).then_inc(L2x_vector_done, 1)
                dve.wait_ge(L2x_vector_done, 226*b + 358)
                dve.tensor_tensor(vv_1[:, :], mv_1[:, :, 1], ssq[:, 1, :], ALU.mult).then_inc(L2x_vector_done, 1)
                dve.tensor_scalar(PT2_0[:, :], e16b_0[:, 0:512], 2.0 ** -6, 1.5 * 2.0 ** 20, ALU.max, ALU.mult).then_inc(L2x_vector_done, 1)
                dve.wait_ge(L2x_vector_done, 226*b + 359)
                dve.tensor_scalar(PT2_1[:, :], e16b_1[:, 0:512], 2.0 ** -6, 1.5 * 2.0 ** 20, ALU.max, ALU.mult).then_inc(L2x_vector_done, 1)
                dve.wait_ge(L2x_scalar_done, 108*b + 180)
                dve.tensor_tensor(rr_0[:, :], rr_0[:, :], srow[:, 1, :], ALU.mult).then_inc(L2x_vector_done, 1)
                dve.wait_ge(L2x_vector_done, 226*b + 363)
                for i in range(4):
                    last = dve.tensor_scalar(qk_0[:, i, :], ps0[:, 1, 128 * i:128 * i + 128], mv_0[:, i, 0:1], rr_0[:, i:i + 1], ALU.subtract, ALU.mult)
                last.then_inc(L2x_vector_done, 1)
                dve.wait_ge(L2x_scalar_done, 108*b + 182)
                dve.tensor_tensor(rr_1[:, :], rr_1[:, :], srow[:, 1, :], ALU.mult).then_inc(L2x_vector_done, 1)
                for i in range(2):
                    last = dve.tensor_scalar(qk_0[:, 4 + i, :], ps0[:, 2, 128 * i:128 * i + 128], mv_0[:, 4 + i, 0:1], rr_0[:, 4 + i:5 + i], ALU.subtract, ALU.mult)
                last.then_inc(L2x_vector_done, 1)
                dve.wait_ge(L2x_vector_done, 226*b + 365)
                for i in range(4):
                    last = dve.tensor_scalar(qk_1[:, i, :], ps1[:, 1, 128 * i:128 * i + 128], mv_1[:, i, 0:1], rr_1[:, i:i + 1], ALU.subtract, ALU.mult)
                last.then_inc(L2x_vector_done, 1)
                for i in range(2):
                    last = dve.tensor_scalar(qk_1[:, 4 + i, :], ps1[:, 2, 128 * i:128 * i + 128], mv_1[:, 4 + i, 0:1], rr_1[:, 4 + i:5 + i], ALU.subtract, ALU.mult)
                last.then_inc(L2x_vector_done, 1)
                dve.wait_ge(L2x_matmul_done, 124*b + 99)
                for i in range(4):
                    dve.bn_stats(s6_0[:, i, :], ps0[:, 1, 128 * i:128 * i + 128])
                dve.wait_ge(L2x_matmul_done, 124*b + 103)
                dve.tensor_reduce(st0[:, 16:20], ps0[:, 2, :].rearrange("p (h s) -> p h s", h=4), AX.X, ALU.max).then_inc(L2x_vector_done, 1)
                dve.wait_ge(L2x_vector_done, 226*b + 369)
                dve.tensor_scalar(st0[:, 16:20], st0[:, 16:20], -0.08838834764831845, None, ALU.mult).then_inc(L2x_vector_done, 1)
                dve.wait_ge(L2x_matmul_done, 124*b + 104)
                dve.tensor_reduce(st1[:, 16:20], ps1[:, 2, :].rearrange("p (h s) -> p h s", h=4), AX.X, ALU.max).then_inc(L2x_vector_done, 1)
                dve.wait_ge(L2x_vector_done, 226*b + 371)
                dve.tensor_scalar(st1[:, 16:20], st1[:, 16:20], -0.08838834764831845, None, ALU.mult).then_inc(L2x_vector_done, 1)
                dve.wait_ge(L2x_scalar_done, 108*b + 187)
                dve.reciprocal(st0[:, 16:20], st0[:, 20:24]).then_inc(L2x_vector_done, 1)
                dve.wait_ge(L2x_scalar_done, 108*b + 188)
                dve.reciprocal(st1[:, 16:20], st1[:, 20:24]).then_inc(L2x_vector_done, 1)
                dve.wait_ge(L2x_matmul_done, 124*b + 106)
                for i in range(4):
                    dve.bn_stats(s6_1[:, i, :], ps1[:, 1, 128 * i:128 * i + 128])
                dve.wait_ge(L2x_matmul_done, 124*b + 109)
                dve.tensor_tensor(P2_0[:, :, :], ps0[:, 3, :].rearrange('p (h t) -> p h t', h=4), smr[:, 20:24].unsqueeze(2).to_broadcast([128, 4, 128]), ALU.mult).then_inc(L2x_vector_done, 1)
                dve.wait_ge(L2x_vector_done, 226*b + 375)
                dve.tensor_scalar(y16_0[:, 0:512], P2f_0[:, :], 448.0, -448.0, ALU.min, ALU.max).then_inc(L2x_vector_done, 1)
                dve.wait_ge(L2x_matmul_done, 124*b + 110)
                for i in range(2):
                    last = dve.bn_stats(s6_0[:, 4 + i, :], ps0[:, 2, 128 * i:128 * i + 128])
                last.then_inc(L2x_vector_done, 1)
                dve.wait_ge(L2x_vector_done, 226*b + 376)
                dve.tensor_scalar(e16_0[:, 0:512], y16u_0[:, 0:512], 0x7F80, None, ALU.bitwise_and)
                dve.wait_ge(L2x_vector_done, 226*b + 377)
                dve.sem_inc(dve_waited, 1)
                for i in range(6):
                    last = dve.bn_aggr(mv_0[:, i, :], s6_0[:, i, :])
                last.then_inc(L2x_vector_done, 1)
                dve.wait_ge(L2x_matmul_done, 124*b + 111)
                dve.tensor_tensor(P2_1[:, :, :], ps1[:, 3, :].rearrange('p (h t) -> p h t', h=4), smr[:, 20:24].unsqueeze(2).to_broadcast([128, 4, 128]), ALU.mult).then_inc(L2x_vector_done, 1)
                dve.wait_ge(L2x_vector_done, 226*b + 378)
                dve.tensor_tensor(vv_0[:, :], mv_0[:, :, 1], ssq[:, 1, :], ALU.mult).then_inc(L2x_vector_done, 1)
                dve.wait_ge(L2x_matmul_done, 124*b + 112)
                for i in range(2):
                    last = dve.bn_stats(s6_1[:, 4 + i, :], ps1[:, 2, 128 * i:128 * i + 128])
                last.then_inc(L2x_vector_done, 1)
                dve.wait_ge(L2x_vector_done, 226*b + 379)
                dve.tensor_scalar(y16_1[:, 0:512], P2f_1[:, :], 448.0, -448.0, ALU.min, ALU.max).then_inc(L2x_vector_done, 1)
                dve.wait_ge(L2x_vector_done, 226*b + 381)
                dve.sem_inc(dve_waited, 1)
                for i in range(6):
                    last = dve.bn_aggr(mv_1[:, i, :], s6_1[:, i, :])
                last.then_inc(L2x_vector_done, 1)
                dve.wait_ge(L2x_vector_done, 226*b + 382)
                dve.tensor_scalar(e16_1[:, 0:512], y16u_1[:, 0:512], 0x7F80, None, ALU.bitwise_and).then_inc(L2x_vector_done, 1)
                dve.wait_ge(L2x_vector_done, 226*b + 383)
                dve.tensor_tensor(vv_1[:, :], mv_1[:, :, 1], ssq[:, 1, :], ALU.mult).then_inc(L2x_vector_done, 1)
                dve.tensor_scalar(PT2_0[:, :], e16b_0[:, 0:512], 2.0 ** -6, 1.5 * 2.0 ** 20, ALU.max, ALU.mult).then_inc(L2x_vector_done, 1)
                dve.wait_ge(L2x_vector_done, 226*b + 384)
                dve.tensor_scalar(PT2_1[:, :], e16b_1[:, 0:512], 2.0 ** -6, 1.5 * 2.0 ** 20, ALU.max, ALU.mult).then_inc(L2x_vector_done, 1)
                dve.wait_ge(L2x_scalar_done, 108*b + 192)
                dve.tensor_tensor(rr_0[:, :], rr_0[:, :], srow[:, 1, :], ALU.mult).then_inc(L2x_vector_done, 1)
                dve.wait_ge(L2x_vector_done, 226*b + 388)
                for i in range(4):
                    last = dve.tensor_scalar(qk_0[:, i, :], ps0[:, 1, 128 * i:128 * i + 128], mv_0[:, i, 0:1], rr_0[:, i:i + 1], ALU.subtract, ALU.mult)
                last.then_inc(L2x_vector_done, 1)
                dve.wait_ge(L2x_scalar_done, 108*b + 194)
                dve.tensor_tensor(rr_1[:, :], rr_1[:, :], srow[:, 1, :], ALU.mult).then_inc(L2x_vector_done, 1)
                for i in range(2):
                    last = dve.tensor_scalar(qk_0[:, 4 + i, :], ps0[:, 2, 128 * i:128 * i + 128], mv_0[:, 4 + i, 0:1], rr_0[:, 4 + i:5 + i], ALU.subtract, ALU.mult)
                last.then_inc(L2x_vector_done, 1)
                dve.wait_ge(L2x_vector_done, 226*b + 390)
                for i in range(4):
                    last = dve.tensor_scalar(qk_1[:, i, :], ps1[:, 1, 128 * i:128 * i + 128], mv_1[:, i, 0:1], rr_1[:, i:i + 1], ALU.subtract, ALU.mult)
                last.then_inc(L2x_vector_done, 1)
                for i in range(2):
                    last = dve.tensor_scalar(qk_1[:, 4 + i, :], ps1[:, 2, 128 * i:128 * i + 128], mv_1[:, 4 + i, 0:1], rr_1[:, 4 + i:5 + i], ALU.subtract, ALU.mult)
                last.then_inc(L2x_vector_done, 1)
                dve.wait_ge(L2x_matmul_done, 124*b + 114)
                for i in range(4):
                    dve.bn_stats(s6_0[:, i, :], ps0[:, 1, 128 * i:128 * i + 128])
                dve.wait_ge(L2x_matmul_done, 124*b + 118)
                dve.tensor_reduce(st0[:, 16:20], ps0[:, 2, :].rearrange("p (h s) -> p h s", h=4), AX.X, ALU.max).then_inc(L2x_vector_done, 1)
                dve.wait_ge(L2x_vector_done, 226*b + 394)
                dve.tensor_scalar(st0[:, 16:20], st0[:, 16:20], -0.08838834764831845, None, ALU.mult).then_inc(L2x_vector_done, 1)
                dve.wait_ge(L2x_matmul_done, 124*b + 119)
                dve.tensor_reduce(st1[:, 16:20], ps1[:, 2, :].rearrange("p (h s) -> p h s", h=4), AX.X, ALU.max).then_inc(L2x_vector_done, 1)
                dve.wait_ge(L2x_vector_done, 226*b + 396)
                dve.tensor_scalar(st1[:, 16:20], st1[:, 16:20], -0.08838834764831845, None, ALU.mult).then_inc(L2x_vector_done, 1)
                dve.wait_ge(L2x_scalar_done, 108*b + 199)
                dve.reciprocal(st0[:, 16:20], st0[:, 20:24]).then_inc(L2x_vector_done, 1)
                dve.wait_ge(L2x_scalar_done, 108*b + 200)
                dve.reciprocal(st1[:, 16:20], st1[:, 20:24]).then_inc(L2x_vector_done, 1)
                dve.wait_ge(L2x_matmul_done, 124*b + 121)
                for i in range(4):
                    dve.bn_stats(s6_1[:, i, :], ps1[:, 1, 128 * i:128 * i + 128])
                dve.wait_ge(L2x_matmul_done, 124*b + 124)
                dve.tensor_tensor(P2_0[:, :, :], ps0[:, 3, :].rearrange('p (h t) -> p h t', h=4), smr[:, 24:28].unsqueeze(2).to_broadcast([128, 4, 128]), ALU.mult).then_inc(L2x_vector_done, 1)
                dve.wait_ge(L2x_vector_done, 226*b + 400)
                dve.tensor_scalar(y16_0[:, 0:512], P2f_0[:, :], 448.0, -448.0, ALU.min, ALU.max).then_inc(L2x_vector_done, 1)
                dve.wait_ge(L2x_matmul_done, 124*b + 125)
                for i in range(2):
                    last = dve.bn_stats(s6_0[:, 4 + i, :], ps0[:, 2, 128 * i:128 * i + 128])
                last.then_inc(L2x_vector_done, 1)
                dve.wait_ge(L2x_vector_done, 226*b + 401)
                dve.tensor_scalar(e16_0[:, 0:512], y16u_0[:, 0:512], 0x7F80, None, ALU.bitwise_and)
                dve.wait_ge(L2x_vector_done, 226*b + 402)
                dve.sem_inc(dve_waited, 1)
                for i in range(6):
                    last = dve.bn_aggr(mv_0[:, i, :], s6_0[:, i, :])
                last.then_inc(L2x_vector_done, 1)
                dve.wait_ge(L2x_matmul_done, 124*b + 126)
                dve.tensor_tensor(P2_1[:, :, :], ps1[:, 3, :].rearrange('p (h t) -> p h t', h=4), smr[:, 24:28].unsqueeze(2).to_broadcast([128, 4, 128]), ALU.mult).then_inc(L2x_vector_done, 1)
                dve.wait_ge(L2x_vector_done, 226*b + 403)
                dve.tensor_tensor(vv_0[:, :], mv_0[:, :, 1], ssq[:, 1, :], ALU.mult).then_inc(L2x_vector_done, 1)
                dve.wait_ge(L2x_matmul_done, 124*b + 127)
                for i in range(2):
                    last = dve.bn_stats(s6_1[:, 4 + i, :], ps1[:, 2, 128 * i:128 * i + 128])
                last.then_inc(L2x_vector_done, 1)
                dve.wait_ge(L2x_vector_done, 226*b + 404)
                dve.tensor_scalar(y16_1[:, 0:512], P2f_1[:, :], 448.0, -448.0, ALU.min, ALU.max).then_inc(L2x_vector_done, 1)
                dve.wait_ge(L2x_vector_done, 226*b + 406)
                dve.sem_inc(dve_waited, 1)
                for i in range(6):
                    last = dve.bn_aggr(mv_1[:, i, :], s6_1[:, i, :])
                last.then_inc(L2x_vector_done, 1)
                dve.wait_ge(L2x_vector_done, 226*b + 407)
                dve.tensor_scalar(e16_1[:, 0:512], y16u_1[:, 0:512], 0x7F80, None, ALU.bitwise_and).then_inc(L2x_vector_done, 1)
                dve.wait_ge(L2x_vector_done, 226*b + 408)
                dve.tensor_tensor(vv_1[:, :], mv_1[:, :, 1], ssq[:, 1, :], ALU.mult).then_inc(L2x_vector_done, 1)
                dve.tensor_scalar(PT2_0[:, :], e16b_0[:, 0:512], 2.0 ** -6, 1.5 * 2.0 ** 20, ALU.max, ALU.mult).then_inc(L2x_vector_done, 1)
                dve.wait_ge(L2x_vector_done, 226*b + 409)
                dve.tensor_scalar(PT2_1[:, :], e16b_1[:, 0:512], 2.0 ** -6, 1.5 * 2.0 ** 20, ALU.max, ALU.mult).then_inc(L2x_vector_done, 1)
                dve.wait_ge(L2x_scalar_done, 108*b + 204)
                dve.tensor_tensor(rr_0[:, :], rr_0[:, :], srow[:, 1, :], ALU.mult).then_inc(L2x_vector_done, 1)
                dve.wait_ge(L2x_vector_done, 226*b + 413)
                for i in range(4):
                    last = dve.tensor_scalar(qk_0[:, i, :], ps0[:, 1, 128 * i:128 * i + 128], mv_0[:, i, 0:1], rr_0[:, i:i + 1], ALU.subtract, ALU.mult)
                last.then_inc(L2x_vector_done, 1)
                dve.wait_ge(L2x_scalar_done, 108*b + 206)
                dve.tensor_tensor(rr_1[:, :], rr_1[:, :], srow[:, 1, :], ALU.mult).then_inc(L2x_vector_done, 1)
                for i in range(2):
                    last = dve.tensor_scalar(qk_0[:, 4 + i, :], ps0[:, 2, 128 * i:128 * i + 128], mv_0[:, 4 + i, 0:1], rr_0[:, 4 + i:5 + i], ALU.subtract, ALU.mult)
                last.then_inc(L2x_vector_done, 1)
                dve.wait_ge(L2x_vector_done, 226*b + 415)
                for i in range(4):
                    last = dve.tensor_scalar(qk_1[:, i, :], ps1[:, 1, 128 * i:128 * i + 128], mv_1[:, i, 0:1], rr_1[:, i:i + 1], ALU.subtract, ALU.mult)
                last.then_inc(L2x_vector_done, 1)
                for i in range(2):
                    last = dve.tensor_scalar(qk_1[:, 4 + i, :], ps1[:, 2, 128 * i:128 * i + 128], mv_1[:, 4 + i, 0:1], rr_1[:, 4 + i:5 + i], ALU.subtract, ALU.mult)
                last.then_inc(L2x_vector_done, 1)
                dve.wait_ge(L2x_matmul_done, 124*b + 132)
                dve.tensor_reduce(st0[:, 16:20], ps0[:, 2, :].rearrange("p (h s) -> p h s", h=4), AX.X, ALU.max).then_inc(L2x_vector_done, 1)
                dve.wait_ge(L2x_vector_done, 226*b + 419)
                dve.tensor_scalar(st0[:, 16:20], st0[:, 16:20], -0.08838834764831845, None, ALU.mult).then_inc(L2x_vector_done, 1)
                dve.wait_ge(L2x_matmul_done, 124*b + 133)
                dve.tensor_reduce(st1[:, 16:20], ps1[:, 2, :].rearrange("p (h s) -> p h s", h=4), AX.X, ALU.max).then_inc(L2x_vector_done, 1)
                dve.wait_ge(L2x_vector_done, 226*b + 421)
                dve.tensor_scalar(st1[:, 16:20], st1[:, 16:20], -0.08838834764831845, None, ALU.mult).then_inc(L2x_vector_done, 1)
                dve.wait_ge(L2x_scalar_done, 108*b + 211)
                dve.reciprocal(st0[:, 16:20], st0[:, 20:24]).then_inc(L2x_vector_done, 1)
                dve.wait_ge(L2x_scalar_done, 108*b + 212)
                dve.reciprocal(st1[:, 16:20], st1[:, 20:24]).then_inc(L2x_vector_done, 1)
                dve.wait_ge(L2x_matmul_done, 124*b + 136)
                dve.tensor_tensor(P2_0[:, :, :], ps0[:, 3, :].rearrange('p (h t) -> p h t', h=4), smr[:, 28:32].unsqueeze(2).to_broadcast([128, 4, 128]), ALU.mult).then_inc(L2x_vector_done, 1)
                dve.wait_ge(L2x_vector_done, 226*b + 425)
                dve.tensor_scalar(y16_0[:, 0:512], P2f_0[:, :], 448.0, -448.0, ALU.min, ALU.max).then_inc(L2x_vector_done, 1)
                dve.wait_ge(L2x_vector_done, 226*b + 426)
                dve.tensor_scalar(e16_0[:, 0:512], y16u_0[:, 0:512], 0x7F80, None, ALU.bitwise_and).then_inc(L2x_vector_done, 1)
                dve.wait_ge(L2x_vector_done, 226*b + 427)
                dve.tensor_scalar(PT2_0[:, :], e16b_0[:, 0:512], 2.0 ** -6, 1.5 * 2.0 ** 20, ALU.max, ALU.mult).then_inc(L2x_vector_done, 1)
                dve.wait_ge(L2x_matmul_done, 124*b + 138)
                dve.tensor_tensor(P2_1[:, :, :], ps1[:, 3, :].rearrange('p (h t) -> p h t', h=4), smr[:, 28:32].unsqueeze(2).to_broadcast([128, 4, 128]), ALU.mult).then_inc(L2x_vector_done, 1)
                dve.wait_ge(L2x_vector_done, 226*b + 429)
                dve.tensor_scalar(y16_1[:, 0:512], P2f_1[:, :], 448.0, -448.0, ALU.min, ALU.max).then_inc(L2x_vector_done, 1)
                dve.wait_ge(L2x_vector_done, 226*b + 430)
                dve.tensor_scalar(e16_1[:, 0:512], y16u_1[:, 0:512], 0x7F80, None, ALU.bitwise_and).then_inc(L2x_vector_done, 1)
                dve.wait_ge(L2x_vector_done, 226*b + 431)
                dve.tensor_scalar(PT2_1[:, :], e16b_1[:, 0:512], 2.0 ** -6, 1.5 * 2.0 ** 20, ALU.max, ALU.mult).then_inc(L2x_vector_done, 1)
                dve.wait_ge(L2x_matmul_done, 124*b + 139)
                dve.scalar_tensor_tensor(x[:, 2*b+0, :], ps0[:, 0, 0:256], wps[:, 0:1], x[:, 2*b+0, :], ALU.mult, ALU.add).then_inc(L2x_vector_done, 1)
                dve.wait_ge(L2x_matmul_done, 124*b + 140)
                dve.scalar_tensor_tensor(x[:, 2*b+1, :], ps1[:, 0, 0:256], wps[:, 0:1], x[:, 2*b+1, :], ALU.mult, ALU.add).then_inc(L2x_vector_done, 1)
                dve.wait_ge(L2x_scalar_done, 108*b + 215)
                dve.tensor_tensor(xs_0[:, :, :, :], unT0[:, :, :].unsqueeze(1).to_broadcast([128, 4, 2, 128]), inrc[:, :, :].unsqueeze(3).to_broadcast([128, 4, 2, 128]), ALU.mult).then_inc(L2x_vector_done, 1)
                dve.wait_ge(L2x_scalar_done, 108*b + 216)
                dve.tensor_tensor(xs_1[:, :, :, :], unT1[:, :, :].unsqueeze(1).to_broadcast([128, 4, 2, 128]), inrc[:, :, :].unsqueeze(3).to_broadcast([128, 4, 2, 128]), ALU.mult).then_inc(L2x_vector_done, 1)
                dve.wait_ge(L2x_vector_done, 226*b + 435)
                dve.tensor_scalar(y16_0[:, :], xsf_0[:, :], 448.0, -448.0, ALU.min, ALU.max).then_inc(L2x_vector_done, 1)
                dve.wait_ge(L2x_vector_done, 226*b + 436)
                dve.tensor_scalar(y16_1[:, :], xsf_1[:, :], 448.0, -448.0, ALU.min, ALU.max).then_inc(L2x_vector_done, 1)
                dve.wait_ge(L2x_vector_done, 226*b + 437)
                dve.tensor_scalar(e16_0[:, 0:1024], y16u_0[:, 0:1024], 0x7F80, None, ALU.bitwise_and).then_inc(L2x_vector_done, 1)
                dve.wait_ge(L2x_vector_done, 226*b + 438)
                dve.tensor_scalar(e16_1[:, 0:1024], y16u_1[:, 0:1024], 0x7F80, None, ALU.bitwise_and).then_inc(L2x_vector_done, 1)
                dve.wait_ge(L2x_vector_done, 226*b + 439)
                dve.tensor_scalar(qq_0[:, :], e16b_0[:, 0:1024], 2.0 ** -6, 1.5 * 2.0 ** 20, ALU.max, ALU.mult).then_inc(L2x_vector_done, 1)
                dve.wait_ge(L2x_vector_done, 226*b + 440)
                dve.tensor_scalar(qq_1[:, :], e16b_1[:, 0:1024], 2.0 ** -6, 1.5 * 2.0 ** 20, ALU.max, ALU.mult).then_inc(L2x_vector_done, 1)
                dve.wait_ge(L2x_pool_done, 52*b + 55)
                dve.tensor_tensor(xs_0[:, :, :, :], xs_0[:, :, :, :], insc[:, :, :].unsqueeze(3).to_broadcast([128, 4, 2, 128]), ALU.mult).then_inc(L2x_vector_done, 1)
                dve.wait_ge(L2x_pool_done, 52*b + 56)
                dve.tensor_tensor(xs_1[:, :, :, :], xs_1[:, :, :, :], insc[:, :, :].unsqueeze(3).to_broadcast([128, 4, 2, 128]), ALU.mult).then_inc(L2x_vector_done, 1)

            dve.sem_inc(L2f_vector_done, 45)
            dve.wait_ge(L2x_vector_done, 1112)
            dve.bn_stats(st0[:, 0:6], x[:, 0, :]).then_inc(L2f_vector_done, 1)
            dve.bn_stats(st1[:, 0:6], x[:, 1, :]).then_inc(L2f_vector_done, 1)
            dve.wait_ge(L2x_scalar_done, 439)
            dve.wait_ge(L2f_vector_done, 46)
            dve.bn_aggr(st0[:, 6:8], st0[:, 0:6]).then_inc(L2f_vector_done, 1)
            dve.wait_ge(L2x_scalar_done, 440)
            dve.wait_ge(L2f_vector_done, 47)
            dve.bn_aggr(st1[:, 6:8], st1[:, 0:6]).then_inc(L2f_vector_done, 1)
            dve.wait_ge(L2f_scalar_done, 35)
            dve.tensor_scalar(u0[:, :], x[:, 0, :], st0[:, 6:7], st0[:, 9:10], ALU.subtract, ALU.mult).then_inc(L2f_vector_done, 1)
            dve.wait_ge(L2f_scalar_done, 36)
            dve.tensor_scalar(u1[:, :], x[:, 1, :], st1[:, 6:7], st1[:, 9:10], ALU.subtract, ALU.mult).then_inc(L2f_vector_done, 1)
            dve.wait_ge(L2f_w_loaded, 128)
            dve.wait_ge(L2x_pool_done, 212)
            dve.wait_ge(L2f_matmul_done, 2)
            with dve.Fori(0, 4) as b:
                dve.wait_ge(L2f_vector_done, 53*b + 1)
                dve.sem_inc(dve_waited, 1)
                dve.bn_stats(st0[:, 0:6], x_next[:, 2*b+0, :]).then_inc(L2f_vector_done, 1)
                dve.wait_ge(L2f_vector_done, 53*b + 2)
                dve.sem_inc(dve_waited, 1)
                dve.bn_stats(st1[:, 0:6], x_next[:, 2*b+1, :]).then_inc(L2f_vector_done, 1)
                dve.wait_ge(L2f_vector_done, 53*b + 52)
                dve.wait_ge(L2f_scalar_done, 37*b + 1)
                dve.sem_inc(dve_waited, 1)
                dve.bn_aggr(st0[:, 6:8], st0[:, 0:6]).then_inc(L2f_vector_done, 1)
                dve.wait_ge(L2f_vector_done, 53*b + 53)
                dve.wait_ge(L2f_scalar_done, 37*b + 2)
                dve.sem_inc(dve_waited, 1)
                dve.bn_aggr(st1[:, 6:8], st1[:, 0:6]).then_inc(L2f_vector_done, 1)
                dve.wait_ge(L2f_scalar_done, 37*b + 40)
                dve.wait_ge(L2f_matmul_done, 29*b + 1)
                dve.tensor_scalar(u0[:, :], x_next[:, 2*b+0, :], st0[:, 6:7], st0[:, 9:10], ALU.subtract, ALU.mult)
                dve.wait_ge(L2f_scalar_done, 37*b + 41)
                dve.wait_ge(L2f_matmul_done, 29*b + 2)
                dve.tensor_scalar(u1[:, :], x_next[:, 2*b+1, :], st1[:, 6:7], st1[:, 9:10], ALU.subtract, ALU.mult)
                dve.wait_ge(L2f_matmul_done, 29*b + 3)
                dve.wait_ge(L2f_pool_done, 18*b + 1)
                dve.tensor_tensor(hb_0[:, :, :], psf0[:, 1024:2048].rearrange('p (j t) -> p j t', j=8), b_u2[:, :].unsqueeze(2).to_broadcast([128, 8, 128]), ALU.add).then_inc(L2f_vector_done, 1)
                dve.wait_ge(L2f_matmul_done, 29*b + 4)
                dve.wait_ge(L2f_pool_done, 18*b + 2)
                dve.tensor_tensor(hb_1[:, :, :], psf1[:, 1024:2048].rearrange('p (j t) -> p j t', j=8), b_u2[:, :].unsqueeze(2).to_broadcast([128, 8, 128]), ALU.add).then_inc(L2f_vector_done, 1)
                dve.wait_ge(L2f_matmul_done, 29*b + 5)
                dve.tensor_scalar(h2T_0[:, :], ps0[:, 1, 0:128], b_d2[:, 0:1], None, ALU.add).then_inc(L2f_vector_done, 1)
                dve.wait_ge(L2f_matmul_done, 29*b + 6)
                dve.tensor_scalar(h2T_1[:, :], ps1[:, 1, 0:128], b_d2[:, 0:1], None, ALU.add).then_inc(L2f_vector_done, 1)
                dve.wait_ge(L2f_scalar_done, 37*b + 46)
                dve.sem_inc(dve_waited, 1)
                for p in range(2):
                    for h in range(8):
                        last = dve.max(v8_0[:, p, h, :], sim_0[:, p, h, :])
                last.then_inc(L2f_vector_done, 1)
                dve.wait_ge(L2f_scalar_done, 37*b + 47)
                dve.sem_inc(dve_waited, 1)
                for p in range(2):
                    for h in range(8):
                        last = dve.max(v8_1[:, p, h, :], sim_1[:, p, h, :])
                last.then_inc(L2f_vector_done, 1)
                dve.wait_ge(L2f_vector_done, 53*b + 60)
                dve.tensor_tensor(c_0[:, 0:2, :, :], v8_0[:, :, :, :], v8_0[:, :, :, 0:1].to_broadcast([128, 2, 8, 8]), ALU.subtract).then_inc(L2f_vector_done, 1)
                dve.wait_ge(L2f_vector_done, 53*b + 61)
                dve.tensor_tensor(c_1[:, 0:2, :, :], v8_1[:, :, :, :], v8_1[:, :, :, 0:1].to_broadcast([128, 2, 8, 8]), ALU.subtract).then_inc(L2f_vector_done, 1)
                dve.wait_ge(L2f_scalar_done, 37*b + 51)
                dve.tensor_tensor(c_0[:, :, :, :], v8_0[:, 0, :, :].unsqueeze(3).to_broadcast([128, 8, 8, 8]), v8_0[:, 1, :, :].unsqueeze(2).to_broadcast([128, 8, 8, 8]), ALU.mult).then_inc(L2f_vector_done, 1)
                dve.wait_ge(L2f_scalar_done, 37*b + 52)
                dve.tensor_tensor(c_1[:, :, :, :], v8_1[:, 0, :, :].unsqueeze(3).to_broadcast([128, 8, 8, 8]), v8_1[:, 1, :, :].unsqueeze(2).to_broadcast([128, 8, 8, 8]), ALU.mult).then_inc(L2f_vector_done, 1)
                dve.wait_ge(L2f_vector_done, 53*b + 64)
                dve.sem_inc(dve_waited, 1)
                for h in range(8):
                    last = dve.max(t8_0[:, h, :], c_0[:, h, :, :])
                last.then_inc(L2f_vector_done, 1)
                dve.wait_ge(L2f_vector_done, 53*b + 65)
                dve.sem_inc(dve_waited, 1)
                for h in range(8):
                    last = dve.max(t8_1[:, h, :], c_1[:, h, :, :])
                last.then_inc(L2f_vector_done, 1)
                dve.wait_ge(L2f_pool_done, 18*b + 7)
                dve.wait_ge(L2f_vector_done, 53*b + 66)
                dve.scalar_tensor_tensor(Qfa_0[:, :], Pfa_0[:, :], t8_0[:, 0, 7:8], Pfa_0[:, :], ALU.is_ge, ALU.mult).then_inc(L2f_vector_done, 1)
                dve.tensor_reduce(d8_0[:, :], t8_0[:, :, :], AX.X, ALU.add).then_inc(L2f_vector_done, 1)
                dve.wait_ge(L2f_vector_done, 53*b + 67)
                dve.tensor_reduce(d8_1[:, :], t8_1[:, :, :], AX.X, ALU.add).then_inc(L2f_vector_done, 1)
                dve.wait_ge(L2f_vector_done, 53*b + 69)
                dve.reciprocal(q8_0[:, :], d8_0[:, :]).then_inc(L2f_vector_done, 1)
                dve.wait_ge(L2f_vector_done, 53*b + 70)
                dve.reciprocal(q8_1[:, :], d8_1[:, :])
                dve.wait_ge(L2f_vector_done, 53*b + 71)
                dve.scalar_tensor_tensor(Qfa_0[:, :], Qfa_0[:, :], q8_0[:, 0:1], z_0[:, 0:2025], ALU.mult, ALU.mult).then_inc(L2f_vector_done, 1)
                dve.wait_ge(L2f_pool_done, 18*b + 8)
                dve.scalar_tensor_tensor(Qfa_1[:, :], Pfa_1[:, :], t8_1[:, 0, 7:8], Pfa_1[:, :], ALU.is_ge, ALU.mult).then_inc(L2f_vector_done, 1)
                dve.wait_ge(L2f_vector_done, 53*b + 73)
                dve.scalar_tensor_tensor(Qfa_1[:, :], Qfa_1[:, :], q8_1[:, 0:1], z_1[:, 0:2025], ALU.mult, ALU.mult).then_inc(L2f_vector_done, 1)
                dve.wait_ge(L2f_pool_done, 18*b + 9)
                dve.scalar_tensor_tensor(Qfb_0[:, :], Pfb_0[:, :], t8_0[:, 1, 7:8], Pfb_0[:, :], ALU.is_ge, ALU.mult).then_inc(L2f_vector_done, 1)
                dve.wait_ge(L2f_pool_done, 18*b + 10)
                dve.scalar_tensor_tensor(Qfb_1[:, :], Pfb_1[:, :], t8_1[:, 1, 7:8], Pfb_1[:, :], ALU.is_ge, ALU.mult).then_inc(L2f_vector_done, 1)
                dve.wait_ge(L2f_vector_done, 53*b + 75)
                dve.scalar_tensor_tensor(Qfb_0[:, :], Qfb_0[:, :], q8_0[:, 1:2], z_0[:, 0:2025], ALU.mult, ALU.mult).then_inc(L2f_vector_done, 1)
                dve.wait_ge(L2f_vector_done, 53*b + 76)
                dve.scalar_tensor_tensor(Qfb_1[:, :], Qfb_1[:, :], q8_1[:, 1:2], z_1[:, 0:2025], ALU.mult, ALU.mult).then_inc(L2f_vector_done, 1)
                dve.wait_ge(L2f_pool_done, 18*b + 11)
                dve.wait_ge(L2f_matmul_done, 29*b + 13)
                dve.scalar_tensor_tensor(Qfa_0[:, :], Pfa_0[:, :], t8_0[:, 2, 7:8], Pfa_0[:, :], ALU.is_ge, ALU.mult).then_inc(L2f_vector_done, 1)
                dve.wait_ge(L2f_matmul_done, 29*b + 14)
                dve.wait_ge(L2f_pool_done, 18*b + 12)
                dve.scalar_tensor_tensor(Qfa_1[:, :], Pfa_1[:, :], t8_1[:, 2, 7:8], Pfa_1[:, :], ALU.is_ge, ALU.mult).then_inc(L2f_vector_done, 1)
                dve.wait_ge(L2f_vector_done, 53*b + 79)
                dve.scalar_tensor_tensor(Qfa_0[:, :], Qfa_0[:, :], q8_0[:, 2:3], z_0[:, 0:2025], ALU.mult, ALU.mult).then_inc(L2f_vector_done, 1)
                dve.wait_ge(L2f_vector_done, 53*b + 80)
                dve.scalar_tensor_tensor(Qfa_1[:, :], Qfa_1[:, :], q8_1[:, 2:3], z_1[:, 0:2025], ALU.mult, ALU.mult).then_inc(L2f_vector_done, 1)
                dve.wait_ge(L2f_pool_done, 18*b + 13)
                dve.wait_ge(L2f_matmul_done, 29*b + 15)
                dve.scalar_tensor_tensor(Qfb_0[:, :], Pfb_0[:, :], t8_0[:, 3, 7:8], Pfb_0[:, :], ALU.is_ge, ALU.mult).then_inc(L2f_vector_done, 1)
                dve.wait_ge(L2f_pool_done, 18*b + 14)
                dve.wait_ge(L2f_matmul_done, 29*b + 16)
                dve.scalar_tensor_tensor(Qfb_1[:, :], Pfb_1[:, :], t8_1[:, 3, 7:8], Pfb_1[:, :], ALU.is_ge, ALU.mult).then_inc(L2f_vector_done, 1)
                dve.wait_ge(L2f_vector_done, 53*b + 83)
                dve.scalar_tensor_tensor(Qfb_0[:, :], Qfb_0[:, :], q8_0[:, 3:4], z_0[:, 0:2025], ALU.mult, ALU.mult).then_inc(L2f_vector_done, 1)
                dve.wait_ge(L2f_vector_done, 53*b + 84)
                dve.scalar_tensor_tensor(Qfb_1[:, :], Qfb_1[:, :], q8_1[:, 3:4], z_1[:, 0:2025], ALU.mult, ALU.mult).then_inc(L2f_vector_done, 1)
                dve.wait_ge(L2f_pool_done, 18*b + 15)
                dve.wait_ge(L2f_matmul_done, 29*b + 17)
                dve.scalar_tensor_tensor(Qfa_0[:, :], Pfa_0[:, :], t8_0[:, 4, 7:8], Pfa_0[:, :], ALU.is_ge, ALU.mult).then_inc(L2f_vector_done, 1)
                dve.wait_ge(L2f_pool_done, 18*b + 16)
                dve.wait_ge(L2f_matmul_done, 29*b + 18)
                dve.scalar_tensor_tensor(Qfa_1[:, :], Pfa_1[:, :], t8_1[:, 4, 7:8], Pfa_1[:, :], ALU.is_ge, ALU.mult).then_inc(L2f_vector_done, 1)
                dve.wait_ge(L2f_vector_done, 53*b + 87)
                dve.scalar_tensor_tensor(Qfa_0[:, :], Qfa_0[:, :], q8_0[:, 4:5], z_0[:, 0:2025], ALU.mult, ALU.mult).then_inc(L2f_vector_done, 1)
                dve.wait_ge(L2f_vector_done, 53*b + 88)
                dve.scalar_tensor_tensor(Qfa_1[:, :], Qfa_1[:, :], q8_1[:, 4:5], z_1[:, 0:2025], ALU.mult, ALU.mult).then_inc(L2f_vector_done, 1)
                dve.wait_ge(L2f_pool_done, 18*b + 17)
                dve.wait_ge(L2f_matmul_done, 29*b + 19)
                dve.scalar_tensor_tensor(Qfb_0[:, :], Pfb_0[:, :], t8_0[:, 5, 7:8], Pfb_0[:, :], ALU.is_ge, ALU.mult).then_inc(L2f_vector_done, 1)
                dve.wait_ge(L2f_pool_done, 18*b + 18)
                dve.wait_ge(L2f_matmul_done, 29*b + 20)
                dve.scalar_tensor_tensor(Qfb_1[:, :], Pfb_1[:, :], t8_1[:, 5, 7:8], Pfb_1[:, :], ALU.is_ge, ALU.mult).then_inc(L2f_vector_done, 1)
                dve.wait_ge(L2f_vector_done, 53*b + 91)
                dve.scalar_tensor_tensor(Qfb_0[:, :], Qfb_0[:, :], q8_0[:, 5:6], z_0[:, 0:2025], ALU.mult, ALU.mult).then_inc(L2f_vector_done, 1)
                dve.wait_ge(L2f_vector_done, 53*b + 92)
                dve.scalar_tensor_tensor(Qfb_1[:, :], Qfb_1[:, :], q8_1[:, 5:6], z_1[:, 0:2025], ALU.mult, ALU.mult).then_inc(L2f_vector_done, 1)
                dve.wait_ge(L2f_pool_done, 18*b + 19)
                dve.wait_ge(L2f_matmul_done, 29*b + 21)
                dve.scalar_tensor_tensor(Qfa_0[:, :], Pfa_0[:, :], t8_0[:, 6, 7:8], Pfa_0[:, :], ALU.is_ge, ALU.mult).then_inc(L2f_vector_done, 1)
                dve.wait_ge(L2f_pool_done, 18*b + 20)
                dve.wait_ge(L2f_matmul_done, 29*b + 22)
                dve.scalar_tensor_tensor(Qfa_1[:, :], Pfa_1[:, :], t8_1[:, 6, 7:8], Pfa_1[:, :], ALU.is_ge, ALU.mult).then_inc(L2f_vector_done, 1)
                dve.wait_ge(L2f_vector_done, 53*b + 95)
                dve.scalar_tensor_tensor(Qfa_0[:, :], Qfa_0[:, :], q8_0[:, 6:7], z_0[:, 0:2025], ALU.mult, ALU.mult).then_inc(L2f_vector_done, 1)
                dve.wait_ge(L2f_vector_done, 53*b + 96)
                dve.scalar_tensor_tensor(Qfa_1[:, :], Qfa_1[:, :], q8_1[:, 6:7], z_1[:, 0:2025], ALU.mult, ALU.mult).then_inc(L2f_vector_done, 1)
                dve.wait_ge(L2f_pool_done, 18*b + 21)
                dve.wait_ge(L2f_matmul_done, 29*b + 23)
                dve.scalar_tensor_tensor(Qfb_0[:, :], Pfb_0[:, :], t8_0[:, 7, 7:8], Pfb_0[:, :], ALU.is_ge, ALU.mult).then_inc(L2f_vector_done, 1)
                dve.wait_ge(L2f_pool_done, 18*b + 22)
                dve.wait_ge(L2f_matmul_done, 29*b + 24)
                dve.scalar_tensor_tensor(Qfb_1[:, :], Pfb_1[:, :], t8_1[:, 7, 7:8], Pfb_1[:, :], ALU.is_ge, ALU.mult).then_inc(L2f_vector_done, 1)
                dve.wait_ge(L2f_vector_done, 53*b + 99)
                dve.scalar_tensor_tensor(Qfb_0[:, :], Qfb_0[:, :], q8_0[:, 7:8], z_0[:, 0:2025], ALU.mult, ALU.mult).then_inc(L2f_vector_done, 1)
                dve.wait_ge(L2f_vector_done, 53*b + 100)
                dve.scalar_tensor_tensor(Qfb_1[:, :], Qfb_1[:, :], q8_1[:, 7:8], z_1[:, 0:2025], ALU.mult, ALU.mult).then_inc(L2f_vector_done, 1)
                dve.wait_ge(L2f_matmul_done, 29*b + 28)
                dve.tensor_tensor(x[:, 2*b+0, :], ps0[:, 0, 0:256], x[:, 2*b+0, :], ALU.add).then_inc(L2f_vector_done, 1)
                dve.wait_ge(L2f_matmul_done, 29*b + 29)
                dve.tensor_tensor(x[:, 2*b+1, :], ps1[:, 0, 0:256], x[:, 2*b+1, :], ALU.add).then_inc(L2f_vector_done, 1)

            dve.sem_inc(L3a_vector_done, 66)
            dve.wait_ge(L2f_scalar_done, 161)
            dve.wait_ge(L2f_pool_done, 64)
            dve.memset(vg_0[:, :, 8:9], 1.0)
            dve.wait_ge(L2f_pool_done, 68)
            dve.memset(vg_1[:, :, 8:9], 1.0)
            dve.wait_ge(L2f_vector_done, 263)
            dve.bn_stats(st0[:, 0:6], x[:, 0, :]).then_inc(L3a_vector_done, 1)
            dve.bn_stats(st1[:, 0:6], x[:, 1, :]).then_inc(L3a_vector_done, 1)
            dve.wait_ge(L3a_vector_done, 67)
            dve.bn_aggr(st0[:, 6:8], st0[:, 0:6]).then_inc(L3a_vector_done, 1)
            dve.wait_ge(L3a_vector_done, 68)
            dve.bn_aggr(st1[:, 6:8], st1[:, 0:6]).then_inc(L3a_vector_done, 1)
            dve.wait_ge(L2f_matmul_done, 117)
            dve.wait_ge(L3a_scalar_done, 38)
            dve.tensor_scalar(u0[:, :], x[:, 0, :], st0[:, 6:7], st0[:, 9:10], ALU.subtract, ALU.mult).then_inc(L3a_vector_done, 1)
            dve.wait_ge(L2f_matmul_done, 118)
            dve.wait_ge(L3a_scalar_done, 39)
            dve.tensor_scalar(u1[:, :], x[:, 1, :], st1[:, 6:7], st1[:, 9:10], ALU.subtract, ALU.mult).then_inc(L3a_vector_done, 1)
            dve.wait_ge(L3a_w_loaded, 128)
            dve.wait_ge(L2f_pool_done, 76)
            dve.wait_ge(L3a_matmul_done, 2)
            with dve.Fori(0, 4) as b:
                dve.wait_ge(L3a_vector_done, 74*b + 1)
                dve.sem_inc(dve_waited, 1)
                dve.bn_stats(st0[:, 0:6], x_next[:, 2*b+0, :]).then_inc(L3a_vector_done, 1)
                dve.wait_ge(L3a_vector_done, 74*b + 2)
                dve.sem_inc(dve_waited, 1)
                dve.bn_stats(st1[:, 0:6], x_next[:, 2*b+1, :]).then_inc(L3a_vector_done, 1)
                dve.wait_ge(L3a_vector_done, 74*b + 73)
                dve.wait_ge(L3a_scalar_done, 40*b + 1)
                dve.sem_inc(dve_waited, 1)
                dve.bn_aggr(st0[:, 6:8], st0[:, 0:6]).then_inc(L3a_vector_done, 1)
                dve.wait_ge(L3a_vector_done, 74*b + 74)
                dve.wait_ge(L3a_scalar_done, 40*b + 2)
                dve.sem_inc(dve_waited, 1)
                dve.bn_aggr(st1[:, 6:8], st1[:, 0:6]).then_inc(L3a_vector_done, 1)
                dve.wait_ge(L3a_scalar_done, 40*b + 43)
                dve.wait_ge(L3a_matmul_done, 56*b + 1)
                dve.tensor_scalar(u0[:, :], x_next[:, 2*b+0, :], st0[:, 6:7], st0[:, 9:10], ALU.subtract, ALU.mult)
                dve.wait_ge(L3a_scalar_done, 40*b + 44)
                dve.wait_ge(L3a_matmul_done, 56*b + 2)
                dve.tensor_scalar(u1[:, :], x_next[:, 2*b+1, :], st1[:, 6:7], st1[:, 9:10], ALU.subtract, ALU.mult)
                dve.wait_ge(L3a_matmul_done, 56*b + 3)
                dve.wait_ge(L3a_pool_done, 3*b + 1)
                for j in range(2):
                    last = dve.tensor_scalar(kT3_0[:, j, :], ps0[:, 1, 256 + 128 * j:384 + 128 * j], b_k3[:, j:j + 1], None, ALU.add)
                last.then_inc(L3a_vector_done, 1)
                for j in range(2):
                    dve.tensor_scalar(qT_0[:, j, :], ps0[:, 1, 128 * j:128 * j + 128], b_q3[:, j:j + 1], None, ALU.add)
                dve.wait_ge(L3a_vector_done, 74*b + 77)
                dve.tensor_tensor(kR_0[:, 0, :, :], kT3_0[:, 0, :].unsqueeze(1).to_broadcast([128, 16, 128]), mask8[:, :].unsqueeze(2).to_broadcast([128, 16, 128]), ALU.mult).then_inc(L3a_vector_done, 1)
                dve.wait_ge(L3a_matmul_done, 56*b + 4)
                dve.wait_ge(L3a_pool_done, 3*b + 2)
                for j in range(2):
                    last = dve.tensor_scalar(kT3_1[:, j, :], ps1[:, 1, 256 + 128 * j:384 + 128 * j], b_k3[:, j:j + 1], None, ALU.add)
                last.then_inc(L3a_vector_done, 1)
                for j in range(2):
                    dve.tensor_scalar(qT_1[:, j, :], ps1[:, 1, 128 * j:128 * j + 128], b_q3[:, j:j + 1], None, ALU.add)
                dve.wait_ge(L3a_vector_done, 74*b + 79)
                dve.tensor_tensor(kR_1[:, 0, :, :], kT3_1[:, 0, :].unsqueeze(1).to_broadcast([128, 16, 128]), mask8[:, :].unsqueeze(2).to_broadcast([128, 16, 128]), ALU.mult).then_inc(L3a_vector_done, 1)
                dve.wait_ge(L3a_matmul_done, 56*b + 5)
                dve.tensor_reduce(st0[:, 16:20], ps0[:, 1, :].rearrange("p (h s) -> p h s", h=4), AX.X, ALU.max).then_inc(L3a_vector_done, 1)
                dve.tensor_tensor(vg_0[:, :, 0:8], ps0[:, 2, 0:64].rearrange('p (h d) -> p h d', h=8), b_v3[:, :].rearrange('p (h d) -> p h d', h=8), ALU.add)
                dve.wait_ge(L3a_vector_done, 74*b + 81)
                dve.tensor_scalar(st0[:, 16:20], st0[:, 16:20], -0.3535533905932738, None, ALU.mult).then_inc(L3a_vector_done, 1)
                dve.tensor_tensor(vg_1[:, :, 0:8], ps1[:, 2, 0:64].rearrange('p (h d) -> p h d', h=8), b_v3[:, :].rearrange('p (h d) -> p h d', h=8), ALU.add)
                dve.wait_ge(L3a_matmul_done, 56*b + 6)
                dve.tensor_reduce(st1[:, 16:20], ps1[:, 1, :].rearrange("p (h s) -> p h s", h=4), AX.X, ALU.max).then_inc(L3a_vector_done, 1)
                dve.wait_ge(L3a_vector_done, 74*b + 83)
                dve.tensor_scalar(st1[:, 16:20], st1[:, 16:20], -0.3535533905932738, None, ALU.mult).then_inc(L3a_vector_done, 1)
                dve.wait_ge(L3a_matmul_done, 56*b + 7)
                dve.tensor_reduce(st0[:, 16:20], ps0[:, 1, :].rearrange("p (h s) -> p h s", h=4), AX.X, ALU.max).then_inc(L3a_vector_done, 1)
                dve.wait_ge(L3a_vector_done, 74*b + 85)
                dve.tensor_scalar(st0[:, 16:20], st0[:, 16:20], -0.3535533905932738, None, ALU.mult).then_inc(L3a_vector_done, 1)
                dve.wait_ge(L3a_matmul_done, 56*b + 9)
                dve.tensor_reduce(st1[:, 16:20], ps1[:, 1, :].rearrange("p (h s) -> p h s", h=4), AX.X, ALU.max).then_inc(L3a_vector_done, 1)
                dve.wait_ge(L3a_matmul_done, 56*b + 11)
                dve.reciprocal(st0[:, 20:24], ps0[:, 3, 0:36].rearrange('p (h e) -> p h e', h=4)[:, :, 8]).then_inc(L3a_vector_done, 1)
                dve.wait_ge(L3a_vector_done, 74*b + 87)
                dve.tensor_scalar(st1[:, 16:20], st1[:, 16:20], -0.3535533905932738, None, ALU.mult).then_inc(L3a_vector_done, 1)
                dve.wait_ge(L3a_vector_done, 74*b + 88)
                dve.tensor_tensor(ao_0[:, 0:32].rearrange('p (h d) -> p h d', h=4), ps0[:, 3, 0:36].rearrange('p (h e) -> p h e', h=4)[:, :, 0:8], st0[:, 20:24].unsqueeze(2).to_broadcast([128, 4, 8]), ALU.mult).then_inc(L3a_vector_done, 1)
                dve.wait_ge(L3a_matmul_done, 56*b + 12)
                dve.tensor_reduce(st0[:, 16:20], ps0[:, 1, :].rearrange("p (h s) -> p h s", h=4), AX.X, ALU.max).then_inc(L3a_vector_done, 1)
                dve.wait_ge(L3a_matmul_done, 56*b + 14)
                dve.reciprocal(st1[:, 20:24], ps1[:, 3, 0:36].rearrange('p (h e) -> p h e', h=4)[:, :, 8]).then_inc(L3a_vector_done, 1)
                dve.wait_ge(L3a_vector_done, 74*b + 91)
                dve.tensor_scalar(st0[:, 16:20], st0[:, 16:20], -0.3535533905932738, None, ALU.mult).then_inc(L3a_vector_done, 1)
                dve.wait_ge(L3a_vector_done, 74*b + 92)
                dve.tensor_tensor(ao_1[:, 0:32].rearrange('p (h d) -> p h d', h=4), ps1[:, 3, 0:36].rearrange('p (h e) -> p h e', h=4)[:, :, 0:8], st1[:, 20:24].unsqueeze(2).to_broadcast([128, 4, 8]), ALU.mult).then_inc(L3a_vector_done, 1)
                dve.wait_ge(L3a_matmul_done, 56*b + 15)
                dve.tensor_reduce(st1[:, 16:20], ps1[:, 1, :].rearrange("p (h s) -> p h s", h=4), AX.X, ALU.max).then_inc(L3a_vector_done, 1)
                dve.wait_ge(L3a_matmul_done, 56*b + 17)
                dve.reciprocal(st0[:, 20:24], ps0[:, 3, 0:36].rearrange('p (h e) -> p h e', h=4)[:, :, 8]).then_inc(L3a_vector_done, 1)
                dve.wait_ge(L3a_vector_done, 74*b + 95)
                dve.tensor_scalar(st1[:, 16:20], st1[:, 16:20], -0.3535533905932738, None, ALU.mult).then_inc(L3a_vector_done, 1)
                dve.wait_ge(L3a_vector_done, 74*b + 96)
                dve.tensor_tensor(ao_0[:, 32:64].rearrange('p (h d) -> p h d', h=4), ps0[:, 3, 0:36].rearrange('p (h e) -> p h e', h=4)[:, :, 0:8], st0[:, 20:24].unsqueeze(2).to_broadcast([128, 4, 8]), ALU.mult).then_inc(L3a_vector_done, 1)
                dve.wait_ge(L3a_matmul_done, 56*b + 18)
                dve.tensor_reduce(st0[:, 16:20], ps0[:, 1, :].rearrange("p (h s) -> p h s", h=4), AX.X, ALU.max).then_inc(L3a_vector_done, 1)
                dve.wait_ge(L3a_matmul_done, 56*b + 20)
                dve.reciprocal(st1[:, 20:24], ps1[:, 3, 0:36].rearrange('p (h e) -> p h e', h=4)[:, :, 8]).then_inc(L3a_vector_done, 1)
                dve.wait_ge(L3a_vector_done, 74*b + 99)
                dve.tensor_scalar(st0[:, 16:20], st0[:, 16:20], -0.3535533905932738, None, ALU.mult).then_inc(L3a_vector_done, 1)
                dve.wait_ge(L3a_vector_done, 74*b + 100)
                dve.tensor_tensor(ao_1[:, 32:64].rearrange('p (h d) -> p h d', h=4), ps1[:, 3, 0:36].rearrange('p (h e) -> p h e', h=4)[:, :, 0:8], st1[:, 20:24].unsqueeze(2).to_broadcast([128, 4, 8]), ALU.mult).then_inc(L3a_vector_done, 1)
                dve.wait_ge(L3a_matmul_done, 56*b + 21)
                dve.tensor_reduce(st1[:, 16:20], ps1[:, 1, :].rearrange("p (h s) -> p h s", h=4), AX.X, ALU.max).then_inc(L3a_vector_done, 1)
                dve.wait_ge(L3a_matmul_done, 56*b + 23)
                dve.reciprocal(st0[:, 20:24], ps0[:, 3, 0:36].rearrange('p (h e) -> p h e', h=4)[:, :, 8]).then_inc(L3a_vector_done, 1)
                dve.wait_ge(L3a_vector_done, 74*b + 103)
                dve.tensor_scalar(st1[:, 16:20], st1[:, 16:20], -0.3535533905932738, None, ALU.mult).then_inc(L3a_vector_done, 1)
                dve.wait_ge(L3a_vector_done, 74*b + 104)
                dve.tensor_tensor(ao_0[:, 64:96].rearrange('p (h d) -> p h d', h=4), ps0[:, 3, 0:36].rearrange('p (h e) -> p h e', h=4)[:, :, 0:8], st0[:, 20:24].unsqueeze(2).to_broadcast([128, 4, 8]), ALU.mult).then_inc(L3a_vector_done, 1)
                dve.wait_ge(L3a_matmul_done, 56*b + 24)
                dve.tensor_reduce(st0[:, 16:20], ps0[:, 1, :].rearrange("p (h s) -> p h s", h=4), AX.X, ALU.max).then_inc(L3a_vector_done, 1)
                dve.wait_ge(L3a_matmul_done, 56*b + 26)
                dve.reciprocal(st1[:, 20:24], ps1[:, 3, 0:36].rearrange('p (h e) -> p h e', h=4)[:, :, 8]).then_inc(L3a_vector_done, 1)
                dve.wait_ge(L3a_vector_done, 74*b + 107)
                dve.tensor_scalar(st0[:, 16:20], st0[:, 16:20], -0.3535533905932738, None, ALU.mult).then_inc(L3a_vector_done, 1)
                dve.wait_ge(L3a_vector_done, 74*b + 108)
                dve.tensor_tensor(ao_1[:, 64:96].rearrange('p (h d) -> p h d', h=4), ps1[:, 3, 0:36].rearrange('p (h e) -> p h e', h=4)[:, :, 0:8], st1[:, 20:24].unsqueeze(2).to_broadcast([128, 4, 8]), ALU.mult).then_inc(L3a_vector_done, 1)
                dve.wait_ge(L3a_matmul_done, 56*b + 27)
                dve.tensor_reduce(st1[:, 16:20], ps1[:, 1, :].rearrange("p (h s) -> p h s", h=4), AX.X, ALU.max).then_inc(L3a_vector_done, 1)
                dve.wait_ge(L3a_matmul_done, 56*b + 29)
                dve.reciprocal(st0[:, 20:24], ps0[:, 3, 0:36].rearrange('p (h e) -> p h e', h=4)[:, :, 8]).then_inc(L3a_vector_done, 1)
                dve.wait_ge(L3a_vector_done, 74*b + 111)
                dve.tensor_scalar(st1[:, 16:20], st1[:, 16:20], -0.3535533905932738, None, ALU.mult).then_inc(L3a_vector_done, 1)
                dve.wait_ge(L3a_vector_done, 74*b + 112)
                dve.tensor_tensor(ao_0[:, 96:128].rearrange('p (h d) -> p h d', h=4), ps0[:, 3, 0:36].rearrange('p (h e) -> p h e', h=4)[:, :, 0:8], st0[:, 20:24].unsqueeze(2).to_broadcast([128, 4, 8]), ALU.mult).then_inc(L3a_vector_done, 1)
                dve.wait_ge(L3a_matmul_done, 56*b + 30)
                dve.tensor_reduce(st0[:, 16:20], ps0[:, 1, :].rearrange("p (h s) -> p h s", h=4), AX.X, ALU.max).then_inc(L3a_vector_done, 1)
                dve.wait_ge(L3a_matmul_done, 56*b + 32)
                dve.reciprocal(st1[:, 20:24], ps1[:, 3, 0:36].rearrange('p (h e) -> p h e', h=4)[:, :, 8]).then_inc(L3a_vector_done, 1)
                dve.wait_ge(L3a_vector_done, 74*b + 115)
                dve.tensor_scalar(st0[:, 16:20], st0[:, 16:20], -0.3535533905932738, None, ALU.mult).then_inc(L3a_vector_done, 1)
                dve.wait_ge(L3a_vector_done, 74*b + 116)
                dve.tensor_tensor(ao_1[:, 96:128].rearrange('p (h d) -> p h d', h=4), ps1[:, 3, 0:36].rearrange('p (h e) -> p h e', h=4)[:, :, 0:8], st1[:, 20:24].unsqueeze(2).to_broadcast([128, 4, 8]), ALU.mult).then_inc(L3a_vector_done, 1)
                dve.wait_ge(L3a_matmul_done, 56*b + 33)
                dve.tensor_reduce(st1[:, 16:20], ps1[:, 1, :].rearrange("p (h s) -> p h s", h=4), AX.X, ALU.max).then_inc(L3a_vector_done, 1)
                dve.wait_ge(L3a_matmul_done, 56*b + 35)
                dve.reciprocal(st0[:, 20:24], ps0[:, 3, 0:36].rearrange('p (h e) -> p h e', h=4)[:, :, 8]).then_inc(L3a_vector_done, 1)
                dve.wait_ge(L3a_vector_done, 74*b + 119)
                dve.tensor_scalar(st1[:, 16:20], st1[:, 16:20], -0.3535533905932738, None, ALU.mult).then_inc(L3a_vector_done, 1)
                dve.wait_ge(L3a_vector_done, 74*b + 120)
                dve.tensor_tensor(ao_0[:, 128:160].rearrange('p (h d) -> p h d', h=4), ps0[:, 3, 0:36].rearrange('p (h e) -> p h e', h=4)[:, :, 0:8], st0[:, 20:24].unsqueeze(2).to_broadcast([128, 4, 8]), ALU.mult).then_inc(L3a_vector_done, 1)
                dve.wait_ge(L3a_matmul_done, 56*b + 36)
                dve.tensor_reduce(st0[:, 16:20], ps0[:, 1, :].rearrange("p (h s) -> p h s", h=4), AX.X, ALU.max).then_inc(L3a_vector_done, 1)
                dve.wait_ge(L3a_matmul_done, 56*b + 38)
                dve.reciprocal(st1[:, 20:24], ps1[:, 3, 0:36].rearrange('p (h e) -> p h e', h=4)[:, :, 8]).then_inc(L3a_vector_done, 1)
                dve.wait_ge(L3a_vector_done, 74*b + 123)
                dve.tensor_scalar(st0[:, 16:20], st0[:, 16:20], -0.3535533905932738, None, ALU.mult).then_inc(L3a_vector_done, 1)
                dve.wait_ge(L3a_vector_done, 74*b + 124)
                dve.tensor_tensor(ao_1[:, 128:160].rearrange('p (h d) -> p h d', h=4), ps1[:, 3, 0:36].rearrange('p (h e) -> p h e', h=4)[:, :, 0:8], st1[:, 20:24].unsqueeze(2).to_broadcast([128, 4, 8]), ALU.mult).then_inc(L3a_vector_done, 1)
                dve.wait_ge(L3a_matmul_done, 56*b + 39)
                dve.tensor_reduce(st1[:, 16:20], ps1[:, 1, :].rearrange("p (h s) -> p h s", h=4), AX.X, ALU.max).then_inc(L3a_vector_done, 1)
                dve.wait_ge(L3a_matmul_done, 56*b + 41)
                dve.reciprocal(st0[:, 20:24], ps0[:, 3, 0:36].rearrange('p (h e) -> p h e', h=4)[:, :, 8]).then_inc(L3a_vector_done, 1)
                dve.wait_ge(L3a_vector_done, 74*b + 127)
                dve.tensor_scalar(st1[:, 16:20], st1[:, 16:20], -0.3535533905932738, None, ALU.mult).then_inc(L3a_vector_done, 1)
                dve.wait_ge(L3a_vector_done, 74*b + 128)
                dve.tensor_tensor(ao_0[:, 160:192].rearrange('p (h d) -> p h d', h=4), ps0[:, 3, 0:36].rearrange('p (h e) -> p h e', h=4)[:, :, 0:8], st0[:, 20:24].unsqueeze(2).to_broadcast([128, 4, 8]), ALU.mult).then_inc(L3a_vector_done, 1)
                dve.wait_ge(L3a_matmul_done, 56*b + 42)
                dve.tensor_reduce(st0[:, 16:20], ps0[:, 1, :].rearrange("p (h s) -> p h s", h=4), AX.X, ALU.max).then_inc(L3a_vector_done, 1)
                dve.wait_ge(L3a_matmul_done, 56*b + 44)
                dve.reciprocal(st1[:, 20:24], ps1[:, 3, 0:36].rearrange('p (h e) -> p h e', h=4)[:, :, 8]).then_inc(L3a_vector_done, 1)
                dve.wait_ge(L3a_vector_done, 74*b + 131)
                dve.tensor_scalar(st0[:, 16:20], st0[:, 16:20], -0.3535533905932738, None, ALU.mult).then_inc(L3a_vector_done, 1)
                dve.wait_ge(L3a_vector_done, 74*b + 132)
                dve.tensor_tensor(ao_1[:, 160:192].rearrange('p (h d) -> p h d', h=4), ps1[:, 3, 0:36].rearrange('p (h e) -> p h e', h=4)[:, :, 0:8], st1[:, 20:24].unsqueeze(2).to_broadcast([128, 4, 8]), ALU.mult).then_inc(L3a_vector_done, 1)
                dve.wait_ge(L3a_matmul_done, 56*b + 45)
                dve.tensor_reduce(st1[:, 16:20], ps1[:, 1, :].rearrange("p (h s) -> p h s", h=4), AX.X, ALU.max).then_inc(L3a_vector_done, 1)
                dve.wait_ge(L3a_matmul_done, 56*b + 47)
                dve.reciprocal(st0[:, 20:24], ps0[:, 3, 0:36].rearrange('p (h e) -> p h e', h=4)[:, :, 8]).then_inc(L3a_vector_done, 1)
                dve.wait_ge(L3a_vector_done, 74*b + 135)
                dve.tensor_scalar(st1[:, 16:20], st1[:, 16:20], -0.3535533905932738, None, ALU.mult).then_inc(L3a_vector_done, 1)
                dve.wait_ge(L3a_vector_done, 74*b + 136)
                dve.tensor_tensor(ao_0[:, 192:224].rearrange('p (h d) -> p h d', h=4), ps0[:, 3, 0:36].rearrange('p (h e) -> p h e', h=4)[:, :, 0:8], st0[:, 20:24].unsqueeze(2).to_broadcast([128, 4, 8]), ALU.mult).then_inc(L3a_vector_done, 1)
                dve.wait_ge(L3a_matmul_done, 56*b + 49)
                dve.reciprocal(st1[:, 20:24], ps1[:, 3, 0:36].rearrange('p (h e) -> p h e', h=4)[:, :, 8]).then_inc(L3a_vector_done, 1)
                dve.wait_ge(L3a_vector_done, 74*b + 139)
                dve.tensor_tensor(ao_1[:, 192:224].rearrange('p (h d) -> p h d', h=4), ps1[:, 3, 0:36].rearrange('p (h e) -> p h e', h=4)[:, :, 0:8], st1[:, 20:24].unsqueeze(2).to_broadcast([128, 4, 8]), ALU.mult).then_inc(L3a_vector_done, 1)
                dve.wait_ge(L3a_matmul_done, 56*b + 51)
                dve.reciprocal(st0[:, 20:24], ps0[:, 3, 0:36].rearrange('p (h e) -> p h e', h=4)[:, :, 8]).then_inc(L3a_vector_done, 1)
                dve.wait_ge(L3a_vector_done, 74*b + 141)
                dve.tensor_tensor(ao_0[:, 224:256].rearrange('p (h d) -> p h d', h=4), ps0[:, 3, 0:36].rearrange('p (h e) -> p h e', h=4)[:, :, 0:8], st0[:, 20:24].unsqueeze(2).to_broadcast([128, 4, 8]), ALU.mult).then_inc(L3a_vector_done, 1)
                dve.wait_ge(L3a_matmul_done, 56*b + 52)
                dve.reciprocal(st1[:, 20:24], ps1[:, 3, 0:36].rearrange('p (h e) -> p h e', h=4)[:, :, 8]).then_inc(L3a_vector_done, 1)
                dve.wait_ge(L3a_vector_done, 74*b + 143)
                dve.tensor_tensor(ao_1[:, 224:256].rearrange('p (h d) -> p h d', h=4), ps1[:, 3, 0:36].rearrange('p (h e) -> p h e', h=4)[:, :, 0:8], st1[:, 20:24].unsqueeze(2).to_broadcast([128, 4, 8]), ALU.mult).then_inc(L3a_vector_done, 1)
                dve.wait_ge(L3a_matmul_done, 56*b + 55)
                dve.tensor_tensor(un0[:, :], ps0[:, 1, 0:256], b_o3[:, :], ALU.add).then_inc(L3a_vector_done, 1)
                dve.wait_ge(L3a_matmul_done, 56*b + 56)
                dve.tensor_tensor(un1[:, :], ps1[:, 1, 0:256], b_o3[:, :], ALU.add).then_inc(L3a_vector_done, 1)

            dve.sem_inc(L3x_vector_done, 18)
            dve.wait_ge(L3a_vector_done, 312)
            dve.wait_ge(L3a_scalar_done, 195)
            dve.wait_ge(L3a_matmul_done, 221)
            dve.memset(v3_0[:, :, 128:129], 1.0)
            dve.memset(v3_1[:, :, 128:129], 1.0)
            dve.wait_ge(L3a_pool_done, 15)
            dve.bn_stats(st0[:, 0:6], x[:, 0, :]).then_inc(L3x_vector_done, 1)
            dve.bn_stats(st1[:, 0:6], x[:, 1, :]).then_inc(L3x_vector_done, 1)
            dve.wait_ge(L3x_vector_done, 19)
            dve.bn_aggr(st0[:, 6:8], st0[:, 0:6]).then_inc(L3x_vector_done, 1)
            dve.wait_ge(L3x_vector_done, 20)
            dve.bn_aggr(st1[:, 6:8], st1[:, 0:6]).then_inc(L3x_vector_done, 1)
            dve.wait_ge(L3a_matmul_done, 225)
            dve.wait_ge(L3x_scalar_done, 16)
            dve.tensor_scalar(u0[:, :], x[:, 0, :], st0[:, 6:7], st0[:, 9:10], ALU.subtract, ALU.mult).then_inc(L3x_vector_done, 1)
            dve.wait_ge(L3a_matmul_done, 226)
            dve.wait_ge(L3x_scalar_done, 17)
            dve.tensor_scalar(u1[:, :], x[:, 1, :], st1[:, 6:7], st1[:, 9:10], ALU.subtract, ALU.mult).then_inc(L3x_vector_done, 1)
            dve.wait_ge(L3x_w_loaded, 64)
            dve.wait_ge(L3x_matmul_done, 15)
            with dve.Fori(0, 4) as b:
                dve.wait_ge(L3x_vector_done, 26*b + 1)
                dve.sem_inc(dve_waited, 1)
                dve.bn_stats(st0[:, 0:6], x_next[:, 2*b+0, :]).then_inc(L3x_vector_done, 1)
                dve.wait_ge(L3x_vector_done, 26*b + 2)
                dve.sem_inc(dve_waited, 1)
                dve.bn_stats(st1[:, 0:6], x_next[:, 2*b+1, :]).then_inc(L3x_vector_done, 1)
                dve.wait_ge(L3x_vector_done, 26*b + 25)
                dve.wait_ge(L3x_scalar_done, 18*b + 3)
                dve.sem_inc(dve_waited, 1)
                dve.bn_aggr(st0[:, 6:8], st0[:, 0:6]).then_inc(L3x_vector_done, 1)
                dve.wait_ge(L3x_vector_done, 26*b + 26)
                dve.wait_ge(L3x_scalar_done, 18*b + 4)
                dve.sem_inc(dve_waited, 1)
                dve.bn_aggr(st1[:, 6:8], st1[:, 0:6]).then_inc(L3x_vector_done, 1)
                dve.wait_ge(L3x_scalar_done, 18*b + 23)
                dve.wait_ge(L3x_matmul_done, 16*b + 14)
                dve.tensor_scalar(u0[:, :], x_next[:, 2*b+0, :], st0[:, 6:7], st0[:, 9:10], ALU.subtract, ALU.mult)
                dve.wait_ge(L3x_matmul_done, 16*b + 16)
                dve.wait_ge(L3x_pool_done, 4*b + 1)
                dve.tensor_tensor(ga_0[:, :], ps0[:, 1, 256:512], b_gx3[:, :], ALU.add).then_inc(L3x_vector_done, 1)
                dve.tensor_scalar(jk0[:, :], ps0[:, 1, 0:256], 0.0, None, ALU.min).then_inc(L3x_vector_done, 1)
                dve.wait_ge(L3x_vector_done, 26*b + 29)
                dve.tensor_scalar(ga_0[:, :], ga_0[:, :], -80.0, None, ALU.max).then_inc(L3x_vector_done, 1)
                dve.wait_ge(L3x_scalar_done, 18*b + 24)
                dve.tensor_scalar(u1[:, :], x_next[:, 2*b+1, :], st1[:, 6:7], st1[:, 9:10], ALU.subtract, ALU.mult)
                dve.wait_ge(L3x_scalar_done, 18*b + 25)
                dve.scalar_tensor_tensor(q3_0[:, :], ps0[:, 1, 0:256], 0.0, jk0[:, :], ALU.max, ALU.add).then_inc(L3x_vector_done, 1)
                dve.wait_ge(L3x_matmul_done, 16*b + 17)
                dve.tensor_scalar(ks_0[:, :], ps0[:, 2, 0:256], 0.0, None, ALU.min).then_inc(L3x_vector_done, 1)
                dve.wait_ge(L3x_pool_done, 4*b + 3)
                dve.reciprocal(ga_0[:, :], ga_0[:, :])
                dve.wait_ge(L3x_matmul_done, 16*b + 18)
                dve.tensor_scalar(ks_1[:, :], ps1[:, 2, 0:256], 0.0, None, ALU.min).then_inc(L3x_vector_done, 1)
                dve.wait_ge(L3x_scalar_done, 18*b + 27)
                dve.scalar_tensor_tensor(k3_0[:, :], ps0[:, 2, 0:256], 0.0, ks_0[:, :], ALU.max, ALU.add).then_inc(L3x_vector_done, 1)
                dve.wait_ge(L3x_matmul_done, 16*b + 19)
                dve.tensor_tensor(ga_1[:, :], ps1[:, 1, 256:512], b_gx3[:, :], ALU.add).then_inc(L3x_vector_done, 1)
                dve.tensor_scalar(jk1[:, :], ps1[:, 1, 0:256], 0.0, None, ALU.min).then_inc(L3x_vector_done, 1)
                dve.wait_ge(L3x_scalar_done, 18*b + 28)
                dve.scalar_tensor_tensor(k3_1[:, :], ps1[:, 2, 0:256], 0.0, ks_1[:, :], ALU.max, ALU.add).then_inc(L3x_vector_done, 1)
                dve.wait_ge(L3x_vector_done, 26*b + 36)
                dve.tensor_scalar(ga_1[:, :], ga_1[:, :], -80.0, None, ALU.max).then_inc(L3x_vector_done, 1)
                dve.wait_ge(L3x_matmul_done, 16*b + 21)
                dve.tensor_tensor(BD_0[:, :, 0:128].rearrange('p c (h e) -> p c h e', h=8), ps0[:, 3, 0:258].rearrange('p (c e) -> p c e', c=2)[:, :, 0:128].rearrange('p c (h e) -> p c h e', h=8), mask16[:, None, :].unsqueeze(3).to_broadcast([128, 2, 8, 16]), ALU.mult)
                dve.wait_ge(L3x_scalar_done, 18*b + 30)
                dve.scalar_tensor_tensor(q3_1[:, :], ps1[:, 1, 0:256], 0.0, jk1[:, :], ALU.max, ALU.add).then_inc(L3x_vector_done, 1)
                for c in range(2):
                    last = dve.tensor_tensor(BD_0[:, c, 128:136], ps0[:, 3, 129 * c + 128:129 * c + 129].to_broadcast([128, 8]), mask16[:, :], ALU.mult)
                last.then_inc(L3x_vector_done, 1)
                dve.wait_ge(L3x_matmul_done, 16*b + 22)
                dve.tensor_tensor(BD_1[:, :, 0:128].rearrange('p c (h e) -> p c h e', h=8), ps1[:, 3, 0:258].rearrange('p (c e) -> p c e', c=2)[:, :, 0:128].rearrange('p c (h e) -> p c h e', h=8), mask16[:, None, :].unsqueeze(3).to_broadcast([128, 2, 8, 16]), ALU.mult)
                for c in range(2):
                    last = dve.tensor_tensor(BD_1[:, c, 128:136], ps1[:, 3, 129 * c + 128:129 * c + 129].to_broadcast([128, 8]), mask16[:, :], ALU.mult)
                last.then_inc(L3x_vector_done, 1)
                dve.wait_ge(L3x_matmul_done, 16*b + 24)
                dve.tensor_scalar(rd_0[:, :].rearrange('p (c h) -> p c h', c=2), ps0[:, 1, 0:272].rearrange('p (c e) -> p c e', c=2)[:, :, 128:136], 1e-6, None, ALU.add).then_inc(L3x_vector_done, 1)
                dve.wait_ge(L3x_pool_done, 4*b + 4)
                dve.reciprocal(ga_1[:, :], ga_1[:, :])
                dve.wait_ge(L3x_matmul_done, 16*b + 25)
                dve.tensor_scalar(rd_1[:, :].rearrange('p (c h) -> p c h', c=2), ps1[:, 1, 0:272].rearrange('p (c e) -> p c e', c=2)[:, :, 128:136], 1e-6, None, ALU.add).then_inc(L3x_vector_done, 1)
                dve.wait_ge(L3x_vector_done, 26*b + 43)
                dve.reciprocal(rd_0[:, :], rd_0[:, :]).then_inc(L3x_vector_done, 1)
                dve.wait_ge(L3x_vector_done, 26*b + 44)
                dve.reciprocal(rd_1[:, :], rd_1[:, :]).then_inc(L3x_vector_done, 1)
                dve.wait_ge(L3x_vector_done, 26*b + 45)
                dve.tensor_tensor(a3_0[:, :].rearrange('p (c h e) -> p c h e', c=2, h=8), ps0[:, 1, 0:272].rearrange('p (c e) -> p c e', c=2)[:, :, 0:128].rearrange('p c (h e) -> p c h e', h=8), rd_0[:, :].rearrange('p (c h) -> p c h', c=2).unsqueeze(3).to_broadcast([128, 2, 8, 16]), ALU.mult).then_inc(L3x_vector_done, 1)
                dve.wait_ge(L3x_vector_done, 26*b + 46)
                dve.tensor_tensor(a3_1[:, :].rearrange('p (c h e) -> p c h e', c=2, h=8), ps1[:, 1, 0:272].rearrange('p (c e) -> p c e', c=2)[:, :, 0:128].rearrange('p c (h e) -> p c h e', h=8), rd_1[:, :].rearrange('p (c h) -> p c h', c=2).unsqueeze(3).to_broadcast([128, 2, 8, 16]), ALU.mult).then_inc(L3x_vector_done, 1)
                dve.wait_ge(L3x_matmul_done, 16*b + 28)
                dve.tensor_tensor(x[:, 2*b+0, :], ps0[:, 1, 0:256], x[:, 2*b+0, :], ALU.add).then_inc(L3x_vector_done, 1)
                dve.wait_ge(L3x_matmul_done, 16*b + 29)
                dve.tensor_tensor(x[:, 2*b+1, :], ps1[:, 1, 0:256], x[:, 2*b+1, :], ALU.add).then_inc(L3x_vector_done, 1)

            dve.sem_inc(L3f_vector_done, 51)
            dve.wait_ge(L3x_vector_done, 116)
            dve.wait_ge(L3x_scalar_done, 85)
            dve.wait_ge(L3x_matmul_done, 70)
            dve.memset(v_0[:, :, 16:17], 1.0)
            dve.wait_ge(L3x_vector_done, 120)
            dve.wait_ge(L3x_matmul_done, 73)
            dve.memset(v_1[:, :, 16:17], 1.0)
            dve.wait_ge(L3x_vector_done, 128)
            dve.bn_stats(st0[:, 0:6], x[:, 0, :]).then_inc(L3f_vector_done, 1)
            dve.bn_stats(st1[:, 0:6], x[:, 1, :]).then_inc(L3f_vector_done, 1)
            dve.wait_ge(L3f_vector_done, 52)
            dve.bn_aggr(st0[:, 6:8], st0[:, 0:6]).then_inc(L3f_vector_done, 1)
            dve.wait_ge(L3f_vector_done, 53)
            dve.bn_aggr(st1[:, 6:8], st1[:, 0:6]).then_inc(L3f_vector_done, 1)
            dve.wait_ge(L3x_matmul_done, 78)
            dve.wait_ge(L3f_scalar_done, 30)
            dve.tensor_scalar(u0[:, :], x[:, 0, :], st0[:, 6:7], st0[:, 9:10], ALU.subtract, ALU.mult).then_inc(L3f_vector_done, 1)
            dve.wait_ge(L3x_matmul_done, 79)
            dve.wait_ge(L3f_scalar_done, 31)
            dve.tensor_scalar(u1[:, :], x[:, 1, :], st1[:, 6:7], st1[:, 9:10], ALU.subtract, ALU.mult).then_inc(L3f_vector_done, 1)
            dve.wait_ge(L3f_w_loaded, 144)
            dve.wait_ge(L3f_scalar_done, 36)
            dve.scalar_tensor_tensor(un0[:, :], u0[:, :], st0[:, 12:13], l1w[:, :], ALU.mult, ALU.mult).then_inc(L3f_vector_done, 1)
            dve.wait_ge(L3f_scalar_done, 37)
            dve.scalar_tensor_tensor(un1[:, :], u1[:, :], st1[:, 12:13], l1w[:, :], ALU.mult, ALU.mult).then_inc(L3f_vector_done, 1)
            dve.wait_ge(L3f_w_loaded, 144)
            dve.wait_ge(L3x_pool_done, 18)
            dve.wait_ge(L3f_matmul_done, 2)
            with dve.Fori(0, 4) as b:
                dve.wait_ge(L3f_vector_done, 61*b + 1)
                dve.sem_inc(dve_waited, 1)
                dve.bn_stats(st0[:, 0:6], x_next[:, 2*b+0, :]).then_inc(L3f_vector_done, 1)
                dve.wait_ge(L3f_vector_done, 61*b + 2)
                dve.sem_inc(dve_waited, 1)
                dve.bn_stats(st1[:, 0:6], x_next[:, 2*b+1, :]).then_inc(L3f_vector_done, 1)
                dve.wait_ge(L3f_vector_done, 61*b + 60)
                dve.wait_ge(L3f_scalar_done, 44*b + 1)
                dve.sem_inc(dve_waited, 1)
                dve.bn_aggr(st0[:, 6:8], st0[:, 0:6]).then_inc(L3f_vector_done, 1)
                dve.wait_ge(L3f_vector_done, 61*b + 61)
                dve.wait_ge(L3f_scalar_done, 44*b + 3)
                dve.sem_inc(dve_waited, 1)
                dve.bn_aggr(st1[:, 6:8], st1[:, 0:6]).then_inc(L3f_vector_done, 1)
                dve.wait_ge(L3f_scalar_done, 44*b + 43)
                dve.wait_ge(L3f_matmul_done, 38*b + 1)
                dve.scalar_tensor_tensor(un0[:, :], u0[:, :], st0[:, 12:13], l2w[:, :], ALU.mult, ALU.mult)
                dve.wait_ge(L3f_scalar_done, 44*b + 44)
                dve.wait_ge(L3f_matmul_done, 38*b + 2)
                dve.scalar_tensor_tensor(un1[:, :], u1[:, :], st1[:, 12:13], l2w[:, :], ALU.mult, ALU.mult)
                dve.wait_ge(L3f_scalar_done, 44*b + 46)
                dve.tensor_tensor(kM3_0[:, 0, :, :], ps0[:, 1, 256:384].unsqueeze(1).to_broadcast([128, 8, 128]), mask16[:, :].unsqueeze(2).to_broadcast([128, 8, 128]), ALU.mult)
                dve.tensor_tensor(kM3_0[:, 1, :, :], ps0[:, 1, 384:512].unsqueeze(1).to_broadcast([128, 8, 128]), mask16[:, :].unsqueeze(2).to_broadcast([128, 8, 128]), ALU.mult).then_inc(L3f_vector_done, 1)
                dve.wait_ge(L3f_scalar_done, 44*b + 48)
                dve.tensor_tensor(kM3_1[:, 0, :, :], ps1[:, 1, 256:384].unsqueeze(1).to_broadcast([128, 8, 128]), mask16[:, :].unsqueeze(2).to_broadcast([128, 8, 128]), ALU.mult)
                dve.tensor_tensor(kM3_1[:, 1, :, :], ps1[:, 1, 384:512].unsqueeze(1).to_broadcast([128, 8, 128]), mask16[:, :].unsqueeze(2).to_broadcast([128, 8, 128]), ALU.mult).then_inc(L3f_vector_done, 1)
                dve.wait_ge(L3f_matmul_done, 38*b + 7)
                dve.tensor_tensor(S_0[:, :, :], ps0[:, 1, :].rearrange("p (h s) -> p h s", h=4), causal[:, None, :].to_broadcast([128, 4, 128]), ALU.add).then_inc(L3f_vector_done, 1)
                dve.wait_ge(L3f_vector_done, 61*b + 66)
                dve.tensor_reduce(st0[:, 16:20], S_0[:, :, :], AX.X, ALU.max).then_inc(L3f_vector_done, 1)
                dve.wait_ge(L3f_matmul_done, 38*b + 8)
                dve.tensor_tensor(S_1[:, :, :], ps1[:, 1, :].rearrange("p (h s) -> p h s", h=4), causal[:, None, :].to_broadcast([128, 4, 128]), ALU.add).then_inc(L3f_vector_done, 1)
                dve.wait_ge(L3f_vector_done, 61*b + 67)
                dve.tensor_scalar(st0[:, 16:20], st0[:, 16:20], -0.25, None, ALU.mult).then_inc(L3f_vector_done, 1)
                dve.wait_ge(L3f_vector_done, 61*b + 68)
                dve.tensor_reduce(st1[:, 16:20], S_1[:, :, :], AX.X, ALU.max).then_inc(L3f_vector_done, 1)
                dve.wait_ge(L3f_vector_done, 61*b + 70)
                dve.tensor_scalar(st1[:, 16:20], st1[:, 16:20], -0.25, None, ALU.mult).then_inc(L3f_vector_done, 1)
                dve.wait_ge(L3f_matmul_done, 38*b + 9)
                dve.tensor_tensor(S_0[:, :, :], ps0[:, 1, :].rearrange("p (h s) -> p h s", h=4), causal[:, None, :].to_broadcast([128, 4, 128]), ALU.add).then_inc(L3f_vector_done, 1)
                dve.wait_ge(L3f_vector_done, 61*b + 72)
                dve.tensor_reduce(st0[:, 16:20], S_0[:, :, :], AX.X, ALU.max).then_inc(L3f_vector_done, 1)
                dve.wait_ge(L3f_vector_done, 61*b + 73)
                dve.tensor_scalar(st0[:, 16:20], st0[:, 16:20], -0.25, None, ALU.mult).then_inc(L3f_vector_done, 1)
                dve.wait_ge(L3f_matmul_done, 38*b + 10)
                dve.tensor_tensor(S_1[:, :, :], ps1[:, 1, :].rearrange("p (h s) -> p h s", h=4), causal[:, None, :].to_broadcast([128, 4, 128]), ALU.add).then_inc(L3f_vector_done, 1)
                dve.wait_ge(L3f_matmul_done, 38*b + 11)
                dve.reciprocal(st0[:, 20:24], ps0[:, 3, 0:68].rearrange('p (h e) -> p h e', h=4)[:, :, 16]).then_inc(L3f_vector_done, 1)
                dve.wait_ge(L3f_vector_done, 61*b + 75)
                dve.tensor_reduce(st1[:, 16:20], S_1[:, :, :], AX.X, ALU.max).then_inc(L3f_vector_done, 1)
                dve.wait_ge(L3f_vector_done, 61*b + 76)
                dve.tensor_tensor(ao_0[:, 0:64].rearrange('p (h d) -> p h d', h=4), ps0[:, 3, 0:68].rearrange('p (h e) -> p h e', h=4)[:, :, 0:16], st0[:, 20:24].unsqueeze(2).to_broadcast([128, 4, 16]), ALU.mult)
                dve.wait_ge(L3f_vector_done, 61*b + 77)
                dve.tensor_scalar(st1[:, 16:20], st1[:, 16:20], -0.25, None, ALU.mult).then_inc(L3f_vector_done, 1)
                dve.wait_ge(L3f_matmul_done, 38*b + 12)
                dve.tensor_tensor(S_0[:, :, :], ps0[:, 1, :].rearrange("p (h s) -> p h s", h=4), causal[:, None, :].to_broadcast([128, 4, 128]), ALU.add).then_inc(L3f_vector_done, 1)
                dve.wait_ge(L3f_matmul_done, 38*b + 13)
                dve.reciprocal(st1[:, 20:24], ps1[:, 3, 0:68].rearrange('p (h e) -> p h e', h=4)[:, :, 16]).then_inc(L3f_vector_done, 1)
                dve.wait_ge(L3f_vector_done, 61*b + 79)
                dve.tensor_reduce(st0[:, 16:20], S_0[:, :, :], AX.X, ALU.max).then_inc(L3f_vector_done, 1)
                dve.wait_ge(L3f_vector_done, 61*b + 80)
                dve.tensor_tensor(ao_1[:, 0:64].rearrange('p (h d) -> p h d', h=4), ps1[:, 3, 0:68].rearrange('p (h e) -> p h e', h=4)[:, :, 0:16], st1[:, 20:24].unsqueeze(2).to_broadcast([128, 4, 16]), ALU.mult)
                dve.wait_ge(L3f_vector_done, 61*b + 81)
                dve.tensor_scalar(st0[:, 16:20], st0[:, 16:20], -0.25, None, ALU.mult).then_inc(L3f_vector_done, 1)
                dve.wait_ge(L3f_matmul_done, 38*b + 14)
                dve.tensor_tensor(S_1[:, :, :], ps1[:, 1, :].rearrange("p (h s) -> p h s", h=4), causal[:, None, :].to_broadcast([128, 4, 128]), ALU.add).then_inc(L3f_vector_done, 1)
                dve.wait_ge(L3f_matmul_done, 38*b + 15)
                dve.reciprocal(st0[:, 20:24], ps0[:, 3, 0:68].rearrange('p (h e) -> p h e', h=4)[:, :, 16]).then_inc(L3f_vector_done, 1)
                dve.wait_ge(L3f_vector_done, 61*b + 83)
                dve.tensor_reduce(st1[:, 16:20], S_1[:, :, :], AX.X, ALU.max).then_inc(L3f_vector_done, 1)
                dve.wait_ge(L3f_vector_done, 61*b + 84)
                dve.tensor_tensor(ao_0[:, 64:128].rearrange('p (h d) -> p h d', h=4), ps0[:, 3, 0:68].rearrange('p (h e) -> p h e', h=4)[:, :, 0:16], st0[:, 20:24].unsqueeze(2).to_broadcast([128, 4, 16]), ALU.mult)
                dve.wait_ge(L3f_vector_done, 61*b + 85)
                dve.tensor_scalar(st1[:, 16:20], st1[:, 16:20], -0.25, None, ALU.mult).then_inc(L3f_vector_done, 1)
                dve.wait_ge(L3f_matmul_done, 38*b + 16)
                dve.tensor_tensor(S_0[:, :, :], ps0[:, 1, :].rearrange("p (h s) -> p h s", h=4), causal[:, None, :].to_broadcast([128, 4, 128]), ALU.add).then_inc(L3f_vector_done, 1)
                dve.wait_ge(L3f_matmul_done, 38*b + 17)
                dve.reciprocal(st1[:, 20:24], ps1[:, 3, 0:68].rearrange('p (h e) -> p h e', h=4)[:, :, 16]).then_inc(L3f_vector_done, 1)
                dve.wait_ge(L3f_vector_done, 61*b + 87)
                dve.tensor_reduce(st0[:, 16:20], S_0[:, :, :], AX.X, ALU.max).then_inc(L3f_vector_done, 1)
                dve.wait_ge(L3f_vector_done, 61*b + 88)
                dve.tensor_tensor(ao_1[:, 64:128].rearrange('p (h d) -> p h d', h=4), ps1[:, 3, 0:68].rearrange('p (h e) -> p h e', h=4)[:, :, 0:16], st1[:, 20:24].unsqueeze(2).to_broadcast([128, 4, 16]), ALU.mult).then_inc(L3f_vector_done, 1)
                dve.wait_ge(L3f_vector_done, 61*b + 89)
                dve.tensor_scalar(st0[:, 16:20], st0[:, 16:20], -0.25, None, ALU.mult).then_inc(L3f_vector_done, 1)
                dve.wait_ge(L3f_matmul_done, 38*b + 18)
                dve.tensor_tensor(S_1[:, :, :], ps1[:, 1, :].rearrange("p (h s) -> p h s", h=4), causal[:, None, :].to_broadcast([128, 4, 128]), ALU.add).then_inc(L3f_vector_done, 1)
                dve.wait_ge(L3f_vector_done, 61*b + 92)
                dve.tensor_reduce(st1[:, 16:20], S_1[:, :, :], AX.X, ALU.max).then_inc(L3f_vector_done, 1)
                dve.wait_ge(L3f_matmul_done, 38*b + 19)
                dve.reciprocal(st0[:, 20:24], ps0[:, 3, 0:68].rearrange('p (h e) -> p h e', h=4)[:, :, 16]).then_inc(L3f_vector_done, 1)
                dve.wait_ge(L3f_vector_done, 61*b + 93)
                dve.tensor_scalar(st1[:, 16:20], st1[:, 16:20], -0.25, None, ALU.mult).then_inc(L3f_vector_done, 1)
                dve.wait_ge(L3f_matmul_done, 38*b + 20)
                dve.reciprocal(st1[:, 20:24], ps1[:, 3, 0:68].rearrange('p (h e) -> p h e', h=4)[:, :, 16]).then_inc(L3f_vector_done, 1)
                dve.wait_ge(L3f_vector_done, 61*b + 94)
                dve.tensor_tensor(ao_0[:, 128:192].rearrange('p (h d) -> p h d', h=4), ps0[:, 3, 0:68].rearrange('p (h e) -> p h e', h=4)[:, :, 0:16], st0[:, 20:24].unsqueeze(2).to_broadcast([128, 4, 16]), ALU.mult).then_inc(L3f_vector_done, 1)
                dve.wait_ge(L3f_vector_done, 61*b + 96)
                dve.tensor_tensor(ao_1[:, 128:192].rearrange('p (h d) -> p h d', h=4), ps1[:, 3, 0:68].rearrange('p (h e) -> p h e', h=4)[:, :, 0:16], st1[:, 20:24].unsqueeze(2).to_broadcast([128, 4, 16]), ALU.mult).then_inc(L3f_vector_done, 1)
                dve.wait_ge(L3f_matmul_done, 38*b + 23)
                dve.reciprocal(st0[:, 20:24], ps0[:, 3, 0:68].rearrange('p (h e) -> p h e', h=4)[:, :, 16]).then_inc(L3f_vector_done, 1)
                dve.wait_ge(L3f_vector_done, 61*b + 99)
                dve.tensor_tensor(ao_0[:, 192:256].rearrange('p (h d) -> p h d', h=4), ps0[:, 3, 0:68].rearrange('p (h e) -> p h e', h=4)[:, :, 0:16], st0[:, 20:24].unsqueeze(2).to_broadcast([128, 4, 16]), ALU.mult).then_inc(L3f_vector_done, 1)
                dve.wait_ge(L3f_matmul_done, 38*b + 24)
                dve.reciprocal(st1[:, 20:24], ps1[:, 3, 0:68].rearrange('p (h e) -> p h e', h=4)[:, :, 16]).then_inc(L3f_vector_done, 1)
                dve.wait_ge(L3f_vector_done, 61*b + 101)
                dve.tensor_tensor(ao_1[:, 192:256].rearrange('p (h d) -> p h d', h=4), ps1[:, 3, 0:68].rearrange('p (h e) -> p h e', h=4)[:, :, 0:16], st1[:, 20:24].unsqueeze(2).to_broadcast([128, 4, 16]), ALU.mult).then_inc(L3f_vector_done, 1)
                dve.wait_ge(L3f_matmul_done, 38*b + 29)
                dve.tensor_scalar(md_0[0:16, :], ps0[0:16, 2, 0:128], 20.0, None, ALU.min).then_inc(L3f_vector_done, 1)
                dve.wait_ge(L3f_matmul_done, 38*b + 32)
                dve.tensor_scalar(md_1[0:16, :], ps1[0:16, 2, 0:128], 20.0, None, ALU.min).then_inc(L3f_vector_done, 1)
                dve.wait_ge(L3f_scalar_done, 44*b + 70)
                dve.tensor_scalar(md_0[0:16, :], md_0[0:16, :], 1.0, None, ALU.add).then_inc(L3f_vector_done, 1)
                dve.wait_ge(L3f_vector_done, 61*b + 105)
                dve.reciprocal(md_0[0:16, :], md_0[0:16, :]).then_inc(L3f_vector_done, 1)
                dve.wait_ge(L3f_scalar_done, 44*b + 72)
                dve.tensor_scalar(md_1[0:16, :], md_1[0:16, :], 1.0, None, ALU.add).then_inc(L3f_vector_done, 1)
                dve.wait_ge(L3f_vector_done, 61*b + 106)
                dve.tensor_scalar(md_0[0:16, :], md_0[0:16, :], -0.2, 0.1, ALU.mult, ALU.add).then_inc(L3f_vector_done, 1)
                dve.wait_ge(L3f_vector_done, 61*b + 107)
                dve.reciprocal(md_1[0:16, :], md_1[0:16, :]).then_inc(L3f_vector_done, 1)
                dve.wait_ge(L3f_matmul_done, 38*b + 33)
                dve.wait_ge(L3f_vector_done, 61*b + 108)
                dve.tensor_tensor(hA_0[0:16, :], ps0[0:16, 2, 128:256], md_0[0:16, :], ALU.mult).then_inc(L3f_vector_done, 1)
                dve.wait_ge(L3f_vector_done, 61*b + 109)
                dve.tensor_scalar(md_1[0:16, :], md_1[0:16, :], -0.2, 0.1, ALU.mult, ALU.add).then_inc(L3f_vector_done, 1)
                dve.wait_ge(L3f_matmul_done, 38*b + 34)
                dve.wait_ge(L3f_vector_done, 61*b + 111)
                dve.tensor_tensor(hA_1[0:16, :], ps1[0:16, 2, 128:256], md_1[0:16, :], ALU.mult).then_inc(L3f_vector_done, 1)
                dve.wait_ge(L3f_scalar_done, 44*b + 73)
                dve.tensor_tensor(m3_0[:, :], tt_0[:, :], psf0[:, 1024:2048], ALU.mult).then_inc(L3f_vector_done, 1)
                dve.wait_ge(L3f_scalar_done, 44*b + 74)
                dve.tensor_tensor(m3_1[:, :], tt_1[:, :], psf1[:, 1024:2048], ALU.mult).then_inc(L3f_vector_done, 1)
                dve.wait_ge(L3f_matmul_done, 38*b + 37)
                dve.tensor_tensor(u0[:, :], u0[:, :], ps0[:, 0, 0:256], ALU.add).then_inc(L3f_vector_done, 1)
                dve.wait_ge(L3f_matmul_done, 38*b + 38)
                dve.tensor_tensor(u1[:, :], u1[:, :], ps1[:, 0, 0:256], ALU.add).then_inc(L3f_vector_done, 1)
                dve.wait_ge(L3f_pool_done, 2*b + 1)
                dve.tensor_scalar(u0[:, :], x_next[:, 2*b+0, :], st0[:, 6:7], st0[:, 9:10], ALU.subtract, ALU.mult).then_inc(L3f_vector_done, 1)
                dve.wait_ge(L3f_pool_done, 2*b + 2)
                dve.tensor_scalar(u1[:, :], x_next[:, 2*b+1, :], st1[:, 6:7], st1[:, 9:10], ALU.subtract, ALU.mult).then_inc(L3f_vector_done, 1)
                dve.wait_ge(L3f_scalar_done, 44*b + 79)
                dve.scalar_tensor_tensor(un0[:, :], u0[:, :], st0[:, 12:13], l1w[:, :], ALU.mult, ALU.mult).then_inc(L3f_vector_done, 1)
                dve.wait_ge(L3f_scalar_done, 44*b + 80)
                dve.scalar_tensor_tensor(un1[:, :], u1[:, :], st1[:, 12:13], l1w[:, :], ALU.mult, ALU.mult).then_inc(L3f_vector_done, 1)

        @block.tensor
        def _(pe):

            pe.wait_ge(L0a_vector_done, 17)
            for k in range(2):
                last = pe.transpose(ps0[:, 0, 128 * k:128 * k + 128], un0[:, 128 * k:128 * k + 128], ident[:, :])
            last.then_inc(L0a_matmul_done, 1)
            pe.wait_ge(L0a_vector_done, 18)
            for k in range(2):
                last = pe.transpose(ps1[:, 0, 128 * k:128 * k + 128], un1[:, 128 * k:128 * k + 128], ident[:, :])
            last.then_inc(L0a_matmul_done, 1)
            pe.wait_ge(L0a_scalar_done, 18)
            with pe.Fori(0, 4) as b:
                pe.wait_ge(L0a_scalar_done, 18*b + 17)
                for j in range(8):
                    for k in range(2):
                        last = pe.matmul(psf0[:, 512 + 128 * j:640 + 128 * j], w_in[:, k, 128 * j:128 * j + 128], unT0[:, k, :], start=k == 0, stop=k == 1)
                last.then_inc(L0a_matmul_done, 1)
                pe.wait_ge(L0a_scalar_done, 18*b + 18)
                for j in range(8):
                    for k in range(2):
                        last = pe.matmul(psf1[:, 512 + 128 * j:640 + 128 * j], w_in[:, k, 128 * j:128 * j + 128], unT1[:, k, :], start=k == 0, stop=k == 1)
                last.then_inc(L0a_matmul_done, 1)
                pe.wait_ge(L0a_scalar_done, 18*b + 23)
                for j in range(2):
                    last = pe.matmul(ps0[:, 3, 128 * j:128 * j + 128], w_dt[:, 128 * j:128 * j + 128], f0[:, 3, :], start=True, stop=True)
                last.then_inc(L0a_matmul_done, 1)
                pe.wait_ge(L0a_scalar_done, 18*b + 24)
                for j in range(2):
                    last = pe.matmul(ps1[:, 3, 128 * j:128 * j + 128], w_dt[:, 128 * j:128 * j + 128], f1[:, 3, :], start=True, stop=True)
                last.then_inc(L0a_matmul_done, 1)
                pe.wait_ge(L0a_vector_done, 20*b + 37)
                for k in range(2):
                    last = pe.transpose(ps0[:, 0, 128 * k:128 * k + 128], un0[:, 128 * k:128 * k + 128], ident[:, :])
                last.then_inc(L0a_matmul_done, 1)
                pe.wait_ge(L0a_vector_done, 20*b + 38)
                for k in range(2):
                    last = pe.transpose(ps1[:, 0, 128 * k:128 * k + 128], un1[:, 128 * k:128 * k + 128], ident[:, :])
                last.then_inc(L0a_matmul_done, 1)
            pe.wait_ge(L0a_vector_done, 96)
            pe.wait_ge(L0a_scalar_done, 90)
            with pe.Fori(0, 32) as n:
                pe.wait_ge(L0a_vector_done, 6*n + 94)
                pe.sem_inc(pe_waited, 1)
                for h in range(2):
                    for q in range(3):
                        last = pe.matmul(ps0[:, h, :], idb[:, ds(n + 32 * 0, 1)].to_broadcast([128, 128]), s3[:, q, 0, 4 * h:4 * h + 4, :], start=q == 0, stop=q == 2)
                last.then_inc(L0a_matmul_done, 1)
                pe.wait_ge(L0a_vector_done, 6*n + 96)
                pe.sem_inc(pe_waited, 1)
                for h in range(2):
                    for q in range(3):
                        last = pe.matmul(ps1[:, h, :], idb[:, ds(n + 32 * 1, 1)].to_broadcast([128, 128]), s3[:, q, 0, 4 * h:4 * h + 4, :], start=q == 0, stop=q == 2)
                last.then_inc(L0a_matmul_done, 1)
                pe.wait_ge(L0a_vector_done, 6*n + 97)
                pe.sem_inc(pe_waited, 1)
                for h in range(2):
                    for q in range(3):
                        last = pe.matmul(ps0[:, 2 + h, :], selC[:, n, :], s3[:, q, 1 + 0, 4 * h:4 * h + 4, :], start=q == 0, stop=q == 2)
                last.then_inc(L0a_matmul_done, 1)
                pe.wait_ge(L0a_vector_done, 6*n + 99)
                pe.sem_inc(pe_waited, 1)
                for h in range(2):
                    for q in range(3):
                        last = pe.matmul(ps1[:, 2 + h, :], selC[:, n, :], s3[:, q, 1 + 1, 4 * h:4 * h + 4, :], start=q == 0, stop=q == 2)
                last.then_inc(L0a_matmul_done, 1)
            pe.wait_ge(L0a_scalar_done, 154)
            pe.wait_ge(L0a_vector_done, 291)
            with pe.Fori(0, 4) as b:
                pe.wait_ge(L0a_vector_done, 12*b + 294)
                for k in range(2):
                    last = pe.matmul(ps0[:, 0, 0:256], sp0[:, k, :], w_mo[:, k, :], start=k == 0, stop=k == 1)
                last.then_inc(L0a_matmul_done, 1)
                pe.wait_ge(L0a_vector_done, 12*b + 295)
                for k in range(2):
                    last = pe.matmul(ps1[:, 0, 0:256], sp1[:, k, :], w_mo[:, k, :], start=k == 0, stop=k == 1)
                last.then_inc(L0a_matmul_done, 1)
                pe.wait_ge(L0a_vector_done, 12*b + 298)
                for k in range(2):
                    last = pe.transpose(ps0[:, 0, 128 * k:128 * k + 128], un0[:, 128 * k:128 * k + 128], ident[:, :])
                last.then_inc(L0a_matmul_done, 1)
                pe.wait_ge(L0a_vector_done, 12*b + 299)
                for k in range(2):
                    last = pe.transpose(ps1[:, 0, 128 * k:128 * k + 128], un1[:, 128 * k:128 * k + 128], ident[:, :])
                last.then_inc(L0a_matmul_done, 1)
                pe.wait_ge(L0a_scalar_done, 12*b + 163)
                for j in range(6):
                    for k in range(2):
                        pe.matmul(psf0[:, 512 + 128 * j:640 + 128 * j], w_gate[:, k, 128 * j:128 * j + 128], unT0[:, k, :], start=k == 0, stop=k == 1)
                pe.wait_ge(L0a_scalar_done, 12*b + 164)
                for j in range(6):
                    for k in range(2):
                        last = pe.matmul(psf1[:, 512 + 128 * j:640 + 128 * j], w_gate[:, k, 128 * j:128 * j + 128], unT1[:, k, :], start=k == 0, stop=k == 1)
                last.then_inc(L0a_matmul_done, 1)
                for j in range(6):
                    for k in range(2):
                        last = pe.matmul(psf0[:, 1280 + 128 * j:1408 + 128 * j], w_up[:, k, 128 * j:128 * j + 128], unT0[:, k, :], start=k == 0, stop=k == 1)
                last.then_inc(L0a_matmul_done, 1)
                for j in range(6):
                    for k in range(2):
                        last = pe.matmul(psf1[:, 1280 + 128 * j:1408 + 128 * j], w_up[:, k, 128 * j:128 * j + 128], unT1[:, k, :], start=k == 0, stop=k == 1)
                last.then_inc(L0a_matmul_done, 1)
                pe.wait_ge(L0a_vector_done, 12*b + 300)
                for k in range(6):
                    last = pe.matmul(ps0[:, 0, 0:256], m0[:, 128 * k:128 * k + 128], w_dn[:, k, :], start=k == 0, stop=k == 5)
                last.then_inc(L0a_matmul_done, 1)
                pe.wait_ge(L0a_vector_done, 12*b + 301)
                for k in range(6):
                    last = pe.matmul(ps1[:, 0, 0:256], m1[:, 128 * k:128 * k + 128], w_dn[:, k, :], start=k == 0, stop=k == 5)
                last.then_inc(L0a_matmul_done, 1)

            pe.wait_ge(L0x_w_loaded, 160)
            pe.wait_ge(L0x_vector_done, 36)
            with pe.Fori(0, 4) as b:
                pe.wait_ge(L0x_vector_done, 38*b + 1)
                pe.sem_inc(pe_waited, 1)
                pe.matmul(ps0[0:64, 0, 0:256], w_th[:, :], ctx[:, 2*b+0, :], start=True, stop=True)
                pe.wait_ge(L0x_vector_done, 38*b + 2)
                pe.sem_inc(pe_waited, 1)
                pe.matmul(ps1[0:64, 0, 0:256], w_th[:, :], ctx[:, 2*b+1, :], start=True, stop=True)
                pe.wait_ge(L0x_vector_done, 38*b + 35)
                pe.matmul(ps0[0:64, 1, 0:256], w_ph[:, :], u0[:, :], start=True, stop=True).then_inc(L0x_matmul_done, 1)
                pe.wait_ge(L0x_vector_done, 38*b + 36)
                pe.matmul(ps1[0:64, 1, 0:256], w_ph[:, :], u1[:, :], start=True, stop=True).then_inc(L0x_matmul_done, 1)
                for k in range(2):
                    last = pe.matmul(ps0[:, 0, 256 + 64 * k:320 + 64 * k], u0[:, 128 * k:128 * k + 128], w_g[:, :], start=True, stop=True)
                last.then_inc(L0x_matmul_done, 1)
                for k in range(2):
                    last = pe.matmul(ps1[:, 0, 256 + 64 * k:320 + 64 * k], u1[:, 128 * k:128 * k + 128], w_g[:, :], start=True, stop=True)
                last.then_inc(L0x_matmul_done, 1)
                pe.wait_ge(L0x_vector_done, 38*b + 37)
                pe.wait_ge(L0x_scalar_done, 12*b + 1)
                for t in range(2):
                    last = pe.matmul(ps0[:, 2, 256 * t:256 * t + 256], thT0[0:64, 128 * t:128 * t + 128], phT0[0:64, :], start=True, stop=True)
                last.then_inc(L0x_matmul_done, 1)
                pe.wait_ge(L0x_vector_done, 38*b + 38)
                pe.wait_ge(L0x_scalar_done, 12*b + 2)
                for t in range(2):
                    last = pe.matmul(ps1[:, 2, 256 * t:256 * t + 256], thT1[0:64, 128 * t:128 * t + 128], phT1[0:64, :], start=True, stop=True)
                last.then_inc(L0x_matmul_done, 1)
                pe.wait_ge(L0x_pool_done, 4*b + 5)
                for c in range(4):
                    last = pe.transpose(ps0[:, 3, 128 * c:128 * c + 128], S0[:, c // 2, 128 * (c % 2):128 * (c % 2) + 128], ident[:, :])
                last.then_inc(L0x_matmul_done, 1)
                pe.wait_ge(L0x_pool_done, 4*b + 6)
                for c in range(4):
                    last = pe.transpose(ps1[:, 3, 128 * c:128 * c + 128], S1[:, c // 2, 128 * (c % 2):128 * (c % 2) + 128], ident[:, :])
                last.then_inc(L0x_matmul_done, 1)
                pe.wait_ge(L0x_scalar_done, 12*b + 15)
                for t in range(2):
                    for s in range(2):
                        last = pe.matmul(ps0[0:64, 1, 128 * t:128 * t + 128], g_0[:, s, :], Pm0[:, 2 * t + s, :], start=s == 0, stop=s == 1)
                last.then_inc(L0x_matmul_done, 1)
                pe.wait_ge(L0x_scalar_done, 12*b + 16)
                for t in range(2):
                    for s in range(2):
                        last = pe.matmul(ps1[0:64, 1, 128 * t:128 * t + 128], g_1[:, s, :], Pm1[:, 2 * t + s, :], start=s == 0, stop=s == 1)
                last.then_inc(L0x_matmul_done, 1)
                pe.wait_ge(L0x_vector_done, 38*b + 50)
                pe.sem_inc(pe_waited, 1)
                pe.matmul(ps0[0:64, 1, 256:258], ones[0:64, 0:64], st0[0:64, 6:8], start=True, stop=True).then_inc(L0x_matmul_done, 1)
                pe.wait_ge(L0x_vector_done, 38*b + 58)
                pe.sem_inc(pe_waited, 1)
                pe.matmul(ps1[0:64, 1, 256:258], ones[0:64, 0:64], st1[0:64, 6:8], start=True, stop=True).then_inc(L0x_matmul_done, 1)
                pe.wait_ge(L0x_vector_done, 38*b + 68)
                pe.matmul(ps0[:, 3, 0:256], w_xo[0:64, :], t_0[0:64, :], start=True, stop=True).then_inc(L0x_matmul_done, 1)
                pe.wait_ge(L0x_vector_done, 38*b + 70)
                pe.matmul(ps1[:, 3, 0:256], w_xo[0:64, :], t_1[0:64, :], start=True, stop=True).then_inc(L0x_matmul_done, 1)

            pe.wait_ge(L0f_vector_done, 15)
            for k in range(2):
                last = pe.transpose(ps0[:, 0, 128 * k:128 * k + 128], u0[:, 128 * k:128 * k + 128], ident[:, :])
            last.then_inc(L0f_matmul_done, 1)
            pe.wait_ge(L0f_vector_done, 16)
            for k in range(2):
                last = pe.transpose(ps1[:, 0, 128 * k:128 * k + 128], u1[:, 128 * k:128 * k + 128], ident[:, :])
            last.then_inc(L0f_matmul_done, 1)
            pe.wait_ge(L0f_w_loaded, 64)
            pe.wait_ge(L0f_scalar_done, 20)
            with pe.Fori(0, 4) as b:
                pe.wait_ge(L0f_vector_done, 18*b + 15)
                pe.wait_ge(L0f_scalar_done, 20*b + 17)
                for k in range(2):
                    last = pe.matmul(ps0[:, 1, :], unT0[:, k, :], w_e0[:, k, 0:512], start=k == 0, stop=k == 1)
                last.then_inc(L0f_matmul_done, 1)
                pe.wait_ge(L0f_vector_done, 18*b + 16)
                pe.wait_ge(L0f_scalar_done, 20*b + 18)
                for k in range(2):
                    last = pe.matmul(ps1[:, 1, :], unT1[:, k, :], w_e0[:, k, 0:512], start=k == 0, stop=k == 1)
                last.then_inc(L0f_matmul_done, 1)
                for k in range(2):
                    last = pe.matmul(ps0[:, 0, 256:264], unT0[:, k, :], w_gt0[:, k, :], start=k == 0, stop=k == 1)
                last.then_inc(L0f_matmul_done, 1)
                for k in range(2):
                    last = pe.matmul(ps1[:, 0, 256:264], unT1[:, k, :], w_gt0[:, k, :], start=k == 0, stop=k == 1)
                last.then_inc(L0f_matmul_done, 1)
                for k in range(2):
                    last = pe.matmul(ps0[:, 2, :], unT0[:, k, :], w_e0[:, k, 512:1024], start=k == 0, stop=k == 1)
                last.then_inc(L0f_matmul_done, 1)
                for k in range(2):
                    last = pe.matmul(ps1[:, 2, :], unT1[:, k, :], w_e0[:, k, 512:1024], start=k == 0, stop=k == 1)
                last.then_inc(L0f_matmul_done, 1)
                for k in range(2):
                    last = pe.matmul(ps0[:, 3, :], unT0[:, k, :], w_e0[:, k, 1024:1536], start=k == 0, stop=k == 1)
                last.then_inc(L0f_matmul_done, 1)
                for k in range(2):
                    last = pe.matmul(ps1[:, 3, :], unT1[:, k, :], w_e0[:, k, 1024:1536], start=k == 0, stop=k == 1)
                last.then_inc(L0f_matmul_done, 1)
                pe.wait_ge(L0f_vector_done, 18*b + 21)
                for k in range(2):
                    last = pe.matmul(ps0[:, 1, :], unT0[:, k, :], w_e0[:, k, 1536:2048], start=k == 0, stop=k == 1)
                last.then_inc(L0f_matmul_done, 1)
                pe.wait_ge(L0f_vector_done, 18*b + 22)
                for k in range(2):
                    last = pe.matmul(ps1[:, 1, :], unT1[:, k, :], w_e0[:, k, 1536:2048], start=k == 0, stop=k == 1)
                last.then_inc(L0f_matmul_done, 1)
                pe.wait_ge(L0f_vector_done, 18*b + 23)
                for k in range(2):
                    last = pe.transpose(ps0[:, 0, 128 * k:128 * k + 128], u0[:, 128 * k:128 * k + 128], ident[:, :])
                last.then_inc(L0f_matmul_done, 1)
                pe.wait_ge(L0f_vector_done, 18*b + 24)
                for k in range(2):
                    last = pe.transpose(ps1[:, 0, 128 * k:128 * k + 128], u1[:, 128 * k:128 * k + 128], ident[:, :])
                last.then_inc(L0f_matmul_done, 1)

            pe.wait_ge(L1a_vector_done, 7)
            for k in range(2):
                last = pe.transpose(ps0[:, 0, 128 * k:128 * k + 128], u0[:, 128 * k:128 * k + 128], ident[:, :])
            last.then_inc(L1a_matmul_done, 1)
            pe.wait_ge(L1a_vector_done, 8)
            for k in range(2):
                last = pe.transpose(ps1[:, 0, 128 * k:128 * k + 128], u1[:, 128 * k:128 * k + 128], ident[:, :])
            last.then_inc(L1a_matmul_done, 1)
            pe.wait_ge(L1a_w_loaded, 32)
            pe.wait_ge(L1a_scalar_done, 11)
            with pe.Fori(0, 4) as b:
                pe.wait_ge(L1a_scalar_done, 11*b + 10)
                for k in range(2):
                    last = pe.matmul(ps0[:, 1, :], unT0[:, k, :], w_qkv1[:, k, 0:512], start=k == 0, stop=k == 1)
                last.then_inc(L1a_matmul_done, 1)
                pe.wait_ge(L1a_scalar_done, 11*b + 11)
                for k in range(2):
                    last = pe.matmul(ps1[:, 1, :], unT1[:, k, :], w_qkv1[:, k, 0:512], start=k == 0, stop=k == 1)
                last.then_inc(L1a_matmul_done, 1)
                pe.wait_ge(L1a_vector_done, 10*b + 7)
                for k in range(2):
                    last = pe.matmul(ps0[:, 2, 0:256], unT0[:, k, :], w_qkv1[:, k, 512:768], start=k == 0, stop=k == 1)
                last.then_inc(L1a_matmul_done, 1)
                pe.wait_ge(L1a_vector_done, 10*b + 8)
                for k in range(2):
                    last = pe.matmul(ps1[:, 2, 0:256], unT1[:, k, :], w_qkv1[:, k, 512:768], start=k == 0, stop=k == 1)
                last.then_inc(L1a_matmul_done, 1)
                pe.wait_ge(L1a_vector_done, 10*b + 13)
                pe.matmul(ps0[:, 3, 0:256], tri[:, :], kv1_0[:, :], start=True, stop=True).then_inc(L1a_matmul_done, 1)
                pe.wait_ge(L1a_vector_done, 10*b + 14)
                pe.matmul(ps1[:, 3, 0:256], tri[:, :], kv1_1[:, :], start=True, stop=True).then_inc(L1a_matmul_done, 1)
                pe.wait_ge(L1a_vector_done, 10*b + 15)
                for k in range(2):
                    last = pe.transpose(ps0[:, 0, 128 * k:128 * k + 128], kv1_0[:, 128 * k:128 * k + 128], ident[:, :])
                last.then_inc(L1a_matmul_done, 1)
                pe.wait_ge(L1a_vector_done, 10*b + 16)
                for k in range(2):
                    last = pe.transpose(ps1[:, 0, 128 * k:128 * k + 128], kv1_1[:, 128 * k:128 * k + 128], ident[:, :])
                last.then_inc(L1a_matmul_done, 1)
                pe.wait_ge(L1a_scalar_done, 11*b + 19)
                for k in range(2):
                    last = pe.matmul(ps0[:, 2, 0:256], vT1_0[:, k, :], w_o1[:, k, :], start=k == 0, stop=k == 1)
                last.then_inc(L1a_matmul_done, 1)
                pe.wait_ge(L1a_scalar_done, 11*b + 20)
                for k in range(2):
                    last = pe.matmul(ps1[:, 2, 0:256], vT1_1[:, k, :], w_o1[:, k, :], start=k == 0, stop=k == 1)
                last.then_inc(L1a_matmul_done, 1)
                for k in range(2):
                    last = pe.transpose(ps0[:, 0, 128 * k:128 * k + 128], u0[:, 128 * k:128 * k + 128], ident[:, :])
                last.then_inc(L1a_matmul_done, 1)
                for k in range(2):
                    last = pe.transpose(ps1[:, 0, 128 * k:128 * k + 128], u1[:, 128 * k:128 * k + 128], ident[:, :])
                last.then_inc(L1a_matmul_done, 1)

            pe.wait_ge(ctx_loaded, 32)
            pe.wait_ge(L1x_w_loaded, 112)
            pe.wait_ge(L1a_vector_done, 45)
            pe.wait_ge(L1a_scalar_done, 55)
            with pe.Fori(0, 4) as b:
                pe.wait_ge(L1x_vector_done, 18*b + 1)
                pe.sem_inc(pe_waited, 1)
                for k in range(2):
                    pe.matmul(ps0[:, 0, 0:128], w_i1[:, k, 0:128], ctxT[:, k, ds(128 * (2*b+0), 128)], start=k == 0, stop=k == 1)
                pe.wait_ge(L1x_vector_done, 18*b + 2)
                pe.sem_inc(pe_waited, 1)
                for k in range(2):
                    pe.matmul(ps1[:, 0, 0:128], w_i1[:, k, 0:128], ctxT[:, k, ds(128 * (2*b+1), 128)], start=k == 0, stop=k == 1)
                for k in range(2):
                    last = pe.matmul(ps0[:, 0, 128:256], w_i1[:, k, 128:256], ctxT[:, k, ds(128 * (2*b+0), 128)], start=k == 0, stop=k == 1)
                last.then_inc(L1x_matmul_done, 1)
                for k in range(2):
                    last = pe.matmul(ps1[:, 0, 128:256], w_i1[:, k, 128:256], ctxT[:, k, ds(128 * (2*b+1), 128)], start=k == 0, stop=k == 1)
                last.then_inc(L1x_matmul_done, 1)
                pe.wait_ge(L1x_vector_done, 18*b + 25)
                for k in range(2):
                    last = pe.matmul(ps0[:, 1, 0:256], mn_0[:, k, :], w_oo1[:, k, :], start=k == 0, stop=k == 1)
                last.then_inc(L1x_matmul_done, 1)
                pe.wait_ge(L1x_vector_done, 18*b + 26)
                for k in range(2):
                    last = pe.matmul(ps1[:, 1, 0:256], mn_1[:, k, :], w_oo1[:, k, :], start=k == 0, stop=k == 1)
                last.then_inc(L1x_matmul_done, 1)

            pe.sem_inc(L1f_matmul_done, 16)
            pe.wait_ge(L1f_vector_done, 53)
            for k in range(2):
                last = pe.transpose(ps0[:, 0, 128 * k:128 * k + 128], u0[:, 128 * k:128 * k + 128], ident[:, :])
            last.then_inc(L1f_matmul_done, 1)
            pe.wait_ge(L1f_vector_done, 54)
            for k in range(2):
                last = pe.transpose(ps1[:, 0, 128 * k:128 * k + 128], u1[:, 128 * k:128 * k + 128], ident[:, :])
            last.then_inc(L1f_matmul_done, 1)
            pe.wait_ge(L1f_w_loaded, 80)
            pe.wait_ge(L1f_scalar_done, 22)
            with pe.Fori(0, 4) as b:
                pe.wait_ge(L1f_vector_done, 56*b + 44)
                pe.wait_ge(L1f_scalar_done, 22*b + 20)
                for j in range(4):
                    for k in range(2):
                        last = pe.matmul(ps0[:, 1, 128 * j:128 * j + 128], w_gu1[:, k, 0 + 128 * j:0 + 128 * j + 128], unT0[:, k, :], start=k == 0, stop=k == 1)
                last.then_inc(L1f_matmul_done, 1)
                pe.wait_ge(L1f_vector_done, 56*b + 46)
                pe.wait_ge(L1f_scalar_done, 22*b + 22)
                for j in range(4):
                    for k in range(2):
                        last = pe.matmul(ps1[:, 1, 128 * j:128 * j + 128], w_gu1[:, k, 0 + 128 * j:0 + 128 * j + 128], unT1[:, k, :], start=k == 0, stop=k == 1)
                last.then_inc(L1f_matmul_done, 1)
                pe.wait_ge(L1f_vector_done, 56*b + 48)
                for j in range(4):
                    for k in range(2):
                        last = pe.matmul(ps0[:, 2, 128 * j:128 * j + 128], w_gu1[:, k, 512 + 128 * j:512 + 128 * j + 128], unT0[:, k, :], start=k == 0, stop=k == 1)
                last.then_inc(L1f_matmul_done, 1)
                pe.wait_ge(L1f_vector_done, 56*b + 50)
                for j in range(4):
                    for k in range(2):
                        last = pe.matmul(ps1[:, 2, 128 * j:128 * j + 128], w_gu1[:, k, 512 + 128 * j:512 + 128 * j + 128], unT1[:, k, :], start=k == 0, stop=k == 1)
                last.then_inc(L1f_matmul_done, 1)
                for k in range(2):
                    last = pe.matmul(ps0[:, 0, 256:263], unT0[:, k, :], w_gt1[:, k, :], start=k == 0, stop=k == 1)
                last.then_inc(L1f_matmul_done, 1)
                for k in range(2):
                    last = pe.matmul(ps1[:, 0, 256:263], unT1[:, k, :], w_gt1[:, k, :], start=k == 0, stop=k == 1)
                last.then_inc(L1f_matmul_done, 1)
                pe.wait_ge(L1f_vector_done, 56*b + 59)
                for j in range(4):
                    for k in range(2):
                        last = pe.matmul(ps0[:, 1, 128 * j:128 * j + 128], w_gu1[:, k, 1024 + 128 * j:1024 + 128 * j + 128], unT0[:, k, :], start=k == 0, stop=k == 1)
                last.then_inc(L1f_matmul_done, 1)
                pe.wait_ge(L1f_vector_done, 56*b + 60)
                for j in range(4):
                    for k in range(2):
                        last = pe.matmul(ps1[:, 1, 128 * j:128 * j + 128], w_gu1[:, k, 1024 + 128 * j:1024 + 128 * j + 128], unT1[:, k, :], start=k == 0, stop=k == 1)
                last.then_inc(L1f_matmul_done, 1)
                for k in range(2):
                    last = pe.matmul(ps0[:, 3, 0:256], m1_0[:, 0, 128 * k:128 * k + 128], w_dn1[:, 0, k, :], start=k == 0, stop=k == 1)
                last.then_inc(L1f_matmul_done, 1)
                for k in range(2):
                    last = pe.matmul(ps1[:, 3, 0:256], m1_1[:, 0, 128 * k:128 * k + 128], w_dn1[:, 0, k, :], start=k == 0, stop=k == 1)
                last.then_inc(L1f_matmul_done, 1)
                pe.wait_ge(L1f_vector_done, 56*b + 61)
                for j in range(4):
                    for k in range(2):
                        last = pe.matmul(ps0[:, 2, 128 * j:128 * j + 128], w_gu1[:, k, 1536 + 128 * j:1536 + 128 * j + 128], unT0[:, k, :], start=k == 0, stop=k == 1)
                last.then_inc(L1f_matmul_done, 1)
                pe.wait_ge(L1f_vector_done, 56*b + 65)
                for j in range(4):
                    for k in range(2):
                        last = pe.matmul(ps1[:, 2, 128 * j:128 * j + 128], w_gu1[:, k, 1536 + 128 * j:1536 + 128 * j + 128], unT1[:, k, :], start=k == 0, stop=k == 1)
                last.then_inc(L1f_matmul_done, 1)
                pe.wait_ge(L1f_vector_done, 56*b + 67)
                for k in range(2):
                    last = pe.matmul(ps0[:, 3, 256:512], m1_0[:, 1, 128 * k:128 * k + 128], w_dn1[:, 1, k, :], start=k == 0, stop=k == 1)
                last.then_inc(L1f_matmul_done, 1)
                pe.wait_ge(L1f_vector_done, 56*b + 69)
                for k in range(2):
                    last = pe.matmul(ps1[:, 3, 256:512], m1_1[:, 1, 128 * k:128 * k + 128], w_dn1[:, 1, k, :], start=k == 0, stop=k == 1)
                last.then_inc(L1f_matmul_done, 1)
                for j in range(4):
                    for k in range(2):
                        last = pe.matmul(ps0[:, 1, 128 * j:128 * j + 128], w_gu1[:, k, 2048 + 128 * j:2048 + 128 * j + 128], unT0[:, k, :], start=k == 0, stop=k == 1)
                last.then_inc(L1f_matmul_done, 1)
                pe.wait_ge(L1f_vector_done, 56*b + 70)
                for j in range(4):
                    for k in range(2):
                        last = pe.matmul(ps1[:, 1, 128 * j:128 * j + 128], w_gu1[:, k, 2048 + 128 * j:2048 + 128 * j + 128], unT1[:, k, :], start=k == 0, stop=k == 1)
                last.then_inc(L1f_matmul_done, 1)
                pe.wait_ge(L1f_vector_done, 56*b + 71)
                for j in range(4):
                    for k in range(2):
                        pe.matmul(ps0[:, 2, 128 * j:128 * j + 128], w_gu1[:, k, 2560 + 128 * j:2560 + 128 * j + 128], unT0[:, k, :], start=k == 0, stop=k == 1)
                pe.wait_ge(L1f_vector_done, 56*b + 72)
                for j in range(4):
                    for k in range(2):
                        pe.matmul(ps1[:, 2, 128 * j:128 * j + 128], w_gu1[:, k, 2560 + 128 * j:2560 + 128 * j + 128], unT1[:, k, :], start=k == 0, stop=k == 1)
                for k in range(2):
                    last = pe.transpose(ps0[:, 0, 128 * k:128 * k + 128], u0[:, 128 * k:128 * k + 128], ident[:, :])
                last.then_inc(L1f_matmul_done, 1)
                for k in range(2):
                    last = pe.transpose(ps1[:, 0, 128 * k:128 * k + 128], u1[:, 128 * k:128 * k + 128], ident[:, :])
                last.then_inc(L1f_matmul_done, 1)
                pe.wait_ge(L1f_vector_done, 56*b + 88)
                for k in range(2):
                    last = pe.matmul(ps0[:, 3, 0:256], m1_0[:, 0, 128 * k:128 * k + 128], w_dn1[:, 2, k, :], start=k == 0, stop=k == 1)
                last.then_inc(L1f_matmul_done, 1)
                pe.wait_ge(L1f_vector_done, 56*b + 90)
                for k in range(2):
                    last = pe.matmul(ps1[:, 3, 0:256], m1_1[:, 0, 128 * k:128 * k + 128], w_dn1[:, 2, k, :], start=k == 0, stop=k == 1)
                last.then_inc(L1f_matmul_done, 1)
                pe.wait_ge(L1f_vector_done, 56*b + 91)
                for k in range(2):
                    last = pe.matmul(ps0[:, 3, 256:512], m1_0[:, 1, 128 * k:128 * k + 128], w_dn1[:, 3, k, :], start=k == 0, stop=k == 1)
                last.then_inc(L1f_matmul_done, 1)
                pe.wait_ge(L1f_vector_done, 56*b + 93)
                for k in range(2):
                    last = pe.matmul(ps1[:, 3, 256:512], m1_1[:, 1, 128 * k:128 * k + 128], w_dn1[:, 3, k, :], start=k == 0, stop=k == 1)
                last.then_inc(L1f_matmul_done, 1)
                for j in range(4):
                    for k in range(2):
                        last = pe.matmul(ps0[:, 1, 128 * j:128 * j + 128], w_gu1[:, k, 3072 + 128 * j:3072 + 128 * j + 128], unT0[:, k, :], start=k == 0, stop=k == 1)
                last.then_inc(L1f_matmul_done, 1)
                pe.wait_ge(L1f_vector_done, 56*b + 94)
                for j in range(4):
                    for k in range(2):
                        last = pe.matmul(ps1[:, 1, 128 * j:128 * j + 128], w_gu1[:, k, 3072 + 128 * j:3072 + 128 * j + 128], unT1[:, k, :], start=k == 0, stop=k == 1)
                last.then_inc(L1f_matmul_done, 1)
                pe.wait_ge(L1f_vector_done, 56*b + 95)
                for k in range(2):
                    last = pe.matmul(ps0[:, 3, 0:256], m1_0[:, 0, 128 * k:128 * k + 128], w_dn1[:, 4, k, :], start=k == 0, stop=k == 1)
                last.then_inc(L1f_matmul_done, 1)
                pe.wait_ge(L1f_vector_done, 56*b + 96)
                for k in range(2):
                    last = pe.matmul(ps1[:, 3, 0:256], m1_1[:, 0, 128 * k:128 * k + 128], w_dn1[:, 4, k, :], start=k == 0, stop=k == 1)
                last.then_inc(L1f_matmul_done, 1)
                pe.wait_ge(L1f_vector_done, 56*b + 97)
                for j in range(4):
                    for k in range(2):
                        last = pe.matmul(ps0[:, 2, 128 * j:128 * j + 128], w_gu1[:, k, 3584 + 128 * j:3584 + 128 * j + 128], unT0[:, k, :], start=k == 0, stop=k == 1)
                last.then_inc(L1f_matmul_done, 1)
                pe.wait_ge(L1f_vector_done, 56*b + 98)
                for j in range(4):
                    for k in range(2):
                        last = pe.matmul(ps1[:, 2, 128 * j:128 * j + 128], w_gu1[:, k, 3584 + 128 * j:3584 + 128 * j + 128], unT1[:, k, :], start=k == 0, stop=k == 1)
                last.then_inc(L1f_matmul_done, 1)
                pe.wait_ge(L1f_vector_done, 56*b + 99)
                for k in range(2):
                    last = pe.matmul(ps0[:, 3, 256:512], m1_0[:, 1, 128 * k:128 * k + 128], w_dn1[:, 5, k, :], start=k == 0, stop=k == 1)
                last.then_inc(L1f_matmul_done, 1)
                pe.wait_ge(L1f_vector_done, 56*b + 101)
                for k in range(2):
                    last = pe.matmul(ps1[:, 3, 256:512], m1_1[:, 1, 128 * k:128 * k + 128], w_dn1[:, 5, k, :], start=k == 0, stop=k == 1)
                last.then_inc(L1f_matmul_done, 1)
                pe.wait_ge(L1f_vector_done, 56*b + 103)
                for k in range(2):
                    last = pe.matmul(ps0[:, 3, 0:256], m1_0[:, 0, 128 * k:128 * k + 128], w_dn1[:, 6, k, :], start=k == 0, stop=k == 1)
                last.then_inc(L1f_matmul_done, 1)
                pe.wait_ge(L1f_vector_done, 56*b + 105)
                for k in range(2):
                    last = pe.matmul(ps1[:, 3, 0:256], m1_1[:, 0, 128 * k:128 * k + 128], w_dn1[:, 6, k, :], start=k == 0, stop=k == 1)
                last.then_inc(L1f_matmul_done, 1)
                pe.wait_ge(L1f_vector_done, 56*b + 107)
                for k in range(2):
                    last = pe.matmul(ps0[:, 3, 256:512], m1_0[:, 1, 128 * k:128 * k + 128], w_dn1[:, 7, k, :], start=k == 0, stop=k == 1)
                last.then_inc(L1f_matmul_done, 1)
                pe.wait_ge(L1f_vector_done, 56*b + 108)
                for k in range(2):
                    last = pe.matmul(ps1[:, 3, 256:512], m1_1[:, 1, 128 * k:128 * k + 128], w_dn1[:, 7, k, :], start=k == 0, stop=k == 1)
                last.then_inc(L1f_matmul_done, 1)

            pe.wait_ge(L2a_vector_done, 44)
            for k in range(2):
                last = pe.transpose(ps0[:, 0, 128 * k:128 * k + 128], u0[:, 128 * k:128 * k + 128], ident[:, :])
            last.then_inc(L2a_matmul_done, 1)
            pe.wait_ge(L2a_vector_done, 45)
            for k in range(2):
                last = pe.transpose(ps1[:, 0, 128 * k:128 * k + 128], u1[:, 128 * k:128 * k + 128], ident[:, :])
            last.then_inc(L2a_matmul_done, 1)
            pe.wait_ge(L2a_w_loaded, 32)
            pe.wait_ge(L2a_scalar_done, 26)
            with pe.Fori(0, 4) as b:
                pe.wait_ge(L2a_vector_done, 47*b + 44)
                pe.wait_ge(L2a_scalar_done, 26*b + 25)
                for j in range(4):
                    for k in range(2):
                        last = pe.matmul(ps0[:, 1, 128 * j:128 * j + 128], w_qkv2[:, k, 128 * j:128 * j + 128], unT0[:, k, :], start=k == 0, stop=k == 1)
                last.then_inc(L2a_matmul_done, 1)
                pe.wait_ge(L2a_scalar_done, 26*b + 26)
                pe.wait_ge(L2a_vector_done, 47*b + 45)
                for j in range(4):
                    for k in range(2):
                        last = pe.matmul(ps1[:, 1, 128 * j:128 * j + 128], w_qkv2[:, k, 128 * j:128 * j + 128], unT1[:, k, :], start=k == 0, stop=k == 1)
                last.then_inc(L2a_matmul_done, 1)
                for k in range(2):
                    last = pe.matmul(ps0[:, 2, 0:256], unT0[:, k, :], w_qkv2[:, k, 512:768], start=k == 0, stop=k == 1)
                last.then_inc(L2a_matmul_done, 1)
                for k in range(2):
                    last = pe.matmul(ps1[:, 2, 0:256], unT1[:, k, :], w_qkv2[:, k, 512:768], start=k == 0, stop=k == 1)
                last.then_inc(L2a_matmul_done, 1)
                pe.wait_ge(L2a_vector_done, 47*b + 51)
                pe.matmul(ps0[:, 1, :], qT_0[:, 0, :], kM_0[:, 0, 0:4, :], start=True, stop=True).then_inc(L2a_matmul_done, 1)
                pe.wait_ge(L2a_vector_done, 47*b + 53)
                pe.matmul(ps1[:, 1, :], qT_1[:, 0, :], kM_1[:, 0, 0:4, :], start=True, stop=True).then_inc(L2a_matmul_done, 1)
                pe.wait_ge(L2a_vector_done, 47*b + 54)
                pe.matmul(ps0[:, 1, :], qT_0[:, 0, :], kM_0[:, 0, 4:8, :], start=True, stop=True).then_inc(L2a_matmul_done, 1)
                pe.wait_ge(L2a_vector_done, 47*b + 56)
                pe.matmul(ps1[:, 1, :], qT_1[:, 0, :], kM_1[:, 0, 4:8, :], start=True, stop=True)
                pe.wait_ge(L2a_scalar_done, 26*b + 33)
                for i in range(4):
                    last = pe.transpose(ps0[:, 2, 128 * i:128 * i + 128], S_0[:, i, :], ident[:, :])
                last.then_inc(L2a_matmul_done, 1)
                pe.wait_ge(L2a_scalar_done, 26*b + 34)
                for i in range(4):
                    last = pe.transpose(ps1[:, 2, 128 * i:128 * i + 128], S_1[:, i, :], ident[:, :])
                last.then_inc(L2a_matmul_done, 1)
                pe.wait_ge(L2a_vector_done, 47*b + 60)
                pe.matmul(ps0[:, 1, :], qT_0[:, 1, :], kM_0[:, 1, 0:4, :], start=True, stop=True)
                pe.wait_ge(L2a_scalar_done, 26*b + 35)
                for i in range(4):
                    last = pe.matmul(ps0[:, 3, 17 * i:17 * i + 17], PT_0[:, i, :], v_0[:, 0 + i, :], start=True, stop=True)
                last.then_inc(L2a_matmul_done, 1)
                pe.wait_ge(L2a_scalar_done, 26*b + 36)
                for i in range(4):
                    last = pe.matmul(ps1[:, 3, 17 * i:17 * i + 17], PT_1[:, i, :], v_1[:, 0 + i, :], start=True, stop=True)
                last.then_inc(L2a_matmul_done, 1)
                pe.wait_ge(L2a_vector_done, 47*b + 62)
                pe.matmul(ps1[:, 1, :], qT_1[:, 1, :], kM_1[:, 1, 0:4, :], start=True, stop=True)
                pe.wait_ge(L2a_scalar_done, 26*b + 37)
                for i in range(4):
                    last = pe.transpose(ps0[:, 2, 128 * i:128 * i + 128], S_0[:, i, :], ident[:, :])
                last.then_inc(L2a_matmul_done, 1)
                pe.wait_ge(L2a_scalar_done, 26*b + 38)
                for i in range(4):
                    last = pe.transpose(ps1[:, 2, 128 * i:128 * i + 128], S_1[:, i, :], ident[:, :])
                last.then_inc(L2a_matmul_done, 1)
                pe.wait_ge(L2a_vector_done, 47*b + 68)
                pe.matmul(ps0[:, 1, :], qT_0[:, 1, :], kM_0[:, 1, 4:8, :], start=True, stop=True)
                pe.wait_ge(L2a_scalar_done, 26*b + 39)
                for i in range(4):
                    last = pe.matmul(ps0[:, 3, 17 * i:17 * i + 17], PT_0[:, i, :], v_0[:, 4 + i, :], start=True, stop=True)
                last.then_inc(L2a_matmul_done, 1)
                pe.wait_ge(L2a_scalar_done, 26*b + 40)
                for i in range(4):
                    last = pe.matmul(ps1[:, 3, 17 * i:17 * i + 17], PT_1[:, i, :], v_1[:, 4 + i, :], start=True, stop=True)
                last.then_inc(L2a_matmul_done, 1)
                pe.wait_ge(L2a_vector_done, 47*b + 70)
                pe.matmul(ps1[:, 1, :], qT_1[:, 1, :], kM_1[:, 1, 4:8, :], start=True, stop=True)
                pe.wait_ge(L2a_scalar_done, 26*b + 41)
                for i in range(4):
                    last = pe.transpose(ps0[:, 2, 128 * i:128 * i + 128], S_0[:, i, :], ident[:, :])
                last.then_inc(L2a_matmul_done, 1)
                pe.wait_ge(L2a_scalar_done, 26*b + 42)
                for i in range(4):
                    last = pe.transpose(ps1[:, 2, 128 * i:128 * i + 128], S_1[:, i, :], ident[:, :])
                last.then_inc(L2a_matmul_done, 1)
                pe.wait_ge(L2a_vector_done, 47*b + 76)
                pe.wait_ge(L2a_scalar_done, 26*b + 43)
                for i in range(4):
                    last = pe.matmul(ps0[:, 3, 17 * i:17 * i + 17], PT_0[:, i, :], v_0[:, 8 + i, :], start=True, stop=True)
                last.then_inc(L2a_matmul_done, 1)
                pe.wait_ge(L2a_vector_done, 47*b + 77)
                pe.wait_ge(L2a_scalar_done, 26*b + 44)
                for i in range(4):
                    last = pe.matmul(ps1[:, 3, 17 * i:17 * i + 17], PT_1[:, i, :], v_1[:, 8 + i, :], start=True, stop=True)
                last.then_inc(L2a_matmul_done, 1)
                pe.wait_ge(L2a_scalar_done, 26*b + 45)
                for i in range(4):
                    last = pe.transpose(ps0[:, 2, 128 * i:128 * i + 128], S_0[:, i, :], ident[:, :])
                last.then_inc(L2a_matmul_done, 1)
                pe.wait_ge(L2a_scalar_done, 26*b + 46)
                for i in range(4):
                    last = pe.transpose(ps1[:, 2, 128 * i:128 * i + 128], S_1[:, i, :], ident[:, :])
                last.then_inc(L2a_matmul_done, 1)
                pe.wait_ge(L2a_scalar_done, 26*b + 47)
                for i in range(4):
                    last = pe.matmul(ps0[:, 3, 17 * i:17 * i + 17], PT_0[:, i, :], v_0[:, 12 + i, :], start=True, stop=True)
                last.then_inc(L2a_matmul_done, 1)
                pe.wait_ge(L2a_vector_done, 47*b + 86)
                pe.wait_ge(L2a_scalar_done, 26*b + 48)
                for i in range(4):
                    last = pe.matmul(ps1[:, 3, 17 * i:17 * i + 17], PT_1[:, i, :], v_1[:, 12 + i, :], start=True, stop=True)
                last.then_inc(L2a_matmul_done, 1)
                pe.wait_ge(L2a_vector_done, 47*b + 88)
                for k in range(2):
                    last = pe.transpose(ps0[:, 0, 128 * k:128 * k + 128], ao_0[:, 128 * k:128 * k + 128], ident[:, :])
                last.then_inc(L2a_matmul_done, 1)
                pe.wait_ge(L2a_vector_done, 47*b + 90)
                for k in range(2):
                    last = pe.transpose(ps1[:, 0, 128 * k:128 * k + 128], ao_1[:, 128 * k:128 * k + 128], ident[:, :])
                last.then_inc(L2a_matmul_done, 1)
                pe.wait_ge(L2a_scalar_done, 26*b + 49)
                for k in range(2):
                    last = pe.matmul(ps0[:, 1, 0:256], unT0[:, k, :], w_o2[:, k, :], start=k == 0, stop=k == 1)
                last.then_inc(L2a_matmul_done, 1)
                pe.wait_ge(L2a_scalar_done, 26*b + 50)
                for k in range(2):
                    last = pe.matmul(ps1[:, 1, 0:256], unT1[:, k, :], w_o2[:, k, :], start=k == 0, stop=k == 1)
                last.then_inc(L2a_matmul_done, 1)
                for k in range(2):
                    last = pe.transpose(ps0[:, 0, 128 * k:128 * k + 128], u0[:, 128 * k:128 * k + 128], ident[:, :])
                last.then_inc(L2a_matmul_done, 1)
                for k in range(2):
                    last = pe.transpose(ps1[:, 0, 128 * k:128 * k + 128], u1[:, 128 * k:128 * k + 128], ident[:, :])
                last.then_inc(L2a_matmul_done, 1)

            pe.sem_inc(L2x_matmul_done, 16)
            pe.wait_ge(L2x_vector_done, 208)
            for k in range(2):
                last = pe.transpose(ps0[:, 0, 128 * k:128 * k + 128], un0[:, 128 * k:128 * k + 128], ident[:, :])
            last.then_inc(L2x_matmul_done, 1)
            pe.wait_ge(L2x_vector_done, 209)
            for k in range(2):
                last = pe.transpose(ps1[:, 0, 128 * k:128 * k + 128], un1[:, 128 * k:128 * k + 128], ident[:, :])
            last.then_inc(L2x_matmul_done, 1)
            pe.wait_ge(L2x_vector_done, 218)
            with pe.Fori(0, 4) as b:
                pe.wait_ge(L2x_vector_done, 226*b + 217)
                for k in range(2):
                    last = pe.matmul(ps0[:, 1, :], xs_0[:, 0, k, :], w_q2[:, k, 0:512], start=k == 0, stop=k == 1)
                last.then_inc(L2x_matmul_done, 1)
                pe.wait_ge(L2x_vector_done, 226*b + 218)
                for k in range(2):
                    last = pe.matmul(ps1[:, 1, :], xs_1[:, 0, k, :], w_q2[:, k, 0:512], start=k == 0, stop=k == 1)
                last.then_inc(L2x_matmul_done, 1)
                pe.wait_ge(L2x_scalar_done, 108*b + 103)
                for k in range(2):
                    pe.matmul(ps0[:, 2, 0:256], xs_0[:, 2, k, :], w_k2[:, k, 0:256], start=k == 0, stop=k == 1)
                pe.wait_ge(L2x_scalar_done, 108*b + 104)
                for k in range(2):
                    pe.matmul(ps1[:, 2, 0:256], xs_1[:, 2, k, :], w_k2[:, k, 0:256], start=k == 0, stop=k == 1)
                for k in range(2):
                    last = pe.matmul(ps0[:, 2, 256:512], xs_0[:, 3, k, :], w_v2[:, k, 0:256], start=k == 0, stop=k == 1)
                last.then_inc(L2x_matmul_done, 1)
                for k in range(2):
                    last = pe.matmul(ps1[:, 2, 256:512], xs_1[:, 3, k, :], w_v2[:, k, 0:256], start=k == 0, stop=k == 1)
                last.then_inc(L2x_matmul_done, 1)
                pe.wait_ge(L2x_vector_done, 226*b + 240)
                for i in range(4):
                    last = pe.transpose(ps0[:, 3, 128 * i:128 * i + 128], qk_0[:, i, :], ident[:, :])
                last.then_inc(L2x_matmul_done, 1)
                for k in range(2):
                    last = pe.matmul(ps0[:, 1, :], xs_0[:, 0, k, :], w_q2[:, k, 512:1024], start=k == 0, stop=k == 1)
                last.then_inc(L2x_matmul_done, 1)
                pe.wait_ge(L2x_vector_done, 226*b + 243)
                for i in range(4):
                    last = pe.transpose(ps1[:, 3, 128 * i:128 * i + 128], qk_1[:, i, :], ident[:, :])
                last.then_inc(L2x_matmul_done, 1)
                pe.wait_ge(L2x_scalar_done, 108*b + 123)
                for i in range(2):
                    last = pe.transpose(ps0[:, 2, 128 * i:128 * i + 128], qk_0[:, 4 + i, :], ident[:, :])
                last.then_inc(L2x_matmul_done, 1)
                pe.wait_ge(L2x_scalar_done, 108*b + 124)
                for i in range(2):
                    last = pe.transpose(ps1[:, 2, 128 * i:128 * i + 128], qk_1[:, 4 + i, :], ident[:, :])
                last.then_inc(L2x_matmul_done, 1)
                for k in range(2):
                    last = pe.matmul(ps1[:, 1, :], xs_1[:, 0, k, :], w_q2[:, k, 512:1024], start=k == 0, stop=k == 1)
                last.then_inc(L2x_matmul_done, 1)
                pe.wait_ge(L2x_scalar_done, 108*b + 125)
                for i in range(4):
                    last = pe.matmul(ps0[:, 2, 128 * i:128 * i + 128], qT2_0[:, 128 * i:128 * i + 128], kT2_0[:, 128 * (i // 2):128 * (i // 2) + 128], start=True, stop=True)
                last.then_inc(L2x_matmul_done, 1)
                pe.wait_ge(L2x_scalar_done, 108*b + 126)
                for i in range(4):
                    last = pe.matmul(ps1[:, 2, 128 * i:128 * i + 128], qT2_1[:, 128 * i:128 * i + 128], kT2_1[:, 128 * (i // 2):128 * (i // 2) + 128], start=True, stop=True)
                last.then_inc(L2x_matmul_done, 1)
                pe.wait_ge(L2x_scalar_done, 108*b + 127)
                for k in range(2):
                    pe.matmul(ps0[:, 2, 0:256], xs_0[:, 2, k, :], w_k2[:, k, 256:512], start=k == 0, stop=k == 1)
                for k in range(2):
                    last = pe.matmul(ps0[:, 2, 256:512], xs_0[:, 3, k, :], w_v2[:, k, 256:512], start=k == 0, stop=k == 1)
                last.then_inc(L2x_matmul_done, 1)
                pe.wait_ge(L2x_pool_done, 52*b + 5)
                for i in range(4):
                    last = pe.transpose(ps0[:, 3, 128 * i:128 * i + 128], P2_0[:, i, :], ident[:, :])
                last.then_inc(L2x_matmul_done, 1)
                pe.wait_ge(L2x_scalar_done, 108*b + 128)
                for k in range(2):
                    pe.matmul(ps1[:, 2, 0:256], xs_1[:, 2, k, :], w_k2[:, k, 256:512], start=k == 0, stop=k == 1)
                pe.wait_ge(L2x_pool_done, 52*b + 6)
                for i in range(4):
                    last = pe.transpose(ps1[:, 3, 128 * i:128 * i + 128], P2_1[:, i, :], ident[:, :])
                last.then_inc(L2x_matmul_done, 1)
                pe.wait_ge(L2x_scalar_done, 108*b + 129)
                for i in range(2):
                    last = pe.matmul(ps0[:, 3, 256 * i:256 * i + 256], v2_0[:, 128 * i:128 * i + 128], PT2_0[:, 256 * i:256 * i + 256], start=True, stop=True)
                last.then_inc(L2x_matmul_done, 1)
                for k in range(2):
                    last = pe.matmul(ps1[:, 2, 256:512], xs_1[:, 3, k, :], w_v2[:, k, 256:512], start=k == 0, stop=k == 1)
                last.then_inc(L2x_matmul_done, 1)
                pe.wait_ge(L2x_scalar_done, 108*b + 132)
                for i in range(2):
                    last = pe.matmul(ps1[:, 3, 256 * i:256 * i + 256], v2_1[:, 128 * i:128 * i + 128], PT2_1[:, 256 * i:256 * i + 256], start=True, stop=True)
                last.then_inc(L2x_matmul_done, 1)
                pe.wait_ge(L2x_vector_done, 226*b + 255)
                for i in range(4):
                    last = pe.transpose(ps0[:, 3, 128 * i:128 * i + 128], qk_0[:, i, :], ident[:, :])
                last.then_inc(L2x_matmul_done, 1)
                for k in range(2):
                    last = pe.matmul(ps0[:, 1, :], xs_0[:, 0, k, :], w_q2[:, k, 1024:1536], start=k == 0, stop=k == 1)
                last.then_inc(L2x_matmul_done, 1)
                pe.wait_ge(L2x_scalar_done, 108*b + 135)
                for i in range(2):
                    last = pe.transpose(ps0[:, 2, 128 * i:128 * i + 128], qk_0[:, 4 + i, :], ident[:, :])
                last.then_inc(L2x_matmul_done, 1)
                pe.wait_ge(L2x_scalar_done, 108*b + 136)
                for i in range(4):
                    last = pe.matmul(ps0[:, 2, 128 * i:128 * i + 128], qT2_0[:, 128 * i:128 * i + 128], kT2_0[:, 128 * (i // 2):128 * (i // 2) + 128], start=True, stop=True)
                last.then_inc(L2x_matmul_done, 1)
                pe.wait_ge(L2x_vector_done, 226*b + 267)
                for i in range(4):
                    last = pe.transpose(ps1[:, 3, 128 * i:128 * i + 128], qk_1[:, i, :], ident[:, :])
                last.then_inc(L2x_matmul_done, 1)
                pe.wait_ge(L2x_scalar_done, 108*b + 137)
                for i in range(2):
                    last = pe.transpose(ps1[:, 2, 128 * i:128 * i + 128], qk_1[:, 4 + i, :], ident[:, :])
                last.then_inc(L2x_matmul_done, 1)
                pe.wait_ge(L2x_pool_done, 52*b + 9)
                for i in range(4):
                    last = pe.matmul(ps0[:, 0, 0:256], P2_0[:, i, :], w_p2[:, 0 + i, :], start=i == 0, stop=False)
                last.then_inc(L2x_matmul_done, 1)
                pe.wait_ge(L2x_scalar_done, 108*b + 138)
                for i in range(4):
                    last = pe.matmul(ps1[:, 2, 128 * i:128 * i + 128], qT2_1[:, 128 * i:128 * i + 128], kT2_1[:, 128 * (i // 2):128 * (i // 2) + 128], start=True, stop=True)
                last.then_inc(L2x_matmul_done, 1)
                pe.wait_ge(L2x_pool_done, 52*b + 10)
                for i in range(4):
                    last = pe.matmul(ps1[:, 0, 0:256], P2_1[:, i, :], w_p2[:, 0 + i, :], start=i == 0, stop=False)
                last.then_inc(L2x_matmul_done, 1)
                for k in range(2):
                    last = pe.matmul(ps1[:, 1, :], xs_1[:, 0, k, :], w_q2[:, k, 1024:1536], start=k == 0, stop=k == 1)
                last.then_inc(L2x_matmul_done, 1)
                pe.wait_ge(L2x_pool_done, 52*b + 11)
                for i in range(4):
                    last = pe.transpose(ps0[:, 3, 128 * i:128 * i + 128], P2_0[:, i, :], ident[:, :])
                last.then_inc(L2x_matmul_done, 1)
                for k in range(2):
                    pe.matmul(ps0[:, 2, 0:256], xs_0[:, 2, k, :], w_k2[:, k, 512:768], start=k == 0, stop=k == 1)
                pe.wait_ge(L2x_scalar_done, 108*b + 140)
                for k in range(2):
                    pe.matmul(ps1[:, 2, 0:256], xs_1[:, 2, k, :], w_k2[:, k, 512:768], start=k == 0, stop=k == 1)
                pe.wait_ge(L2x_pool_done, 52*b + 12)
                for i in range(4):
                    last = pe.transpose(ps1[:, 3, 128 * i:128 * i + 128], P2_1[:, i, :], ident[:, :])
                last.then_inc(L2x_matmul_done, 1)
                pe.wait_ge(L2x_scalar_done, 108*b + 141)
                for i in range(2):
                    last = pe.matmul(ps0[:, 3, 256 * i:256 * i + 256], v2_0[:, 128 * i:128 * i + 128], PT2_0[:, 256 * i:256 * i + 256], start=True, stop=True)
                last.then_inc(L2x_matmul_done, 1)
                for k in range(2):
                    last = pe.matmul(ps0[:, 2, 256:512], xs_0[:, 3, k, :], w_v2[:, k, 512:768], start=k == 0, stop=k == 1)
                last.then_inc(L2x_matmul_done, 1)
                pe.wait_ge(L2x_scalar_done, 108*b + 142)
                for i in range(2):
                    last = pe.matmul(ps1[:, 3, 256 * i:256 * i + 256], v2_1[:, 128 * i:128 * i + 128], PT2_1[:, 256 * i:256 * i + 256], start=True, stop=True)
                last.then_inc(L2x_matmul_done, 1)
                for k in range(2):
                    last = pe.matmul(ps1[:, 2, 256:512], xs_1[:, 3, k, :], w_v2[:, k, 512:768], start=k == 0, stop=k == 1)
                last.then_inc(L2x_matmul_done, 1)
                pe.wait_ge(L2x_vector_done, 226*b + 289)
                for i in range(4):
                    last = pe.transpose(ps0[:, 3, 128 * i:128 * i + 128], qk_0[:, i, :], ident[:, :])
                last.then_inc(L2x_matmul_done, 1)
                for k in range(2):
                    last = pe.matmul(ps0[:, 1, :], xs_0[:, 0, k, :], w_q2[:, k, 1536:2048], start=k == 0, stop=k == 1)
                last.then_inc(L2x_matmul_done, 1)
                pe.wait_ge(L2x_vector_done, 226*b + 292)
                for i in range(4):
                    last = pe.transpose(ps1[:, 3, 128 * i:128 * i + 128], qk_1[:, i, :], ident[:, :])
                last.then_inc(L2x_matmul_done, 1)
                pe.wait_ge(L2x_scalar_done, 108*b + 147)
                for i in range(2):
                    last = pe.transpose(ps0[:, 2, 128 * i:128 * i + 128], qk_0[:, 4 + i, :], ident[:, :])
                last.then_inc(L2x_matmul_done, 1)
                pe.wait_ge(L2x_scalar_done, 108*b + 148)
                for i in range(2):
                    last = pe.transpose(ps1[:, 2, 128 * i:128 * i + 128], qk_1[:, 4 + i, :], ident[:, :])
                last.then_inc(L2x_matmul_done, 1)
                pe.wait_ge(L2x_pool_done, 52*b + 15)
                for i in range(4):
                    pe.matmul(ps0[:, 0, 0:256], P2_0[:, i, :], w_p2[:, 4 + i, :], start=False, stop=False)
                pe.wait_ge(L2x_scalar_done, 108*b + 149)
                for i in range(4):
                    last = pe.matmul(ps0[:, 2, 128 * i:128 * i + 128], qT2_0[:, 128 * i:128 * i + 128], kT2_0[:, 128 * (i // 2):128 * (i // 2) + 128], start=True, stop=True)
                last.then_inc(L2x_matmul_done, 1)
                pe.wait_ge(L2x_scalar_done, 108*b + 150)
                for i in range(4):
                    last = pe.matmul(ps1[:, 2, 128 * i:128 * i + 128], qT2_1[:, 128 * i:128 * i + 128], kT2_1[:, 128 * (i // 2):128 * (i // 2) + 128], start=True, stop=True)
                last.then_inc(L2x_matmul_done, 1)
                pe.wait_ge(L2x_pool_done, 52*b + 16)
                for i in range(4):
                    last = pe.matmul(ps1[:, 0, 0:256], P2_1[:, i, :], w_p2[:, 4 + i, :], start=False, stop=False)
                last.then_inc(L2x_matmul_done, 1)
                for k in range(2):
                    last = pe.matmul(ps1[:, 1, :], xs_1[:, 0, k, :], w_q2[:, k, 1536:2048], start=k == 0, stop=k == 1)
                last.then_inc(L2x_matmul_done, 1)
                pe.wait_ge(L2x_pool_done, 52*b + 17)
                for i in range(4):
                    last = pe.transpose(ps0[:, 3, 128 * i:128 * i + 128], P2_0[:, i, :], ident[:, :])
                last.then_inc(L2x_matmul_done, 1)
                for k in range(2):
                    pe.matmul(ps0[:, 2, 0:256], xs_0[:, 2, k, :], w_k2[:, k, 768:1024], start=k == 0, stop=k == 1)
                pe.wait_ge(L2x_scalar_done, 108*b + 152)
                for k in range(2):
                    pe.matmul(ps1[:, 2, 0:256], xs_1[:, 2, k, :], w_k2[:, k, 768:1024], start=k == 0, stop=k == 1)
                pe.wait_ge(L2x_pool_done, 52*b + 18)
                for i in range(4):
                    last = pe.transpose(ps1[:, 3, 128 * i:128 * i + 128], P2_1[:, i, :], ident[:, :])
                last.then_inc(L2x_matmul_done, 1)
                pe.wait_ge(L2x_scalar_done, 108*b + 153)
                for i in range(2):
                    last = pe.matmul(ps0[:, 3, 256 * i:256 * i + 256], v2_0[:, 128 * i:128 * i + 128], PT2_0[:, 256 * i:256 * i + 256], start=True, stop=True)
                last.then_inc(L2x_matmul_done, 1)
                for k in range(2):
                    last = pe.matmul(ps0[:, 2, 256:512], xs_0[:, 3, k, :], w_v2[:, k, 768:1024], start=k == 0, stop=k == 1)
                last.then_inc(L2x_matmul_done, 1)
                pe.wait_ge(L2x_scalar_done, 108*b + 154)
                for i in range(2):
                    last = pe.matmul(ps1[:, 3, 256 * i:256 * i + 256], v2_1[:, 128 * i:128 * i + 128], PT2_1[:, 256 * i:256 * i + 256], start=True, stop=True)
                last.then_inc(L2x_matmul_done, 1)
                for k in range(2):
                    last = pe.matmul(ps1[:, 2, 256:512], xs_1[:, 3, k, :], w_v2[:, k, 768:1024], start=k == 0, stop=k == 1)
                last.then_inc(L2x_matmul_done, 1)
                pe.wait_ge(L2x_vector_done, 226*b + 314)
                for i in range(4):
                    last = pe.transpose(ps0[:, 3, 128 * i:128 * i + 128], qk_0[:, i, :], ident[:, :])
                last.then_inc(L2x_matmul_done, 1)
                for k in range(2):
                    last = pe.matmul(ps0[:, 1, :], xs_0[:, 1, k, :], w_qx2[:, k, 0:512], start=k == 0, stop=k == 1)
                last.then_inc(L2x_matmul_done, 1)
                pe.wait_ge(L2x_vector_done, 226*b + 317)
                for i in range(4):
                    last = pe.transpose(ps1[:, 3, 128 * i:128 * i + 128], qk_1[:, i, :], ident[:, :])
                last.then_inc(L2x_matmul_done, 1)
                pe.wait_ge(L2x_scalar_done, 108*b + 159)
                for i in range(2):
                    last = pe.transpose(ps0[:, 2, 128 * i:128 * i + 128], qk_0[:, 4 + i, :], ident[:, :])
                last.then_inc(L2x_matmul_done, 1)
                pe.wait_ge(L2x_scalar_done, 108*b + 160)
                for i in range(2):
                    last = pe.transpose(ps1[:, 2, 128 * i:128 * i + 128], qk_1[:, 4 + i, :], ident[:, :])
                last.then_inc(L2x_matmul_done, 1)
                pe.wait_ge(L2x_pool_done, 52*b + 21)
                for i in range(4):
                    pe.matmul(ps0[:, 0, 0:256], P2_0[:, i, :], w_p2[:, 8 + i, :], start=False, stop=False)
                pe.wait_ge(L2x_scalar_done, 108*b + 161)
                for i in range(4):
                    last = pe.matmul(ps0[:, 2, 128 * i:128 * i + 128], qT2_0[:, 128 * i:128 * i + 128], kT2_0[:, 128 * (i // 2):128 * (i // 2) + 128], start=True, stop=True)
                last.then_inc(L2x_matmul_done, 1)
                pe.wait_ge(L2x_scalar_done, 108*b + 162)
                for i in range(4):
                    last = pe.matmul(ps1[:, 2, 128 * i:128 * i + 128], qT2_1[:, 128 * i:128 * i + 128], kT2_1[:, 128 * (i // 2):128 * (i // 2) + 128], start=True, stop=True)
                last.then_inc(L2x_matmul_done, 1)
                pe.wait_ge(L2x_pool_done, 52*b + 22)
                for i in range(4):
                    last = pe.matmul(ps1[:, 0, 0:256], P2_1[:, i, :], w_p2[:, 8 + i, :], start=False, stop=False)
                last.then_inc(L2x_matmul_done, 1)
                for k in range(2):
                    last = pe.matmul(ps1[:, 1, :], xs_1[:, 1, k, :], w_qx2[:, k, 0:512], start=k == 0, stop=k == 1)
                last.then_inc(L2x_matmul_done, 1)
                pe.wait_ge(L2x_pool_done, 52*b + 23)
                for i in range(4):
                    last = pe.transpose(ps0[:, 3, 128 * i:128 * i + 128], P2_0[:, i, :], ident[:, :])
                last.then_inc(L2x_matmul_done, 1)
                for k in range(2):
                    pe.matmul(ps0[:, 2, 0:256], cx_0[:, k, :], w_kv2[:, k, 0:256], start=k == 0, stop=k == 1)
                pe.wait_ge(L2x_scalar_done, 108*b + 164)
                for k in range(2):
                    pe.matmul(ps1[:, 2, 0:256], cx_1[:, k, :], w_kv2[:, k, 0:256], start=k == 0, stop=k == 1)
                pe.wait_ge(L2x_pool_done, 52*b + 24)
                for i in range(4):
                    last = pe.transpose(ps1[:, 3, 128 * i:128 * i + 128], P2_1[:, i, :], ident[:, :])
                last.then_inc(L2x_matmul_done, 1)
                pe.wait_ge(L2x_scalar_done, 108*b + 165)
                for i in range(2):
                    last = pe.matmul(ps0[:, 3, 256 * i:256 * i + 256], v2_0[:, 128 * i:128 * i + 128], PT2_0[:, 256 * i:256 * i + 256], start=True, stop=True)
                last.then_inc(L2x_matmul_done, 1)
                for k in range(2):
                    last = pe.matmul(ps0[:, 2, 256:512], cx_0[:, k, :], w_kv2[:, k, 1024:1280], start=k == 0, stop=k == 1)
                last.then_inc(L2x_matmul_done, 1)
                pe.wait_ge(L2x_scalar_done, 108*b + 166)
                for i in range(2):
                    last = pe.matmul(ps1[:, 3, 256 * i:256 * i + 256], v2_1[:, 128 * i:128 * i + 128], PT2_1[:, 256 * i:256 * i + 256], start=True, stop=True)
                last.then_inc(L2x_matmul_done, 1)
                for k in range(2):
                    last = pe.matmul(ps1[:, 2, 256:512], cx_1[:, k, :], w_kv2[:, k, 1024:1280], start=k == 0, stop=k == 1)
                last.then_inc(L2x_matmul_done, 1)
                pe.wait_ge(L2x_vector_done, 226*b + 339)
                for i in range(4):
                    last = pe.transpose(ps0[:, 3, 128 * i:128 * i + 128], qk_0[:, i, :], ident[:, :])
                last.then_inc(L2x_matmul_done, 1)
                for k in range(2):
                    last = pe.matmul(ps0[:, 1, :], xs_0[:, 1, k, :], w_qx2[:, k, 512:1024], start=k == 0, stop=k == 1)
                last.then_inc(L2x_matmul_done, 1)
                pe.wait_ge(L2x_vector_done, 226*b + 342)
                for i in range(4):
                    last = pe.transpose(ps1[:, 3, 128 * i:128 * i + 128], qk_1[:, i, :], ident[:, :])
                last.then_inc(L2x_matmul_done, 1)
                pe.wait_ge(L2x_scalar_done, 108*b + 171)
                for i in range(2):
                    last = pe.transpose(ps0[:, 2, 128 * i:128 * i + 128], qk_0[:, 4 + i, :], ident[:, :])
                last.then_inc(L2x_matmul_done, 1)
                pe.wait_ge(L2x_scalar_done, 108*b + 172)
                for i in range(2):
                    last = pe.transpose(ps1[:, 2, 128 * i:128 * i + 128], qk_1[:, 4 + i, :], ident[:, :])
                last.then_inc(L2x_matmul_done, 1)
                pe.wait_ge(L2x_pool_done, 52*b + 27)
                for i in range(4):
                    pe.matmul(ps0[:, 0, 0:256], P2_0[:, i, :], w_p2[:, 12 + i, :], start=False, stop=False)
                pe.wait_ge(L2x_scalar_done, 108*b + 173)
                for i in range(4):
                    last = pe.matmul(ps0[:, 2, 128 * i:128 * i + 128], qT2_0[:, 128 * i:128 * i + 128], kT2_0[:, 128 * (i // 2):128 * (i // 2) + 128], start=True, stop=True)
                last.then_inc(L2x_matmul_done, 1)
                pe.wait_ge(L2x_scalar_done, 108*b + 174)
                for i in range(4):
                    last = pe.matmul(ps1[:, 2, 128 * i:128 * i + 128], qT2_1[:, 128 * i:128 * i + 128], kT2_1[:, 128 * (i // 2):128 * (i // 2) + 128], start=True, stop=True)
                last.then_inc(L2x_matmul_done, 1)
                pe.wait_ge(L2x_pool_done, 52*b + 28)
                for i in range(4):
                    last = pe.matmul(ps1[:, 0, 0:256], P2_1[:, i, :], w_p2[:, 12 + i, :], start=False, stop=False)
                last.then_inc(L2x_matmul_done, 1)
                for k in range(2):
                    last = pe.matmul(ps1[:, 1, :], xs_1[:, 1, k, :], w_qx2[:, k, 512:1024], start=k == 0, stop=k == 1)
                last.then_inc(L2x_matmul_done, 1)
                pe.wait_ge(L2x_pool_done, 52*b + 29)
                for i in range(4):
                    last = pe.transpose(ps0[:, 3, 128 * i:128 * i + 128], P2_0[:, i, :], ident[:, :])
                last.then_inc(L2x_matmul_done, 1)
                for k in range(2):
                    pe.matmul(ps0[:, 2, 0:256], cx_0[:, k, :], w_kv2[:, k, 256:512], start=k == 0, stop=k == 1)
                pe.wait_ge(L2x_scalar_done, 108*b + 176)
                for k in range(2):
                    pe.matmul(ps1[:, 2, 0:256], cx_1[:, k, :], w_kv2[:, k, 256:512], start=k == 0, stop=k == 1)
                pe.wait_ge(L2x_pool_done, 52*b + 30)
                for i in range(4):
                    last = pe.transpose(ps1[:, 3, 128 * i:128 * i + 128], P2_1[:, i, :], ident[:, :])
                last.then_inc(L2x_matmul_done, 1)
                pe.wait_ge(L2x_scalar_done, 108*b + 177)
                for i in range(2):
                    last = pe.matmul(ps0[:, 3, 256 * i:256 * i + 256], v2_0[:, 128 * i:128 * i + 128], PT2_0[:, 256 * i:256 * i + 256], start=True, stop=True)
                last.then_inc(L2x_matmul_done, 1)
                for k in range(2):
                    last = pe.matmul(ps0[:, 2, 256:512], cx_0[:, k, :], w_kv2[:, k, 1280:1536], start=k == 0, stop=k == 1)
                last.then_inc(L2x_matmul_done, 1)
                pe.wait_ge(L2x_scalar_done, 108*b + 178)
                for i in range(2):
                    last = pe.matmul(ps1[:, 3, 256 * i:256 * i + 256], v2_1[:, 128 * i:128 * i + 128], PT2_1[:, 256 * i:256 * i + 256], start=True, stop=True)
                last.then_inc(L2x_matmul_done, 1)
                for k in range(2):
                    last = pe.matmul(ps1[:, 2, 256:512], cx_1[:, k, :], w_kv2[:, k, 1280:1536], start=k == 0, stop=k == 1)
                last.then_inc(L2x_matmul_done, 1)
                pe.wait_ge(L2x_vector_done, 226*b + 364)
                for i in range(4):
                    last = pe.transpose(ps0[:, 3, 128 * i:128 * i + 128], qk_0[:, i, :], ident[:, :])
                last.then_inc(L2x_matmul_done, 1)
                for k in range(2):
                    last = pe.matmul(ps0[:, 1, :], xs_0[:, 1, k, :], w_qx2[:, k, 1024:1536], start=k == 0, stop=k == 1)
                last.then_inc(L2x_matmul_done, 1)
                pe.wait_ge(L2x_vector_done, 226*b + 367)
                for i in range(4):
                    last = pe.transpose(ps1[:, 3, 128 * i:128 * i + 128], qk_1[:, i, :], ident[:, :])
                last.then_inc(L2x_matmul_done, 1)
                pe.wait_ge(L2x_scalar_done, 108*b + 183)
                for i in range(2):
                    last = pe.transpose(ps0[:, 2, 128 * i:128 * i + 128], qk_0[:, 4 + i, :], ident[:, :])
                last.then_inc(L2x_matmul_done, 1)
                pe.wait_ge(L2x_scalar_done, 108*b + 184)
                for i in range(2):
                    last = pe.transpose(ps1[:, 2, 128 * i:128 * i + 128], qk_1[:, 4 + i, :], ident[:, :])
                last.then_inc(L2x_matmul_done, 1)
                pe.wait_ge(L2x_pool_done, 52*b + 33)
                for i in range(4):
                    pe.matmul(ps0[:, 0, 0:256], P2_0[:, i, :], w_p2[:, 16 + i, :], start=False, stop=False)
                pe.wait_ge(L2x_scalar_done, 108*b + 185)
                for i in range(4):
                    last = pe.matmul(ps0[:, 2, 128 * i:128 * i + 128], qT2_0[:, 128 * i:128 * i + 128], kT2_0[:, 128 * (i // 2):128 * (i // 2) + 128], start=True, stop=True)
                last.then_inc(L2x_matmul_done, 1)
                pe.wait_ge(L2x_scalar_done, 108*b + 186)
                for i in range(4):
                    last = pe.matmul(ps1[:, 2, 128 * i:128 * i + 128], qT2_1[:, 128 * i:128 * i + 128], kT2_1[:, 128 * (i // 2):128 * (i // 2) + 128], start=True, stop=True)
                last.then_inc(L2x_matmul_done, 1)
                pe.wait_ge(L2x_pool_done, 52*b + 34)
                for i in range(4):
                    last = pe.matmul(ps1[:, 0, 0:256], P2_1[:, i, :], w_p2[:, 16 + i, :], start=False, stop=False)
                last.then_inc(L2x_matmul_done, 1)
                for k in range(2):
                    last = pe.matmul(ps1[:, 1, :], xs_1[:, 1, k, :], w_qx2[:, k, 1024:1536], start=k == 0, stop=k == 1)
                last.then_inc(L2x_matmul_done, 1)
                pe.wait_ge(L2x_pool_done, 52*b + 35)
                for i in range(4):
                    last = pe.transpose(ps0[:, 3, 128 * i:128 * i + 128], P2_0[:, i, :], ident[:, :])
                last.then_inc(L2x_matmul_done, 1)
                for k in range(2):
                    pe.matmul(ps0[:, 2, 0:256], cx_0[:, k, :], w_kv2[:, k, 512:768], start=k == 0, stop=k == 1)
                pe.wait_ge(L2x_scalar_done, 108*b + 188)
                for k in range(2):
                    pe.matmul(ps1[:, 2, 0:256], cx_1[:, k, :], w_kv2[:, k, 512:768], start=k == 0, stop=k == 1)
                pe.wait_ge(L2x_pool_done, 52*b + 36)
                for i in range(4):
                    last = pe.transpose(ps1[:, 3, 128 * i:128 * i + 128], P2_1[:, i, :], ident[:, :])
                last.then_inc(L2x_matmul_done, 1)
                pe.wait_ge(L2x_scalar_done, 108*b + 189)
                for i in range(2):
                    last = pe.matmul(ps0[:, 3, 256 * i:256 * i + 256], v2_0[:, 128 * i:128 * i + 128], PT2_0[:, 256 * i:256 * i + 256], start=True, stop=True)
                last.then_inc(L2x_matmul_done, 1)
                for k in range(2):
                    last = pe.matmul(ps0[:, 2, 256:512], cx_0[:, k, :], w_kv2[:, k, 1536:1792], start=k == 0, stop=k == 1)
                last.then_inc(L2x_matmul_done, 1)
                pe.wait_ge(L2x_scalar_done, 108*b + 190)
                for i in range(2):
                    last = pe.matmul(ps1[:, 3, 256 * i:256 * i + 256], v2_1[:, 128 * i:128 * i + 128], PT2_1[:, 256 * i:256 * i + 256], start=True, stop=True)
                last.then_inc(L2x_matmul_done, 1)
                for k in range(2):
                    last = pe.matmul(ps1[:, 2, 256:512], cx_1[:, k, :], w_kv2[:, k, 1536:1792], start=k == 0, stop=k == 1)
                last.then_inc(L2x_matmul_done, 1)
                pe.wait_ge(L2x_vector_done, 226*b + 389)
                for i in range(4):
                    last = pe.transpose(ps0[:, 3, 128 * i:128 * i + 128], qk_0[:, i, :], ident[:, :])
                last.then_inc(L2x_matmul_done, 1)
                for k in range(2):
                    last = pe.matmul(ps0[:, 1, :], xs_0[:, 1, k, :], w_qx2[:, k, 1536:2048], start=k == 0, stop=k == 1)
                last.then_inc(L2x_matmul_done, 1)
                pe.wait_ge(L2x_vector_done, 226*b + 392)
                for i in range(4):
                    last = pe.transpose(ps1[:, 3, 128 * i:128 * i + 128], qk_1[:, i, :], ident[:, :])
                last.then_inc(L2x_matmul_done, 1)
                pe.wait_ge(L2x_scalar_done, 108*b + 195)
                for i in range(2):
                    last = pe.transpose(ps0[:, 2, 128 * i:128 * i + 128], qk_0[:, 4 + i, :], ident[:, :])
                last.then_inc(L2x_matmul_done, 1)
                pe.wait_ge(L2x_scalar_done, 108*b + 196)
                for i in range(2):
                    last = pe.transpose(ps1[:, 2, 128 * i:128 * i + 128], qk_1[:, 4 + i, :], ident[:, :])
                last.then_inc(L2x_matmul_done, 1)
                pe.wait_ge(L2x_pool_done, 52*b + 39)
                for i in range(4):
                    pe.matmul(ps0[:, 0, 0:256], P2_0[:, i, :], w_p2[:, 20 + i, :], start=False, stop=False)
                pe.wait_ge(L2x_scalar_done, 108*b + 197)
                for i in range(4):
                    last = pe.matmul(ps0[:, 2, 128 * i:128 * i + 128], qT2_0[:, 128 * i:128 * i + 128], kT2_0[:, 128 * (i // 2):128 * (i // 2) + 128], start=True, stop=True)
                last.then_inc(L2x_matmul_done, 1)
                pe.wait_ge(L2x_scalar_done, 108*b + 198)
                for i in range(4):
                    last = pe.matmul(ps1[:, 2, 128 * i:128 * i + 128], qT2_1[:, 128 * i:128 * i + 128], kT2_1[:, 128 * (i // 2):128 * (i // 2) + 128], start=True, stop=True)
                last.then_inc(L2x_matmul_done, 1)
                pe.wait_ge(L2x_pool_done, 52*b + 40)
                for i in range(4):
                    last = pe.matmul(ps1[:, 0, 0:256], P2_1[:, i, :], w_p2[:, 20 + i, :], start=False, stop=False)
                last.then_inc(L2x_matmul_done, 1)
                for k in range(2):
                    last = pe.matmul(ps1[:, 1, :], xs_1[:, 1, k, :], w_qx2[:, k, 1536:2048], start=k == 0, stop=k == 1)
                last.then_inc(L2x_matmul_done, 1)
                pe.wait_ge(L2x_pool_done, 52*b + 41)
                for i in range(4):
                    last = pe.transpose(ps0[:, 3, 128 * i:128 * i + 128], P2_0[:, i, :], ident[:, :])
                last.then_inc(L2x_matmul_done, 1)
                for k in range(2):
                    pe.matmul(ps0[:, 2, 0:256], cx_0[:, k, :], w_kv2[:, k, 768:1024], start=k == 0, stop=k == 1)
                pe.wait_ge(L2x_scalar_done, 108*b + 200)
                for k in range(2):
                    pe.matmul(ps1[:, 2, 0:256], cx_1[:, k, :], w_kv2[:, k, 768:1024], start=k == 0, stop=k == 1)
                pe.wait_ge(L2x_pool_done, 52*b + 42)
                for i in range(4):
                    last = pe.transpose(ps1[:, 3, 128 * i:128 * i + 128], P2_1[:, i, :], ident[:, :])
                last.then_inc(L2x_matmul_done, 1)
                pe.wait_ge(L2x_scalar_done, 108*b + 201)
                for i in range(2):
                    last = pe.matmul(ps0[:, 3, 256 * i:256 * i + 256], v2_0[:, 128 * i:128 * i + 128], PT2_0[:, 256 * i:256 * i + 256], start=True, stop=True)
                last.then_inc(L2x_matmul_done, 1)
                for k in range(2):
                    last = pe.matmul(ps0[:, 2, 256:512], cx_0[:, k, :], w_kv2[:, k, 1792:2048], start=k == 0, stop=k == 1)
                last.then_inc(L2x_matmul_done, 1)
                pe.wait_ge(L2x_scalar_done, 108*b + 202)
                for i in range(2):
                    last = pe.matmul(ps1[:, 3, 256 * i:256 * i + 256], v2_1[:, 128 * i:128 * i + 128], PT2_1[:, 256 * i:256 * i + 256], start=True, stop=True)
                last.then_inc(L2x_matmul_done, 1)
                for k in range(2):
                    last = pe.matmul(ps1[:, 2, 256:512], cx_1[:, k, :], w_kv2[:, k, 1792:2048], start=k == 0, stop=k == 1)
                last.then_inc(L2x_matmul_done, 1)
                pe.wait_ge(L2x_vector_done, 226*b + 414)
                for i in range(4):
                    last = pe.transpose(ps0[:, 3, 128 * i:128 * i + 128], qk_0[:, i, :], ident[:, :])
                last.then_inc(L2x_matmul_done, 1)
                pe.wait_ge(L2x_vector_done, 226*b + 417)
                for i in range(4):
                    last = pe.transpose(ps1[:, 3, 128 * i:128 * i + 128], qk_1[:, i, :], ident[:, :])
                last.then_inc(L2x_matmul_done, 1)
                pe.wait_ge(L2x_scalar_done, 108*b + 207)
                for i in range(2):
                    last = pe.transpose(ps0[:, 2, 128 * i:128 * i + 128], qk_0[:, 4 + i, :], ident[:, :])
                last.then_inc(L2x_matmul_done, 1)
                pe.wait_ge(L2x_pool_done, 52*b + 45)
                for i in range(4):
                    pe.matmul(ps0[:, 0, 0:256], P2_0[:, i, :], w_p2[:, 24 + i, :], start=False, stop=False)
                pe.wait_ge(L2x_scalar_done, 108*b + 208)
                for i in range(2):
                    last = pe.transpose(ps1[:, 2, 128 * i:128 * i + 128], qk_1[:, 4 + i, :], ident[:, :])
                last.then_inc(L2x_matmul_done, 1)
                pe.wait_ge(L2x_scalar_done, 108*b + 209)
                for i in range(4):
                    last = pe.matmul(ps0[:, 2, 128 * i:128 * i + 128], qT2_0[:, 128 * i:128 * i + 128], kT2_0[:, 128 * (i // 2):128 * (i // 2) + 128], start=True, stop=True)
                last.then_inc(L2x_matmul_done, 1)
                pe.wait_ge(L2x_scalar_done, 108*b + 210)
                for i in range(4):
                    last = pe.matmul(ps1[:, 2, 128 * i:128 * i + 128], qT2_1[:, 128 * i:128 * i + 128], kT2_1[:, 128 * (i // 2):128 * (i // 2) + 128], start=True, stop=True)
                last.then_inc(L2x_matmul_done, 1)
                pe.wait_ge(L2x_pool_done, 52*b + 46)
                for i in range(4):
                    last = pe.matmul(ps1[:, 0, 0:256], P2_1[:, i, :], w_p2[:, 24 + i, :], start=False, stop=False)
                last.then_inc(L2x_matmul_done, 1)
                pe.wait_ge(L2x_pool_done, 52*b + 47)
                for i in range(4):
                    last = pe.transpose(ps0[:, 3, 128 * i:128 * i + 128], P2_0[:, i, :], ident[:, :])
                last.then_inc(L2x_matmul_done, 1)
                pe.wait_ge(L2x_scalar_done, 108*b + 213)
                for i in range(2):
                    last = pe.matmul(ps0[:, 3, 256 * i:256 * i + 256], v2_0[:, 128 * i:128 * i + 128], PT2_0[:, 256 * i:256 * i + 256], start=True, stop=True)
                last.then_inc(L2x_matmul_done, 1)
                pe.wait_ge(L2x_pool_done, 52*b + 48)
                for i in range(4):
                    last = pe.transpose(ps1[:, 3, 128 * i:128 * i + 128], P2_1[:, i, :], ident[:, :])
                last.then_inc(L2x_matmul_done, 1)
                pe.wait_ge(L2x_scalar_done, 108*b + 214)
                for i in range(2):
                    last = pe.matmul(ps1[:, 3, 256 * i:256 * i + 256], v2_1[:, 128 * i:128 * i + 128], PT2_1[:, 256 * i:256 * i + 256], start=True, stop=True)
                last.then_inc(L2x_matmul_done, 1)
                pe.wait_ge(L2x_pool_done, 52*b + 50)
                for i in range(4):
                    last = pe.matmul(ps0[:, 0, 0:256], P2_0[:, i, :], w_p2[:, 28 + i, :], start=False, stop=i == 3)
                last.then_inc(L2x_matmul_done, 1)
                pe.wait_ge(L2x_pool_done, 52*b + 52)
                for i in range(4):
                    last = pe.matmul(ps1[:, 0, 0:256], P2_1[:, i, :], w_p2[:, 28 + i, :], start=False, stop=i == 3)
                last.then_inc(L2x_matmul_done, 1)
                pe.wait_ge(L2x_vector_done, 226*b + 433)
                for k in range(2):
                    last = pe.transpose(ps0[:, 0, 128 * k:128 * k + 128], un0[:, 128 * k:128 * k + 128], ident[:, :])
                last.then_inc(L2x_matmul_done, 1)
                pe.wait_ge(L2x_vector_done, 226*b + 434)
                for k in range(2):
                    last = pe.transpose(ps1[:, 0, 128 * k:128 * k + 128], un1[:, 128 * k:128 * k + 128], ident[:, :])
                last.then_inc(L2x_matmul_done, 1)

            pe.wait_ge(L2f_vector_done, 50)
            for k in range(2):
                last = pe.transpose(ps0[:, 0, 128 * k:128 * k + 128], u0[:, 128 * k:128 * k + 128], ident[:, :])
            last.then_inc(L2f_matmul_done, 1)
            pe.wait_ge(L2f_vector_done, 51)
            for k in range(2):
                last = pe.transpose(ps1[:, 0, 128 * k:128 * k + 128], u1[:, 128 * k:128 * k + 128], ident[:, :])
            last.then_inc(L2f_matmul_done, 1)
            pe.wait_ge(L2f_w_loaded, 128)
            pe.wait_ge(L2f_ue_loaded, 32)
            pe.wait_ge(L2f_scalar_done, 37)
            with pe.Fori(0, 4) as b:
                pe.wait_ge(L2f_vector_done, 53*b + 3)
                pe.wait_ge(L2f_scalar_done, 37*b + 36)
                for j in range(8):
                    for k in range(2):
                        last = pe.matmul(psf0[:, 1024 + 128 * j:1152 + 128 * j], w_u2[:, k, 128 * j:128 * j + 128], unT0[:, k, :], start=k == 0, stop=k == 1)
                last.then_inc(L2f_matmul_done, 1)
                pe.wait_ge(L2f_vector_done, 53*b + 4)
                pe.wait_ge(L2f_scalar_done, 37*b + 37)
                for j in range(8):
                    for k in range(2):
                        last = pe.matmul(psf1[:, 1024 + 128 * j:1152 + 128 * j], w_u2[:, k, 128 * j:128 * j + 128], unT1[:, k, :], start=k == 0, stop=k == 1)
                last.then_inc(L2f_matmul_done, 1)
                pe.wait_ge(L2f_scalar_done, 37*b + 42)
                for k in range(8):
                    last = pe.matmul(ps0[:, 1, 0:128], w_d2[:, k, :], he_0[:, k, :], start=k == 0, stop=k == 7)
                last.then_inc(L2f_matmul_done, 1)
                pe.wait_ge(L2f_scalar_done, 37*b + 43)
                for k in range(8):
                    last = pe.matmul(ps1[:, 1, 0:128], w_d2[:, k, :], he_1[:, k, :], start=k == 0, stop=k == 7)
                last.then_inc(L2f_matmul_done, 1)
                pe.wait_ge(L2f_vector_done, 53*b + 58)
                for j in range(8):
                    last = pe.matmul(psf0[:, 1024 + 128 * j:1152 + 128 * j], w_q2f[:, 128 * j:128 * j + 128], h2T_0[:, :], start=True, stop=True)
                last.then_inc(L2f_matmul_done, 1)
                pe.wait_ge(L2f_vector_done, 53*b + 59)
                for j in range(8):
                    last = pe.matmul(psf1[:, 1024 + 128 * j:1152 + 128 * j], w_q2f[:, 128 * j:128 * j + 128], h2T_1[:, :], start=True, stop=True)
                last.then_inc(L2f_matmul_done, 1)
                pe.wait_ge(L2f_scalar_done, 37*b + 44)
                for p in range(2):
                    for g in range(4):
                        last = pe.matmul(psf0[:, 512 * p + 90 * g:512 * p + 90 * g + 90], qc_0[:, 4 * p + g, :], keys[:, 4 * p + g, :], start=True, stop=True)
                last.then_inc(L2f_matmul_done, 1)
                pe.wait_ge(L2f_scalar_done, 37*b + 45)
                for p in range(2):
                    for g in range(4):
                        last = pe.matmul(psf1[:, 512 * p + 90 * g:512 * p + 90 * g + 90], qc_1[:, 4 * p + g, :], keys[:, 4 * p + g, :], start=True, stop=True)
                last.then_inc(L2f_matmul_done, 1)
                pe.wait_ge(L2f_scalar_done, 37*b + 46)
                for c in range(4):
                    last = pe.matmul(psf0[:, 512 * c:min(512 * c + 512, 2025)], h2T_0[:, :], de[:, 512 * c:min(512 * c + 512, 2025)], start=True, stop=True)
                last.then_inc(L2f_matmul_done, 1)
                pe.wait_ge(L2f_scalar_done, 37*b + 47)
                for c in range(4):
                    last = pe.matmul(psf1[:, 512 * c:min(512 * c + 512, 2025)], h2T_1[:, :], de[:, 512 * c:min(512 * c + 512, 2025)], start=True, stop=True)
                last.then_inc(L2f_matmul_done, 1)
                pe.wait_ge(L2f_scalar_done, 37*b + 53)
                for c in range(15):
                    pe.matmul(psf0[:, 128 * c:128 * c + 128], Qfa_0[:, 128 * c:128 * c + 128], ident[:, :], start=c % 4 == 0, stop=False, skip_group_check=True)
                pe.wait_ge(L2f_scalar_done, 37*b + 54)
                for c in range(15):
                    pe.matmul(psf1[:, 128 * c:128 * c + 128], Qfa_1[:, 128 * c:128 * c + 128], ident[:, :], start=c % 4 == 0, stop=False, skip_group_check=True)
                pe.matmul(psf0[0:105, 1920:2048], Qfa_0[:, 1920:2025], ident[:, :], start=False, stop=False, skip_group_check=True).then_inc(L2f_matmul_done, 1)
                pe.matmul(psf1[0:105, 1920:2048], Qfa_1[:, 1920:2025], ident[:, :], start=False, stop=False, skip_group_check=True).then_inc(L2f_matmul_done, 1)
                pe.wait_ge(L2f_scalar_done, 37*b + 55)
                for c in range(15):
                    pe.matmul(psf0[:, 128 * c:128 * c + 128], Qfb_0[:, 128 * c:128 * c + 128], ident[:, :], start=False, stop=False, skip_group_check=True)
                pe.wait_ge(L2f_scalar_done, 37*b + 56)
                for c in range(15):
                    pe.matmul(psf1[:, 128 * c:128 * c + 128], Qfb_1[:, 128 * c:128 * c + 128], ident[:, :], start=False, stop=False, skip_group_check=True)
                pe.matmul(psf0[0:105, 1920:2048], Qfb_0[:, 1920:2025], ident[:, :], start=False, stop=False, skip_group_check=True).then_inc(L2f_matmul_done, 1)
                pe.matmul(psf1[0:105, 1920:2048], Qfb_1[:, 1920:2025], ident[:, :], start=False, stop=False, skip_group_check=True).then_inc(L2f_matmul_done, 1)
                pe.wait_ge(L2f_scalar_done, 37*b + 57)
                for c in range(15):
                    pe.matmul(psf0[:, 128 * c:128 * c + 128], Qfa_0[:, 128 * c:128 * c + 128], ident[:, :], start=False, stop=False, skip_group_check=True)
                pe.wait_ge(L2f_scalar_done, 37*b + 58)
                for c in range(15):
                    pe.matmul(psf1[:, 128 * c:128 * c + 128], Qfa_1[:, 128 * c:128 * c + 128], ident[:, :], start=False, stop=False, skip_group_check=True)
                pe.matmul(psf0[0:105, 1920:2048], Qfa_0[:, 1920:2025], ident[:, :], start=False, stop=False, skip_group_check=True).then_inc(L2f_matmul_done, 1)
                pe.matmul(psf1[0:105, 1920:2048], Qfa_1[:, 1920:2025], ident[:, :], start=False, stop=False, skip_group_check=True).then_inc(L2f_matmul_done, 1)
                pe.wait_ge(L2f_scalar_done, 37*b + 59)
                for c in range(15):
                    pe.matmul(psf0[:, 128 * c:128 * c + 128], Qfb_0[:, 128 * c:128 * c + 128], ident[:, :], start=False, stop=False, skip_group_check=True)
                pe.wait_ge(L2f_scalar_done, 37*b + 60)
                for c in range(15):
                    pe.matmul(psf1[:, 128 * c:128 * c + 128], Qfb_1[:, 128 * c:128 * c + 128], ident[:, :], start=False, stop=False, skip_group_check=True)
                pe.matmul(psf0[0:105, 1920:2048], Qfb_0[:, 1920:2025], ident[:, :], start=False, stop=False, skip_group_check=True).then_inc(L2f_matmul_done, 1)
                pe.matmul(psf1[0:105, 1920:2048], Qfb_1[:, 1920:2025], ident[:, :], start=False, stop=False, skip_group_check=True).then_inc(L2f_matmul_done, 1)
                pe.wait_ge(L2f_scalar_done, 37*b + 61)
                for c in range(15):
                    pe.matmul(psf0[:, 128 * c:128 * c + 128], Qfa_0[:, 128 * c:128 * c + 128], ident[:, :], start=False, stop=False, skip_group_check=True)
                pe.wait_ge(L2f_scalar_done, 37*b + 62)
                for c in range(15):
                    pe.matmul(psf1[:, 128 * c:128 * c + 128], Qfa_1[:, 128 * c:128 * c + 128], ident[:, :], start=False, stop=False, skip_group_check=True)
                pe.matmul(psf0[0:105, 1920:2048], Qfa_0[:, 1920:2025], ident[:, :], start=False, stop=False, skip_group_check=True).then_inc(L2f_matmul_done, 1)
                pe.matmul(psf1[0:105, 1920:2048], Qfa_1[:, 1920:2025], ident[:, :], start=False, stop=False, skip_group_check=True).then_inc(L2f_matmul_done, 1)
                pe.wait_ge(L2f_scalar_done, 37*b + 63)
                for c in range(15):
                    pe.matmul(psf0[:, 128 * c:128 * c + 128], Qfb_0[:, 128 * c:128 * c + 128], ident[:, :], start=False, stop=False, skip_group_check=True)
                pe.wait_ge(L2f_scalar_done, 37*b + 64)
                for c in range(15):
                    pe.matmul(psf1[:, 128 * c:128 * c + 128], Qfb_1[:, 128 * c:128 * c + 128], ident[:, :], start=False, stop=False, skip_group_check=True)
                pe.matmul(psf0[0:105, 1920:2048], Qfb_0[:, 1920:2025], ident[:, :], start=False, stop=False, skip_group_check=True).then_inc(L2f_matmul_done, 1)
                pe.matmul(psf1[0:105, 1920:2048], Qfb_1[:, 1920:2025], ident[:, :], start=False, stop=False, skip_group_check=True).then_inc(L2f_matmul_done, 1)
                pe.wait_ge(L2f_scalar_done, 37*b + 65)
                for c in range(15):
                    pe.matmul(psf0[:, 128 * c:128 * c + 128], Qfa_0[:, 128 * c:128 * c + 128], ident[:, :], start=False, stop=False, skip_group_check=True)
                pe.wait_ge(L2f_scalar_done, 37*b + 66)
                for c in range(15):
                    pe.matmul(psf1[:, 128 * c:128 * c + 128], Qfa_1[:, 128 * c:128 * c + 128], ident[:, :], start=False, stop=False, skip_group_check=True)
                pe.matmul(psf0[0:105, 1920:2048], Qfa_0[:, 1920:2025], ident[:, :], start=False, stop=False, skip_group_check=True)
                pe.matmul(psf1[0:105, 1920:2048], Qfa_1[:, 1920:2025], ident[:, :], start=False, stop=False, skip_group_check=True)
                pe.wait_ge(L2f_scalar_done, 37*b + 67)
                for c in range(15):
                    pe.matmul(psf0[:, 128 * c:128 * c + 128], Qfb_0[:, 128 * c:128 * c + 128], ident[:, :], start=False, stop=True, skip_group_check=True)
                pe.wait_ge(L2f_scalar_done, 37*b + 68)
                for c in range(15):
                    pe.matmul(psf1[:, 128 * c:128 * c + 128], Qfb_1[:, 128 * c:128 * c + 128], ident[:, :], start=False, stop=True, skip_group_check=True)
                pe.matmul(psf0[0:105, 1920:2048], Qfb_0[:, 1920:2025], ident[:, :], start=False, stop=True, skip_group_check=True).then_inc(L2f_matmul_done, 1)
                pe.matmul(psf1[0:105, 1920:2048], Qfb_1[:, 1920:2025], ident[:, :], start=False, stop=True, skip_group_check=True).then_inc(L2f_matmul_done, 1)
                pe.wait_ge(L2f_scalar_done, 37*b + 69)
                for c in range(15):
                    last = pe.matmul(ps0[:, 0, 0:256], GT_0[:, c, :], ue[:, c, :], start=c == 0, stop=False)
                last.then_inc(L2f_matmul_done, 1)
                pe.wait_ge(L2f_scalar_done, 37*b + 70)
                for c in range(15):
                    pe.matmul(ps1[:, 0, 0:256], GT_1[:, c, :], ue[:, c, :], start=c == 0, stop=False)
                pe.wait_ge(L2f_scalar_done, 37*b + 71)
                pe.matmul(ps0[:, 0, 0:256], GT_0[0:105, 15, :], ue[0:105, 15, :], start=False, stop=True).then_inc(L2f_matmul_done, 1)
                pe.wait_ge(L2f_scalar_done, 37*b + 72)
                pe.matmul(ps1[:, 0, 0:256], GT_1[0:105, 15, :], ue[0:105, 15, :], start=False, stop=True).then_inc(L2f_matmul_done, 1)
                pe.wait_ge(L2f_vector_done, 53*b + 103)
                for k in range(2):
                    last = pe.transpose(ps0[:, 0, 128 * k:128 * k + 128], u0[:, 128 * k:128 * k + 128], ident[:, :])
                last.then_inc(L2f_matmul_done, 1)
                pe.wait_ge(L2f_vector_done, 53*b + 104)
                for k in range(2):
                    last = pe.transpose(ps1[:, 0, 128 * k:128 * k + 128], u1[:, 128 * k:128 * k + 128], ident[:, :])
                last.then_inc(L2f_matmul_done, 1)

            pe.wait_ge(L3a_vector_done, 71)
            for k in range(2):
                last = pe.transpose(ps0[:, 0, 128 * k:128 * k + 128], u0[:, 128 * k:128 * k + 128], ident[:, :])
            last.then_inc(L3a_matmul_done, 1)
            pe.wait_ge(L3a_vector_done, 72)
            for k in range(2):
                last = pe.transpose(ps1[:, 0, 128 * k:128 * k + 128], u1[:, 128 * k:128 * k + 128], ident[:, :])
            last.then_inc(L3a_matmul_done, 1)
            pe.wait_ge(L3a_w_loaded, 128)
            pe.wait_ge(L2f_pool_done, 76)
            pe.wait_ge(L3a_scalar_done, 40)
            with pe.Fori(0, 4) as b:
                pe.wait_ge(L3a_vector_done, 74*b + 71)
                pe.wait_ge(L3a_scalar_done, 40*b + 39)
                for j in range(2):
                    for k in range(2):
                        pe.matmul(ps0[:, 1, 128 * j:128 * j + 128], w_q3[:, k, 128 * j:128 * j + 128], unT0[:, k, :], start=k == 0, stop=k == 1)
                pe.wait_ge(L3a_vector_done, 74*b + 72)
                pe.wait_ge(L3a_scalar_done, 40*b + 40)
                for j in range(2):
                    for k in range(2):
                        pe.matmul(ps1[:, 1, 128 * j:128 * j + 128], w_q3[:, k, 128 * j:128 * j + 128], unT1[:, k, :], start=k == 0, stop=k == 1)
                for j in range(2):
                    for k in range(2):
                        last = pe.matmul(ps0[:, 1, 256 + 128 * j:384 + 128 * j], w_kr3[:, k, 128 * j:128 * j + 128], unT0[:, k, :], start=k == 0, stop=k == 1)
                last.then_inc(L3a_matmul_done, 1)
                for j in range(2):
                    for k in range(2):
                        last = pe.matmul(ps1[:, 1, 256 + 128 * j:384 + 128 * j], w_kr3[:, k, 128 * j:128 * j + 128], unT1[:, k, :], start=k == 0, stop=k == 1)
                last.then_inc(L3a_matmul_done, 1)
                for k in range(2):
                    pe.matmul(ps0[:, 2, 0:64], unT0[:, k, :], w_v3[:, k, :], start=k == 0, stop=k == 1)
                for k in range(2):
                    pe.matmul(ps1[:, 2, 0:64], unT1[:, k, :], w_v3[:, k, :], start=k == 0, stop=k == 1)
                pe.wait_ge(L3a_vector_done, 74*b + 78)
                pe.matmul(ps0[:, 1, :], qT_0[:, 0, :], kR_0[:, 0, 0:4, :], start=True, stop=True).then_inc(L3a_matmul_done, 1)
                pe.wait_ge(L3a_vector_done, 74*b + 80)
                pe.matmul(ps1[:, 1, :], qT_1[:, 0, :], kR_1[:, 0, 0:4, :], start=True, stop=True).then_inc(L3a_matmul_done, 1)
                pe.wait_ge(L3a_scalar_done, 40*b + 45)
                pe.matmul(ps0[:, 1, :], qT_0[:, 0, :], kR_0[:, 0, 4:8, :], start=True, stop=True).then_inc(L3a_matmul_done, 1)
                for i in range(4):
                    last = pe.transpose(ps0[:, 2, 128 * i:128 * i + 128], S_0[:, i, :], ident[:, :])
                last.then_inc(L3a_matmul_done, 1)
                pe.wait_ge(L3a_scalar_done, 40*b + 46)
                pe.matmul(ps1[:, 1, :], qT_1[:, 0, :], kR_1[:, 0, 4:8, :], start=True, stop=True).then_inc(L3a_matmul_done, 1)
                for i in range(4):
                    last = pe.transpose(ps1[:, 2, 128 * i:128 * i + 128], S_1[:, i, :], ident[:, :])
                last.then_inc(L3a_matmul_done, 1)
                pe.wait_ge(L3a_scalar_done, 40*b + 47)
                for i in range(4):
                    last = pe.matmul(ps0[:, 3, 9 * i:9 * i + 9], PT_0[:, i, :], vg_0[:, 0, :], start=True, stop=True)
                last.then_inc(L3a_matmul_done, 1)
                pe.wait_ge(L3a_scalar_done, 40*b + 48)
                pe.matmul(ps0[:, 1, :], qT_0[:, 0, :], kR_0[:, 0, 8:12, :], start=True, stop=True).then_inc(L3a_matmul_done, 1)
                for i in range(4):
                    last = pe.transpose(ps0[:, 2, 128 * i:128 * i + 128], S_0[:, i, :], ident[:, :])
                last.then_inc(L3a_matmul_done, 1)
                pe.wait_ge(L3a_scalar_done, 40*b + 49)
                for i in range(4):
                    last = pe.matmul(ps1[:, 3, 9 * i:9 * i + 9], PT_1[:, i, :], vg_1[:, 0, :], start=True, stop=True)
                last.then_inc(L3a_matmul_done, 1)
                pe.wait_ge(L3a_scalar_done, 40*b + 50)
                pe.matmul(ps1[:, 1, :], qT_1[:, 0, :], kR_1[:, 0, 8:12, :], start=True, stop=True).then_inc(L3a_matmul_done, 1)
                for i in range(4):
                    last = pe.transpose(ps1[:, 2, 128 * i:128 * i + 128], S_1[:, i, :], ident[:, :])
                last.then_inc(L3a_matmul_done, 1)
                pe.wait_ge(L3a_vector_done, 74*b + 90)
                pe.wait_ge(L3a_scalar_done, 40*b + 51)
                for i in range(4):
                    last = pe.matmul(ps0[:, 3, 9 * i:9 * i + 9], PT_0[:, i, :], vg_0[:, 1, :], start=True, stop=True)
                last.then_inc(L3a_matmul_done, 1)
                pe.wait_ge(L3a_scalar_done, 40*b + 52)
                pe.matmul(ps0[:, 1, :], qT_0[:, 0, :], kR_0[:, 0, 12:16, :], start=True, stop=True).then_inc(L3a_matmul_done, 1)
                for i in range(4):
                    last = pe.transpose(ps0[:, 2, 128 * i:128 * i + 128], S_0[:, i, :], ident[:, :])
                last.then_inc(L3a_matmul_done, 1)
                pe.wait_ge(L3a_vector_done, 74*b + 94)
                pe.wait_ge(L3a_scalar_done, 40*b + 53)
                for i in range(4):
                    last = pe.matmul(ps1[:, 3, 9 * i:9 * i + 9], PT_1[:, i, :], vg_1[:, 1, :], start=True, stop=True)
                last.then_inc(L3a_matmul_done, 1)
                pe.wait_ge(L3a_scalar_done, 40*b + 54)
                pe.matmul(ps1[:, 1, :], qT_1[:, 0, :], kR_1[:, 0, 12:16, :], start=True, stop=True).then_inc(L3a_matmul_done, 1)
                for i in range(4):
                    last = pe.transpose(ps1[:, 2, 128 * i:128 * i + 128], S_1[:, i, :], ident[:, :])
                last.then_inc(L3a_matmul_done, 1)
                pe.wait_ge(L3a_vector_done, 74*b + 98)
                pe.wait_ge(L3a_scalar_done, 40*b + 55)
                for i in range(4):
                    last = pe.matmul(ps0[:, 3, 9 * i:9 * i + 9], PT_0[:, i, :], vg_0[:, 2, :], start=True, stop=True)
                last.then_inc(L3a_matmul_done, 1)
                pe.wait_ge(L3a_pool_done, 3*b + 4)
                pe.wait_ge(L3a_scalar_done, 40*b + 56)
                pe.matmul(ps0[:, 1, :], qT_0[:, 1, :], kR_0[:, 1, 0:4, :], start=True, stop=True).then_inc(L3a_matmul_done, 1)
                for i in range(4):
                    last = pe.transpose(ps0[:, 2, 128 * i:128 * i + 128], S_0[:, i, :], ident[:, :])
                last.then_inc(L3a_matmul_done, 1)
                pe.wait_ge(L3a_vector_done, 74*b + 102)
                pe.wait_ge(L3a_scalar_done, 40*b + 57)
                for i in range(4):
                    last = pe.matmul(ps1[:, 3, 9 * i:9 * i + 9], PT_1[:, i, :], vg_1[:, 2, :], start=True, stop=True)
                last.then_inc(L3a_matmul_done, 1)
                pe.wait_ge(L3a_pool_done, 3*b + 5)
                pe.wait_ge(L3a_scalar_done, 40*b + 58)
                pe.matmul(ps1[:, 1, :], qT_1[:, 1, :], kR_1[:, 1, 0:4, :], start=True, stop=True).then_inc(L3a_matmul_done, 1)
                for i in range(4):
                    last = pe.transpose(ps1[:, 2, 128 * i:128 * i + 128], S_1[:, i, :], ident[:, :])
                last.then_inc(L3a_matmul_done, 1)
                pe.wait_ge(L3a_vector_done, 74*b + 106)
                pe.wait_ge(L3a_scalar_done, 40*b + 59)
                for i in range(4):
                    last = pe.matmul(ps0[:, 3, 9 * i:9 * i + 9], PT_0[:, i, :], vg_0[:, 3, :], start=True, stop=True)
                last.then_inc(L3a_matmul_done, 1)
                pe.wait_ge(L3a_scalar_done, 40*b + 60)
                pe.matmul(ps0[:, 1, :], qT_0[:, 1, :], kR_0[:, 1, 4:8, :], start=True, stop=True).then_inc(L3a_matmul_done, 1)
                for i in range(4):
                    last = pe.transpose(ps0[:, 2, 128 * i:128 * i + 128], S_0[:, i, :], ident[:, :])
                last.then_inc(L3a_matmul_done, 1)
                pe.wait_ge(L3a_vector_done, 74*b + 110)
                pe.wait_ge(L3a_scalar_done, 40*b + 61)
                for i in range(4):
                    last = pe.matmul(ps1[:, 3, 9 * i:9 * i + 9], PT_1[:, i, :], vg_1[:, 3, :], start=True, stop=True)
                last.then_inc(L3a_matmul_done, 1)
                pe.wait_ge(L3a_scalar_done, 40*b + 62)
                pe.matmul(ps1[:, 1, :], qT_1[:, 1, :], kR_1[:, 1, 4:8, :], start=True, stop=True).then_inc(L3a_matmul_done, 1)
                for i in range(4):
                    last = pe.transpose(ps1[:, 2, 128 * i:128 * i + 128], S_1[:, i, :], ident[:, :])
                last.then_inc(L3a_matmul_done, 1)
                pe.wait_ge(L3a_vector_done, 74*b + 114)
                pe.wait_ge(L3a_scalar_done, 40*b + 63)
                for i in range(4):
                    last = pe.matmul(ps0[:, 3, 9 * i:9 * i + 9], PT_0[:, i, :], vg_0[:, 4, :], start=True, stop=True)
                last.then_inc(L3a_matmul_done, 1)
                pe.wait_ge(L3a_scalar_done, 40*b + 64)
                pe.matmul(ps0[:, 1, :], qT_0[:, 1, :], kR_0[:, 1, 8:12, :], start=True, stop=True).then_inc(L3a_matmul_done, 1)
                for i in range(4):
                    last = pe.transpose(ps0[:, 2, 128 * i:128 * i + 128], S_0[:, i, :], ident[:, :])
                last.then_inc(L3a_matmul_done, 1)
                pe.wait_ge(L3a_vector_done, 74*b + 118)
                pe.wait_ge(L3a_scalar_done, 40*b + 65)
                for i in range(4):
                    last = pe.matmul(ps1[:, 3, 9 * i:9 * i + 9], PT_1[:, i, :], vg_1[:, 4, :], start=True, stop=True)
                last.then_inc(L3a_matmul_done, 1)
                pe.wait_ge(L3a_scalar_done, 40*b + 66)
                pe.matmul(ps1[:, 1, :], qT_1[:, 1, :], kR_1[:, 1, 8:12, :], start=True, stop=True).then_inc(L3a_matmul_done, 1)
                for i in range(4):
                    last = pe.transpose(ps1[:, 2, 128 * i:128 * i + 128], S_1[:, i, :], ident[:, :])
                last.then_inc(L3a_matmul_done, 1)
                pe.wait_ge(L3a_vector_done, 74*b + 122)
                pe.wait_ge(L3a_scalar_done, 40*b + 67)
                for i in range(4):
                    last = pe.matmul(ps0[:, 3, 9 * i:9 * i + 9], PT_0[:, i, :], vg_0[:, 5, :], start=True, stop=True)
                last.then_inc(L3a_matmul_done, 1)
                pe.wait_ge(L3a_scalar_done, 40*b + 68)
                pe.matmul(ps0[:, 1, :], qT_0[:, 1, :], kR_0[:, 1, 12:16, :], start=True, stop=True).then_inc(L3a_matmul_done, 1)
                for i in range(4):
                    last = pe.transpose(ps0[:, 2, 128 * i:128 * i + 128], S_0[:, i, :], ident[:, :])
                last.then_inc(L3a_matmul_done, 1)
                pe.wait_ge(L3a_vector_done, 74*b + 126)
                pe.wait_ge(L3a_scalar_done, 40*b + 69)
                for i in range(4):
                    last = pe.matmul(ps1[:, 3, 9 * i:9 * i + 9], PT_1[:, i, :], vg_1[:, 5, :], start=True, stop=True)
                last.then_inc(L3a_matmul_done, 1)
                pe.wait_ge(L3a_scalar_done, 40*b + 70)
                pe.matmul(ps1[:, 1, :], qT_1[:, 1, :], kR_1[:, 1, 12:16, :], start=True, stop=True).then_inc(L3a_matmul_done, 1)
                for i in range(4):
                    last = pe.transpose(ps1[:, 2, 128 * i:128 * i + 128], S_1[:, i, :], ident[:, :])
                last.then_inc(L3a_matmul_done, 1)
                pe.wait_ge(L3a_vector_done, 74*b + 130)
                pe.wait_ge(L3a_scalar_done, 40*b + 71)
                for i in range(4):
                    last = pe.matmul(ps0[:, 3, 9 * i:9 * i + 9], PT_0[:, i, :], vg_0[:, 6, :], start=True, stop=True)
                last.then_inc(L3a_matmul_done, 1)
                pe.wait_ge(L3a_scalar_done, 40*b + 72)
                for i in range(4):
                    last = pe.transpose(ps0[:, 2, 128 * i:128 * i + 128], S_0[:, i, :], ident[:, :])
                last.then_inc(L3a_matmul_done, 1)
                pe.wait_ge(L3a_vector_done, 74*b + 134)
                pe.wait_ge(L3a_scalar_done, 40*b + 73)
                for i in range(4):
                    last = pe.matmul(ps1[:, 3, 9 * i:9 * i + 9], PT_1[:, i, :], vg_1[:, 6, :], start=True, stop=True)
                last.then_inc(L3a_matmul_done, 1)
                pe.wait_ge(L3a_scalar_done, 40*b + 74)
                for i in range(4):
                    last = pe.transpose(ps1[:, 2, 128 * i:128 * i + 128], S_1[:, i, :], ident[:, :])
                last.then_inc(L3a_matmul_done, 1)
                pe.wait_ge(L3a_vector_done, 74*b + 138)
                pe.wait_ge(L3a_scalar_done, 40*b + 75)
                for i in range(4):
                    last = pe.matmul(ps0[:, 3, 9 * i:9 * i + 9], PT_0[:, i, :], vg_0[:, 7, :], start=True, stop=True)
                last.then_inc(L3a_matmul_done, 1)
                pe.wait_ge(L3a_vector_done, 74*b + 140)
                pe.wait_ge(L3a_scalar_done, 40*b + 76)
                for i in range(4):
                    last = pe.matmul(ps1[:, 3, 9 * i:9 * i + 9], PT_1[:, i, :], vg_1[:, 7, :], start=True, stop=True)
                last.then_inc(L3a_matmul_done, 1)
                pe.wait_ge(L3a_vector_done, 74*b + 142)
                for k in range(2):
                    last = pe.transpose(ps0[:, 0, 128 * k:128 * k + 128], ao_0[:, 128 * k:128 * k + 128], ident[:, :])
                last.then_inc(L3a_matmul_done, 1)
                pe.wait_ge(L3a_vector_done, 74*b + 144)
                for k in range(2):
                    last = pe.transpose(ps1[:, 0, 128 * k:128 * k + 128], ao_1[:, 128 * k:128 * k + 128], ident[:, :])
                last.then_inc(L3a_matmul_done, 1)
                pe.wait_ge(L3a_scalar_done, 40*b + 77)
                for k in range(2):
                    last = pe.matmul(ps0[:, 1, 0:256], unT0[:, k, :], w_o3[:, k, :], start=k == 0, stop=k == 1)
                last.then_inc(L3a_matmul_done, 1)
                pe.wait_ge(L3a_scalar_done, 40*b + 78)
                for k in range(2):
                    last = pe.matmul(ps1[:, 1, 0:256], unT1[:, k, :], w_o3[:, k, :], start=k == 0, stop=k == 1)
                last.then_inc(L3a_matmul_done, 1)
                for k in range(2):
                    last = pe.transpose(ps0[:, 0, 128 * k:128 * k + 128], u0[:, 128 * k:128 * k + 128], ident[:, :])
                last.then_inc(L3a_matmul_done, 1)
                for k in range(2):
                    last = pe.transpose(ps1[:, 0, 128 * k:128 * k + 128], u1[:, 128 * k:128 * k + 128], ident[:, :])
                last.then_inc(L3a_matmul_done, 1)

            pe.sem_inc(L3x_matmul_done, 13)
            pe.wait_ge(L3x_vector_done, 23)
            for k in range(2):
                last = pe.transpose(ps0[:, 0, 128 * k:128 * k + 128], u0[:, 128 * k:128 * k + 128], ident[:, :])
            last.then_inc(L3x_matmul_done, 1)
            pe.wait_ge(L3x_vector_done, 24)
            for k in range(2):
                last = pe.transpose(ps1[:, 0, 128 * k:128 * k + 128], u1[:, 128 * k:128 * k + 128], ident[:, :])
            last.then_inc(L3x_matmul_done, 1)
            pe.wait_ge(L3x_w_loaded, 64)
            pe.wait_ge(L3x_scalar_done, 18)
            with pe.Fori(0, 4) as b:
                pe.wait_ge(L3x_vector_done, 26*b + 23)
                pe.wait_ge(L3x_scalar_done, 18*b + 18)
                for k in range(2):
                    last = pe.matmul(ps0[:, 1, :], unT0[:, k, :], w_qg3[:, k, :], start=k == 0, stop=k == 1)
                last.then_inc(L3x_matmul_done, 1)
                pe.wait_ge(L3x_scalar_done, 18*b + 19)
                for k in range(2):
                    last = pe.matmul(ps0[:, 2, :], cT_0[:, k, :], w_kv3[:, k, :], start=k == 0, stop=k == 1)
                last.then_inc(L3x_matmul_done, 1)
                pe.wait_ge(L3x_scalar_done, 18*b + 20)
                for k in range(2):
                    last = pe.matmul(ps1[:, 2, :], cT_1[:, k, :], w_kv3[:, k, :], start=k == 0, stop=k == 1)
                last.then_inc(L3x_matmul_done, 1)
                pe.wait_ge(L3x_vector_done, 26*b + 24)
                for k in range(2):
                    last = pe.matmul(ps1[:, 1, :], unT1[:, k, :], w_qg3[:, k, :], start=k == 0, stop=k == 1)
                last.then_inc(L3x_matmul_done, 1)
                pe.wait_ge(L3x_vector_done, 26*b + 32)
                for k in range(2):
                    last = pe.transpose(ps0[:, 0, 128 * k:128 * k + 128], q3_0[:, 128 * k:128 * k + 128], ident[:, :])
                last.then_inc(L3x_matmul_done, 1)
                pe.wait_ge(L3x_scalar_done, 18*b + 29)
                for c in range(2):
                    last = pe.matmul(ps0[:, 3, 129 * c:129 * c + 129], k3_0[:, 128 * c:128 * c + 128], v3_0[:, c, :], start=True, stop=True)
                last.then_inc(L3x_matmul_done, 1)
                pe.wait_ge(L3x_scalar_done, 18*b + 31)
                for c in range(2):
                    last = pe.matmul(ps1[:, 3, 129 * c:129 * c + 129], k3_1[:, 128 * c:128 * c + 128], v3_1[:, c, :], start=True, stop=True)
                last.then_inc(L3x_matmul_done, 1)
                pe.wait_ge(L3x_vector_done, 26*b + 40)
                for k in range(2):
                    last = pe.transpose(ps1[:, 0, 128 * k:128 * k + 128], q3_1[:, 128 * k:128 * k + 128], ident[:, :])
                last.then_inc(L3x_matmul_done, 1)
                pe.wait_ge(L3x_vector_done, 26*b + 41)
                for c in range(2):
                    last = pe.matmul(ps0[:, 1, 136 * c:136 * c + 136], unT0[:, c, :], BD_0[:, c, :], start=True, stop=True)
                last.then_inc(L3x_matmul_done, 1)
                pe.wait_ge(L3x_scalar_done, 18*b + 33)
                pe.wait_ge(L3x_vector_done, 26*b + 42)
                for c in range(2):
                    last = pe.matmul(ps1[:, 1, 136 * c:136 * c + 136], unT1[:, c, :], BD_1[:, c, :], start=True, stop=True)
                last.then_inc(L3x_matmul_done, 1)
                pe.wait_ge(L3x_pool_done, 4*b + 5)
                for k in range(2):
                    last = pe.transpose(ps0[:, 0, 128 * k:128 * k + 128], a3_0[:, 128 * k:128 * k + 128], ident[:, :])
                last.then_inc(L3x_matmul_done, 1)
                pe.wait_ge(L3x_pool_done, 4*b + 6)
                for k in range(2):
                    last = pe.transpose(ps1[:, 0, 128 * k:128 * k + 128], a3_1[:, 128 * k:128 * k + 128], ident[:, :])
                last.then_inc(L3x_matmul_done, 1)
                pe.wait_ge(L3x_scalar_done, 18*b + 34)
                for k in range(2):
                    last = pe.matmul(ps0[:, 1, 0:256], unT0[:, k, :], w_ox3[:, k, :], start=k == 0, stop=k == 1)
                last.then_inc(L3x_matmul_done, 1)
                pe.wait_ge(L3x_scalar_done, 18*b + 35)
                for k in range(2):
                    last = pe.matmul(ps1[:, 1, 0:256], unT1[:, k, :], w_ox3[:, k, :], start=k == 0, stop=k == 1)
                last.then_inc(L3x_matmul_done, 1)
                for k in range(2):
                    last = pe.transpose(ps0[:, 0, 128 * k:128 * k + 128], u0[:, 128 * k:128 * k + 128], ident[:, :])
                last.then_inc(L3x_matmul_done, 1)
                for k in range(2):
                    last = pe.transpose(ps1[:, 0, 128 * k:128 * k + 128], u1[:, 128 * k:128 * k + 128], ident[:, :])
                last.then_inc(L3x_matmul_done, 1)

            pe.wait_ge(L3f_vector_done, 58)
            for k in range(2):
                last = pe.transpose(ps0[:, 0, 128 * k:128 * k + 128], un0[:, 128 * k:128 * k + 128], ident[:, :])
            last.then_inc(L3f_matmul_done, 1)
            pe.wait_ge(L3f_vector_done, 59)
            for k in range(2):
                last = pe.transpose(ps1[:, 0, 128 * k:128 * k + 128], un1[:, 128 * k:128 * k + 128], ident[:, :])
            last.then_inc(L3f_matmul_done, 1)
            pe.wait_ge(L3x_pool_done, 18)
            pe.wait_ge(L3f_scalar_done, 38)
            with pe.Fori(0, 4) as b:
                pe.wait_ge(L3f_vector_done, 61*b + 26)
                pe.wait_ge(L3f_scalar_done, 44*b + 37)
                for j in range(4):
                    for k in range(2):
                        last = pe.matmul(ps0[:, 1, 128 * j:128 * j + 128], w_qkv3[:, k, 128 * j:128 * j + 128], unT0[:, k, :], start=k == 0, stop=k == 1)
                last.then_inc(L3f_matmul_done, 1)
                pe.wait_ge(L3f_vector_done, 61*b + 31)
                pe.wait_ge(L3f_scalar_done, 44*b + 38)
                for j in range(4):
                    for k in range(2):
                        last = pe.matmul(ps1[:, 1, 128 * j:128 * j + 128], w_qkv3[:, k, 128 * j:128 * j + 128], unT1[:, k, :], start=k == 0, stop=k == 1)
                last.then_inc(L3f_matmul_done, 1)
                pe.wait_ge(L3f_vector_done, 61*b + 52)
                for k in range(2):
                    last = pe.matmul(ps0[:, 2, 0:256], unT0[:, k, :], w_qkv3[:, k, 512:768], start=k == 0, stop=k == 1)
                last.then_inc(L3f_matmul_done, 1)
                pe.wait_ge(L3f_vector_done, 61*b + 53)
                for k in range(2):
                    last = pe.matmul(ps1[:, 2, 0:256], unT1[:, k, :], w_qkv3[:, k, 512:768], start=k == 0, stop=k == 1)
                last.then_inc(L3f_matmul_done, 1)
                pe.wait_ge(L3f_vector_done, 61*b + 64)
                pe.matmul(ps0[:, 1, :], qT_0[:, 0, :], kM3_0[:, 0, 0:4, :], start=True, stop=True).then_inc(L3f_matmul_done, 1)
                pe.wait_ge(L3f_vector_done, 61*b + 65)
                pe.matmul(ps1[:, 1, :], qT_1[:, 0, :], kM3_1[:, 0, 0:4, :], start=True, stop=True).then_inc(L3f_matmul_done, 1)
                pe.wait_ge(L3f_vector_done, 61*b + 66)
                pe.matmul(ps0[:, 1, :], qT_0[:, 0, :], kM3_0[:, 0, 4:8, :], start=True, stop=True)
                pe.wait_ge(L3f_vector_done, 61*b + 68)
                pe.matmul(ps1[:, 1, :], qT_1[:, 0, :], kM3_1[:, 0, 4:8, :], start=True, stop=True)
                pe.wait_ge(L3f_scalar_done, 44*b + 49)
                for i in range(4):
                    last = pe.transpose(ps0[:, 2, 128 * i:128 * i + 128], S_0[:, i, :], ident[:, :])
                last.then_inc(L3f_matmul_done, 1)
                pe.wait_ge(L3f_vector_done, 61*b + 72)
                pe.matmul(ps0[:, 1, :], qT_0[:, 1, :], kM3_0[:, 1, 0:4, :], start=True, stop=True)
                pe.wait_ge(L3f_scalar_done, 44*b + 50)
                for i in range(4):
                    last = pe.transpose(ps1[:, 2, 128 * i:128 * i + 128], S_1[:, i, :], ident[:, :])
                last.then_inc(L3f_matmul_done, 1)
                pe.wait_ge(L3f_scalar_done, 44*b + 51)
                for i in range(4):
                    last = pe.matmul(ps0[:, 3, 17 * i:17 * i + 17], PT_0[:, i, :], v_0[:, 0 + i, :], start=True, stop=True)
                last.then_inc(L3f_matmul_done, 1)
                pe.wait_ge(L3f_vector_done, 61*b + 75)
                pe.matmul(ps1[:, 1, :], qT_1[:, 1, :], kM3_1[:, 1, 0:4, :], start=True, stop=True)
                pe.wait_ge(L3f_scalar_done, 44*b + 52)
                for i in range(4):
                    last = pe.transpose(ps0[:, 2, 128 * i:128 * i + 128], S_0[:, i, :], ident[:, :])
                last.then_inc(L3f_matmul_done, 1)
                pe.wait_ge(L3f_scalar_done, 44*b + 53)
                for i in range(4):
                    last = pe.matmul(ps1[:, 3, 17 * i:17 * i + 17], PT_1[:, i, :], v_1[:, 0 + i, :], start=True, stop=True)
                last.then_inc(L3f_matmul_done, 1)
                pe.wait_ge(L3f_vector_done, 61*b + 79)
                pe.matmul(ps0[:, 1, :], qT_0[:, 1, :], kM3_0[:, 1, 4:8, :], start=True, stop=True)
                pe.wait_ge(L3f_scalar_done, 44*b + 54)
                for i in range(4):
                    last = pe.transpose(ps1[:, 2, 128 * i:128 * i + 128], S_1[:, i, :], ident[:, :])
                last.then_inc(L3f_matmul_done, 1)
                pe.wait_ge(L3f_scalar_done, 44*b + 55)
                for i in range(4):
                    last = pe.matmul(ps0[:, 3, 17 * i:17 * i + 17], PT_0[:, i, :], v_0[:, 4 + i, :], start=True, stop=True)
                last.then_inc(L3f_matmul_done, 1)
                pe.wait_ge(L3f_vector_done, 61*b + 83)
                pe.matmul(ps1[:, 1, :], qT_1[:, 1, :], kM3_1[:, 1, 4:8, :], start=True, stop=True)
                pe.wait_ge(L3f_scalar_done, 44*b + 56)
                for i in range(4):
                    last = pe.transpose(ps0[:, 2, 128 * i:128 * i + 128], S_0[:, i, :], ident[:, :])
                last.then_inc(L3f_matmul_done, 1)
                pe.wait_ge(L3f_scalar_done, 44*b + 57)
                for i in range(4):
                    last = pe.matmul(ps1[:, 3, 17 * i:17 * i + 17], PT_1[:, i, :], v_1[:, 4 + i, :], start=True, stop=True)
                last.then_inc(L3f_matmul_done, 1)
                pe.wait_ge(L3f_scalar_done, 44*b + 58)
                for i in range(4):
                    last = pe.transpose(ps1[:, 2, 128 * i:128 * i + 128], S_1[:, i, :], ident[:, :])
                last.then_inc(L3f_matmul_done, 1)
                pe.wait_ge(L3f_scalar_done, 44*b + 59)
                for i in range(4):
                    last = pe.matmul(ps0[:, 3, 17 * i:17 * i + 17], PT_0[:, i, :], v_0[:, 8 + i, :], start=True, stop=True)
                last.then_inc(L3f_matmul_done, 1)
                pe.wait_ge(L3f_vector_done, 61*b + 90)
                pe.wait_ge(L3f_scalar_done, 44*b + 60)
                for i in range(4):
                    last = pe.matmul(ps1[:, 3, 17 * i:17 * i + 17], PT_1[:, i, :], v_1[:, 8 + i, :], start=True, stop=True)
                last.then_inc(L3f_matmul_done, 1)
                pe.wait_ge(L3f_scalar_done, 44*b + 61)
                for i in range(4):
                    last = pe.transpose(ps0[:, 2, 128 * i:128 * i + 128], S_0[:, i, :], ident[:, :])
                last.then_inc(L3f_matmul_done, 1)
                pe.wait_ge(L3f_scalar_done, 44*b + 62)
                for i in range(4):
                    last = pe.transpose(ps1[:, 2, 128 * i:128 * i + 128], S_1[:, i, :], ident[:, :])
                last.then_inc(L3f_matmul_done, 1)
                pe.wait_ge(L3f_vector_done, 61*b + 97)
                pe.wait_ge(L3f_scalar_done, 44*b + 63)
                for i in range(4):
                    last = pe.matmul(ps0[:, 3, 17 * i:17 * i + 17], PT_0[:, i, :], v_0[:, 12 + i, :], start=True, stop=True)
                last.then_inc(L3f_matmul_done, 1)
                pe.wait_ge(L3f_vector_done, 61*b + 98)
                pe.wait_ge(L3f_scalar_done, 44*b + 64)
                for i in range(4):
                    last = pe.matmul(ps1[:, 3, 17 * i:17 * i + 17], PT_1[:, i, :], v_1[:, 12 + i, :], start=True, stop=True)
                last.then_inc(L3f_matmul_done, 1)
                pe.wait_ge(L3f_vector_done, 61*b + 100)
                for k in range(2):
                    last = pe.transpose(ps0[:, 0, 128 * k:128 * k + 128], ao_0[:, 128 * k:128 * k + 128], ident[:, :])
                last.then_inc(L3f_matmul_done, 1)
                pe.wait_ge(L3f_vector_done, 61*b + 102)
                for k in range(2):
                    last = pe.transpose(ps1[:, 0, 128 * k:128 * k + 128], ao_1[:, 128 * k:128 * k + 128], ident[:, :])
                last.then_inc(L3f_matmul_done, 1)
                pe.wait_ge(L3f_scalar_done, 44*b + 65)
                for j in range(2):
                    for k in range(2):
                        last = pe.matmul(ps0[:, 1, 128 * j:128 * j + 128], w_o3f[:, k, 128 * j:128 * j + 128], unT0[:, k, :], start=k == 0, stop=k == 1)
                last.then_inc(L3f_matmul_done, 1)
                pe.wait_ge(L3f_scalar_done, 44*b + 66)
                for j in range(2):
                    for k in range(2):
                        last = pe.matmul(ps1[:, 1, 128 * j:128 * j + 128], w_o3f[:, k, 128 * j:128 * j + 128], unT1[:, k, :], start=k == 0, stop=k == 1)
                last.then_inc(L3f_matmul_done, 1)
                pe.wait_ge(L3f_scalar_done, 44*b + 67)
                for k in range(2):
                    last = pe.matmul(ps0[0:16, 2, 0:128], w_A[:, k, :], qT_0[:, k, :], start=k == 0, stop=k == 1)
                last.then_inc(L3f_matmul_done, 1)
                for k in range(2):
                    last = pe.transpose(ps0[:, 0, 128 * k:128 * k + 128], un0[:, 128 * k:128 * k + 128], ident[:, :])
                last.then_inc(L3f_matmul_done, 1)
                for k in range(2):
                    last = pe.transpose(ps1[:, 0, 128 * k:128 * k + 128], un1[:, 128 * k:128 * k + 128], ident[:, :])
                last.then_inc(L3f_matmul_done, 1)
                pe.wait_ge(L3f_scalar_done, 44*b + 68)
                for k in range(2):
                    last = pe.matmul(ps1[0:16, 2, 0:128], w_A[:, k, :], qT_1[:, k, :], start=k == 0, stop=k == 1)
                last.then_inc(L3f_matmul_done, 1)
                pe.wait_ge(L3f_vector_done, 61*b + 103)
                pe.wait_ge(L3f_scalar_done, 44*b + 69)
                for k in range(2):
                    last = pe.matmul(ps0[0:16, 2, 128:256], w_A[:, k, :], unT0[:, k, :], start=k == 0, stop=k == 1)
                last.then_inc(L3f_matmul_done, 1)
                for k in range(2):
                    pe.matmul(psf0[:, 0:128], w_in3[:, k, 0:128], unT0[:, k, :], start=k == 0, stop=False)
                pe.wait_ge(L3f_vector_done, 61*b + 104)
                pe.wait_ge(L3f_scalar_done, 44*b + 71)
                for k in range(2):
                    last = pe.matmul(ps1[0:16, 2, 128:256], w_A[:, k, :], unT1[:, k, :], start=k == 0, stop=k == 1)
                last.then_inc(L3f_matmul_done, 1)
                for k in range(2):
                    pe.matmul(psf1[:, 0:128], w_in3[:, k, 0:128], unT1[:, k, :], start=k == 0, stop=False)
                for k in range(2):
                    pe.matmul(psf0[:, 512:640], w_in3[:, k, 512:640], unT0[:, k, :], start=k == 0, stop=False)
                for k in range(2):
                    pe.matmul(psf1[:, 512:640], w_in3[:, k, 512:640], unT1[:, k, :], start=k == 0, stop=False)
                pe.wait_ge(L3f_vector_done, 61*b + 110)
                pe.matmul(psf0[:, 0:128], w_B[0:16, 0:128], hA_0[0:16, :], start=False, stop=True)
                pe.matmul(psf0[:, 512:640], w_B[0:16, 512:640], hA_0[0:16, :], start=False, stop=True)
                for k in range(2):
                    pe.matmul(psf0[:, 128:256], w_in3[:, k, 128:256], unT0[:, k, :], start=k == 0, stop=False)
                pe.wait_ge(L3f_vector_done, 61*b + 112)
                pe.matmul(psf1[:, 0:128], w_B[0:16, 0:128], hA_1[0:16, :], start=False, stop=True)
                pe.matmul(psf1[:, 512:640], w_B[0:16, 512:640], hA_1[0:16, :], start=False, stop=True)
                for k in range(2):
                    pe.matmul(psf1[:, 128:256], w_in3[:, k, 128:256], unT1[:, k, :], start=k == 0, stop=False)
                for k in range(2):
                    pe.matmul(psf0[:, 640:768], w_in3[:, k, 640:768], unT0[:, k, :], start=k == 0, stop=False)
                for k in range(2):
                    pe.matmul(psf1[:, 640:768], w_in3[:, k, 640:768], unT1[:, k, :], start=k == 0, stop=False)
                for j in range(8):
                    for k in range(2):
                        pe.matmul(psf0[:, 1024 + 128 * j:1152 + 128 * j], w_up3[:, k, 128 * j:128 * j + 128], unT0[:, k, :], start=k == 0, stop=k == 1)
                for j in range(8):
                    for k in range(2):
                        pe.matmul(psf1[:, 1024 + 128 * j:1152 + 128 * j], w_up3[:, k, 128 * j:128 * j + 128], unT1[:, k, :], start=k == 0, stop=k == 1)
                pe.matmul(psf0[:, 128:256], w_B[0:16, 128:256], hA_0[0:16, :], start=False, stop=True)
                pe.matmul(psf1[:, 128:256], w_B[0:16, 128:256], hA_1[0:16, :], start=False, stop=True)
                pe.matmul(psf0[:, 640:768], w_B[0:16, 640:768], hA_0[0:16, :], start=False, stop=True)
                pe.matmul(psf1[:, 640:768], w_B[0:16, 640:768], hA_1[0:16, :], start=False, stop=True)
                for k in range(2):
                    pe.matmul(psf0[:, 256:384], w_in3[:, k, 256:384], unT0[:, k, :], start=k == 0, stop=False)
                for k in range(2):
                    pe.matmul(psf1[:, 256:384], w_in3[:, k, 256:384], unT1[:, k, :], start=k == 0, stop=False)
                for k in range(2):
                    pe.matmul(psf0[:, 768:896], w_in3[:, k, 768:896], unT0[:, k, :], start=k == 0, stop=False)
                for k in range(2):
                    pe.matmul(psf1[:, 768:896], w_in3[:, k, 768:896], unT1[:, k, :], start=k == 0, stop=False)
                pe.matmul(psf0[:, 256:384], w_B[0:16, 256:384], hA_0[0:16, :], start=False, stop=True)
                pe.matmul(psf1[:, 256:384], w_B[0:16, 256:384], hA_1[0:16, :], start=False, stop=True)
                pe.matmul(psf0[:, 768:896], w_B[0:16, 768:896], hA_0[0:16, :], start=False, stop=True)
                pe.matmul(psf1[:, 768:896], w_B[0:16, 768:896], hA_1[0:16, :], start=False, stop=True)
                for k in range(2):
                    pe.matmul(psf0[:, 384:512], w_in3[:, k, 384:512], unT0[:, k, :], start=k == 0, stop=False)
                for k in range(2):
                    pe.matmul(psf1[:, 384:512], w_in3[:, k, 384:512], unT1[:, k, :], start=k == 0, stop=False)
                for k in range(2):
                    pe.matmul(psf0[:, 896:1024], w_in3[:, k, 896:1024], unT0[:, k, :], start=k == 0, stop=False)
                for k in range(2):
                    pe.matmul(psf1[:, 896:1024], w_in3[:, k, 896:1024], unT1[:, k, :], start=k == 0, stop=False)
                pe.matmul(psf0[:, 384:512], w_B[0:16, 384:512], hA_0[0:16, :], start=False, stop=True)
                pe.matmul(psf1[:, 384:512], w_B[0:16, 384:512], hA_1[0:16, :], start=False, stop=True)
                pe.matmul(psf0[:, 896:1024], w_B[0:16, 896:1024], hA_0[0:16, :], start=False, stop=True).then_inc(L3f_matmul_done, 1)
                pe.matmul(psf1[:, 896:1024], w_B[0:16, 896:1024], hA_1[0:16, :], start=False, stop=True).then_inc(L3f_matmul_done, 1)
                pe.wait_ge(L3f_vector_done, 61*b + 113)
                for k in range(8):
                    last = pe.matmul(ps0[:, 0, 0:256], m3_0[:, 128 * k:128 * k + 128], w_dn3[:, k, :], start=k == 0, stop=k == 7)
                last.then_inc(L3f_matmul_done, 1)
                pe.wait_ge(L3f_vector_done, 61*b + 114)
                for k in range(8):
                    last = pe.matmul(ps1[:, 0, 0:256], m3_1[:, 128 * k:128 * k + 128], w_dn3[:, k, :], start=k == 0, stop=k == 7)
                last.then_inc(L3f_matmul_done, 1)
                pe.wait_ge(L3f_vector_done, 61*b + 119)
                for k in range(2):
                    last = pe.transpose(ps0[:, 0, 128 * k:128 * k + 128], un0[:, 128 * k:128 * k + 128], ident[:, :])
                last.then_inc(L3f_matmul_done, 1)
                pe.wait_ge(L3f_vector_done, 61*b + 120)
                for k in range(2):
                    last = pe.transpose(ps1[:, 0, 128 * k:128 * k + 128], un1[:, 128 * k:128 * k + 128], ident[:, :])
                last.then_inc(L3f_matmul_done, 1)


def feature_rows(w):
    return w.reshape(w.shape[0] // 128, 128, w.shape[1]).transpose(1, 0, 2)


def per_feature(v):
    return v.reshape(-1, 128).T


def mamba_columns(w):
    x_rows = np.repeat(w[256:320].reshape(2, 1, 32, 256), 4, axis=1).reshape(256, 256)
    return np.concatenate([w[0:256], x_rows, w[320:384], w[320:384], w[384:640], w[640:768]]).T


def per_query_head(w):
    return np.repeat(w.reshape(8, 1, 8, -1), 4, axis=1).reshape(256, -1) if w.ndim > 1 else np.repeat(w.reshape(8, 1, 8), 4, axis=1).reshape(256)


def head_rows(w):
    return w.reshape(4, 8, 8, -1).transpose(1, 0, 2, 3).reshape(256, -1)


def expert_columns(s1, sg, w1, wg):
    parts = [s1, sg]
    for e in range(w1.shape[0]):
        parts += [w1[e], wg[e]]
    return feature_rows(np.concatenate(parts, axis=1))


def kernel(x, ctx_2048, L0_attn_in_proj_w, L0_attn_dt_proj_w, L0_attn_dt_proj_b, L0_attn_A_log, L0_attn_D_param, L0_attn_out_proj_w, L0_attn_gate_w, L0_attn_up_w, L0_attn_down_w, L0_attn_norm1_w, L0_attn_norm2_w, L0_xattn_theta_w, L0_xattn_theta_b, L0_xattn_phi_w, L0_xattn_phi_b, L0_xattn_g_w, L0_xattn_g_b, L0_xattn_ln_gamma, L0_xattn_ln_beta, L0_xattn_out_w, L0_xattn_out_b, L0_ffn_gate_w, L0_ffn_gate_b, L0_ffn_expert_w, L0_ffn_expert_b, L1_attn_Wq, L1_attn_Wk, L1_attn_Wv, L1_attn_Wo, L1_xattn_decay, L1_xattn_W_in, L1_xattn_b_in, L1_xattn_W_out, L1_xattn_b_out, L1_xattn_gamma, L1_xattn_beta, L1_ffn_W1, L1_ffn_Wg, L1_ffn_W2, L1_ffn_Ws1, L1_ffn_Wsg, L1_ffn_Ws2, L1_ffn_gate_w, L1_ffn_gate_b, L1_ffn_biases, L2_attn_W_qkv, L2_attn_W_o, L2_xattn_ln_w, L2_xattn_ln_b, L2_xattn_wq, L2_xattn_wq_scale, L2_xattn_q_in_scale, L2_xattn_wqx, L2_xattn_wqx_scale, L2_xattn_qx_in_scale, L2_xattn_wk, L2_xattn_wk_scale, L2_xattn_k_in_scale, L2_xattn_wv, L2_xattn_wv_scale, L2_xattn_v_in_scale, L2_xattn_w_kv_x, L2_xattn_qln_w, L2_xattn_qln_b, L2_xattn_kln_w, L2_xattn_kln_b, L2_xattn_qxln_w, L2_xattn_qxln_b, L2_xattn_kxln_w, L2_xattn_kxln_b, L2_xattn_wproj, L2_xattn_proj_w_scale, L2_xattn_proj_in_scale, L2_xattn_proj_smooth, L2_ffn_W_up, L2_ffn_b_up, L2_ffn_W_down, L2_ffn_b_down, L2_ffn_W_q, L2_ffn_keys, L2_ffn_down_embed, L2_ffn_up_embed, L3_attn_Wq, L3_attn_bq, L3_attn_Wk, L3_attn_bk, L3_attn_Wv, L3_attn_bv, L3_attn_Wo, L3_attn_bo, L3_xattn_Wq, L3_xattn_Wg, L3_xattn_bg, L3_xattn_Wkv, L3_xattn_Wo, L3_ffn_ln1_w, L3_ffn_ln2_w, L3_ffn_Wq, L3_ffn_Wk, L3_ffn_Wv, L3_ffn_Wo, L3_ffn_A, L3_ffn_B, L3_ffn_W_in_base, L3_ffn_W_up_base, L3_ffn_W_down):

    import concourse.bacc as _bacc
    from concourse.bass_utils import run_bass_kernel_spmd as _run

    weights = {
        'x_d': x.transpose(1, 0, 2),
        'ctx_d': ctx_2048.transpose(1, 0, 2),
        'ctxT_d': ctx_2048.reshape(1024, 2, 128).transpose(2, 1, 0),
        'w_in_d': feature_rows(mamba_columns(L0_attn_in_proj_w)),
        'w_dt_d': L0_attn_dt_proj_w.T,
        'b_dt_d': per_feature(L0_attn_dt_proj_b),
        'A_d': L0_attn_A_log.reshape(2, 128, 32).transpose(1, 0, 2),
        'Dp_d': per_feature(L0_attn_D_param),
        'w_mo_d': feature_rows(L0_attn_out_proj_w.T),
        'w_gate_d': feature_rows(L0_attn_gate_w.T),
        'w_up_d': feature_rows(L0_attn_up_w.T),
        'w_dn_d': feature_rows(L0_attn_down_w.T[0:640]),
        'w_dn_rest_d': L0_attn_down_w.T[640:704],
        'n1_d': L0_attn_norm1_w.reshape(1, 256),
        'n2_d': L0_attn_norm2_w.reshape(1, 256),
        'w_th_d': L0_xattn_theta_w.T,
        'w_ph_d': L0_xattn_phi_w.T,
        'w_g_d': L0_xattn_g_w.T,
        'gam0_d': L0_xattn_ln_gamma,
        'bet0_d': L0_xattn_ln_beta,
        'w_xo_d': L0_xattn_out_w.T,
        'b_th_d': L0_xattn_theta_b.reshape(64, 1),
        'b_ph_d': L0_xattn_phi_b.reshape(64, 1),
        'b_xo_d': L0_xattn_out_b.reshape(128, 1),
        'b_g_d': L0_xattn_g_b.reshape(1, 64),
        'w_e0_d': L0_ffn_expert_w.transpose(1, 0, 2).reshape(2, 128, 2048).transpose(1, 0, 2),
        'b_e0_d': L0_ffn_expert_b.reshape(1, 2048),
        'w_gt0_d': feature_rows(L0_ffn_gate_w),
        'b_gt0_d': L0_ffn_gate_b.reshape(1, 8),
        'w_qkv1_d': feature_rows(np.concatenate([L1_attn_Wq, L1_attn_Wk, L1_attn_Wv]).T),
        'w_o1_d': feature_rows(L1_attn_Wo.T),
        'w_i1_d': feature_rows(L1_xattn_W_in.T),
        'w_oo1_d': feature_rows(L1_xattn_W_out.T),
        'b_i1_d': per_feature(L1_xattn_b_in),
        'b_oo1_d': L1_xattn_b_out.reshape(1, 256),
        'gam1_d': L1_xattn_gamma.reshape(1, 256),
        'bet1_d': L1_xattn_beta.reshape(1, 256),
        'dec_d': L1_xattn_decay.reshape(1, 1),
        'w_gu1_d': expert_columns(L1_ffn_Ws1, L1_ffn_Wsg, L1_ffn_W1, L1_ffn_Wg),
        'w_dn1_d': np.concatenate([L1_ffn_Ws2[None], L1_ffn_W2]).reshape(8, 2, 128, 256).transpose(2, 0, 1, 3),
        'w_gt1_d': feature_rows(L1_ffn_gate_w),
        'b_gt1_d': L1_ffn_gate_b.reshape(1, 7),
        'bi1_d': L1_ffn_biases.reshape(1, 7),
        'w_qkv2_d': feature_rows(L2_attn_W_qkv),
        'w_o2_d': feature_rows(L2_attn_W_o),
        'w_q2_d': feature_rows(L2_xattn_wq.T),
        'w_qx2_d': feature_rows(L2_xattn_wqx.T),
        'w_k2_d': feature_rows(L2_xattn_wk.T),
        'w_v2_d': feature_rows(L2_xattn_wv.T),
        'w_kv2_d': feature_rows(L2_xattn_w_kv_x.T),
        'w_p2_d': feature_rows(L2_xattn_wproj.T),
        'insc_d': np.stack([L2_xattn_q_in_scale, L2_xattn_qx_in_scale, L2_xattn_k_in_scale, L2_xattn_v_in_scale]).reshape(4, 2, 128).transpose(2, 0, 1),
        'lnb2_d': np.stack([L2_xattn_ln_w, L2_xattn_ln_b]).reshape(1, 2, 256),
        'nw2_d': np.stack([np.stack([L2_xattn_qln_w, L2_xattn_qln_b]), np.stack([L2_xattn_qxln_w, L2_xattn_qxln_b]), np.stack([L2_xattn_kln_w, L2_xattn_kln_b]), np.stack([L2_xattn_kxln_w, L2_xattn_kxln_b])]).transpose(2, 0, 1),
        'smo_d': per_feature(L2_xattn_proj_smooth),
        'wsc_d': np.stack([L2_xattn_wq_scale, L2_xattn_wqx_scale, L2_xattn_wk_scale, L2_xattn_wv_scale, L2_xattn_proj_w_scale, L2_xattn_proj_in_scale]).reshape(1, 6),
        'w_u2_d': feature_rows(L2_ffn_W_up.T),
        'b_u2_d': per_feature(L2_ffn_b_up),
        'w_d2_d': feature_rows(L2_ffn_W_down.T),
        'b_d2_d': L2_ffn_b_down.reshape(128, 1),
        'w_q2f_d': L2_ffn_W_q.T,
        'keys_even_d': L2_ffn_keys[0::2].transpose(3, 2, 0, 1).reshape(64, 8, 45),
        'keys_odd_d': L2_ffn_keys[1::2].transpose(3, 2, 0, 1).reshape(64, 8, 45),
        'de_d': L2_ffn_down_embed[0:2025].T,
        'ue_d': feature_rows(L2_ffn_up_embed[0:1920]),
        'ue_rest_d': L2_ffn_up_embed[1920:2025],
        'w_q3_d': feature_rows(L3_attn_Wq.T),
        'w_kr3_d': feature_rows(per_query_head(L3_attn_Wk).T),
        'w_v3_d': feature_rows(L3_attn_Wv.T),
        'w_o3_d': feature_rows(head_rows(L3_attn_Wo.T)),
        'b_q3_d': per_feature(L3_attn_bq),
        'b_k3_d': per_feature(per_query_head(L3_attn_bk)),
        'b_v3_d': L3_attn_bv.reshape(1, 64),
        'b_o3_d': L3_attn_bo.reshape(1, 256),
        'w_qg3_d': feature_rows(np.concatenate([L3_xattn_Wq, L3_xattn_Wg]).T),
        'w_kv3_d': feature_rows(L3_xattn_Wkv.T),
        'w_ox3_d': feature_rows(L3_xattn_Wo.T),
        'b_gx3_d': L3_xattn_bg.reshape(1, 256),
        'w_qkv3_d': feature_rows(np.concatenate([L3_ffn_Wq, L3_ffn_Wk, L3_ffn_Wv]).T),
        'w_o3f_d': feature_rows(L3_ffn_Wo.T),
        'w_A_d': feature_rows(L3_ffn_A),
        'w_B_d': L3_ffn_B,
        'w_in3_d': feature_rows(L3_ffn_W_in_base.T),
        'w_up3_d': feature_rows(L3_ffn_W_up_base.T),
        'w_dn3_d': feature_rows(L3_ffn_W_down.T),
        'l1w_d': L3_ffn_ln1_w.reshape(1, 256),
        'l2w_d': L3_ffn_ln2_w.reshape(1, 256),
    }
    nc = _bacc.Bacc("TRN2", target_bir_lowering=False, num_devices=1)
    arrays, dram = {}, {}
    for name in _WEIGHTS:
        a = np.ascontiguousarray(weights[name])
        arrays[name] = a
        dram[name] = nc.dram_tensor(name, a.shape, mybir.dt.from_np(a.dtype), kind="ExternalInput").ap()
    out = nc.dram_tensor("out_d", (128, 8, 256), F32, kind="ExternalOutput").ap()
    build_program(nc, dram, out)
    r = _run(nc, [arrays], core_ids=[0])
    return np.ascontiguousarray(r.results[0]["out_d"].transpose(1, 0, 2))
```
